# Optimizing a Trainium2 kernel written in Bass

```python
import numpy as np
import jax
import jax.numpy as jnp

def _softmax(x, axis=-1):
    return jax.nn.softmax(x, axis=axis)

def _gelu(x):
    return jax.nn.gelu(x, approximate=True)

def _silu(x):
    return jax.nn.silu(x)

def _sigmoid(x):
    return jax.nn.sigmoid(x)

def _layernorm(x, axis=-1, eps=1e-05):
    m = jnp.mean(x, axis=axis, keepdims=True)
    v = jnp.var(x, axis=axis, keepdims=True)
    return (x - m) / jnp.sqrt(v + eps)

def _scatter_add(tgt, idx, src, axis=0):
    return tgt.at[idx].add(src)

def _segment_sum(src, seg, n):
    return jax.ops.segment_sum(src, seg, n)
kernel_name = 'mk_adaln_attn_ffn_d4_seqx_r8_e0e7a2'

def setup_inputs(seed: int=0):
    np.random.seed(seed)
    _w = jnp.asarray

    def _rec_inputs():
        import jax
        import jax.numpy as jnp
        _rk = jax.random.key(seed)
        x = -0.0002928 + 1 * jax.random.normal(jax.random.fold_in(_rk, 1), (2, 512, 128), jnp.float32)
        _lenS = 512 - jax.random.randint(jax.random.fold_in(_rk, 7), (2,), 0, max(1, 512 // 4) + 1, jnp.int32)
        _lenS2 = 512 - jax.random.randint(jax.random.fold_in(_rk, 8), (2,), 0, max(1, 512 // 4) + 1, jnp.int32)
        cond_64 = -0.0184271 + 1.00439 * jax.random.normal(jax.random.fold_in(_rk, 12), (2, 64), jnp.float32)
        fside_16xSxS_0 = -5.72187e-05 + 0.999849 * jax.random.normal(jax.random.fold_in(_rk, 13), (16, 512, 512), jnp.float32)
        _validS = jnp.arange(512)[None, :] < _lenS[:, None]
        _validS2 = jnp.arange(512)[None, :] < _lenS2[:, None]
        _causal = jnp.tril(jnp.ones((512, 512), dtype=bool))
        mask_BxS_bf1 = jnp.ones((2, 512), dtype=bool)
        mask_BxS_bk0 = jnp.logical_not(jnp.broadcast_to(_validS[:, :], (2, 512)))
        return (x, cond_64, fside_16xSxS_0, mask_BxS_bf1, mask_BxS_bk0)
    x, cond_64, fside_16xSxS_0, mask_BxS_bf1, mask_BxS_bk0 = _rec_inputs()

    def _L0_cond_setup():
        import jax, jax.numpy as jnp
        import numpy as np
        DIM = 128
        HEADS = 16
        DIM_HEAD = 64
        SCALE = 8.0

        def ln(x, g, eps=1e-05):
            mean = x.mean(axis=-1, keepdims=True)
            var = ((x - mean) ** 2).mean(axis=-1, keepdims=True)
            return (x - mean) * jax.lax.rsqrt(var + eps) * g

        def l2norm(t):
            n = jnp.maximum(jnp.linalg.norm(t, axis=-1, keepdims=True), 1e-12)
            return t / n

        def rel_pos_bias(n, w0, b0, g0, w1, b1, g1, w2, b2, dtype):
            pos = jnp.arange(-n + 1, n, dtype=dtype)[:, None]
            h = jax.nn.silu(ln(pos @ w0 + b0, g0))
            h = jax.nn.silu(ln(h @ w1 + b1, g1))
            h = h @ w2 + b2
            i = jnp.arange(n)
            idx = i[:, None] - i[None, :] + n - 1
            bias = h[idx]
            return jnp.transpose(bias, (2, 0, 1))
        key = jax.random.key(seed)
        ks = jax.random.split(key, 16)
        b, n = (2, 256)
        inner = HEADS * DIM_HEAD
        s = 0.02
        return {'x': jax.random.normal(ks[0], (b, n, DIM), jnp.float32), 'mask': jnp.ones((b, n), dtype=bool), 'g_norm': jnp.ones((DIM,), jnp.float32), 'Wq': jax.random.normal(ks[1], (DIM, inner), jnp.float32) * s, 'Wkv': jax.random.normal(ks[2], (DIM, 2 * DIM_HEAD), jnp.float32) * s, 'q_scale': jnp.ones((DIM_HEAD,), jnp.float32), 'k_scale': jnp.ones((DIM_HEAD,), jnp.float32), 'null_kv': jax.random.normal(ks[3], (2, DIM_HEAD), jnp.float32), 'null_attn_bias': jax.random.normal(ks[4], (HEADS,), jnp.float32), 'w0': jax.random.normal(ks[5], (1, DIM), jnp.float32) * s, 'b0': jnp.zeros((DIM,), jnp.float32), 'g0': jnp.ones((DIM,), jnp.float32), 'w1': jax.random.normal(ks[6], (DIM, DIM), jnp.float32) * s, 'b1': jnp.zeros((DIM,), jnp.float32), 'g1': jnp.ones((DIM,), jnp.float32), 'w2': jax.random.normal(ks[7], (DIM, HEADS), jnp.float32) * s, 'b2': jnp.zeros((HEADS,), jnp.float32), 'Wout': jax.random.normal(ks[8], (inner, DIM), jnp.float32) * s, 'g_out': jnp.ones((DIM,), jnp.float32)}
    _L0_cond_all = _L0_cond_setup()
    _L0_cond_in = {k: v for k, v in _L0_cond_all.items() if k in ('g_norm', 'Wq', 'Wkv', 'q_scale', 'k_scale', 'null_attn_bias', 'w0', 'b0', 'g0', 'w1', 'b1', 'g1', 'w2', 'b2', 'Wout', 'g_out')}
    del _L0_cond_all

    def _L0_attn_setup():
        import math
        import jax, jax.numpy as jnp
        import numpy as np
        D_MODEL = 128
        HEADS = 16
        DH = D_MODEL // HEADS
        MAX_REL = 128
        LN_EPS = 1e-05

        def _layernorm(x, gamma, beta):
            mu = jnp.mean(x, axis=-1, keepdims=True)
            var = jnp.mean(jnp.square(x - mu), axis=-1, keepdims=True)
            return (x - mu) * jax.lax.rsqrt(var + LN_EPS) * gamma + beta
        key = jax.random.key(seed)
        ks = jax.random.split(key, 6)
        B, T = (4, 256)
        scale = 1.0 / math.sqrt(D_MODEL)
        x = jax.random.normal(ks[0], (B, T, D_MODEL), dtype=jnp.float32)
        Wq = jax.random.normal(ks[1], (D_MODEL, D_MODEL), dtype=jnp.float32) * scale
        Wk = jax.random.normal(ks[2], (D_MODEL, D_MODEL), dtype=jnp.float32) * scale
        Wv = jax.random.normal(ks[3], (D_MODEL, D_MODEL), dtype=jnp.float32) * scale
        Wo = jax.random.normal(ks[4], (D_MODEL, D_MODEL), dtype=jnp.float32) * scale
        rel = jnp.tile(jnp.linspace(0.0, -2.0, MAX_REL + 1, dtype=jnp.float32)[None, :], (HEADS, 1))
        ln_gamma = jnp.ones((D_MODEL,), dtype=jnp.float32)
        ln_beta = jnp.zeros((D_MODEL,), dtype=jnp.float32)
        return {'x': x, 'Wq': Wq, 'Wk': Wk, 'Wv': Wv, 'Wo': Wo, 'rel': rel, 'ln_gamma': ln_gamma, 'ln_beta': ln_beta}
    _L0_attn_all = _L0_attn_setup()
    _L0_attn_in = {k: v for k, v in _L0_attn_all.items() if k in ('Wq', 'Wk', 'Wv', 'Wo', 'rel', 'ln_gamma', 'ln_beta')}
    del _L0_attn_all

    def _L0_cond2_setup():
        import jax, jax.numpy as jnp
        import numpy as np
        B, N, DIM, H, DH = (2, 256, 128, 16, 64)
        INNER = H * DH
        EPS = 1e-05

        def layernorm(x, g):
            mean = jnp.mean(x, axis=-1, keepdims=True)
            var = jnp.var(x, axis=-1, keepdims=True)
            return (x - mean) * jax.lax.rsqrt(var + EPS) * g
        key = jax.random.key(seed)
        ks = jax.random.split(key, 10)
        x = jax.random.normal(ks[0], (B, N, DIM), dtype=jnp.float32)
        attn_bias = jax.random.normal(ks[1], (H, N, N), dtype=jnp.float32)
        mask = jax.random.randint(ks[2], (B, N), 0, 2).astype(bool)
        g_in = jnp.ones((DIM,), dtype=jnp.float32)
        null_attn_bias = jax.random.normal(ks[3], (H,), dtype=jnp.float32)
        null_kv = jax.random.normal(ks[4], (2, DH), dtype=jnp.float32)
        Wq = jax.random.normal(ks[5], (DIM, INNER), dtype=jnp.float32) * 0.02
        Wkv = jax.random.normal(ks[6], (DIM, 2 * DH), dtype=jnp.float32) * 0.02
        Wo = jax.random.normal(ks[7], (INNER, DIM), dtype=jnp.float32) * 0.02
        g_out = jnp.ones((DIM,), dtype=jnp.float32)
        return {'x': x, 'attn_bias': attn_bias, 'mask': mask, 'g_in': g_in, 'null_attn_bias': null_attn_bias, 'null_kv': null_kv, 'Wq': Wq, 'Wkv': Wkv, 'Wo': Wo, 'g_out': g_out}
    _L0_cond2_all = _L0_cond2_setup()
    _L0_cond2_in = {k: v for k, v in _L0_cond2_all.items() if k in ('g_in', 'null_attn_bias', 'Wq', 'Wkv', 'Wo', 'g_out')}
    del _L0_cond2_all

    def _L0_ffn_setup():
        import jax, jax.numpy as jnp
        import numpy as np
        E = 8
        K = 2
        S = 1
        THRESHOLD = 0.7
        NORM_TOPK = True
        H = 128
        F = 128
        B, SEQ = (2, 128)
        key = jax.random.key(seed)
        k1, k2, k3, k4, k5 = jax.random.split(key, 5)
        hidden_states = jax.random.normal(k1, (B, SEQ, H), jnp.float32)
        gate_weight = jax.random.normal(k2, (E, H), jnp.float32) * 0.02
        gate_up_proj = jax.random.normal(k3, (E, 2 * F, H), jnp.float32) * 0.02
        down_proj = jax.random.normal(k4, (E, H, F), jnp.float32) * 0.02
        sim = jax.random.uniform(k5, (E, E), jnp.float32)
        sim = (sim + sim.T) / 2.0
        sim = sim.at[jnp.arange(E), jnp.arange(E)].set(1.0)
        return {'hidden_states': hidden_states, 'gate_weight': gate_weight, 'gate_up_proj': gate_up_proj, 'down_proj': down_proj, 'similarity_matrix': sim}
    _L0_ffn_all = _L0_ffn_setup()
    _L0_ffn_in = {k: v for k, v in _L0_ffn_all.items() if k in ('gate_weight', 'gate_up_proj', 'down_proj', 'similarity_matrix')}
    del _L0_ffn_all

    def _L1_cond_setup():
        import jax, jax.numpy as jnp
        import numpy as np
        B, S, H = (4, 256, 128)
        E = 8
        M = 64
        K = 2
        N_SHARED = 2
        SM = M * N_SHARED
        G = 64
        GE_TEMP = 1.0
        ALPHA = 0.001
        SEQ_AUX = True
        NORM_TOPK = True
        COS_TEMP = 0.78
        CONS_ALPHA = 0.01
        LEAKY_SLOPE = 0.01
        EPS_COS = 1e-08

        def _leaky(x):
            return jnp.where(x >= 0, x, LEAKY_SLOPE * x)

        def _moe_forward(hidden_states, g, wt, wg, w_gate, w_up, w_down, sw_gate, sw_up, sw_down):
            b, s, h = hidden_states.shape
            x = hidden_states.reshape(-1, h)
            T = x.shape[0]
            logits_h = x @ wt.T
            logits_g = g @ wg.T
            logits_g = jnp.repeat(logits_g, s, axis=0)
            logits = (logits_h + logits_g / GE_TEMP) / (1.0 + 1.0 / GE_TEMP)
            scores = jax.nn.softmax(logits, axis=-1)
            topk_w, topk_idx = jax.lax.top_k(scores, K)
            if K > 1 and NORM_TOPK:
                topk_w = topk_w / (topk_w.sum(-1, keepdims=True) + 1e-20)
            onehot = jax.nn.one_hot(topk_idx.reshape(b, s * K), E, dtype=jnp.float32)
            ce = onehot.sum(1) / (s * K / E)
            aux_loss = (ce * scores.reshape(b, s, E).mean(1)).sum(1).mean() * ALPHA
            gp = _leaky(jnp.einsum('th,ehm->etm', x, w_gate))
            up = jnp.einsum('th,ehm->etm', x, w_up)
            y_all = jnp.einsum('etm,emh->eth', gp * up, w_down)
            y_sel = y_all[topk_idx, jnp.arange(T)[:, None], :]
            y = (y_sel * topk_w[..., None]).sum(1).reshape(b, s, h)
            p = _leaky(hidden_states @ sw_gate) * (hidden_states @ sw_up) @ sw_down
            y = y + p
            num = jnp.sum(y * p, -1)
            den = jnp.maximum(jnp.linalg.norm(y, axis=-1), EPS_COS) * jnp.maximum(jnp.linalg.norm(p, axis=-1), EPS_COS)
            closs = CONS_ALPHA * jnp.mean(num / den / (1.0 + COS_TEMP))
            return (y, aux_loss + closs)
        key = jax.random.key(seed)
        ks = jax.random.split(key, 12)
        sh = 1.0 / np.sqrt(H)
        sm = 1.0 / np.sqrt(M)
        ssm = 1.0 / np.sqrt(SM)
        sg = 1.0 / np.sqrt(G)
        return {'hidden_states': jax.random.normal(ks[0], (B, S, H), jnp.float32), 'g': jax.random.normal(ks[1], (B, G), jnp.float32), 'wt': jax.random.uniform(ks[2], (E, H), jnp.float32, -sh, sh), 'wg': jax.random.uniform(ks[3], (E, G), jnp.float32, -sg, sg), 'w_gate': jax.random.uniform(ks[4], (E, H, M), jnp.float32, -sh, sh), 'w_up': jax.random.uniform(ks[5], (E, H, M), jnp.float32, -sh, sh), 'w_down': jax.random.uniform(ks[6], (E, M, H), jnp.float32, -sm, sm), 'sw_gate': jax.random.uniform(ks[7], (H, SM), jnp.float32, -sh, sh), 'sw_up': jax.random.uniform(ks[8], (H, SM), jnp.float32, -sh, sh), 'sw_down': jax.random.uniform(ks[9], (SM, H), jnp.float32, -ssm, ssm)}
    _L1_cond_all = _L1_cond_setup()
    _L1_cond_in = {k: v for k, v in _L1_cond_all.items() if k in ('wt', 'wg', 'w_gate', 'w_up', 'w_down', 'sw_gate', 'sw_up', 'sw_down')}
    del _L1_cond_all

    def _L1_attn_setup():
        import jax, jax.numpy as jnp
        import numpy as np
        DIM = 128
        HEADS = 16
        HEAD_DIM = DIM // HEADS
        FEAT = 32
        B, N = (4, 512)

        def _elu1(x):
            return jnp.where(x > 0, x + 1.0, jnp.exp(x))
        key = jax.random.key(seed)
        k_x, k_qkv, k_proj, k_wo, k_bo = jax.random.split(key, 5)
        x = jax.random.normal(k_x, (B, N, DIM), dtype=jnp.float32)
        w_qkv = jax.random.normal(k_qkv, (DIM, 3 * DIM), dtype=jnp.float32) * (1.0 / np.sqrt(DIM))
        proj_matrix = jax.random.normal(k_proj, (HEADS, HEAD_DIM, FEAT), dtype=jnp.float32) * (1.0 / np.sqrt(HEAD_DIM))
        w_out = jax.random.normal(k_wo, (DIM, DIM), dtype=jnp.float32) * (1.0 / np.sqrt(DIM))
        b_out = jax.random.normal(k_bo, (DIM,), dtype=jnp.float32) * 0.01
        return {'x': x, 'w_qkv': w_qkv, 'proj_matrix': proj_matrix, 'w_out': w_out, 'b_out': b_out}
    _L1_attn_all = _L1_attn_setup()
    _L1_attn_in = {k: v for k, v in _L1_attn_all.items() if k in ('w_qkv', 'proj_matrix', 'w_out', 'b_out')}
    del _L1_attn_all

    def _L1_cond2_setup():
        import jax, jax.numpy as jnp
        import numpy as np
        B, N, DIM, H, DH = (2, 256, 128, 16, 64)
        INNER = H * DH
        EPS = 1e-05

        def layernorm(x, g):
            mean = jnp.mean(x, axis=-1, keepdims=True)
            var = jnp.var(x, axis=-1, keepdims=True)
            return (x - mean) * jax.lax.rsqrt(var + EPS) * g
        key = jax.random.key(seed)
        ks = jax.random.split(key, 10)
        x = jax.random.normal(ks[0], (B, N, DIM), dtype=jnp.float32)
        attn_bias = jax.random.normal(ks[1], (H, N, N), dtype=jnp.float32)
        mask = jax.random.randint(ks[2], (B, N), 0, 2).astype(bool)
        g_in = jnp.ones((DIM,), dtype=jnp.float32)
        null_attn_bias = jax.random.normal(ks[3], (H,), dtype=jnp.float32)
        null_kv = jax.random.normal(ks[4], (2, DH), dtype=jnp.float32)
        Wq = jax.random.normal(ks[5], (DIM, INNER), dtype=jnp.float32) * 0.02
        Wkv = jax.random.normal(ks[6], (DIM, 2 * DH), dtype=jnp.float32) * 0.02
        Wo = jax.random.normal(ks[7], (INNER, DIM), dtype=jnp.float32) * 0.02
        g_out = jnp.ones((DIM,), dtype=jnp.float32)
        return {'x': x, 'attn_bias': attn_bias, 'mask': mask, 'g_in': g_in, 'null_attn_bias': null_attn_bias, 'null_kv': null_kv, 'Wq': Wq, 'Wkv': Wkv, 'Wo': Wo, 'g_out': g_out}
    _L1_cond2_all = _L1_cond2_setup()
    _L1_cond2_in = {k: v for k, v in _L1_cond2_all.items() if k in ('g_in', 'null_attn_bias', 'Wq', 'Wkv', 'Wo', 'g_out')}
    del _L1_cond2_all

    def _L1_ffn_setup():
        import jax, jax.numpy as jnp
        import numpy as np
        B, S, D_MODEL, D_FF = (4, 256, 128, 512)

        def _quantum_transform(hidden, theta, w_real, w_imag):
            imag = w_imag * jnp.sin(theta + hidden * 0.1)
            quantum_phase = jnp.cos(theta) * w_real + jnp.sin(theta) * w_imag
            return hidden + quantum_phase * imag * 0.1
        key = jax.random.key(seed)
        ks = jax.random.split(key, 8)
        return {'x': jax.random.normal(ks[0], (B, S, D_MODEL), dtype=jnp.float32), 'W1': jax.random.normal(ks[1], (D_MODEL, D_FF), dtype=jnp.float32) * (1.0 / np.sqrt(D_MODEL)), 'b1': jnp.zeros((D_FF,), dtype=jnp.float32), 'quantum_phases': jax.random.normal(ks[2], (D_FF,), dtype=jnp.float32) * (2.0 * np.pi), 'quantum_weights_real': jax.random.normal(ks[3], (D_FF,), dtype=jnp.float32) * 0.1, 'quantum_weights_imag': jax.random.normal(ks[4], (D_FF,), dtype=jnp.float32) * 0.1, 'W2': jax.random.normal(ks[5], (D_FF, D_MODEL), dtype=jnp.float32) * (1.0 / np.sqrt(D_FF)), 'b2': jnp.zeros((D_MODEL,), dtype=jnp.float32)}
    _L1_ffn_all = _L1_ffn_setup()
    _L1_ffn_in = {k: v for k, v in _L1_ffn_all.items() if k in ('W1', 'b1', 'quantum_phases', 'quantum_weights_real', 'quantum_weights_imag', 'W2', 'b2')}
    del _L1_ffn_all

    def _L2_cond_setup():
        import jax, jax.numpy as jnp
        import numpy as np
        B, S, H = (4, 256, 128)
        E = 8
        M = 64
        K = 2
        N_SHARED = 2
        SM = M * N_SHARED
        G = 64
        GE_TEMP = 1.0
        ALPHA = 0.001
        SEQ_AUX = True
        NORM_TOPK = True
        COS_TEMP = 0.78
        CONS_ALPHA = 0.01
        LEAKY_SLOPE = 0.01
        EPS_COS = 1e-08

        def _leaky(x):
            return jnp.where(x >= 0, x, LEAKY_SLOPE * x)

        def _moe_forward(hidden_states, g, wt, wg, w_gate, w_up, w_down, sw_gate, sw_up, sw_down):
            b, s, h = hidden_states.shape
            x = hidden_states.reshape(-1, h)
            T = x.shape[0]
            logits_h = x @ wt.T
            logits_g = g @ wg.T
            logits_g = jnp.repeat(logits_g, s, axis=0)
            logits = (logits_h + logits_g / GE_TEMP) / (1.0 + 1.0 / GE_TEMP)
            scores = jax.nn.softmax(logits, axis=-1)
            topk_w, topk_idx = jax.lax.top_k(scores, K)
            if K > 1 and NORM_TOPK:
                topk_w = topk_w / (topk_w.sum(-1, keepdims=True) + 1e-20)
            onehot = jax.nn.one_hot(topk_idx.reshape(b, s * K), E, dtype=jnp.float32)
            ce = onehot.sum(1) / (s * K / E)
            aux_loss = (ce * scores.reshape(b, s, E).mean(1)).sum(1).mean() * ALPHA
            gp = _leaky(jnp.einsum('th,ehm->etm', x, w_gate))
            up = jnp.einsum('th,ehm->etm', x, w_up)
            y_all = jnp.einsum('etm,emh->eth', gp * up, w_down)
            y_sel = y_all[topk_idx, jnp.arange(T)[:, None], :]
            y = (y_sel * topk_w[..., None]).sum(1).reshape(b, s, h)
            p = _leaky(hidden_states @ sw_gate) * (hidden_states @ sw_up) @ sw_down
            y = y + p
            num = jnp.sum(y * p, -1)
            den = jnp.maximum(jnp.linalg.norm(y, axis=-1), EPS_COS) * jnp.maximum(jnp.linalg.norm(p, axis=-1), EPS_COS)
            closs = CONS_ALPHA * jnp.mean(num / den / (1.0 + COS_TEMP))
            return (y, aux_loss + closs)
        key = jax.random.key(seed)
        ks = jax.random.split(key, 12)
        sh = 1.0 / np.sqrt(H)
        sm = 1.0 / np.sqrt(M)
        ssm = 1.0 / np.sqrt(SM)
        sg = 1.0 / np.sqrt(G)
        return {'hidden_states': jax.random.normal(ks[0], (B, S, H), jnp.float32), 'g': jax.random.normal(ks[1], (B, G), jnp.float32), 'wt': jax.random.uniform(ks[2], (E, H), jnp.float32, -sh, sh), 'wg': jax.random.uniform(ks[3], (E, G), jnp.float32, -sg, sg), 'w_gate': jax.random.uniform(ks[4], (E, H, M), jnp.float32, -sh, sh), 'w_up': jax.random.uniform(ks[5], (E, H, M), jnp.float32, -sh, sh), 'w_down': jax.random.uniform(ks[6], (E, M, H), jnp.float32, -sm, sm), 'sw_gate': jax.random.uniform(ks[7], (H, SM), jnp.float32, -sh, sh), 'sw_up': jax.random.uniform(ks[8], (H, SM), jnp.float32, -sh, sh), 'sw_down': jax.random.uniform(ks[9], (SM, H), jnp.float32, -ssm, ssm)}
    _L2_cond_all = _L2_cond_setup()
    _L2_cond_in = {k: v for k, v in _L2_cond_all.items() if k in ('wt', 'wg', 'w_gate', 'w_up', 'w_down', 'sw_gate', 'sw_up', 'sw_down')}
    del _L2_cond_all

    def _L2_attn_setup():
        import jax, jax.numpy as jnp
        import numpy as np
        DIM = 128
        NUM_HEADS = 16
        NUM_KV_HEADS = 2
        HEAD_DIM = DIM // NUM_HEADS
        REPEATS = NUM_HEADS // NUM_KV_HEADS
        WINDOW = 32
        HALF = WINDOW // 2
        BATCH, SEQ = (2, 256)
        key = jax.random.key(seed)
        ks = jax.random.split(key, 9)
        sc = 1.0 / np.sqrt(DIM)
        return {'x': jax.random.normal(ks[0], (BATCH, SEQ, DIM), jnp.float32), 'Wq': jax.random.normal(ks[1], (DIM, NUM_HEADS * HEAD_DIM), jnp.float32) * sc, 'bq': jax.random.normal(ks[2], (NUM_HEADS * HEAD_DIM,), jnp.float32) * 0.01, 'Wk': jax.random.normal(ks[3], (DIM, NUM_KV_HEADS * HEAD_DIM), jnp.float32) * sc, 'bk': jax.random.normal(ks[4], (NUM_KV_HEADS * HEAD_DIM,), jnp.float32) * 0.01, 'Wv': jax.random.normal(ks[5], (DIM, NUM_KV_HEADS * HEAD_DIM), jnp.float32) * sc, 'bv': jax.random.normal(ks[6], (NUM_KV_HEADS * HEAD_DIM,), jnp.float32) * 0.01, 'Wo': jax.random.normal(ks[7], (DIM, DIM), jnp.float32) * sc, 'bo': jax.random.normal(ks[8], (DIM,), jnp.float32) * 0.01}
    _L2_attn_all = _L2_attn_setup()
    _L2_attn_in = {k: v for k, v in _L2_attn_all.items() if k in ('Wq', 'bq', 'Wk', 'bk', 'Wv', 'bv', 'Wo', 'bo')}
    del _L2_attn_all

    def _L2_cond2_setup():
        import jax, jax.numpy as jnp
        import numpy as np
        B, S, H = (4, 256, 128)
        E = 8
        M = 64
        K = 2
        N_SHARED = 2
        SM = M * N_SHARED
        G = 64
        GE_TEMP = 1.0
        ALPHA = 0.001
        SEQ_AUX = True
        NORM_TOPK = True
        COS_TEMP = 0.78
        CONS_ALPHA = 0.01
        LEAKY_SLOPE = 0.01
        EPS_COS = 1e-08

        def _leaky(x):
            return jnp.where(x >= 0, x, LEAKY_SLOPE * x)

        def _moe_forward(hidden_states, g, wt, wg, w_gate, w_up, w_down, sw_gate, sw_up, sw_down):
            b, s, h = hidden_states.shape
            x = hidden_states.reshape(-1, h)
            T = x.shape[0]
            logits_h = x @ wt.T
            logits_g = g @ wg.T
            logits_g = jnp.repeat(logits_g, s, axis=0)
            logits = (logits_h + logits_g / GE_TEMP) / (1.0 + 1.0 / GE_TEMP)
            scores = jax.nn.softmax(logits, axis=-1)
            topk_w, topk_idx = jax.lax.top_k(scores, K)
            if K > 1 and NORM_TOPK:
                topk_w = topk_w / (topk_w.sum(-1, keepdims=True) + 1e-20)
            onehot = jax.nn.one_hot(topk_idx.reshape(b, s * K), E, dtype=jnp.float32)
            ce = onehot.sum(1) / (s * K / E)
            aux_loss = (ce * scores.reshape(b, s, E).mean(1)).sum(1).mean() * ALPHA
            gp = _leaky(jnp.einsum('th,ehm->etm', x, w_gate))
            up = jnp.einsum('th,ehm->etm', x, w_up)
            y_all = jnp.einsum('etm,emh->eth', gp * up, w_down)
            y_sel = y_all[topk_idx, jnp.arange(T)[:, None], :]
            y = (y_sel * topk_w[..., None]).sum(1).reshape(b, s, h)
            p = _leaky(hidden_states @ sw_gate) * (hidden_states @ sw_up) @ sw_down
            y = y + p
            num = jnp.sum(y * p, -1)
            den = jnp.maximum(jnp.linalg.norm(y, axis=-1), EPS_COS) * jnp.maximum(jnp.linalg.norm(p, axis=-1), EPS_COS)
            closs = CONS_ALPHA * jnp.mean(num / den / (1.0 + COS_TEMP))
            return (y, aux_loss + closs)
        key = jax.random.key(seed)
        ks = jax.random.split(key, 12)
        sh = 1.0 / np.sqrt(H)
        sm = 1.0 / np.sqrt(M)
        ssm = 1.0 / np.sqrt(SM)
        sg = 1.0 / np.sqrt(G)
        return {'hidden_states': jax.random.normal(ks[0], (B, S, H), jnp.float32), 'g': jax.random.normal(ks[1], (B, G), jnp.float32), 'wt': jax.random.uniform(ks[2], (E, H), jnp.float32, -sh, sh), 'wg': jax.random.uniform(ks[3], (E, G), jnp.float32, -sg, sg), 'w_gate': jax.random.uniform(ks[4], (E, H, M), jnp.float32, -sh, sh), 'w_up': jax.random.uniform(ks[5], (E, H, M), jnp.float32, -sh, sh), 'w_down': jax.random.uniform(ks[6], (E, M, H), jnp.float32, -sm, sm), 'sw_gate': jax.random.uniform(ks[7], (H, SM), jnp.float32, -sh, sh), 'sw_up': jax.random.uniform(ks[8], (H, SM), jnp.float32, -sh, sh), 'sw_down': jax.random.uniform(ks[9], (SM, H), jnp.float32, -ssm, ssm)}
    _L2_cond2_all = _L2_cond2_setup()
    _L2_cond2_in = {k: v for k, v in _L2_cond2_all.items() if k in ('wt', 'wg', 'w_gate', 'w_up', 'w_down', 'sw_gate', 'sw_up', 'sw_down')}
    del _L2_cond2_all

    def _L2_ffn_setup():
        import jax, jax.numpy as jnp
        import numpy as np
        D_MODEL, D_FF, N_EXP = (128, 512, 8)
        key = jax.random.key(seed)
        ks = jax.random.split(key, 8)
        s = lambda fan_in: 1.0 / np.sqrt(fan_in)
        x = jax.random.normal(ks[0], (4, 256, D_MODEL), dtype=jnp.float32)
        Wr = jax.random.uniform(ks[1], (N_EXP, D_MODEL), jnp.float32, -s(D_MODEL), s(D_MODEL))
        br = jax.random.uniform(ks[2], (N_EXP,), jnp.float32, -s(D_MODEL), s(D_MODEL))
        W1 = jax.random.uniform(ks[3], (N_EXP, D_FF, D_MODEL), jnp.float32, -s(D_MODEL), s(D_MODEL))
        b1 = jax.random.uniform(ks[4], (N_EXP, D_FF), jnp.float32, -s(D_MODEL), s(D_MODEL))
        W2 = jax.random.uniform(ks[5], (N_EXP, D_MODEL, D_FF), jnp.float32, -s(D_FF), s(D_FF))
        b2 = jax.random.uniform(ks[6], (N_EXP, D_MODEL), jnp.float32, -s(D_FF), s(D_FF))
        return {'x': x, 'Wr': Wr, 'br': br, 'W1': W1, 'b1': b1, 'W2': W2, 'b2': b2}
    _L2_ffn_all = _L2_ffn_setup()
    _L2_ffn_in = {k: v for k, v in _L2_ffn_all.items() if k in ('Wr', 'br', 'W1', 'b1', 'W2', 'b2')}
    del _L2_ffn_all

    def _L3_cond_setup():
        import jax, jax.numpy as jnp
        import numpy as np
        B, S, H = (4, 256, 128)
        E = 8
        M = 64
        K = 2
        N_SHARED = 2
        SM = M * N_SHARED
        G = 64
        GE_TEMP = 1.0
        ALPHA = 0.001
        SEQ_AUX = True
        NORM_TOPK = True
        COS_TEMP = 0.78
        CONS_ALPHA = 0.01
        LEAKY_SLOPE = 0.01
        EPS_COS = 1e-08

        def _leaky(x):
            return jnp.where(x >= 0, x, LEAKY_SLOPE * x)

        def _moe_forward(hidden_states, g, wt, wg, w_gate, w_up, w_down, sw_gate, sw_up, sw_down):
            b, s, h = hidden_states.shape
            x = hidden_states.reshape(-1, h)
            T = x.shape[0]
            logits_h = x @ wt.T
            logits_g = g @ wg.T
            logits_g = jnp.repeat(logits_g, s, axis=0)
            logits = (logits_h + logits_g / GE_TEMP) / (1.0 + 1.0 / GE_TEMP)
            scores = jax.nn.softmax(logits, axis=-1)
            topk_w, topk_idx = jax.lax.top_k(scores, K)
            if K > 1 and NORM_TOPK:
                topk_w = topk_w / (topk_w.sum(-1, keepdims=True) + 1e-20)
            onehot = jax.nn.one_hot(topk_idx.reshape(b, s * K), E, dtype=jnp.float32)
            ce = onehot.sum(1) / (s * K / E)
            aux_loss = (ce * scores.reshape(b, s, E).mean(1)).sum(1).mean() * ALPHA
            gp = _leaky(jnp.einsum('th,ehm->etm', x, w_gate))
            up = jnp.einsum('th,ehm->etm', x, w_up)
            y_all = jnp.einsum('etm,emh->eth', gp * up, w_down)
            y_sel = y_all[topk_idx, jnp.arange(T)[:, None], :]
            y = (y_sel * topk_w[..., None]).sum(1).reshape(b, s, h)
            p = _leaky(hidden_states @ sw_gate) * (hidden_states @ sw_up) @ sw_down
            y = y + p
            num = jnp.sum(y * p, -1)
            den = jnp.maximum(jnp.linalg.norm(y, axis=-1), EPS_COS) * jnp.maximum(jnp.linalg.norm(p, axis=-1), EPS_COS)
            closs = CONS_ALPHA * jnp.mean(num / den / (1.0 + COS_TEMP))
            return (y, aux_loss + closs)
        key = jax.random.key(seed)
        ks = jax.random.split(key, 12)
        sh = 1.0 / np.sqrt(H)
        sm = 1.0 / np.sqrt(M)
        ssm = 1.0 / np.sqrt(SM)
        sg = 1.0 / np.sqrt(G)
        return {'hidden_states': jax.random.normal(ks[0], (B, S, H), jnp.float32), 'g': jax.random.normal(ks[1], (B, G), jnp.float32), 'wt': jax.random.uniform(ks[2], (E, H), jnp.float32, -sh, sh), 'wg': jax.random.uniform(ks[3], (E, G), jnp.float32, -sg, sg), 'w_gate': jax.random.uniform(ks[4], (E, H, M), jnp.float32, -sh, sh), 'w_up': jax.random.uniform(ks[5], (E, H, M), jnp.float32, -sh, sh), 'w_down': jax.random.uniform(ks[6], (E, M, H), jnp.float32, -sm, sm), 'sw_gate': jax.random.uniform(ks[7], (H, SM), jnp.float32, -sh, sh), 'sw_up': jax.random.uniform(ks[8], (H, SM), jnp.float32, -sh, sh), 'sw_down': jax.random.uniform(ks[9], (SM, H), jnp.float32, -ssm, ssm)}
    _L3_cond_all = _L3_cond_setup()
    _L3_cond_in = {k: v for k, v in _L3_cond_all.items() if k in ('wt', 'wg', 'w_gate', 'w_up', 'w_down', 'sw_gate', 'sw_up', 'sw_down')}
    del _L3_cond_all

    def _L3_attn_setup():
        import jax, jax.numpy as jnp
        import numpy as np
        B, T, DIM = (2, 512, 128)
        DEPTH, HEADS = (4, 8)
        DH = DIM // HEADS
        NLOCAL, WINDOW, BUCKET = (4, 128, 64)
        MULT = 4

        def layer_norm(x, g, b, eps=1e-05):
            m = jnp.mean(x, -1, keepdims=True)
            v = jnp.mean(jnp.square(x - m), -1, keepdims=True)
            return (x - m) * jax.lax.rsqrt(v + eps) * g + b

        def causal_linear_attn(q, k, v):
            b, h, n, e = q.shape
            u = n // BUCKET
            q = jax.nn.softmax(q, axis=-1)
            k = jax.nn.elu(k) + 1.0
            bq = q.reshape(b, h, u, BUCKET, e)
            bk = k.reshape(b, h, u, BUCKET, e)
            bv = v.reshape(b, h, u, BUCKET, e)
            k_cum = jnp.cumsum(bk.sum(axis=-2), axis=-2)
            ctx = jnp.einsum('bhund,bhune->bhude', bk, bv)
            ctx = jnp.cumsum(ctx, axis=2)
            ctx = ctx / (k_cum[..., None] + 1e-06)
            ctx = jnp.pad(ctx, ((0, 0), (0, 0), (1, 0), (0, 0), (0, 0)))[:, :, :-1]
            out = jnp.einsum('bhund,bhude->bhune', bq, ctx)
            return out.reshape(b, h, n, e)

        def local_attn(q, k, v):
            b, lh, t, e = q.shape
            bh = b * lh
            nb = t // WINDOW
            bq = q.reshape(bh, nb, WINDOW, e)
            bk = k.reshape(bh, nb, WINDOW, e)
            bv = v.reshape(bh, nb, WINDOW, e)

            def look_around(x):
                padded = jnp.pad(x, ((0, 0), (1, 0), (0, 0), (0, 0)))
                return jnp.concatenate([padded[:, :-1], padded[:, 1:]], axis=2)
            bk2 = look_around(bk)
            bv2 = look_around(bv)
            tix = jnp.arange(t).reshape(1, nb, WINDOW)
            tpad = jnp.pad(tix, ((0, 0), (1, 0), (0, 0)), constant_values=-1)
            kix = jnp.concatenate([tpad[:, :-1], tpad[:, 1:]], axis=2)
            dots = jnp.einsum('bwie,bwje->bwij', bq, bk2) * e ** (-0.5)
            mask_value = -jnp.finfo(dots.dtype).max
            causal_mask = tix[:, :, :, None] < kix[:, :, None, :]
            pad_mask = (kix == -1)[:, :, None, :]
            dots = jnp.where(causal_mask | pad_mask, mask_value, dots)
            attn = jax.nn.softmax(dots, axis=-1)
            out = jnp.einsum('bwij,bwje->bwie', attn, bv2)
            return out.reshape(b, lh, t, e)

        def self_attention(x, Wq, Wk, Wv, Wo, bo):
            b, t, _ = x.shape
            mh = lambda z: z.reshape(b, t, HEADS, DH).transpose(0, 2, 1, 3)
            q, k, v = (mh(x @ Wq), mh(x @ Wk), mh(x @ Wv))
            lo = local_attn(q[:, :NLOCAL], k[:, :NLOCAL], v[:, :NLOCAL])
            go = causal_linear_attn(q[:, NLOCAL:], k[:, NLOCAL:], v[:, NLOCAL:])
            out = jnp.concatenate([lo, go], axis=1)
            out = out.transpose(0, 2, 1, 3).reshape(b, t, DIM)
            return out @ Wo + bo
        key = jax.random.key(seed)
        ks = jax.random.split(key, 8)
        s = 0.02
        rn = lambda k, shape: jax.random.normal(k, shape, dtype=jnp.float32) * s
        return {'x': jax.random.normal(ks[0], (B, T, DIM), dtype=jnp.float32), 'Wq': rn(ks[1], (DEPTH, DIM, DIM)), 'Wk': rn(ks[2], (DEPTH, DIM, DIM)), 'Wv': rn(ks[3], (DEPTH, DIM, DIM)), 'Wo': rn(ks[4], (DEPTH, DIM, DIM)), 'bo': jnp.zeros((DEPTH, DIM), jnp.float32), 'ln1_g': jnp.ones((DEPTH, DIM), jnp.float32), 'ln1_b': jnp.zeros((DEPTH, DIM), jnp.float32), 'W1': rn(ks[5], (DEPTH, DIM, DIM * MULT)), 'b1': jnp.zeros((DEPTH, DIM * MULT), jnp.float32), 'W2': rn(ks[6], (DEPTH, DIM * MULT, DIM)), 'b2': jnp.zeros((DEPTH, DIM), jnp.float32), 'ln2_g': jnp.ones((DEPTH, DIM), jnp.float32), 'ln2_b': jnp.zeros((DEPTH, DIM), jnp.float32)}
    _L3_attn_all = _L3_attn_setup()
    _L3_attn_in = {k: v for k, v in _L3_attn_all.items() if k in ('Wq', 'Wk', 'Wv', 'Wo', 'bo', 'ln1_g', 'ln1_b', 'W1', 'b1', 'W2', 'b2', 'ln2_g', 'ln2_b')}
    del _L3_attn_all

    def _L3_cond2_setup():
        import jax, jax.numpy as jnp
        import numpy as np
        DIM = 128
        HEADS = 16
        DIM_HEAD = 64
        SCALE = 8.0

        def ln(x, g, eps=1e-05):
            mean = x.mean(axis=-1, keepdims=True)
            var = ((x - mean) ** 2).mean(axis=-1, keepdims=True)
            return (x - mean) * jax.lax.rsqrt(var + eps) * g

        def l2norm(t):
            n = jnp.maximum(jnp.linalg.norm(t, axis=-1, keepdims=True), 1e-12)
            return t / n

        def rel_pos_bias(n, w0, b0, g0, w1, b1, g1, w2, b2, dtype):
            pos = jnp.arange(-n + 1, n, dtype=dtype)[:, None]
            h = jax.nn.silu(ln(pos @ w0 + b0, g0))
            h = jax.nn.silu(ln(h @ w1 + b1, g1))
            h = h @ w2 + b2
            i = jnp.arange(n)
            idx = i[:, None] - i[None, :] + n - 1
            bias = h[idx]
            return jnp.transpose(bias, (2, 0, 1))
        key = jax.random.key(seed)
        ks = jax.random.split(key, 16)
        b, n = (2, 256)
        inner = HEADS * DIM_HEAD
        s = 0.02
        return {'x': jax.random.normal(ks[0], (b, n, DIM), jnp.float32), 'mask': jnp.ones((b, n), dtype=bool), 'g_norm': jnp.ones((DIM,), jnp.float32), 'Wq': jax.random.normal(ks[1], (DIM, inner), jnp.float32) * s, 'Wkv': jax.random.normal(ks[2], (DIM, 2 * DIM_HEAD), jnp.float32) * s, 'q_scale': jnp.ones((DIM_HEAD,), jnp.float32), 'k_scale': jnp.ones((DIM_HEAD,), jnp.float32), 'null_kv': jax.random.normal(ks[3], (2, DIM_HEAD), jnp.float32), 'null_attn_bias': jax.random.normal(ks[4], (HEADS,), jnp.float32), 'w0': jax.random.normal(ks[5], (1, DIM), jnp.float32) * s, 'b0': jnp.zeros((DIM,), jnp.float32), 'g0': jnp.ones((DIM,), jnp.float32), 'w1': jax.random.normal(ks[6], (DIM, DIM), jnp.float32) * s, 'b1': jnp.zeros((DIM,), jnp.float32), 'g1': jnp.ones((DIM,), jnp.float32), 'w2': jax.random.normal(ks[7], (DIM, HEADS), jnp.float32) * s, 'b2': jnp.zeros((HEADS,), jnp.float32), 'Wout': jax.random.normal(ks[8], (inner, DIM), jnp.float32) * s, 'g_out': jnp.ones((DIM,), jnp.float32)}
    _L3_cond2_all = _L3_cond2_setup()
    _L3_cond2_in = {k: v for k, v in _L3_cond2_all.items() if k in ('g_norm', 'Wq', 'Wkv', 'q_scale', 'k_scale', 'null_attn_bias', 'w0', 'b0', 'g0', 'w1', 'b1', 'g1', 'w2', 'b2', 'Wout', 'g_out')}
    del _L3_cond2_all

    def _L3_ffn_setup():
        import math
        import jax, jax.numpy as jnp
        import numpy as np
        D_MODEL = 128
        D_HIDDEN = 512
        N_EXPERTS = 8
        TOP_K = 2
        CAPACITY_FACTOR = 1.25
        key = jax.random.key(seed)
        ks = jax.random.split(key, 8)
        s = 0.02
        x = jax.random.normal(ks[0], (4, 256, D_MODEL), dtype=jnp.float32)
        router_w = jax.random.normal(ks[1], (D_MODEL, N_EXPERTS), dtype=jnp.float32) * s
        router_b = jnp.zeros((N_EXPERTS,), dtype=jnp.float32)
        w1 = jax.random.normal(ks[2], (N_EXPERTS, D_MODEL, D_HIDDEN), dtype=jnp.float32) * s
        b1 = jnp.zeros((N_EXPERTS, D_HIDDEN), dtype=jnp.float32)
        w2 = jax.random.normal(ks[3], (N_EXPERTS, D_HIDDEN, D_MODEL), dtype=jnp.float32) * s
        b2 = jnp.zeros((N_EXPERTS, D_MODEL), dtype=jnp.float32)
        return {'x': x, 'router_w': router_w, 'router_b': router_b, 'w1': w1, 'b1': b1, 'w2': w2, 'b2': b2}
    _L3_ffn_all = _L3_ffn_setup()
    _L3_ffn_in = {k: v for k, v in _L3_ffn_all.items() if k in ('router_w', 'router_b', 'w1', 'b1', 'w2', 'b2')}
    del _L3_ffn_all
    return {'x': x, 'cond_64': cond_64, 'fside_16xSxS_0': fside_16xSxS_0, 'mask_BxS_bf1': mask_BxS_bf1, 'mask_BxS_bk0': mask_BxS_bk0, 'L0_cond_g_norm': _L0_cond_in['g_norm'], 'L0_cond_Wq': _L0_cond_in['Wq'], 'L0_cond_Wkv': _L0_cond_in['Wkv'], 'L0_cond_q_scale': _L0_cond_in['q_scale'], 'L0_cond_k_scale': _L0_cond_in['k_scale'], 'L0_cond_null_attn_bias': _L0_cond_in['null_attn_bias'], 'L0_cond_w0': _L0_cond_in['w0'], 'L0_cond_b0': _L0_cond_in['b0'], 'L0_cond_g0': _L0_cond_in['g0'], 'L0_cond_w1': _L0_cond_in['w1'], 'L0_cond_b1': _L0_cond_in['b1'], 'L0_cond_g1': _L0_cond_in['g1'], 'L0_cond_w2': _L0_cond_in['w2'], 'L0_cond_b2': _L0_cond_in['b2'], 'L0_cond_Wout': _L0_cond_in['Wout'], 'L0_cond_g_out': _L0_cond_in['g_out'], 'L0_attn_Wq': _L0_attn_in['Wq'], 'L0_attn_Wk': _L0_attn_in['Wk'], 'L0_attn_Wv': _L0_attn_in['Wv'], 'L0_attn_Wo': _L0_attn_in['Wo'], 'L0_attn_rel': _L0_attn_in['rel'], 'L0_attn_ln_gamma': _L0_attn_in['ln_gamma'], 'L0_attn_ln_beta': _L0_attn_in['ln_beta'], 'L0_cond2_g_in': _L0_cond2_in['g_in'], 'L0_cond2_null_attn_bias': _L0_cond2_in['null_attn_bias'], 'L0_cond2_Wq': _L0_cond2_in['Wq'], 'L0_cond2_Wkv': _L0_cond2_in['Wkv'], 'L0_cond2_Wo': _L0_cond2_in['Wo'], 'L0_cond2_g_out': _L0_cond2_in['g_out'], 'L0_ffn_gate_weight': _L0_ffn_in['gate_weight'], 'L0_ffn_gate_up_proj': _L0_ffn_in['gate_up_proj'], 'L0_ffn_down_proj': _L0_ffn_in['down_proj'], 'L0_ffn_similarity_matrix': _L0_ffn_in['similarity_matrix'], 'L1_cond_wt': _L1_cond_in['wt'], 'L1_cond_wg': _L1_cond_in['wg'], 'L1_cond_w_gate': _L1_cond_in['w_gate'], 'L1_cond_w_up': _L1_cond_in['w_up'], 'L1_cond_w_down': _L1_cond_in['w_down'], 'L1_cond_sw_gate': _L1_cond_in['sw_gate'], 'L1_cond_sw_up': _L1_cond_in['sw_up'], 'L1_cond_sw_down': _L1_cond_in['sw_down'], 'L1_attn_w_qkv': _L1_attn_in['w_qkv'], 'L1_attn_proj_matrix': _L1_attn_in['proj_matrix'], 'L1_attn_w_out': _L1_attn_in['w_out'], 'L1_attn_b_out': _L1_attn_in['b_out'], 'L1_cond2_g_in': _L1_cond2_in['g_in'], 'L1_cond2_null_attn_bias': _L1_cond2_in['null_attn_bias'], 'L1_cond2_Wq': _L1_cond2_in['Wq'], 'L1_cond2_Wkv': _L1_cond2_in['Wkv'], 'L1_cond2_Wo': _L1_cond2_in['Wo'], 'L1_cond2_g_out': _L1_cond2_in['g_out'], 'L1_ffn_W1': _L1_ffn_in['W1'], 'L1_ffn_b1': _L1_ffn_in['b1'], 'L1_ffn_quantum_phases': _L1_ffn_in['quantum_phases'], 'L1_ffn_quantum_weights_real': _L1_ffn_in['quantum_weights_real'], 'L1_ffn_quantum_weights_imag': _L1_ffn_in['quantum_weights_imag'], 'L1_ffn_W2': _L1_ffn_in['W2'], 'L1_ffn_b2': _L1_ffn_in['b2'], 'L2_cond_wt': _L2_cond_in['wt'], 'L2_cond_wg': _L2_cond_in['wg'], 'L2_cond_w_gate': _L2_cond_in['w_gate'], 'L2_cond_w_up': _L2_cond_in['w_up'], 'L2_cond_w_down': _L2_cond_in['w_down'], 'L2_cond_sw_gate': _L2_cond_in['sw_gate'], 'L2_cond_sw_up': _L2_cond_in['sw_up'], 'L2_cond_sw_down': _L2_cond_in['sw_down'], 'L2_attn_Wq': _L2_attn_in['Wq'], 'L2_attn_bq': _L2_attn_in['bq'], 'L2_attn_Wk': _L2_attn_in['Wk'], 'L2_attn_bk': _L2_attn_in['bk'], 'L2_attn_Wv': _L2_attn_in['Wv'], 'L2_attn_bv': _L2_attn_in['bv'], 'L2_attn_Wo': _L2_attn_in['Wo'], 'L2_attn_bo': _L2_attn_in['bo'], 'L2_cond2_wt': _L2_cond2_in['wt'], 'L2_cond2_wg': _L2_cond2_in['wg'], 'L2_cond2_w_gate': _L2_cond2_in['w_gate'], 'L2_cond2_w_up': _L2_cond2_in['w_up'], 'L2_cond2_w_down': _L2_cond2_in['w_down'], 'L2_cond2_sw_gate': _L2_cond2_in['sw_gate'], 'L2_cond2_sw_up': _L2_cond2_in['sw_up'], 'L2_cond2_sw_down': _L2_cond2_in['sw_down'], 'L2_ffn_Wr': _L2_ffn_in['Wr'], 'L2_ffn_br': _L2_ffn_in['br'], 'L2_ffn_W1': _L2_ffn_in['W1'], 'L2_ffn_b1': _L2_ffn_in['b1'], 'L2_ffn_W2': _L2_ffn_in['W2'], 'L2_ffn_b2': _L2_ffn_in['b2'], 'L3_cond_wt': _L3_cond_in['wt'], 'L3_cond_wg': _L3_cond_in['wg'], 'L3_cond_w_gate': _L3_cond_in['w_gate'], 'L3_cond_w_up': _L3_cond_in['w_up'], 'L3_cond_w_down': _L3_cond_in['w_down'], 'L3_cond_sw_gate': _L3_cond_in['sw_gate'], 'L3_cond_sw_up': _L3_cond_in['sw_up'], 'L3_cond_sw_down': _L3_cond_in['sw_down'], 'L3_attn_Wq': _L3_attn_in['Wq'], 'L3_attn_Wk': _L3_attn_in['Wk'], 'L3_attn_Wv': _L3_attn_in['Wv'], 'L3_attn_Wo': _L3_attn_in['Wo'], 'L3_attn_bo': _L3_attn_in['bo'], 'L3_attn_ln1_g': _L3_attn_in['ln1_g'], 'L3_attn_ln1_b': _L3_attn_in['ln1_b'], 'L3_attn_W1': _L3_attn_in['W1'], 'L3_attn_b1': _L3_attn_in['b1'], 'L3_attn_W2': _L3_attn_in['W2'], 'L3_attn_b2': _L3_attn_in['b2'], 'L3_attn_ln2_g': _L3_attn_in['ln2_g'], 'L3_attn_ln2_b': _L3_attn_in['ln2_b'], 'L3_cond2_g_norm': _L3_cond2_in['g_norm'], 'L3_cond2_Wq': _L3_cond2_in['Wq'], 'L3_cond2_Wkv': _L3_cond2_in['Wkv'], 'L3_cond2_q_scale': _L3_cond2_in['q_scale'], 'L3_cond2_k_scale': _L3_cond2_in['k_scale'], 'L3_cond2_null_attn_bias': _L3_cond2_in['null_attn_bias'], 'L3_cond2_w0': _L3_cond2_in['w0'], 'L3_cond2_b0': _L3_cond2_in['b0'], 'L3_cond2_g0': _L3_cond2_in['g0'], 'L3_cond2_w1': _L3_cond2_in['w1'], 'L3_cond2_b1': _L3_cond2_in['b1'], 'L3_cond2_g1': _L3_cond2_in['g1'], 'L3_cond2_w2': _L3_cond2_in['w2'], 'L3_cond2_b2': _L3_cond2_in['b2'], 'L3_cond2_Wout': _L3_cond2_in['Wout'], 'L3_cond2_g_out': _L3_cond2_in['g_out'], 'L3_ffn_router_w': _L3_ffn_in['router_w'], 'L3_ffn_router_b': _L3_ffn_in['router_b'], 'L3_ffn_w1': _L3_ffn_in['w1'], 'L3_ffn_b1': _L3_ffn_in['b1'], 'L3_ffn_w2': _L3_ffn_in['w2'], 'L3_ffn_b2': _L3_ffn_in['b2']}

def reference(x, cond_64, fside_16xSxS_0, mask_BxS_bf1, mask_BxS_bk0, L0_cond_g_norm, L0_cond_Wq, L0_cond_Wkv, L0_cond_q_scale, L0_cond_k_scale, L0_cond_null_attn_bias, L0_cond_w0, L0_cond_b0, L0_cond_g0, L0_cond_w1, L0_cond_b1, L0_cond_g1, L0_cond_w2, L0_cond_b2, L0_cond_Wout, L0_cond_g_out, L0_attn_Wq, L0_attn_Wk, L0_attn_Wv, L0_attn_Wo, L0_attn_rel, L0_attn_ln_gamma, L0_attn_ln_beta, L0_cond2_g_in, L0_cond2_null_attn_bias, L0_cond2_Wq, L0_cond2_Wkv, L0_cond2_Wo, L0_cond2_g_out, L0_ffn_gate_weight, L0_ffn_gate_up_proj, L0_ffn_down_proj, L0_ffn_similarity_matrix, L1_cond_wt, L1_cond_wg, L1_cond_w_gate, L1_cond_w_up, L1_cond_w_down, L1_cond_sw_gate, L1_cond_sw_up, L1_cond_sw_down, L1_attn_w_qkv, L1_attn_proj_matrix, L1_attn_w_out, L1_attn_b_out, L1_cond2_g_in, L1_cond2_null_attn_bias, L1_cond2_Wq, L1_cond2_Wkv, L1_cond2_Wo, L1_cond2_g_out, L1_ffn_W1, L1_ffn_b1, L1_ffn_quantum_phases, L1_ffn_quantum_weights_real, L1_ffn_quantum_weights_imag, L1_ffn_W2, L1_ffn_b2, L2_cond_wt, L2_cond_wg, L2_cond_w_gate, L2_cond_w_up, L2_cond_w_down, L2_cond_sw_gate, L2_cond_sw_up, L2_cond_sw_down, L2_attn_Wq, L2_attn_bq, L2_attn_Wk, L2_attn_bk, L2_attn_Wv, L2_attn_bv, L2_attn_Wo, L2_attn_bo, L2_cond2_wt, L2_cond2_wg, L2_cond2_w_gate, L2_cond2_w_up, L2_cond2_w_down, L2_cond2_sw_gate, L2_cond2_sw_up, L2_cond2_sw_down, L2_ffn_Wr, L2_ffn_br, L2_ffn_W1, L2_ffn_b1, L2_ffn_W2, L2_ffn_b2, L3_cond_wt, L3_cond_wg, L3_cond_w_gate, L3_cond_w_up, L3_cond_w_down, L3_cond_sw_gate, L3_cond_sw_up, L3_cond_sw_down, L3_attn_Wq, L3_attn_Wk, L3_attn_Wv, L3_attn_Wo, L3_attn_bo, L3_attn_ln1_g, L3_attn_ln1_b, L3_attn_W1, L3_attn_b1, L3_attn_W2, L3_attn_b2, L3_attn_ln2_g, L3_attn_ln2_b, L3_cond2_g_norm, L3_cond2_Wq, L3_cond2_Wkv, L3_cond2_q_scale, L3_cond2_k_scale, L3_cond2_null_attn_bias, L3_cond2_w0, L3_cond2_b0, L3_cond2_g0, L3_cond2_w1, L3_cond2_b1, L3_cond2_g1, L3_cond2_w2, L3_cond2_b2, L3_cond2_Wout, L3_cond2_g_out, L3_ffn_router_w, L3_ffn_router_b, L3_ffn_w1, L3_ffn_b1, L3_ffn_w2, L3_ffn_b2):
    import jax
    import jax.numpy as jnp

    def _L0_cond_ref(x, mask, g_norm, Wq, Wkv, q_scale, k_scale, null_kv, null_attn_bias, w0, b0, g0, w1, b1, g1, w2, b2, Wout, g_out):
        import jax, jax.numpy as jnp
        import numpy as np
        DIM = 128
        HEADS = 16
        DIM_HEAD = 64
        SCALE = 8.0

        def ln(x, g, eps=1e-05):
            mean = x.mean(axis=-1, keepdims=True)
            var = ((x - mean) ** 2).mean(axis=-1, keepdims=True)
            return (x - mean) * jax.lax.rsqrt(var + eps) * g

        def l2norm(t):
            n = jnp.maximum(jnp.linalg.norm(t, axis=-1, keepdims=True), 1e-12)
            return t / n

        def rel_pos_bias(n, w0, b0, g0, w1, b1, g1, w2, b2, dtype):
            pos = jnp.arange(-n + 1, n, dtype=dtype)[:, None]
            h = jax.nn.silu(ln(pos @ w0 + b0, g0))
            h = jax.nn.silu(ln(h @ w1 + b1, g1))
            h = h @ w2 + b2
            i = jnp.arange(n)
            idx = i[:, None] - i[None, :] + n - 1
            bias = h[idx]
            return jnp.transpose(bias, (2, 0, 1))
        b, n, _ = x.shape
        xn = ln(x, g_norm)
        q = (xn @ Wq).reshape(b, n, HEADS, DIM_HEAD).transpose(0, 2, 1, 3)
        kv = xn @ Wkv
        k, v = (kv[..., :DIM_HEAD], kv[..., DIM_HEAD:])
        nk = jnp.broadcast_to(null_kv[0], (b, 1, DIM_HEAD))
        nv = jnp.broadcast_to(null_kv[1], (b, 1, DIM_HEAD))
        k = jnp.concatenate([nk, k], axis=1)
        v = jnp.concatenate([nv, v], axis=1)
        q = l2norm(q) * q_scale
        k = l2norm(k) * k_scale
        sim = jnp.einsum('bhid,bjd->bhij', q, k) * SCALE
        bias = rel_pos_bias(n, w0, b0, g0, w1, b1, g1, w2, b2, q.dtype)
        null_bias = jnp.broadcast_to(null_attn_bias[:, None, None], (HEADS, n, 1))
        attn_bias = jnp.concatenate([null_bias, bias], axis=-1)
        sim = sim + attn_bias
        neg = -jnp.finfo(sim.dtype).max
        causal = jnp.triu(jnp.ones((n, n + 1), dtype=bool), k=2)
        sim = jnp.where(causal, neg, sim)
        m = jnp.pad(mask, ((0, 0), (1, 0)), constant_values=True)[:, None, None, :]
        sim = jnp.where(m, sim, neg)
        attn = jax.nn.softmax(sim, axis=-1)
        out = jnp.einsum('bhij,bjd->bhid', attn, v)
        out = out.transpose(0, 2, 1, 3).reshape(b, n, HEADS * DIM_HEAD)
        return ln(out @ Wout, g_out)

    def _L0_attn_ref(x, Wq, Wk, Wv, Wo, rel, ln_gamma, ln_beta):
        import math
        import jax, jax.numpy as jnp
        import numpy as np
        D_MODEL = 128
        HEADS = 16
        DH = D_MODEL // HEADS
        MAX_REL = 128
        LN_EPS = 1e-05

        def _layernorm(x, gamma, beta):
            mu = jnp.mean(x, axis=-1, keepdims=True)
            var = jnp.mean(jnp.square(x - mu), axis=-1, keepdims=True)
            return (x - mu) * jax.lax.rsqrt(var + LN_EPS) * gamma + beta
        B, T, D = x.shape
        x0 = x
        xn = _layernorm(x, ln_gamma, ln_beta)

        def proj(W):
            return (xn @ W.T).reshape(B, T, HEADS, DH).transpose(0, 2, 1, 3)
        q = proj(Wq) / math.sqrt(DH)
        k = proj(Wk)
        v = proj(Wv)
        scores = jnp.einsum('bhid,bhjd->bhij', q, k)
        i = jnp.arange(T)
        dist = jnp.clip(i[:, None] - i[None, :], 0, MAX_REL)
        bias = rel[:, dist]
        scores = scores + bias[None]
        causal = i[:, None] >= i[None, :]
        scores = jnp.where(causal[None, None], scores, -jnp.inf)
        attn = jax.nn.softmax(scores, axis=-1)
        y = jnp.einsum('bhij,bhjd->bhid', attn, v)
        y = y.transpose(0, 2, 1, 3).reshape(B, T, D)
        y = y @ Wo.T
        return x0 + y

    def _L0_cond2_ref(x, attn_bias, mask, g_in, null_attn_bias, null_kv, Wq, Wkv, Wo, g_out):
        import jax, jax.numpy as jnp
        import numpy as np
        B, N, DIM, H, DH = (2, 256, 128, 16, 64)
        INNER = H * DH
        EPS = 1e-05

        def layernorm(x, g):
            mean = jnp.mean(x, axis=-1, keepdims=True)
            var = jnp.var(x, axis=-1, keepdims=True)
            return (x - mean) * jax.lax.rsqrt(var + EPS) * g
        b, n, _ = x.shape
        scale = DH ** (-0.5)
        xn = layernorm(x, g_in)
        q = (xn @ Wq).reshape(b, n, H, DH).transpose(0, 2, 1, 3) * scale
        kv = xn @ Wkv
        k, v = (kv[..., :DH], kv[..., DH:])
        nk = jnp.broadcast_to(null_kv[0], (b, 1, DH))
        nv = jnp.broadcast_to(null_kv[1], (b, 1, DH))
        k = jnp.concatenate([nk, k], axis=1)
        v = jnp.concatenate([nv, v], axis=1)
        sim = jnp.einsum('bhid,bjd->bhij', q, k)
        null_col = jnp.broadcast_to(null_attn_bias[:, None, None], (H, n, 1))
        bias = jnp.concatenate([null_col, attn_bias], axis=-1)
        sim = sim + bias
        neg = -jnp.finfo(sim.dtype).max
        j = n + 1
        causal_mask = jnp.triu(jnp.ones((n, j), dtype=bool), k=j - n + 1)
        sim = jnp.where(causal_mask, neg, sim)
        mask_p = jnp.pad(mask, ((0, 0), (1, 0)), constant_values=True)
        sim = jnp.where(mask_p[:, None, None, :], sim, neg)
        attn = jax.nn.softmax(sim, axis=-1)
        out = jnp.einsum('bhij,bjd->bhid', attn, v)
        out = out.transpose(0, 2, 1, 3).reshape(b, n, INNER)
        out = out @ Wo
        return layernorm(out, g_out)

    def _L0_ffn_ref(hidden_states, gate_weight, gate_up_proj, down_proj, similarity_matrix):
        import jax, jax.numpy as jnp
        import numpy as np
        E = 8
        K = 2
        S = 1
        THRESHOLD = 0.7
        NORM_TOPK = True
        H = 128
        F = 128
        B, SEQ = (2, 128)
        b, s, h = hidden_states.shape
        x = hidden_states.reshape(-1, h)
        N = x.shape[0]
        logits = x @ gate_weight.T
        probs = jax.nn.softmax(logits.astype(jnp.float32), axis=-1)
        top_w, top_i = jax.lax.top_k(probs, K)
        if NORM_TOPK:
            top_w = top_w / jnp.clip(jnp.sum(top_w, -1, keepdims=True), 1e-12)
        primary_mask = jnp.zeros((E,), bool).at[top_i[:, :S].reshape(-1)].set(True)
        sim = jnp.where(primary_mask[None, :], similarity_matrix.astype(jnp.float32), -jnp.inf)
        best_j = jnp.argmax(sim, axis=-1)
        best_sim = jnp.max(sim, axis=-1)
        ids = jnp.arange(E)
        expert_map = jnp.where(~primary_mask & (best_sim >= THRESHOLD), best_j, ids)
        rerouted = expert_map[top_i]
        rows = jnp.arange(N)[:, None]
        dense = jnp.zeros((N, E), top_w.dtype).at[rows, rerouted].add(top_w)
        fw, fi = jax.lax.top_k(dense, K)
        combine = jnp.zeros((N, E), fw.dtype).at[rows, fi].add(jnp.where(fw > 0, fw, 0.0))
        gu = jnp.einsum('nh,efh->enf', x, gate_up_proj)
        g, u = jnp.split(gu, 2, axis=-1)
        hmid = jax.nn.silu(g) * u
        y = jnp.einsum('enf,ehf->enh', hmid, down_proj)
        out = jnp.einsum('ne,enh->nh', combine, y)
        return out.reshape(b, s, h)

    def _L1_cond_ref(hidden_states, g, wt, wg, w_gate, w_up, w_down, sw_gate, sw_up, sw_down):
        import jax, jax.numpy as jnp
        import numpy as np
        B, S, H = (4, 256, 128)
        E = 8
        M = 64
        K = 2
        N_SHARED = 2
        SM = M * N_SHARED
        G = 64
        GE_TEMP = 1.0
        ALPHA = 0.001
        SEQ_AUX = True
        NORM_TOPK = True
        COS_TEMP = 0.78
        CONS_ALPHA = 0.01
        LEAKY_SLOPE = 0.01
        EPS_COS = 1e-08

        def _leaky(x):
            return jnp.where(x >= 0, x, LEAKY_SLOPE * x)

        def _moe_forward(hidden_states, g, wt, wg, w_gate, w_up, w_down, sw_gate, sw_up, sw_down):
            b, s, h = hidden_states.shape
            x = hidden_states.reshape(-1, h)
            T = x.shape[0]
            logits_h = x @ wt.T
            logits_g = g @ wg.T
            logits_g = jnp.repeat(logits_g, s, axis=0)
            logits = (logits_h + logits_g / GE_TEMP) / (1.0 + 1.0 / GE_TEMP)
            scores = jax.nn.softmax(logits, axis=-1)
            topk_w, topk_idx = jax.lax.top_k(scores, K)
            if K > 1 and NORM_TOPK:
                topk_w = topk_w / (topk_w.sum(-1, keepdims=True) + 1e-20)
            onehot = jax.nn.one_hot(topk_idx.reshape(b, s * K), E, dtype=jnp.float32)
            ce = onehot.sum(1) / (s * K / E)
            aux_loss = (ce * scores.reshape(b, s, E).mean(1)).sum(1).mean() * ALPHA
            gp = _leaky(jnp.einsum('th,ehm->etm', x, w_gate))
            up = jnp.einsum('th,ehm->etm', x, w_up)
            y_all = jnp.einsum('etm,emh->eth', gp * up, w_down)
            y_sel = y_all[topk_idx, jnp.arange(T)[:, None], :]
            y = (y_sel * topk_w[..., None]).sum(1).reshape(b, s, h)
            p = _leaky(hidden_states @ sw_gate) * (hidden_states @ sw_up) @ sw_down
            y = y + p
            num = jnp.sum(y * p, -1)
            den = jnp.maximum(jnp.linalg.norm(y, axis=-1), EPS_COS) * jnp.maximum(jnp.linalg.norm(p, axis=-1), EPS_COS)
            closs = CONS_ALPHA * jnp.mean(num / den / (1.0 + COS_TEMP))
            return (y, aux_loss + closs)
        y, _ = _moe_forward(hidden_states, g, wt, wg, w_gate, w_up, w_down, sw_gate, sw_up, sw_down)
        return y

    def _L1_attn_ref(x, w_qkv, proj_matrix, w_out, b_out):
        import jax, jax.numpy as jnp
        import numpy as np
        DIM = 128
        HEADS = 16
        HEAD_DIM = DIM // HEADS
        FEAT = 32
        B, N = (4, 512)

        def _elu1(x):
            return jnp.where(x > 0, x + 1.0, jnp.exp(x))
        b, n, d = x.shape
        h, hd = (HEADS, HEAD_DIM)
        qkv = x @ w_qkv
        q, k, v = jnp.split(qkv, 3, axis=-1)
        to_heads = lambda t: t.reshape(b, n, h, hd).transpose(0, 2, 1, 3)
        q, k, v = (to_heads(q), to_heads(k), to_heads(v))
        q_proj = _elu1(jnp.einsum('bhnd,hdf->bhnf', q, proj_matrix))
        k_proj = _elu1(jnp.einsum('bhnd,hdf->bhnf', k, proj_matrix))
        kv = jnp.einsum('bhnf,bhnd->bhfd', k_proj, v)
        attn = jnp.einsum('bhnf,bhfd->bhnd', q_proj, kv)
        k_sum = k_proj.sum(axis=2)
        z = 1.0 / (jnp.einsum('bhnf,bhf->bhn', q_proj, k_sum) + 1e-08)
        attn = attn * z[..., None]
        out = attn.transpose(0, 2, 1, 3).reshape(b, n, d)
        return out @ w_out + b_out

    def _L1_cond2_ref(x, attn_bias, mask, g_in, null_attn_bias, null_kv, Wq, Wkv, Wo, g_out):
        import jax, jax.numpy as jnp
        import numpy as np
        B, N, DIM, H, DH = (2, 256, 128, 16, 64)
        INNER = H * DH
        EPS = 1e-05

        def layernorm(x, g):
            mean = jnp.mean(x, axis=-1, keepdims=True)
            var = jnp.var(x, axis=-1, keepdims=True)
            return (x - mean) * jax.lax.rsqrt(var + EPS) * g
        b, n, _ = x.shape
        scale = DH ** (-0.5)
        xn = layernorm(x, g_in)
        q = (xn @ Wq).reshape(b, n, H, DH).transpose(0, 2, 1, 3) * scale
        kv = xn @ Wkv
        k, v = (kv[..., :DH], kv[..., DH:])
        nk = jnp.broadcast_to(null_kv[0], (b, 1, DH))
        nv = jnp.broadcast_to(null_kv[1], (b, 1, DH))
        k = jnp.concatenate([nk, k], axis=1)
        v = jnp.concatenate([nv, v], axis=1)
        sim = jnp.einsum('bhid,bjd->bhij', q, k)
        null_col = jnp.broadcast_to(null_attn_bias[:, None, None], (H, n, 1))
        bias = jnp.concatenate([null_col, attn_bias], axis=-1)
        sim = sim + bias
        neg = -jnp.finfo(sim.dtype).max
        j = n + 1
        causal_mask = jnp.triu(jnp.ones((n, j), dtype=bool), k=j - n + 1)
        sim = jnp.where(causal_mask, neg, sim)
        mask_p = jnp.pad(mask, ((0, 0), (1, 0)), constant_values=True)
        sim = jnp.where(mask_p[:, None, None, :], sim, neg)
        attn = jax.nn.softmax(sim, axis=-1)
        out = jnp.einsum('bhij,bjd->bhid', attn, v)
        out = out.transpose(0, 2, 1, 3).reshape(b, n, INNER)
        out = out @ Wo
        return layernorm(out, g_out)

    def _L1_ffn_ref(x, W1, b1, quantum_phases, quantum_weights_real, quantum_weights_imag, W2, b2):
        import jax, jax.numpy as jnp
        import numpy as np
        B, S, D_MODEL, D_FF = (4, 256, 128, 512)

        def _quantum_transform(hidden, theta, w_real, w_imag):
            imag = w_imag * jnp.sin(theta + hidden * 0.1)
            quantum_phase = jnp.cos(theta) * w_real + jnp.sin(theta) * w_imag
            return hidden + quantum_phase * imag * 0.1
        hidden = jnp.einsum('bsd,df->bsf', x, W1) + b1
        q = _quantum_transform(hidden, quantum_phases, quantum_weights_real, quantum_weights_imag)
        act = jax.nn.relu(q)
        return jnp.einsum('bsf,fd->bsd', act, W2) + b2

    def _L2_cond_ref(hidden_states, g, wt, wg, w_gate, w_up, w_down, sw_gate, sw_up, sw_down):
        import jax, jax.numpy as jnp
        import numpy as np
        B, S, H = (4, 256, 128)
        E = 8
        M = 64
        K = 2
        N_SHARED = 2
        SM = M * N_SHARED
        G = 64
        GE_TEMP = 1.0
        ALPHA = 0.001
        SEQ_AUX = True
        NORM_TOPK = True
        COS_TEMP = 0.78
        CONS_ALPHA = 0.01
        LEAKY_SLOPE = 0.01
        EPS_COS = 1e-08

        def _leaky(x):
            return jnp.where(x >= 0, x, LEAKY_SLOPE * x)

        def _moe_forward(hidden_states, g, wt, wg, w_gate, w_up, w_down, sw_gate, sw_up, sw_down):
            b, s, h = hidden_states.shape
            x = hidden_states.reshape(-1, h)
            T = x.shape[0]
            logits_h = x @ wt.T
            logits_g = g @ wg.T
            logits_g = jnp.repeat(logits_g, s, axis=0)
            logits = (logits_h + logits_g / GE_TEMP) / (1.0 + 1.0 / GE_TEMP)
            scores = jax.nn.softmax(logits, axis=-1)
            topk_w, topk_idx = jax.lax.top_k(scores, K)
            if K > 1 and NORM_TOPK:
                topk_w = topk_w / (topk_w.sum(-1, keepdims=True) + 1e-20)
            onehot = jax.nn.one_hot(topk_idx.reshape(b, s * K), E, dtype=jnp.float32)
            ce = onehot.sum(1) / (s * K / E)
            aux_loss = (ce * scores.reshape(b, s, E).mean(1)).sum(1).mean() * ALPHA
            gp = _leaky(jnp.einsum('th,ehm->etm', x, w_gate))
            up = jnp.einsum('th,ehm->etm', x, w_up)
            y_all = jnp.einsum('etm,emh->eth', gp * up, w_down)
            y_sel = y_all[topk_idx, jnp.arange(T)[:, None], :]
            y = (y_sel * topk_w[..., None]).sum(1).reshape(b, s, h)
            p = _leaky(hidden_states @ sw_gate) * (hidden_states @ sw_up) @ sw_down
            y = y + p
            num = jnp.sum(y * p, -1)
            den = jnp.maximum(jnp.linalg.norm(y, axis=-1), EPS_COS) * jnp.maximum(jnp.linalg.norm(p, axis=-1), EPS_COS)
            closs = CONS_ALPHA * jnp.mean(num / den / (1.0 + COS_TEMP))
            return (y, aux_loss + closs)
        y, _ = _moe_forward(hidden_states, g, wt, wg, w_gate, w_up, w_down, sw_gate, sw_up, sw_down)
        return y

    def _L2_attn_ref(x, Wq, bq, Wk, bk, Wv, bv, Wo, bo):
        import jax, jax.numpy as jnp
        import numpy as np
        DIM = 128
        NUM_HEADS = 16
        NUM_KV_HEADS = 2
        HEAD_DIM = DIM // NUM_HEADS
        REPEATS = NUM_HEADS // NUM_KV_HEADS
        WINDOW = 32
        HALF = WINDOW // 2
        BATCH, SEQ = (2, 256)
        b, s, _ = x.shape
        q = (x @ Wq + bq).reshape(b, s, NUM_HEADS, HEAD_DIM).transpose(0, 2, 1, 3)
        k = (x @ Wk + bk).reshape(b, s, NUM_KV_HEADS, HEAD_DIM).transpose(0, 2, 1, 3)
        v = (x @ Wv + bv).reshape(b, s, NUM_KV_HEADS, HEAD_DIM).transpose(0, 2, 1, 3)
        kp = jnp.pad(k, ((0, 0), (0, 0), (HALF, HALF), (0, 0)))
        vp = jnp.pad(v, ((0, 0), (0, 0), (HALF, HALF), (0, 0)))
        idx = jnp.arange(s)[:, None] + jnp.arange(WINDOW)[None, :]
        k_win = kp[:, :, idx]
        v_win = vp[:, :, idx]
        qg = q.reshape(b, NUM_KV_HEADS, REPEATS, s, HEAD_DIM)
        scores = jnp.einsum('bgrsd,bgswd->bgrsw', qg, k_win)
        probs = jax.nn.softmax(scores, axis=-1)
        out = jnp.einsum('bgrsw,bgswd->bgrsd', probs, v_win)
        out = out.reshape(b, NUM_HEADS, s, HEAD_DIM).transpose(0, 2, 1, 3).reshape(b, s, DIM)
        return out @ Wo + bo

    def _L2_cond2_ref(hidden_states, g, wt, wg, w_gate, w_up, w_down, sw_gate, sw_up, sw_down):
        import jax, jax.numpy as jnp
        import numpy as np
        B, S, H = (4, 256, 128)
        E = 8
        M = 64
        K = 2
        N_SHARED = 2
        SM = M * N_SHARED
        G = 64
        GE_TEMP = 1.0
        ALPHA = 0.001
        SEQ_AUX = True
        NORM_TOPK = True
        COS_TEMP = 0.78
        CONS_ALPHA = 0.01
        LEAKY_SLOPE = 0.01
        EPS_COS = 1e-08

        def _leaky(x):
            return jnp.where(x >= 0, x, LEAKY_SLOPE * x)

        def _moe_forward(hidden_states, g, wt, wg, w_gate, w_up, w_down, sw_gate, sw_up, sw_down):
            b, s, h = hidden_states.shape
            x = hidden_states.reshape(-1, h)
            T = x.shape[0]
            logits_h = x @ wt.T
            logits_g = g @ wg.T
            logits_g = jnp.repeat(logits_g, s, axis=0)
            logits = (logits_h + logits_g / GE_TEMP) / (1.0 + 1.0 / GE_TEMP)
            scores = jax.nn.softmax(logits, axis=-1)
            topk_w, topk_idx = jax.lax.top_k(scores, K)
            if K > 1 and NORM_TOPK:
                topk_w = topk_w / (topk_w.sum(-1, keepdims=True) + 1e-20)
            onehot = jax.nn.one_hot(topk_idx.reshape(b, s * K), E, dtype=jnp.float32)
            ce = onehot.sum(1) / (s * K / E)
            aux_loss = (ce * scores.reshape(b, s, E).mean(1)).sum(1).mean() * ALPHA
            gp = _leaky(jnp.einsum('th,ehm->etm', x, w_gate))
            up = jnp.einsum('th,ehm->etm', x, w_up)
            y_all = jnp.einsum('etm,emh->eth', gp * up, w_down)
            y_sel = y_all[topk_idx, jnp.arange(T)[:, None], :]
            y = (y_sel * topk_w[..., None]).sum(1).reshape(b, s, h)
            p = _leaky(hidden_states @ sw_gate) * (hidden_states @ sw_up) @ sw_down
            y = y + p
            num = jnp.sum(y * p, -1)
            den = jnp.maximum(jnp.linalg.norm(y, axis=-1), EPS_COS) * jnp.maximum(jnp.linalg.norm(p, axis=-1), EPS_COS)
            closs = CONS_ALPHA * jnp.mean(num / den / (1.0 + COS_TEMP))
            return (y, aux_loss + closs)
        y, _ = _moe_forward(hidden_states, g, wt, wg, w_gate, w_up, w_down, sw_gate, sw_up, sw_down)
        return y

    def _L2_ffn_ref(x, Wr, br, W1, b1, W2, b2):
        import jax, jax.numpy as jnp
        import numpy as np
        D_MODEL, D_FF, N_EXP = (128, 512, 8)
        B, S, D = x.shape
        xf = x.reshape(-1, D)
        logits = xf @ Wr.T + br
        expert_idx = jnp.argmax(logits, axis=-1)
        h = jax.nn.relu(jnp.einsum('td,efd->etf', xf, W1) + b1[:, None, :])
        y = jnp.einsum('etf,edf->etd', h, W2) + b2[:, None, :]
        out = y[expert_idx, jnp.arange(xf.shape[0])]
        return out.reshape(B, S, D)

    def _L3_cond_ref(hidden_states, g, wt, wg, w_gate, w_up, w_down, sw_gate, sw_up, sw_down):
        import jax, jax.numpy as jnp
        import numpy as np
        B, S, H = (4, 256, 128)
        E = 8
        M = 64
        K = 2
        N_SHARED = 2
        SM = M * N_SHARED
        G = 64
        GE_TEMP = 1.0
        ALPHA = 0.001
        SEQ_AUX = True
        NORM_TOPK = True
        COS_TEMP = 0.78
        CONS_ALPHA = 0.01
        LEAKY_SLOPE = 0.01
        EPS_COS = 1e-08

        def _leaky(x):
            return jnp.where(x >= 0, x, LEAKY_SLOPE * x)

        def _moe_forward(hidden_states, g, wt, wg, w_gate, w_up, w_down, sw_gate, sw_up, sw_down):
            b, s, h = hidden_states.shape
            x = hidden_states.reshape(-1, h)
            T = x.shape[0]
            logits_h = x @ wt.T
            logits_g = g @ wg.T
            logits_g = jnp.repeat(logits_g, s, axis=0)
            logits = (logits_h + logits_g / GE_TEMP) / (1.0 + 1.0 / GE_TEMP)
            scores = jax.nn.softmax(logits, axis=-1)
            topk_w, topk_idx = jax.lax.top_k(scores, K)
            if K > 1 and NORM_TOPK:
                topk_w = topk_w / (topk_w.sum(-1, keepdims=True) + 1e-20)
            onehot = jax.nn.one_hot(topk_idx.reshape(b, s * K), E, dtype=jnp.float32)
            ce = onehot.sum(1) / (s * K / E)
            aux_loss = (ce * scores.reshape(b, s, E).mean(1)).sum(1).mean() * ALPHA
            gp = _leaky(jnp.einsum('th,ehm->etm', x, w_gate))
            up = jnp.einsum('th,ehm->etm', x, w_up)
            y_all = jnp.einsum('etm,emh->eth', gp * up, w_down)
            y_sel = y_all[topk_idx, jnp.arange(T)[:, None], :]
            y = (y_sel * topk_w[..., None]).sum(1).reshape(b, s, h)
            p = _leaky(hidden_states @ sw_gate) * (hidden_states @ sw_up) @ sw_down
            y = y + p
            num = jnp.sum(y * p, -1)
            den = jnp.maximum(jnp.linalg.norm(y, axis=-1), EPS_COS) * jnp.maximum(jnp.linalg.norm(p, axis=-1), EPS_COS)
            closs = CONS_ALPHA * jnp.mean(num / den / (1.0 + COS_TEMP))
            return (y, aux_loss + closs)
        y, _ = _moe_forward(hidden_states, g, wt, wg, w_gate, w_up, w_down, sw_gate, sw_up, sw_down)
        return y

    def _L3_attn_ref(x, Wq, Wk, Wv, Wo, bo, ln1_g, ln1_b, W1, b1, W2, b2, ln2_g, ln2_b):
        import jax, jax.numpy as jnp
        import numpy as np
        B, T, DIM = (2, 512, 128)
        DEPTH, HEADS = (4, 8)
        DH = DIM // HEADS
        NLOCAL, WINDOW, BUCKET = (4, 128, 64)
        MULT = 4

        def layer_norm(x, g, b, eps=1e-05):
            m = jnp.mean(x, -1, keepdims=True)
            v = jnp.mean(jnp.square(x - m), -1, keepdims=True)
            return (x - m) * jax.lax.rsqrt(v + eps) * g + b

        def causal_linear_attn(q, k, v):
            b, h, n, e = q.shape
            u = n // BUCKET
            q = jax.nn.softmax(q, axis=-1)
            k = jax.nn.elu(k) + 1.0
            bq = q.reshape(b, h, u, BUCKET, e)
            bk = k.reshape(b, h, u, BUCKET, e)
            bv = v.reshape(b, h, u, BUCKET, e)
            k_cum = jnp.cumsum(bk.sum(axis=-2), axis=-2)
            ctx = jnp.einsum('bhund,bhune->bhude', bk, bv)
            ctx = jnp.cumsum(ctx, axis=2)
            ctx = ctx / (k_cum[..., None] + 1e-06)
            ctx = jnp.pad(ctx, ((0, 0), (0, 0), (1, 0), (0, 0), (0, 0)))[:, :, :-1]
            out = jnp.einsum('bhund,bhude->bhune', bq, ctx)
            return out.reshape(b, h, n, e)

        def local_attn(q, k, v):
            b, lh, t, e = q.shape
            bh = b * lh
            nb = t // WINDOW
            bq = q.reshape(bh, nb, WINDOW, e)
            bk = k.reshape(bh, nb, WINDOW, e)
            bv = v.reshape(bh, nb, WINDOW, e)

            def look_around(x):
                padded = jnp.pad(x, ((0, 0), (1, 0), (0, 0), (0, 0)))
                return jnp.concatenate([padded[:, :-1], padded[:, 1:]], axis=2)
            bk2 = look_around(bk)
            bv2 = look_around(bv)
            tix = jnp.arange(t).reshape(1, nb, WINDOW)
            tpad = jnp.pad(tix, ((0, 0), (1, 0), (0, 0)), constant_values=-1)
            kix = jnp.concatenate([tpad[:, :-1], tpad[:, 1:]], axis=2)
            dots = jnp.einsum('bwie,bwje->bwij', bq, bk2) * e ** (-0.5)
            mask_value = -jnp.finfo(dots.dtype).max
            causal_mask = tix[:, :, :, None] < kix[:, :, None, :]
            pad_mask = (kix == -1)[:, :, None, :]
            dots = jnp.where(causal_mask | pad_mask, mask_value, dots)
            attn = jax.nn.softmax(dots, axis=-1)
            out = jnp.einsum('bwij,bwje->bwie', attn, bv2)
            return out.reshape(b, lh, t, e)

        def self_attention(x, Wq, Wk, Wv, Wo, bo):
            b, t, _ = x.shape
            mh = lambda z: z.reshape(b, t, HEADS, DH).transpose(0, 2, 1, 3)
            q, k, v = (mh(x @ Wq), mh(x @ Wk), mh(x @ Wv))
            lo = local_attn(q[:, :NLOCAL], k[:, :NLOCAL], v[:, :NLOCAL])
            go = causal_linear_attn(q[:, NLOCAL:], k[:, NLOCAL:], v[:, NLOCAL:])
            out = jnp.concatenate([lo, go], axis=1)
            out = out.transpose(0, 2, 1, 3).reshape(b, t, DIM)
            return out @ Wo + bo
        for i in range(DEPTH):
            x = x + self_attention(layer_norm(x, ln1_g[i], ln1_b[i]), Wq[i], Wk[i], Wv[i], Wo[i], bo[i])
            h = layer_norm(x, ln2_g[i], ln2_b[i])
            x = x + (jax.nn.gelu(h @ W1[i] + b1[i], approximate=False) @ W2[i] + b2[i])
        return x

    def _L3_cond2_ref(x, mask, g_norm, Wq, Wkv, q_scale, k_scale, null_kv, null_attn_bias, w0, b0, g0, w1, b1, g1, w2, b2, Wout, g_out):
        import jax, jax.numpy as jnp
        import numpy as np
        DIM = 128
        HEADS = 16
        DIM_HEAD = 64
        SCALE = 8.0

        def ln(x, g, eps=1e-05):
            mean = x.mean(axis=-1, keepdims=True)
            var = ((x - mean) ** 2).mean(axis=-1, keepdims=True)
            return (x - mean) * jax.lax.rsqrt(var + eps) * g

        def l2norm(t):
            n = jnp.maximum(jnp.linalg.norm(t, axis=-1, keepdims=True), 1e-12)
            return t / n

        def rel_pos_bias(n, w0, b0, g0, w1, b1, g1, w2, b2, dtype):
            pos = jnp.arange(-n + 1, n, dtype=dtype)[:, None]
            h = jax.nn.silu(ln(pos @ w0 + b0, g0))
            h = jax.nn.silu(ln(h @ w1 + b1, g1))
            h = h @ w2 + b2
            i = jnp.arange(n)
            idx = i[:, None] - i[None, :] + n - 1
            bias = h[idx]
            return jnp.transpose(bias, (2, 0, 1))
        b, n, _ = x.shape
        xn = ln(x, g_norm)
        q = (xn @ Wq).reshape(b, n, HEADS, DIM_HEAD).transpose(0, 2, 1, 3)
        kv = xn @ Wkv
        k, v = (kv[..., :DIM_HEAD], kv[..., DIM_HEAD:])
        nk = jnp.broadcast_to(null_kv[0], (b, 1, DIM_HEAD))
        nv = jnp.broadcast_to(null_kv[1], (b, 1, DIM_HEAD))
        k = jnp.concatenate([nk, k], axis=1)
        v = jnp.concatenate([nv, v], axis=1)
        q = l2norm(q) * q_scale
        k = l2norm(k) * k_scale
        sim = jnp.einsum('bhid,bjd->bhij', q, k) * SCALE
        bias = rel_pos_bias(n, w0, b0, g0, w1, b1, g1, w2, b2, q.dtype)
        null_bias = jnp.broadcast_to(null_attn_bias[:, None, None], (HEADS, n, 1))
        attn_bias = jnp.concatenate([null_bias, bias], axis=-1)
        sim = sim + attn_bias
        neg = -jnp.finfo(sim.dtype).max
        causal = jnp.triu(jnp.ones((n, n + 1), dtype=bool), k=2)
        sim = jnp.where(causal, neg, sim)
        m = jnp.pad(mask, ((0, 0), (1, 0)), constant_values=True)[:, None, None, :]
        sim = jnp.where(m, sim, neg)
        attn = jax.nn.softmax(sim, axis=-1)
        out = jnp.einsum('bhij,bjd->bhid', attn, v)
        out = out.transpose(0, 2, 1, 3).reshape(b, n, HEADS * DIM_HEAD)
        return ln(out @ Wout, g_out)

    def _L3_ffn_ref(x, router_w, router_b, w1, b1, w2, b2):
        import math
        import jax, jax.numpy as jnp
        import numpy as np
        D_MODEL = 128
        D_HIDDEN = 512
        N_EXPERTS = 8
        TOP_K = 2
        CAPACITY_FACTOR = 1.25
        B, T, D = x.shape
        N = B * T
        E = N_EXPERTS
        capacity = max(1, math.ceil(N / E * CAPACITY_FACTOR))
        x_flat = x.reshape(N, D)
        logits = x_flat.astype(jnp.float32) @ router_w + router_b
        gates = jax.nn.softmax(logits, axis=-1)
        _, topk_idx = jax.lax.top_k(gates, TOP_K)
        expert_mask = jax.nn.one_hot(topk_idx, E, dtype=jnp.int32).sum(1)
        pos = jnp.cumsum(expert_mask, axis=0) - 1
        expert_mask = expert_mask * (pos < capacity)
        valid = expert_mask > 0
        pos_c = jnp.where(valid, pos, capacity)
        e_idx = jnp.broadcast_to(jnp.arange(E), (N, E))
        dispatched = x_flat[:, None, :] * valid[:, :, None].astype(x.dtype)
        buf = jnp.zeros((E, capacity + 1, D), x.dtype).at[e_idx.ravel(), pos_c.ravel()].add(dispatched.reshape(N * E, D))
        buf = buf[:, :capacity]
        h = jax.nn.gelu(jnp.einsum('ecd,edh->ech', buf, w1) + b1[:, None, :], approximate=False)
        out = jnp.einsum('ech,ehd->ecd', h, w2) + b2[:, None, :]
        pos_g = jnp.minimum(pos_c, capacity - 1)
        gathered = out[e_idx, pos_g]
        weights = (gates * valid).astype(x.dtype)
        y = jnp.einsum('ned,ne->nd', gathered, weights)
        return y.reshape(B, T, D)
    x = x + _L0_attn_ref(_L0_cond_ref(x, mask_BxS_bf1, L0_cond_g_norm, L0_cond_Wq, L0_cond_Wkv, L0_cond_q_scale, L0_cond_k_scale, cond_64, L0_cond_null_attn_bias, L0_cond_w0, L0_cond_b0, L0_cond_g0, L0_cond_w1, L0_cond_b1, L0_cond_g1, L0_cond_w2, L0_cond_b2, L0_cond_Wout, L0_cond_g_out), L0_attn_Wq, L0_attn_Wk, L0_attn_Wv, L0_attn_Wo, L0_attn_rel, L0_attn_ln_gamma, L0_attn_ln_beta)
    x = x + _L0_ffn_ref(_L0_cond2_ref(x, fside_16xSxS_0, mask_BxS_bk0, L0_cond2_g_in, L0_cond2_null_attn_bias, cond_64, L0_cond2_Wq, L0_cond2_Wkv, L0_cond2_Wo, L0_cond2_g_out), L0_ffn_gate_weight, L0_ffn_gate_up_proj, L0_ffn_down_proj, L0_ffn_similarity_matrix)
    x = x + _L1_attn_ref(_L1_cond_ref(x, cond_64, L1_cond_wt, L1_cond_wg, L1_cond_w_gate, L1_cond_w_up, L1_cond_w_down, L1_cond_sw_gate, L1_cond_sw_up, L1_cond_sw_down), L1_attn_w_qkv, L1_attn_proj_matrix, L1_attn_w_out, L1_attn_b_out)
    x = x + _L1_ffn_ref(_L1_cond2_ref(x, fside_16xSxS_0, mask_BxS_bk0, L1_cond2_g_in, L1_cond2_null_attn_bias, cond_64, L1_cond2_Wq, L1_cond2_Wkv, L1_cond2_Wo, L1_cond2_g_out), L1_ffn_W1, L1_ffn_b1, L1_ffn_quantum_phases, L1_ffn_quantum_weights_real, L1_ffn_quantum_weights_imag, L1_ffn_W2, L1_ffn_b2)
    x = x + _L2_attn_ref(_L2_cond_ref(x, cond_64, L2_cond_wt, L2_cond_wg, L2_cond_w_gate, L2_cond_w_up, L2_cond_w_down, L2_cond_sw_gate, L2_cond_sw_up, L2_cond_sw_down), L2_attn_Wq, L2_attn_bq, L2_attn_Wk, L2_attn_bk, L2_attn_Wv, L2_attn_bv, L2_attn_Wo, L2_attn_bo)
    x = x + _L2_ffn_ref(_L2_cond2_ref(x, cond_64, L2_cond2_wt, L2_cond2_wg, L2_cond2_w_gate, L2_cond2_w_up, L2_cond2_w_down, L2_cond2_sw_gate, L2_cond2_sw_up, L2_cond2_sw_down), L2_ffn_Wr, L2_ffn_br, L2_ffn_W1, L2_ffn_b1, L2_ffn_W2, L2_ffn_b2)
    x = x + _L3_attn_ref(_L3_cond_ref(x, cond_64, L3_cond_wt, L3_cond_wg, L3_cond_w_gate, L3_cond_w_up, L3_cond_w_down, L3_cond_sw_gate, L3_cond_sw_up, L3_cond_sw_down), L3_attn_Wq, L3_attn_Wk, L3_attn_Wv, L3_attn_Wo, L3_attn_bo, L3_attn_ln1_g, L3_attn_ln1_b, L3_attn_W1, L3_attn_b1, L3_attn_W2, L3_attn_b2, L3_attn_ln2_g, L3_attn_ln2_b)
    x = x + _L3_ffn_ref(_L3_cond2_ref(x, mask_BxS_bf1, L3_cond2_g_norm, L3_cond2_Wq, L3_cond2_Wkv, L3_cond2_q_scale, L3_cond2_k_scale, cond_64, L3_cond2_null_attn_bias, L3_cond2_w0, L3_cond2_b0, L3_cond2_g0, L3_cond2_w1, L3_cond2_b1, L3_cond2_g1, L3_cond2_w2, L3_cond2_b2, L3_cond2_Wout, L3_cond2_g_out), L3_ffn_router_w, L3_ffn_router_b, L3_ffn_w1, L3_ffn_b1, L3_ffn_w2, L3_ffn_b2)
    return x

_drawn_inputs = setup_inputs


def setup_inputs(seed=0):
    import zlib

    import numpy as np

    out = dict(_drawn_inputs(seed))
    spreads = {'L0_cond_g_norm': (1.0, 0.2),
     'L0_cond_q_scale': (1.0, 0.2),
     'L0_cond_k_scale': (1.0, 0.2),
     'L0_cond_b0': (0.0, 0.373),
     'L0_cond_g0': (1.0, 0.6),
     'L0_cond_b1': (0.0, 0.1),
     'L0_cond_g1': (1.0, 0.6),
     'L0_cond_b2': (0.0, 0.282),
     'L0_cond_g_out': (1.0, 0.2),
     'L0_attn_ln_gamma': (1.0, 0.2),
     'L0_attn_ln_beta': (0.0, 0.1),
     'L0_cond2_g_in': (1.0, 0.6),
     'L0_cond2_g_out': (1.0, 0.6),
     'L1_cond2_g_in': (1.0, 0.2),
     'L1_cond2_g_out': (1.0, 0.2),
     'L1_ffn_b1': (0.0, 0.1),
     'L1_ffn_b2': (0.0, 0.1),
     'L3_attn_bo': (0.0, 0.8),
     'L3_attn_ln1_g': (1.0, 0.6),
     'L3_attn_ln1_b': (0.0, 2.0),
     'L3_attn_b1': (0.0, 2.0),
     'L3_attn_b2': (0.0, 0.8),
     'L3_attn_ln2_g': (1.0, 0.6),
     'L3_attn_ln2_b': (0.0, 2.0),
     'L3_cond2_g_norm': (1.0, 0.6),
     'L3_cond2_q_scale': (1.0, 0.6),
     'L3_cond2_k_scale': (1.0, 0.6),
     'L3_cond2_b0': (0.0, 2.0),
     'L3_cond2_g0': (1.0, 0.6),
     'L3_cond2_b1': (0.0, 2.0),
     'L3_cond2_g1': (1.0, 0.6),
     'L3_cond2_b2': (0.0, 2.0),
     'L3_cond2_g_out': (1.0, 0.6),
     'L3_ffn_router_b': (0.0, 2.0),
     'L3_ffn_b1': (0.0, 2.0),
     'L3_ffn_b2': (0.0, 2.0)}
    factors = {'L0_cond2_null_attn_bias': 8.0,
     'L0_cond2_Wq': 8.0,
     'L0_cond2_Wkv': 8.0,
     'L0_cond2_Wo': 7.79,
     'L0_ffn_gate_weight': 6.998,
     'L0_ffn_gate_up_proj': 7.883,
     'L0_ffn_down_proj': 7.845,
     'L0_ffn_similarity_matrix': 8.0,
     'L1_cond_wt': 2.726,
     'L1_cond_wg': 3.013,
     'L1_attn_proj_matrix': 8.0,
     'L1_attn_b_out': 4.578,
     'L1_cond2_Wq': 2.745,
     'L1_ffn_quantum_phases': 8.0,
     'L1_ffn_quantum_weights_real': 8.0,
     'L1_ffn_quantum_weights_imag': 8.0,
     'L2_attn_bq': 8.0,
     'L2_attn_bk': 64.0,
     'L2_attn_bv': 4.261,
     'L2_attn_bo': 4.347,
     'L2_ffn_b1': 28.448,
     'L2_ffn_b2': 22.528,
     'L3_attn_Wq': 64.0,
     'L3_attn_Wk': 64.0,
     'L3_cond2_Wq': 64.0,
     'L3_cond2_Wkv': 51.392,
     'L3_cond2_null_attn_bias': 64.0,
     'L3_cond2_w0': 64.0,
     'L3_cond2_w1': 64.0,
     'L3_cond2_w2': 64.0,
     'L3_cond2_Wout': 55.091,
     'L3_ffn_router_w': 64.0,
     'L3_ffn_w1': 64.0,
     'L3_ffn_w2': 64.0,
     'L3_cond_wg': 2.863,
     'L3_attn_Wv': 8.0,
     'L3_attn_Wo': 8.0,
     'L3_attn_W1': 8.0,
     'L3_attn_W2': 8.0}
    for name, (base, spread) in spreads.items():
        noise = np.random.default_rng([zlib.crc32(name.encode()), seed]).standard_normal(out[name].shape)
        drawn = base * np.exp(spread * noise) if base else spread * noise
        out[name] = jnp.asarray(drawn.astype(out[name].dtype))
    for name, factor in factors.items():
        out[name] = (out[name] * factor).astype(out[name].dtype)
    return out
```

```python
from contextlib import ExitStack

import concourse.bass as bass
from concourse import mybir

F32 = mybir.dt.float32
BF16 = mybir.dt.bfloat16
I32 = mybir.dt.int32
U8 = mybir.dt.uint8
ALU = mybir.AluOpType
ACT = mybir.ActivationFunctionType
AX = mybir.AxisListType

P = 128
B, N, D = 2, 512, 128
TOK = B * N
NT = TOK // P
TPB = N // P
HEADS = 16
DH = 64
INNER = HEADS * DH
E = 8
NEG = -1.0e30
EPS = 1e-5
TOEP = N + P - 1

DEBUG_NAMES = []
UPTO = 99


class Chain:

    def __init__(self, eng, sem):
        self.eng, self.sem, self.n = eng, sem, 0

    def __call__(self, ins, wait=True):
        ins.then_inc(self.sem, 1)
        self.n += 1
        if wait:
            self.eng.wait_ge(self.sem, self.n)

    def join(self):
        self.eng.wait_ge(self.sem, self.n)


class Stage:

    cleared = []

    def __init__(self, nc, name):
        self.nc, self.name, self.ctx, self.sems = nc, name, ExitStack(), []

    def sb(self, name, shape, dt=F32):
        return self.ctx.enter_context(self.nc.sbuf_tensor(f"{self.name}_{name}", shape, dt))

    def ps(self, name, shape, dt=F32):
        return self.ctx.enter_context(self.nc.psum_tensor(f"{self.name}_{name}", shape, dt))

    def sem(self, name):
        s = self.nc.alloc_semaphore(f"{self.name}_{name}")
        self.sems.append(s)
        return s

    def block(self):
        return self.ctx.enter_context(self.nc.Block())

    def __enter__(self):
        return self

    def __exit__(self, *a):
        done = self.ctx.__exit__(*a)
        if a[0] is None:
            for s in self.sems:
                self.nc.gpsimd.sem_clear(s)
            for s in Stage.cleared:
                self.nc.release_semaphore(s)
            Stage.cleared = self.sems
        return done


def dram_view(ap, offset, pattern):
    return bass.AP(tensor=ap.tensor, offset=offset, ap=pattern)


def row_to_all(ap, n, offset=0):
    if len(ap.shape) == 2 and ap.shape[0] == 1:
        return ap.partition_broadcast(P).rearrange("p a n -> p (a n)")
    return dram_view(ap, offset, [[0, P], [1, n]])


def rsqrt_rows(link, act_sqrt, var, root, r, t, eps):
    v = nc_vec(link)
    link(v.tensor_scalar(var, var, eps, None, ALU.add))
    act_sqrt()
    link(v.reciprocal(r, root))
    link(v.tensor_tensor(t, r, r, ALU.mult))
    link(v.tensor_tensor(t, t, var, ALU.mult))
    link(v.tensor_scalar(t, t, -0.5, 1.5, ALU.mult, ALU.add))
    link(v.tensor_tensor(r, r, t, ALU.mult))


def nc_vec(link):
    return link.eng


def layer_norm(nc, name, src, dst, gain, shift=None, dst_cols=None, ident=None, tiles=NT, silu=False):
    with Stage(nc, name) as st:
        g = st.sb("g", [P, D])
        s = st.sb("s", [P, D])
        stats = st.sb("stats", [P, tiles, 6])
        mv = st.sb("mv", [P, tiles, 2])
        var = st.sb("var", [P, tiles])
        root = st.sb("root", [P, tiles])
        rstd = st.sb("rstd", [P, tiles])
        tmp = st.sb("tmp", [P, tiles])
        turned = st.ps("turned", [P, tiles, P])
        loaded, chain, var_ready, root_ready, rows_ready, rows_silu, turned_ready, chain_act = (
            st.sem(x) for x in ("loaded", "chain", "var_ready", "root_ready", "rows_ready", "rows_silu",
                                "turned_ready", "chain_act"))
        n_loads = 16 * (1 + (shift is not None))
        block = st.block()

        @block.sync
        def _(sp):
            sp.dma_start(g[:, :], row_to_all(gain, D)).then_inc(loaded, 16)
            if shift is not None:
                sp.dma_start(s[:, :], row_to_all(shift, D)).then_inc(loaded, 16)

        @block.vector
        def _(dve):
            link = Chain(dve, chain)
            for t in range(tiles):
                link(dve.bn_stats(stats[:, t, :], src[:, t, :]), wait=False)
            for t in range(tiles):
                dve.wait_ge(chain, t + 1)
                link(dve.bn_aggr(mv[:, t, :], stats[:, t, :]), wait=False)
            link.join()
            link(dve.tensor_scalar(var[:, :], mv[:, :, 1], EPS, None, ALU.add))
            dve.engine_nop().then_inc(var_ready, 1)
            dve.wait_ge(root_ready, 1)
            link(dve.reciprocal(rstd[:, :], root[:, :]))
            link(dve.tensor_tensor(tmp[:, :], rstd[:, :], rstd[:, :], ALU.mult))
            link(dve.tensor_tensor(tmp[:, :], tmp[:, :], var[:, :], ALU.mult))
            link(dve.tensor_scalar(tmp[:, :], tmp[:, :], -0.5, 1.5, ALU.mult, ALU.add))
            link(dve.tensor_tensor(rstd[:, :], rstd[:, :], tmp[:, :], ALU.mult))
            for t in range(tiles):
                link(dve.tensor_scalar(dst[:, t, :], src[:, t, :], mv[:, t, 0:1], rstd[:, t:t + 1],
                                       ALU.subtract, ALU.mult), wait=False)
            dve.wait_ge(loaded, n_loads)
            link.join()
            for h in range(0, tiles, TPB):
                part = dst[:, h:h + TPB, :]
                mul = dve.tensor_tensor(part, part, g[:, None, :].to_broadcast([P, TPB, D]), ALU.mult)
                if shift is not None:
                    link(mul)
                    mul = dve.tensor_tensor(part, part, s[:, None, :].to_broadcast([P, TPB, D]), ALU.add)
                mul.then_inc(rows_ready, 1)
            if dst_cols is not None:
                dve.wait_ge(turned_ready, 1)
                dve.tensor_copy(dst_cols[:, 0:N], turned[:, 0:TPB, :])

        @block.scalar
        def _(act):
            act.wait_ge(var_ready, 1)
            act.activation(root[:, :], var[:, :], ACT.Sqrt).then_inc(root_ready, 1)
            if silu:
                for h in range(0, tiles, TPB):
                    act.wait_ge(rows_ready, h // TPB + 1)
                    part = dst[:, h:h + TPB, :]
                    act.activation(part, part, ACT.Silu).then_inc(rows_silu, 1)
            if dst_cols is not None and tiles > TPB:
                act.wait_ge(turned_ready, 2)
                act.activation(dst_cols[:, N:2 * N], turned[:, TPB:2 * TPB, :], ACT.Copy)

        @block.tensor
        def _(pe):
            if dst_cols is not None:
                for h in range(0, tiles, TPB):
                    pe.wait_ge(rows_silu if silu else rows_ready, h // TPB + 1)
                    for t in range(h, h + TPB):
                        last = pe.transpose(turned[:, t, :], dst[:, t, :], ident[:, :])
                    last.then_inc(turned_ready, 1)


def rows_to_columns(nc, name, src, dst_cols, ident):
    with Stage(nc, name) as st:
        turned = st.ps("turned", [P, NT, P])
        turned_ready = st.sem("turned_ready")
        block = st.block()

        @block.tensor
        def _(pe):
            for t in range(NT):
                last = pe.transpose(turned[:, t, :], src[:, t, :], ident[:, :])
                if t % TPB == TPB - 1:
                    last.then_inc(turned_ready, 1)

        @block.vector
        def _(dve):
            dve.wait_ge(turned_ready, 1)
            dve.tensor_copy(dst_cols[:, 0:N], turned[:, 0:TPB, :])

        @block.scalar
        def _(act):
            act.wait_ge(turned_ready, 2)
            act.activation(dst_cols[:, N:2 * N], turned[:, TPB:NT, :], ACT.Copy)


def add_columns(nc, name, cols, rows, ident, add=True):
    with Stage(nc, name) as st:
        turned = st.ps("turned", [P, NT, P])
        turned_ready = st.sem("turned_ready")
        block = st.block()

        @block.tensor
        def _(pe):
            for t in range(NT):
                last = pe.transpose(turned[:, t, :], cols[:, t * P:(t + 1) * P], ident[:, :])
                if t % TPB == TPB - 1:
                    last.then_inc(turned_ready, 1)

        @block.vector
        def _(dve):
            for h in range(2):
                dve.wait_ge(turned_ready, h + 1)
                part = rows[:, h * TPB:(h + 1) * TPB, :]
                if add:
                    dve.tensor_tensor(part, part, turned[:, h * TPB:(h + 1) * TPB, :], ALU.add)
                else:
                    dve.tensor_copy(part, turned[:, h * TPB:(h + 1) * TPB, :])


def shared_kv(nc, name, xn_cols, w_kv, null_kv, kT, k_null, v_rows, v_null, ident, k_gain=None, q_gain=None):
    with Stage(nc, name) as st:
        wkv = st.sb("wkv", [P, 2 * DH])
        kk = st.sb("kk", [P, NT, 2, DH])
        sq = st.sb("sq", [P, NT, DH])
        gain = st.sb("gain", [P, 2, DH])
        gcol = st.sb("gcol", [P, 2])
        nrm = st.sb("nrm", [P, NT + 1])
        root = st.sb("root", [P, NT + 1])
        rec = st.sb("rec", [P, NT + 1])
        tmp = st.sb("tmp", [P, NT + 1])
        sqn = st.sb("sqn", [P, 1])
        ones = st.sb("ones", [P, P])
        kv = st.ps("kv", [P, NT, 2 * DH])
        turned = st.ps("turned", [P, NT, P])
        nn = st.ps("nn", [P, 1])
        loaded, kv_ready, chain, k_ready, turned_ready, nrm_ready, root_ready, null_sq, null_len = (
            st.sem(x) for x in ("loaded", "kv_ready", "chain", "k_ready", "turned_ready", "nrm_ready",
                                "root_ready", "null_sq", "null_len"))
        n_loads = 16 * (4 + (6 if k_gain is not None else 0))
        block = st.block()

        @block.sync
        def _(sp):
            sp.dma_start(wkv[:, :], w_kv).then_inc(loaded, 16)
            sp.dma_start(v_null[:, :], row_to_all(null_kv, DH, DH)).then_inc(loaded, 16)
            for c in range(2):
                sp.dma_start(k_null[c * DH:(c + 1) * DH, :], dram_view(null_kv, 0, [[1, DH], [1, 1]]))\
                    .then_inc(loaded, 16)
            if k_gain is not None:
                for n, v in enumerate((k_gain, q_gain)):
                    sp.dma_start(gain[:, n, :], row_to_all(v, DH)).then_inc(loaded, 16)
                    for c in range(2):
                        sp.dma_start(gcol[c * DH:(c + 1) * DH, n:n + 1], dram_view(v, 0, [[1, DH], [1, 1]]))\
                            .then_inc(loaded, 16)

        @block.tensor
        def _(pe):
            pe.wait_ge(loaded, n_loads)
            for t in range(NT):
                last = pe.matmul(kv[:, t, :], xn_cols[:, t * P:(t + 1) * P], wkv[:, :], start=True, stop=True)
                if t % TPB == TPB - 1:
                    last.then_inc(kv_ready, 1)
            if k_gain is not None:
                pe.wait_ge(null_sq, 1)
                pe.matmul(nn[:, :], ones[0:DH, :], sqn[0:DH, :], start=True, stop=True).then_inc(null_len, 1)
            pe.wait_ge(k_ready, 1)
            for t in range(NT):
                last = pe.transpose(turned[:, t, :], kk[:, t, :, :], ident[:, :])
                if t % TPB == TPB - 1:
                    last.then_inc(turned_ready, 1)

        @block.scalar
        def _(act):
            if k_gain is not None:
                act.wait_ge(nrm_ready, 1)
                act.activation(root[:, :], nrm[:, :], ACT.Sqrt).then_inc(root_ready, 1)
            act.wait_ge(turned_ready, 2)
            act.activation(kT[:, N:2 * N], turned[:, TPB:NT, :], ACT.Copy)

        @block.vector
        def _(dve):
            link = Chain(dve, chain)
            link(dve.memset(ones[:, :], 1.0))
            dve.wait_ge(loaded, n_loads)
            dve.wait_ge(kv_ready, 2)
            link(dve.tensor_tensor(v_rows[:, :, :], kv[:, :, DH:2 * DH],
                                   v_null[:, None, :].to_broadcast([P, NT, DH]), ALU.subtract), wait=False)
            if k_gain is None:
                for c in range(2):
                    link(dve.tensor_scalar(kk[:, :, c, :], kv[:, :, 0:DH], DH ** -0.5, None, ALU.mult), wait=False)
                link(dve.tensor_scalar(k_null[:, :], k_null[:, :], DH ** -0.5, None, ALU.mult))
            else:
                link(dve.tensor_copy(kk[:, :, 0, :], kv[:, :, 0:DH]))
                link(dve.tensor_tensor(sq[:, :, :], kk[:, :, 0, :], kk[:, :, 0, :], ALU.mult))
                link(dve.tensor_reduce(nrm[:, 0:NT], sq[:, :, :], AX.X, ALU.add))
                dve.tensor_tensor(sqn[:, :], k_null[:, :], k_null[:, :], ALU.mult).then_inc(null_sq, 1)
                dve.wait_ge(null_len, 1)
                link(dve.tensor_copy(nrm[:, NT:NT + 1], nn[:, :]))
                link(dve.tensor_scalar(nrm[:, :], nrm[:, :], 1e-24, None, ALU.max))
                dve.engine_nop().then_inc(nrm_ready, 1)
                dve.wait_ge(root_ready, 1)
                link(dve.reciprocal(rec[:, :], root[:, :]))
                link(dve.tensor_tensor(tmp[:, :], rec[:, :], rec[:, :], ALU.mult))
                link(dve.tensor_tensor(tmp[:, :], tmp[:, :], nrm[:, :], ALU.mult))
                link(dve.tensor_scalar(tmp[:, :], tmp[:, :], -0.5, 1.5, ALU.mult, ALU.add))
                link(dve.tensor_tensor(rec[:, :], rec[:, :], tmp[:, :], ALU.mult))
                link(dve.tensor_tensor(gain[:, 0, :], gain[:, 0, :], gain[:, 1, :], ALU.mult))
                link(dve.tensor_tensor(kk[:, :, 0, :], kk[:, :, 0, :],
                                       rec[:, 0:NT, None].to_broadcast([P, NT, DH]), ALU.mult))
                link(dve.tensor_tensor(kk[:, :, 0, :], kk[:, :, 0, :],
                                       gain[:, 0:1, :].to_broadcast([P, NT, DH]), ALU.mult))
                link(dve.tensor_copy(kk[:, :, 1, :], kk[:, :, 0, :]))
                link(dve.tensor_tensor(gcol[:, 0:1], gcol[:, 0:1], gcol[:, 1:2], ALU.mult))
                link(dve.tensor_scalar(k_null[:, :], k_null[:, :], rec[:, NT:NT + 1], gcol[:, 0:1],
                                       ALU.mult, ALU.mult))
            dve.engine_nop().then_inc(k_ready, 1)
            dve.wait_ge(turned_ready, 1)
            dve.tensor_copy(kT[:, 0:N], turned[:, 0:TPB, :])


def query_lengths(nc, name, xn_cols, w_q, scale, rq):
    with Stage(nc, name) as st:
        wq = st.sb("wq", [P, INNER])
        sq = st.sb("sq", [P, 2, INNER])
        nrm = st.sb("nrm", [P, NT * HEADS])
        root = st.sb("root", [P, NT * HEADS])
        tmp = st.sb("tmp", [P, NT * HEADS])
        q = st.ps("q", [P, 2, INNER])
        loaded, q_ready, sq_ready, sq_read, nrm_ready, root_ready, chain = (
            st.sem(x) for x in ("loaded", "q_ready", "sq_ready", "sq_read", "nrm_ready", "root_ready", "chain"))
        block = st.block()

        @block.sync
        def _(sp):
            sp.dma_start(wq[:, :], w_q).then_inc(loaded, 16)

        @block.tensor
        def _(pe):
            pe.wait_ge(loaded, 16)
            for t in range(NT):
                if t >= 2:
                    pe.wait_ge(sq_ready, t - 1)
                for h in range(2):
                    last = pe.matmul(q[:, t % 2, h * N:(h + 1) * N], xn_cols[:, t * P:(t + 1) * P],
                                     wq[:, h * N:(h + 1) * N], start=True, stop=True)
                last.then_inc(q_ready, 1)

        @block.scalar
        def _(act):
            for t in range(NT):
                act.wait_ge(q_ready, t + 1)
                if t >= 2:
                    act.wait_ge(sq_read, t - 1)
                act.activation(sq[:, t % 2, :], q[:, t % 2, :], ACT.Square).then_inc(sq_ready, 1)
            act.wait_ge(nrm_ready, 1)
            act.activation(root[:, :], nrm[:, :], ACT.Sqrt).then_inc(root_ready, 1)

        @block.vector
        def _(dve):
            link = Chain(dve, chain)
            r = rq[:, :, :].rearrange("p t h -> p (t h)")
            for t in range(NT):
                dve.wait_ge(sq_ready, t + 1)
                dve.tensor_reduce(nrm[:, t * HEADS:(t + 1) * HEADS],
                                  sq[:, t % 2, :].rearrange("p (h d) -> p h d", h=HEADS), AX.X, ALU.add)\
                    .then_inc(sq_read, 1)
            dve.wait_ge(sq_read, NT)
            link(dve.tensor_scalar(nrm[:, :], nrm[:, :], 1e-24, None, ALU.max))
            dve.engine_nop().then_inc(nrm_ready, 1)
            dve.wait_ge(root_ready, 1)
            link(dve.reciprocal(r, root[:, :]))
            link(dve.tensor_tensor(tmp[:, :], r, r, ALU.mult))
            link(dve.tensor_tensor(tmp[:, :], tmp[:, :], nrm[:, :], ALU.mult))
            link(dve.tensor_scalar(tmp[:, :], tmp[:, :], -0.5 * scale, 1.5 * scale, ALU.mult, ALU.add))
            link(dve.tensor_tensor(r, r, tmp[:, :], ALU.mult))


def attend(nc, name, x_cols, w_q, O, v_rows, ident, identb, onesb, trib, dh=DH, w_k=None, q_scale=1.0, kT=None,
           k_null=None, null_row=None, v_null=None, key_mask=None, rq=None, side=None, toeplitz=None):
    null = k_null is not None
    UNITS = 2 * B * TPB
    PAIRS = HEADS // 2
    with Stage(nc, name) as st:
        wbuf = st.sb("wbuf", [P, 2, P])
        qbuf = st.sb("qbuf", [P, B, N])
        kbuf = st.sb("kbuf", [P, B, N]) if w_k is not None else None
        bias = st.sb("bias", [P, 4, TPB, N + 1]) if side is not None else None
        nrow = st.sb("nrow", [1, HEADS])
        onef = st.sb("onef", [1, P])
        S = st.sb("S", [P, 2, N + 1])
        Pr = st.sb("Pr", [P, 2, N + 1])
        PT = st.sb("PT", [P, 2, N])
        nmax = st.sb("nmax", [P, 8])
        rsum = st.sb("rsum", [P, 8])
        rinv = st.sb("rinv", [P, 8])
        psS = st.ps("psS", [P, 2, 2 * N])
        psT = st.ps("psT", [P, 2, N])
        psO = st.ps("psO", [P, N])
        psQ = st.ps("psQ", [P, N])
        (w_in, q_out, q_in, s_out, biased, maxed, probs, pt_out, pt_even, pt_odd, pv_out, inv, o_in,
         consts, w_clear, cleared) = (
            st.sem(x) for x in ("w_in", "q_out", "q_in", "s_out", "biased", "maxed", "probs", "pt_out",
                                "pt_even", "pt_odd", "pv_out", "inv", "o_in", "consts", "w_clear",
                                "cleared"))
        bias_in = [st.sem(f"bias_in{hh}") for hh in range(2)]
        NQ = 1 if w_k is None else 2
        W_INC = 16 * (2 if w_k is None else 4)
        block = st.block()

        def unit(u):
            b, hh, qt = u // (2 * TPB), u // TPB % 2, u % TPB
            return b, hh, qt, (qt + 1) * P

        def mod4(pair, hh):
            return (pair % 2) * 2 + hh

        @block.sync
        def _(sp):
            if null_row is not None:
                sp.dma_start(nrow[:, :], dram_view(null_row, 0, [[HEADS, 1], [1, HEADS]])).then_inc(consts, 16)
            if dh < DH:
                sp.wait_ge(w_clear, 1)

            def load_weights(pair):
                for n, w in enumerate((w_q, w_k)[:NQ]):
                    for hh in range(2):
                        sp.dma_start(wbuf[:, n, hh * DH:hh * DH + dh], w[:, bass.ds(pair * (2 * dh) + hh * dh, dh)])\
                            .then_inc(w_in, 16)

            def load_bias(pair, first):
                for hh in range(2):
                    if not first:
                        sp.wait_ge(biased, pair * UNITS - UNITS + TPB * hh + 1)
                    for qt in range(TPB):
                        n = (qt + 1) * P
                        src = side[bass.ds(pair * 2 + hh, 1), qt * P:(qt + 1) * P, 0:n]\
                            .rearrange("a p j -> p (a j)")
                        sp.dma_start(bias[:, bass.ds(mod4(pair, hh), 1), qt, N - n:N]
                                     .rearrange("p a j -> p (a j)"), src).then_inc(bias_in[hh], 16)

            load_weights(0)
            if side is not None:
                load_bias(0, True)
            with sp.Fori(1, PAIRS) as pair:
                sp.wait_ge(q_out, pair * (2 * NQ))
                load_weights(pair)
                if side is not None:
                    load_bias(pair, False)

        @block.tensor
        def _(pe):
            def project(pair, b):
                pe.wait_ge(w_in, pair * W_INC + W_INC)
                for n in range(NQ):
                    if b or n or not isinstance(pair, int) or pair:
                        pe.wait_ge(q_in, pair * (2 * NQ) + b * NQ + n)
                    pe.matmul(psQ[:, :], wbuf[:, n, :], x_cols[:, b * N:(b + 1) * N],
                              start=True, stop=True).then_inc(q_out, 1)

            def scores(pair, u, first):
                b, hh, qt, n = unit(u)
                g = pair * UNITS + u
                if u % (2 * TPB) == 0:
                    pe.wait_ge(q_in, pair * (2 * NQ) + (b + 1) * NQ)
                if not first or u >= 2:
                    pe.wait_ge(biased, g - 1)
                rows = slice(hh * DH, hh * DH + dh)
                q = qbuf[rows, b, qt * P:(qt + 1) * P]
                keys = kbuf[rows, b, 0:n] if w_k is not None else kT[rows, b * N:b * N + n]
                out = psS[:, u % 2, :]
                if key_mask is not None:
                    pe.matmul(out[:, 0:n], onesb[:, :], key_mask[:, b * N:b * N + n], start=True, stop=False,
                              skip_group_check=True)
                if side is not None:
                    pe.matmul(out[:, n - P:n], identb[:, :], trib[:, :], start=key_mask is None, stop=False,
                              skip_group_check=True)
                last = pe.matmul(out[:, 0:n], q, keys, start=key_mask is None and side is None, stop=True,
                                 skip_group_check=True)
                if null:
                    last = pe.matmul(out[:, n:n + 1], q, k_null[rows, :], start=n == N,
                                     stop=null_row is None, skip_group_check=True)
                    if null_row is not None:
                        last = pe.matmul(out[:, n:n + 1], onef[:, :], nrow[:, bass.ds(pair * 2 + hh, 1)],
                                         start=False, stop=True, skip_group_check=True)
                last.then_inc(s_out, 1)

            def turn(pair, u, first):
                _, _, qt, n = unit(u % UNITS)
                g = pair * UNITS + u
                pe.wait_ge(probs, g + 1)
                if not first or u >= 2:
                    pe.wait_ge((pt_even, pt_odd)[u % 2], pair * (UNITS // 2) + u // 2)
                for k in range(qt + 1):
                    last = pe.transpose(psT[:, u % 2, k * P:(k + 1) * P], Pr[:, u % 2, k * P:(k + 1) * P],
                                        ident[:, :])
                last.then_inc(pt_out, 1)

            def values(pair, u, first):
                b, hh, qt, n = unit(u % UNITS)
                g = pair * UNITS + u
                pe.wait_ge((pt_even, pt_odd)[u % 2], pair * (UNITS // 2) + u // 2 + 1)
                if not first or u >= 1:
                    pe.wait_ge(o_in, g)
                for k in range(qt + 1):
                    v = v_rows[:, b * TPB + k, :] if kT is not None else \
                        v_rows[:, b * TPB + k, bass.ds(pair * (2 * dh) + hh * dh, dh)]
                    last = pe.matmul(psO[:, 0:dh], PT[:, u % 2, k * P:(k + 1) * P], v,
                                     start=k == 0, stop=k == qt)
                last.then_inc(pv_out, 1)

            def body(pair, first, last):
                for u in range(UNITS):
                    if u == 0:
                        project(pair, 1)
                    if u == UNITS // 2 and not last:
                        project(pair + 1, 0)
                    scores(pair, u, first)
                    if u >= 1:
                        turn(pair, u - 1, first)
                    elif not first:
                        turn(pair - 1, UNITS - 1, False)
                    if u >= 2:
                        values(pair, u - 2, first)
                    elif not first:
                        values(pair - 1, UNITS - 2 + u, False)

            pe.wait_ge(consts, 1 + (16 if null_row is not None else 0))
            project(0, 0)
            body(0, True, False)
            with pe.Fori(1, PAIRS - 1) as pair:
                body(pair, False, False)
            body(PAIRS - 1, False, True)
            turn(PAIRS - 1, UNITS - 1, False)
            values(PAIRS - 1, UNITS - 2, False)
            values(PAIRS - 1, UNITS - 1, False)

        @block.scalar
        def _(act):
            def copy_q(pair, b, first):
                for n in range(NQ):
                    m = pair * (2 * NQ) + b * NQ + n
                    act.wait_ge(q_out, m + 1)
                    if n == 0 and not (first and (b or isinstance(pair, int) and pair == 0)):
                        act.wait_ge(s_out, pair * UNITS - UNITS // 2 * (1 - b))
                    dst = (qbuf, kbuf)[n][:, b, :]
                    act.activation(dst, psQ[:, :], ACT.Copy, scale=q_scale if n == 0 else 1.0).then_inc(q_in, 1)

            def exps(pair, u, first):
                _, _, _, n = unit(u)
                g = pair * UNITS + u
                act.wait_ge(maxed, g + 1)
                if not first or u >= 2:
                    act.wait_ge(pt_out, g - 1)
                w = n + null
                act.activation(Pr[:, u % 2, 0:w], S[:, u % 2, 0:w], ACT.Exp, bias=nmax[:, u % 8:u % 8 + 1],
                               accum_out=rsum[:, u % 8:u % 8 + 1]).then_inc(probs, 1)

            def copy_pt(pair, u, first):
                _, _, _, n = unit(u)
                g = pair * UNITS + u
                act.wait_ge(pt_out, g + 1)
                if not first or u >= 2:
                    act.wait_ge(pv_out, g - 1)
                act.activation(PT[:, 0, 0:n], psT[:, 0, 0:n], ACT.Copy).then_inc(pt_even, 1)

            def body(pair, first, last):
                for u in range(UNITS):
                    if u == 0:
                        copy_q(pair, 1, first)
                    if u == UNITS // 2 and not last:
                        copy_q(pair + 1, 0, False)
                    exps(pair, u, first)
                    if u % 2:
                        copy_pt(pair, u - 1, first)

            copy_q(0, 0, True)
            body(0, True, False)
            with act.Fori(1, PAIRS - 1) as pair:
                body(pair, False, False)
            body(PAIRS - 1, False, True)

        @block.vector
        def _(dve):
            def score_bias(pair, u, first):
                b, hh, qt, n = unit(u)
                g = pair * UNITS + u
                w = n + null
                dve.wait_ge(s_out, g + 1)
                if not first or u >= 2:
                    dve.wait_ge(probs, g - 1)
                if side is not None and u in (0, TPB):
                    dve.wait_ge(bias_in[hh], pair * (16 * TPB) + 16 * TPB)
                if side is not None:
                    add = bias[:, bass.ds(mod4(pair, hh), 1), qt, N - n:N - n + w]
                else:
                    add = toeplitz[:, bass.ds(pair * 2 + hh, 1), N - n:N - n + w]
                add = add.rearrange("p a j -> p (a j)")
                scale = 1.0 if rq is None else \
                    rq[:, b * TPB + qt, bass.ds(pair * 2 + hh, 1)]
                dve.scalar_tensor_tensor(out=S[:, u % 2, 0:w], in0=psS[:, u % 2, 0:w], scalar=scale, in1=add,
                                         op0=ALU.mult, op1=ALU.add).then_inc(biased, 1)
                dve.wait_ge(biased, g + 1)
                dve.tensor_reduce(nmax[:, u % 8:u % 8 + 1], S[:, u % 2, 0:w], AX.X, ALU.max, negate=True)\
                    .then_inc(maxed, 1)

            def copy_pt(pair, u, first):
                _, _, _, n = unit(u)
                g = pair * UNITS + u
                dve.wait_ge(pt_out, g + 1)
                if not first or u >= 2:
                    dve.wait_ge(pv_out, g - 1)
                dve.tensor_copy(PT[:, 1, 0:n], psT[:, 1, 0:n]).then_inc(pt_odd, 1)

            def outputs(pair, u):
                b, hh, qt, _ = unit(u)
                g = pair * UNITS + u
                s = u % 8
                dve.wait_ge(pv_out, g + 1)
                dve.reciprocal(rinv[:, s:s + 1], rsum[:, s:s + 1]).then_inc(inv, 1)
                dve.wait_ge(inv, g + 1)
                dst = O[:, b * TPB + qt, bass.ds(pair * (2 * dh) + hh * dh, dh)]
                if null:
                    dve.scalar_tensor_tensor(out=dst, in0=psO[:, 0:dh], scalar=rinv[:, s:s + 1],
                                             in1=v_null[:, :], op0=ALU.mult, op1=ALU.add).then_inc(o_in, 1)
                else:
                    dve.tensor_scalar(dst, psO[:, 0:dh], rinv[:, s:s + 1], None, ALU.mult)\
                        .then_inc(o_in, 1)

            def body(pair, first, last):
                for u in range(UNITS):
                    if u >= 3:
                        outputs(pair, u - 3)
                    elif not first:
                        outputs(pair - 1, UNITS - 3 + u)
                    score_bias(pair, u, first)
                    if u % 2 == 0 and u:
                        copy_pt(pair, u - 1, first)
                    elif u == 0 and not first:
                        copy_pt(pair - 1, UNITS - 1, False)

            dve.memset(onef[:, :], 1.0).then_inc(consts, 1)
            if dh < DH:
                dve.memset(wbuf[:, :, :], 0.0).then_inc(w_clear, 1)
            if side is not None:
                dve.memset(bias[:, :, :, N:N + 1], 0.0).then_inc(cleared, 1)
            if side is not None:
                dve.wait_ge(cleared, 1)
            body(0, True, False)
            with dve.Fori(1, PAIRS - 1) as pair:
                body(pair, False, False)
            body(PAIRS - 1, False, True)
            outputs(PAIRS - 1, UNITS - 3)
            copy_pt(PAIRS - 1, UNITS - 1, False)
            for u in range(UNITS - 2, UNITS):
                outputs(PAIRS - 1, u)


def project_rows(nc, name, O, width, w_out, dst, addends, ident):
    CH = width // P
    with Stage(nc, name) as st:
        w = st.sb("w", [P, CH, D])
        OT = st.sb("OT", [P, 2, CH, P])
        turned = st.ps("turned", [P, 2, CH * P if CH > 1 else N])
        y = st.ps("y", [P, 2, N])
        loaded, turned_ready, ot_ready, y_ready, y_read, chain = (
            st.sem(x) for x in ("loaded", "turned_ready", "ot_ready", "y_ready", "y_read", "chain"))
        block = st.block()

        @block.sync
        def _(sp):
            sp.dma_start(w[:, :, :], w_out.rearrange("(c p) n -> p c n", p=P)).then_inc(loaded, 16)

        @block.tensor
        def _(pe):
            def product(t):
                if t == 0:
                    pe.wait_ge(loaded, 16)
                pe.wait_ge(ot_ready, t + 1)
                if t >= 2:
                    pe.wait_ge(y_read, t - 1)
                for c in range(CH):
                    last = pe.matmul(y[:, t % 2, 0:D], OT[:, t % 2, c, :], w[:, c, :], start=c == 0, stop=c == CH - 1)
                last.then_inc(y_ready, 1)

            for t in range(NT):
                if t >= 2:
                    pe.wait_ge(ot_ready, t - 1)
                for c in range(CH):
                    last = pe.transpose(turned[:, t % 2, c * P:(c + 1) * P], O[:, t, c * P:(c + 1) * P], ident[:, :])
                last.then_inc(turned_ready, 1)
                if t >= 1:
                    product(t - 1)
            product(NT - 1)

        @block.scalar
        def _(act):
            for t in range(NT):
                act.wait_ge(turned_ready, t + 1)
                if t >= 2:
                    act.wait_ge(y_ready, t - 1)
                act.activation(OT[:, t % 2, :, :], turned[:, t % 2, 0:CH * P], ACT.Copy).then_inc(ot_ready, 1)

        @block.vector
        def _(dve):
            link = Chain(dve, chain)
            for t in range(NT):
                dve.wait_ge(y_ready, t + 1)
                if not addends:
                    dve.tensor_copy(dst[:, t, :], y[:, t % 2, 0:D]).then_inc(y_read, 1)
                    continue
                dve.tensor_tensor(dst[:, t, :], y[:, t % 2, 0:D], addends[0](t), ALU.add).then_inc(y_read, 1)
                for a in addends[1:]:
                    dve.wait_ge(y_read, t + 1)
                    link(dve.tensor_tensor(dst[:, t, :], dst[:, t, :], a(t), ALU.add))


def toeplitz_from_table(nc, name, table, scratch, T, C, null_bias=None):
    with Stage(nc, name) as st:
        nb = st.sb("nb", [P, HEADS])
        turned = st.sb("turned", [P, HEADS, N])
        ps = st.ps("ps", [P, 4, N])
        stored, loaded, flipped, out_v, out_a = (
            st.sem(x) for x in ("stored", "loaded", "flipped", "out_v", "out_a"))
        spread = [st.sem(f"spread{h}") for h in range(4)]
        block = st.block()

        @block.sync
        def _(sp):
            sp.dma_start(scratch, table[:, :]).then_inc(stored, 16)
            if null_bias is not None:
                sp.dma_start(nb[:, :], row_to_all(null_bias, HEADS)).then_inc(loaded, 16)
            sp.wait_ge(stored, 16)
            for q in range(4):
                sp.dma_start(turned[:, q * 4:(q + 1) * 4, :],
                             dram_view(scratch, q * 4 * TOEP, [[1, P], [TOEP, 4], [1, N]])).then_inc(spread[q], 16)

        @block.tensor
        def _(pe):
            for h in range(HEADS):
                if h % 4 == 0:
                    pe.wait_ge(spread[h // 4], 16)
                if h >= 4:
                    pe.wait_ge((out_v, out_a)[h % 2], (h - 4) // 2 + 1)
                pe.matmul(ps[:, h % 4, :], C.flip[:, :], turned[:, h, :], start=True, stop=True)\
                    .then_inc(flipped, 1)

        @block.scalar
        def _(act):
            for h in range(1, HEADS, 2):
                act.wait_ge(flipped, h + 1)
                act.activation(T[:, h, 0:N], ps[:, h % 4, :], ACT.Copy).then_inc(out_a, 1)

        @block.vector
        def _(dve):
            for h in range(0, HEADS, 2):
                dve.wait_ge(flipped, h + 1)
                dve.tensor_copy(T[:, h, 0:N], ps[:, h % 4, :]).then_inc(out_v, 1)
            if null_bias is not None:
                dve.wait_ge(loaded, 16)
                dve.tensor_copy(T[:, :, N], nb[:, :])


def position_bias(nc, name, I, pre, T, scratch, C):
    ident = C.ident
    h = nc.sbuf_tensor
    with ExitStack() as ctx:
        rows = ctx.enter_context(h(f"{name}_rows", [P, TPB, D], F32))
        cols = ctx.enter_context(h(f"{name}_cols", [P, N], F32))
        table = ctx.enter_context(h(f"{name}_table", [HEADS, TOEP], F32))
        with Stage(nc, name + "_in") as st:
            w0 = st.sb("w0", [P, D])
            b0 = st.sb("b0", [P, D])
            posi = st.sb("posi", [P, TPB], I32)
            pos = st.sb("pos", [P, TPB])
            loaded, made, conv = (st.sem(x) for x in ("loaded", "made", "conv"))
            block = st.block()

            @block.sync
            def _(sp):
                sp.dma_start(w0[:, :], row_to_all(I[pre + "w0"], D)).then_inc(loaded, 16)
                sp.dma_start(b0[:, :], row_to_all(I[pre + "b0"], D)).then_inc(loaded, 16)

            @block.gpsimd
            def _(pool):
                pool.iota(posi[:, :], pattern=[[-P, TPB]], base=N - 1, channel_multiplier=-1).then_inc(made, 1)

            @block.vector
            def _(dve):
                dve.wait_ge(made, 1)
                dve.tensor_copy(pos[:, :], posi[:, :]).then_inc(conv, 1)
                dve.wait_ge(conv, 1)
                dve.wait_ge(loaded, 32)
                for t in range(TPB):
                    dve.scalar_tensor_tensor(out=rows[:, t, :], in0=w0[:, :], scalar=pos[:, t:t + 1], in1=b0[:, :],
                                             op0=ALU.mult, op1=ALU.add)

        layer_norm(nc, name + "_n0", rows, rows, I[pre + "g0"], dst_cols=cols, ident=ident, tiles=TPB, silu=True)
        with Stage(nc, name + "_mid") as st:
            w1 = st.sb("w1", [P, D])
            b1 = st.sb("b1", [P, D])
            y = st.ps("y", [P, TPB, D])
            loaded, y_ready = (st.sem(x) for x in ("loaded", "y_ready"))
            block = st.block()

            @block.sync
            def _(sp):
                sp.dma_start(w1[:, :], I[pre + "w1"]).then_inc(loaded, 16)
                sp.dma_start(b1[:, :], row_to_all(I[pre + "b1"], D)).then_inc(loaded, 16)

            @block.tensor
            def _(pe):
                pe.wait_ge(loaded, 32)
                for t in range(TPB):
                    last = pe.matmul(y[:, t, :], cols[:, t * P:(t + 1) * P], w1[:, :], start=True, stop=True)
                last.then_inc(y_ready, 1)

            @block.vector
            def _(dve):
                dve.wait_ge(y_ready, 1)
                dve.wait_ge(loaded, 32)
                dve.tensor_tensor(rows[:, :, :], y[:, :, :], b1[:, None, :].to_broadcast([P, TPB, D]), ALU.add)

        layer_norm(nc, name + "_n1", rows, rows, I[pre + "g1"], dst_cols=cols, ident=ident, tiles=TPB, silu=True)
        with Stage(nc, name + "_out") as st:
            w2 = st.sb("w2", [P, HEADS])
            b2 = st.sb("b2", [HEADS, 1])
            y = st.ps("y", [HEADS, N])
            loaded, y_ready = (st.sem(x) for x in ("loaded", "y_ready"))
            block = st.block()

            @block.sync
            def _(sp):
                sp.dma_start(w2[:, :], I[pre + "w2"]).then_inc(loaded, 16)
                sp.dma_start(b2[:, :], dram_view(I[pre + "b2"], 0, [[1, HEADS], [1, 1]])).then_inc(loaded, 16)

            @block.tensor
            def _(pe):
                pe.wait_ge(loaded, 32)
                pe.matmul(y[:, :], w2[:, :], cols[:, :], start=True, stop=True).then_inc(y_ready, 1)

            @block.vector
            def _(dve):
                dve.memset(table[:, N:TOEP], NEG)
                dve.wait_ge(loaded, 32)
                dve.wait_ge(y_ready, 1)
                dve.tensor_scalar(table[:, 0:N], y[:, :], b2[:, 0:1], None, ALU.add)

        toeplitz_from_table(nc, name + "_spread", table, scratch, T, C, I[pre + "null_attn_bias"])


def distance_bias(nc, name, rel, T, scratch, C):
    R = rel.shape[1]
    with ExitStack() as ctx:
        table = ctx.enter_context(nc.sbuf_tensor(f"{name}_table", [HEADS, TOEP], F32))
        with Stage(nc, name + "_in") as st:
            r = st.sb("r", [HEADS, R])
            loaded = st.sem("loaded")
            block = st.block()

            @block.sync
            def _(sp):
                sp.dma_start(r[:, :], rel).then_inc(loaded, 16)

            @block.vector
            def _(dve):
                dve.memset(table[:, N:TOEP], NEG)
                dve.wait_ge(loaded, 16)
                dve.tensor_copy(table[:, N - R + 1:N], r[:, 1:R])
                dve.tensor_copy(table[:, 0:N - R + 1], r[:, 0:1].to_broadcast([HEADS, N - R + 1]))
        toeplitz_from_table(nc, name + "_spread", table, scratch, T, C)


def cosine_attention(nc, name, I, pre, src, dst, C, scratch):
    with ExitStack() as ctx:
        def sb(n, shape, dt=F32):
            return ctx.enter_context(nc.sbuf_tensor(f"{name}_{n}", shape, dt))
        T = sb("T", [P, HEADS, N + 1])
        xn = sb("xn", [P, NT, D])
        xn_cols = sb("xn_cols", [P, TOK])
        kT = sb("kT", [P, TOK])
        k_null = sb("k_null", [P, 1])
        v_rows = sb("v_rows", [P, NT, DH])
        v_null = sb("v_null", [P, DH])
        rq = sb("rq", [P, NT, HEADS])
        O = sb("O", [P, NT, INNER])
        position_bias(nc, name + "_pos", I, pre, T, scratch, C)
        layer_norm(nc, name + "_ln", src, xn, I[pre + "g_norm"], dst_cols=xn_cols, ident=C.ident)
        shared_kv(nc, name + "_kv", xn_cols, I[pre + "Wkv"], I["cond_64"], kT, k_null, v_rows, v_null, C.ident,
                  I[pre + "k_scale"], I[pre + "q_scale"])
        query_lengths(nc, name + "_ql", xn_cols, I[pre + "Wq"], 8.0, rq)
        attend(nc, name + "_at", xn_cols, I[pre + "Wq"], O, v_rows, C.ident, C.identb, C.onesb, C.trib, kT=kT,
               k_null=k_null, v_null=v_null, key_mask=C.mask_bf1, rq=rq, toeplitz=T)
        project_rows(nc, name + "_o", O, INNER, I[pre + "Wout"], dst, (), C.ident)
    layer_norm(nc, name + "_ln2", dst, dst, I[pre + "g_out"])


def biased_attention(nc, name, I, pre, src, dst, dst_cols, C):
    with ExitStack() as ctx:
        def sb(n, shape, dt=F32):
            return ctx.enter_context(nc.sbuf_tensor(f"{name}_{n}", shape, dt))
        xn = sb("xn", [P, NT, D])
        xn_cols = sb("xn_cols", [P, TOK])
        kT = sb("kT", [P, TOK])
        k_null = sb("k_null", [P, 1])
        v_rows = sb("v_rows", [P, NT, DH])
        v_null = sb("v_null", [P, DH])
        O = sb("O", [P, NT, INNER])
        layer_norm(nc, name + "_ln", src, xn, I[pre + "g_in"], dst_cols=xn_cols, ident=C.ident)
        shared_kv(nc, name + "_kv", xn_cols, I[pre + "Wkv"], I["cond_64"], kT, k_null, v_rows, v_null, C.ident)
        attend(nc, name + "_at", xn_cols, I[pre + "Wq"], O, v_rows, C.ident, C.identb, C.onesb, C.trib, kT=kT,
               k_null=k_null, null_row=I[pre + "null_attn_bias"], v_null=v_null, key_mask=C.mask_bk0,
               side=I["fside_16xSxS_0"])
        project_rows(nc, name + "_o", O, INNER, I[pre + "Wo"], dst, (), C.ident)
    layer_norm(nc, name + "_ln2", dst, dst, I[pre + "g_out"], dst_cols=dst_cols, ident=C.ident)


def distance_attention(nc, name, I, pre, src, X, C, scratch):
    with ExitStack() as ctx:
        def sb(n, shape, dt=F32):
            return ctx.enter_context(nc.sbuf_tensor(f"{name}_{n}", shape, dt))
        T = sb("T", [P, HEADS, N + 1])
        xn = sb("xn", [P, NT, D])
        xn_cols = sb("xn_cols", [P, TOK])
        v_rows = sb("v_rows", [P, NT, D])
        O = sb("O", [P, NT, D])
        distance_bias(nc, name + "_b", I[pre + "rel"], T, scratch, C)
        layer_norm(nc, name + "_ln", src, xn, I[pre + "ln_gamma"], I[pre + "ln_beta"], dst_cols=xn_cols,
                   ident=C.ident)
        linear_rows(nc, name + "_v", xn_cols, I[pre + "Wv"], D, v_rows)
        attend(nc, name + "_at", xn_cols, I[pre + "Wq"], O, v_rows, C.ident, C.identb, C.onesb, C.trib, dh=8,
               w_k=I[pre + "Wk"], q_scale=8 ** -0.5, toeplitz=T)
        project_rows(nc, name + "_o", O, D, I[pre + "Wo"], X,
                     (lambda t: X[:, t, :], lambda t: src[:, t, :]), C.ident)


def linear_rows(nc, name, x_cols, w, width, dst):
    with Stage(nc, name) as st:
        ws = st.sb("w", [P, width])
        y = st.ps("y", [P, NT, width])
        loaded, y_ready = (st.sem(x) for x in ("loaded", "y_ready"))
        block = st.block()

        @block.sync
        def _(sp):
            sp.dma_start(ws[:, :], w).then_inc(loaded, 16)

        @block.tensor
        def _(pe):
            pe.wait_ge(loaded, 16)
            for t in range(NT):
                last = pe.matmul(y[:, t, :], x_cols[:, t * P:(t + 1) * P], ws[:, :], start=True, stop=True)
            last.then_inc(y_ready, 1)

        @block.vector
        def _(dve):
            dve.wait_ge(y_ready, 1)
            dve.tensor_copy(dst[:, :, :], y[:, :, :])


def first_maximum(link, dve, s, best, onehot, place, C):
    shape = [s.shape[0], s.shape[1], E]
    desc = C.desc[0:shape[0], None, :].to_broadcast(shape)
    link(dve.tensor_reduce(best, s, AX.X, ALU.max))
    link(dve.tensor_tensor(onehot, s, best.unsqueeze(2).to_broadcast(shape), ALU.is_equal))
    link(dve.tensor_tensor(onehot, onehot, desc, ALU.mult))
    link(dve.tensor_reduce(place, onehot, AX.X, ALU.max))
    link(dve.tensor_tensor(onehot, desc, place.unsqueeze(2).to_broadcast(shape), ALU.is_equal))


def route(nc, name, x_cols, w, C, cT, softmax=True, temper=1.0, group=None, bias=None, top=2, norm=None,
          capacity=None, similarity=None):
    with Stage(nc, name) as st:
        ws = st.sb("w", [P, E])
        wg = st.sb("wg", [DH, E])
        gcol = st.sb("gcol", [DH, B])
        gb = st.sb("gb", [DH, B, P])
        br = st.sb("br", [P, E])
        s = st.sb("s", [P, NT, E])
        r = st.sb("r", [P, NT, E])
        oh1 = st.sb("oh1", [P, NT, E])
        oh2 = st.sb("oh2", [P, NT, E])
        m1, m2, den, place = (st.sb(x, [P, NT]) for x in ("m1", "m2", "den", "place"))
        sim = st.sb("sim", [E, 1, E])
        simm = st.sb("simm", [E, 1, E])
        move = st.sb("move", [E, 1, E])
        prim = st.sb("prim", [E, 1, E])
        cond = st.sb("cond", [E, 4])
        c0 = st.sb("c0", [E, TOK])
        L = st.ps("L", [P, NT, E])
        cnt = st.ps("cnt", [P, NT, E])
        tot = st.ps("tot", [P, NT, E])
        turned = st.ps("turned", [E, TOK])
        moved = st.ps("moved", [E, TOK])
        loaded, gb_ready, logits, chain, shifted, expd, w_ready, turned_ready, c0_ready, moved_ready, counted, mask_ready = (
            st.sem(x) for x in ("loaded", "gb_ready", "logits", "chain", "shifted", "expd", "w_ready",
                                "turned_ready", "c0_ready", "moved_ready", "counted", "mask_ready"))
        n_loads = 16 * (1 + (2 if group else 0) + (bias is not None) + (similarity is not None))
        block = st.block()

        @block.sync
        def _(sp):
            sp.dma_start(ws[:, :], w).then_inc(loaded, 16)
            if group:
                sp.dma_start(wg[:, :], group[0]).then_inc(loaded, 16)
                sp.dma_start(gcol[:, :], group[1]).then_inc(loaded, 16)
            if bias is not None:
                sp.dma_start(br[:, :], row_to_all(bias, E)).then_inc(loaded, 16)
            if similarity is not None:
                sp.dma_start(sim[:, 0, :], similarity).then_inc(loaded, 16)

        @block.tensor
        def _(pe):
            pe.wait_ge(loaded, n_loads)
            if group:
                pe.wait_ge(gb_ready, 1)
            for t in range(NT):
                last = pe.matmul(L[:, t, :], x_cols[:, t * P:(t + 1) * P], ws[:, :], start=True, stop=not group)
                if group:
                    last = pe.matmul(L[:, t, :], gb[:, t // TPB, :], wg[:, :], start=False, stop=True)
            last.then_inc(logits, 1)
            if similarity is not None:
                pe.wait_ge(mask_ready, 1)
                for t in range(NT):
                    pe.matmul(cnt[0:E, 0, :], C.ones[:, 0:E], oh1[:, t, :], start=t == 0, stop=t == NT - 1)
                for t in range(NT):
                    last = pe.matmul(tot[0:E, 0, 0:1], oh1[:, t, :], C.ones[:, 0:1], start=t == 0, stop=t == NT - 1)
                last.then_inc(counted, 1)
            if capacity is not None:
                pe.wait_ge(mask_ready, 1)
                pe.matmul(cnt[:, :, :], C.upto[:, :], oh2[:, :, :], start=True, stop=True)
                pe.matmul(tot[:, :, :], C.ones[:, :], oh2[:, :, :], start=True, stop=True).then_inc(counted, 1)
            pe.wait_ge(w_ready, 1)
            for t in range(NT):
                last = pe.transpose(turned[:, t * P:(t + 1) * P], r[:, t, :], C.ident[:, :])
            last.then_inc(turned_ready, 1)
            if similarity is not None:
                pe.wait_ge(c0_ready, 1)
                for h in range(B):
                    last = pe.matmul(moved[:, h * N:(h + 1) * N], move[:, 0, :], c0[:, h * N:(h + 1) * N],
                                     start=True, stop=True)
                last.then_inc(moved_ready, 1)

        @block.scalar
        def _(act):
            if softmax:
                act.wait_ge(shifted, 1)
                act.activation(s[:, :, :], s[:, :, :], ACT.Exp, scale=temper).then_inc(expd, 1)

        @block.vector
        def _(dve):
            link = Chain(dve, chain)
            dve.wait_ge(loaded, n_loads)
            if group:
                for b in range(B):
                    last = dve.tensor_copy(gb[:, b, :], gcol[:, b:b + 1].to_broadcast([DH, P]))
                last.then_inc(gb_ready, 1)
            dve.wait_ge(logits, 1)

            def over(x):
                return x[:, :].unsqueeze(2).to_broadcast([P, NT, E])

            if bias is not None:
                link(dve.tensor_tensor(s[:, :, :], L[:, :, :], br[:, None, :].to_broadcast([P, NT, E]), ALU.add))
            else:
                link(dve.tensor_copy(s[:, :, :], L[:, :, :]))
            if softmax:
                link(dve.tensor_reduce(m1[:, :], s[:, :, :], AX.X, ALU.max))
                link(dve.tensor_tensor(s[:, :, :], s[:, :, :], over(m1), ALU.subtract))
                dve.engine_nop().then_inc(shifted, 1)
                dve.wait_ge(expd, 1)
                link(dve.tensor_reduce(den[:, :], s[:, :, :], AX.X, ALU.add))
                link(dve.reciprocal(den[:, :], den[:, :]))
                link(dve.tensor_tensor(s[:, :, :], s[:, :, :], over(den), ALU.mult))
            first_maximum(link, dve, s[:, :, :], m1[:, :], oh1[:, :, :], place[:, :], C)
            if similarity is not None:
                dve.engine_nop().then_inc(mask_ready, 1)
            if top == 1:
                link(dve.tensor_copy(r[:, :, :], oh1[:, :, :]))
            else:
                link(dve.scalar_tensor_tensor(out=r[:, :, :], in0=oh1[:, :, :], scalar=-4.0, in1=s[:, :, :],
                                              op0=ALU.mult, op1=ALU.add))
                first_maximum(link, dve, r[:, :, :], m2[:, :], oh2[:, :, :], place[:, :], C)
                link(dve.tensor_tensor(oh2[:, :, :], oh1[:, :, :], oh2[:, :, :], ALU.add))
                link(dve.tensor_tensor(r[:, :, :], s[:, :, :], oh2[:, :, :], ALU.mult))
            if norm is not None:
                link(dve.tensor_tensor(den[:, :], m1[:, :], m2[:, :], ALU.add))
                link(dve.tensor_scalar(den[:, :], den[:, :], norm[1], None, norm[0]))
                link(dve.reciprocal(den[:, :], den[:, :]))
                link(dve.tensor_tensor(r[:, :, :], r[:, :, :], over(den), ALU.mult))
            if capacity is not None:
                dve.engine_nop().then_inc(mask_ready, 1)
                dve.wait_ge(counted, 1)
                link(dve.memset(s[:, 0, :], 0.0))
                for t in range(1, NT):
                    link(dve.tensor_tensor(s[:, t, :], s[:, t - 1, :], tot[:, t - 1, :], ALU.add))
                link(dve.tensor_tensor(s[:, :, :], s[:, :, :], cnt[:, :, :], ALU.add))
                link(dve.tensor_scalar(s[:, :, :], s[:, :, :], float(capacity), None, ALU.is_le))
                link(dve.tensor_tensor(r[:, :, :], r[:, :, :], s[:, :, :], ALU.mult))
            if similarity is not None:
                dve.wait_ge(counted, 1)
                link(dve.tensor_scalar(prim[:, :, :], cnt[0:E, 0:1, :], 1.0, None, ALU.min))
                link(dve.tensor_tensor(simm[:, :, :], sim[:, :, :], prim[:, :, :], ALU.mult))
                link(dve.tensor_scalar(prim[:, :, :], prim[:, :, :], 1.0, -NEG, ALU.subtract, ALU.mult))
                link(dve.tensor_tensor(simm[:, :, :], simm[:, :, :], prim[:, :, :], ALU.add))
                first_maximum(link, dve, simm[:, :, :], cond[:, 0:1], move[:, :, :], cond[:, 1:2], C)
                link(dve.tensor_scalar(cond[:, 2:3], tot[0:E, 0, 0:1], 0.5, None, ALU.is_lt))
                link(dve.tensor_scalar(cond[:, 0:1], cond[:, 0:1], 0.7, cond[:, 2:3], ALU.is_ge, ALU.mult))
                link(dve.tensor_scalar(cond[:, 3:4], cond[:, 0:1], -1.0, 1.0, ALU.mult, ALU.add))
                link(dve.tensor_scalar(move[:, 0, :], move[:, 0, :], cond[:, 0:1], None, ALU.mult))
                link(dve.scalar_tensor_tensor(out=move[:, 0, :], in0=C.ident[0:E, 0:E], scalar=cond[:, 3:4],
                                              in1=move[:, 0, :], op0=ALU.mult, op1=ALU.add))
            dve.engine_nop().then_inc(w_ready, 1)
            dve.wait_ge(turned_ready, 1)
            if similarity is None:
                dve.tensor_copy(cT[:, :], turned[:, :])
            else:
                dve.tensor_copy(c0[:, :], turned[:, :]).then_inc(c0_ready, 1)
                dve.wait_ge(moved_ready, 1)
                dve.tensor_copy(cT[:, :], moved[:, :])


def gated_experts(nc, name, x_cols, w_gate, w_up, w_down, chunk, n_chunks, shared, leaky, cT, C, dst):
    per = P // chunk
    units = n_chunks * P
    steps = [(c, h) for c in range(n_chunks) for h in range(B)]
    if shared:
        steps = [(-1, h) for h in range(B)] + steps
    with Stage(nc, name) as st:
        wg = st.sb("wg", [P, units])
        wu = st.sb("wu", [P, units])
        wd = st.sb("wd", [P, n_chunks, D])
        sg = st.sb("sg", [P, 3, P])
        sel = st.sb("sel", [E, n_chunks, P])
        gs = st.sb("gs", [P, 2, N])
        lk = st.sb("lk", [P, 2, N])
        hid = st.sb("hid", [P, 2, N])
        psG = st.ps("psG", [P, N])
        psU = st.ps("psU", [P, 2, N])
        psB = st.ps("psB", [P, 2, N])
        psY = st.ps("psY", [P, B, N])
        (loaded, sel_made, g_out, u_out, g_in, chain, hid_ready, y_out, scaled) = (
            st.sem(x) for x in ("loaded", "sel_made", "g_out", "u_out", "g_in", "chain", "hid_ready", "y_out",
                                "scaled"))
        shared_in = st.sem("shared_in")
        block = st.block()

        @block.sync
        def _(sp):
            if shared:
                for n, w in enumerate(shared):
                    sp.dma_start(sg[:, n, :], w).then_inc(shared_in, 16)
            sp.dma_start(wg[:, :], w_gate).then_inc(loaded, 16)
            sp.dma_start(wu[:, :], w_up).then_inc(loaded, 16)
            sp.dma_start(wd[:, :, :], w_down.rearrange("(c p) n -> p c n", p=P)).then_inc(loaded, 16)

        @block.gpsimd
        def _(pool):
            pool.memset(sel[:, :, :], 0.0).then_inc(sel_made, 1)
            pool.wait_ge(sel_made, 1)
            v = sel[:, :, :].rearrange("e c (k m) -> e c k m", k=per)
            pool.affine_select(out=v, in_=v, compare_op=ALU.not_equal, fill=1.0, base=0,
                               pattern=[[-per, n_chunks], [-1, per], [0, chunk]], channel_multiplier=1)\
                .then_inc(sel_made, 1)

        @block.tensor
        def _(pe):
            def down(k):
                c, h = steps[k]
                pe.wait_ge(hid_ready, k + 1)
                w = sg[:, 2, :] if c < 0 else wd[:, c, :]
                pe.matmul(psY[:, h, :], w, hid[:, k % 2, :], start=k < 2, stop=k >= len(steps) - 2,
                          skip_group_check=True).then_inc(y_out, 1)

            pe.wait_ge(sel_made, 2)
            for k, (c, h) in enumerate(steps):
                if c < 0:
                    pe.wait_ge(shared_in, 48)
                else:
                    pe.wait_ge(loaded, 48)
                x = x_cols[:, h * N:(h + 1) * N]
                if k >= 1:
                    pe.wait_ge(g_in, k)
                g, u = (sg[:, 0, :], sg[:, 1, :]) if c < 0 else (wg[:, c * P:(c + 1) * P], wu[:, c * P:(c + 1) * P])
                pe.matmul(psG[:, :], g, x, start=True, stop=True).then_inc(g_out, 1)
                if k >= 2:
                    pe.wait_ge(hid_ready, k - 1)
                last = pe.matmul(psU[:, k % 2, :], u, x, start=True, stop=True)
                if c >= 0:
                    last = pe.matmul(psB[:, k % 2, :], sel[:, c, :], cT[:, h * N:(h + 1) * N], start=True, stop=True)
                last.then_inc(u_out, 1)
                if k >= 1:
                    down(k - 1)
            down(len(steps) - 1)

        @block.scalar
        def _(act):
            for k in range(len(steps)):
                act.wait_ge(g_out, k + 1)
                if k >= 2:
                    act.wait_ge(scaled, k - 1)
                act.activation(gs[:, k % 2, :], psG[:, :], ACT.Copy if leaky else ACT.Silu).then_inc(g_in, 1)
            act.wait_ge(y_out, len(steps))
            act.activation(dst[:, N:2 * N], psY[:, 1, :], ACT.Copy)

        @block.vector
        def _(dve):
            link = Chain(dve, chain)
            for k, (c, h) in enumerate(steps):
                dve.wait_ge(g_in, k + 1)
                a = gs[:, k % 2, :]
                if leaky:
                    link(dve.scalar_tensor_tensor(out=lk[:, k % 2, :], in0=a, scalar=0.01, in1=a,
                                                  op0=ALU.mult, op1=ALU.max))
                    a = lk[:, k % 2, :]
                dve.wait_ge(u_out, k + 1)
                if k >= 2:
                    dve.wait_ge(y_out, k - 1)
                mul = dve.tensor_tensor(hid[:, k % 2, :], a, psU[:, k % 2, :], ALU.mult)
                mul.then_inc(scaled, 1)
                dve.wait_ge(scaled, k + 1)
                if c >= 0:
                    dve.tensor_tensor(hid[:, k % 2, :], hid[:, k % 2, :], psB[:, k % 2, :], ALU.mult)\
                        .then_inc(hid_ready, 1)
                else:
                    dve.engine_nop().then_inc(hid_ready, 1)
            dve.wait_ge(y_out, len(steps))
            dve.tensor_copy(dst[:, 0:N], psY[:, 0, :])


def grouped_experts(nc, name, I, pre, x_cols, dst, C):
    with ExitStack() as ctx:
        cT = ctx.enter_context(nc.sbuf_tensor(f"{name}_cT", [E, TOK], F32))
        route(nc, name + "_r", x_cols, I[pre + "wt"], C, cT, temper=0.5, group=(I[pre + "wg"], I["cond_64_T"]),
              norm=(ALU.add, 1e-20))
        gated_experts(nc, name + "_x", x_cols, I[pre + "w_gate"], I[pre + "w_up"],
                      I[pre + "w_down"], DH, E * DH // P,
                      tuple(I[pre + w] for w in ("sw_gate", "sw_up", "sw_down")), True, cT, C, dst)


def rerouted_experts(nc, name, I, pre, x_cols, dst, C):
    with ExitStack() as ctx:
        cT = ctx.enter_context(nc.sbuf_tensor(f"{name}_cT", [E, TOK], F32))
        route(nc, name + "_r", x_cols, I[pre + "gate_weight"], C, cT, norm=(ALU.max, 1e-12),
              similarity=I[pre + "similarity_matrix"])
        gated_experts(nc, name + "_x", x_cols, I[pre + "gate"], I[pre + "up"], I[pre + "down"], P, E, None,
                      False, cT, C, dst)


def linear_attention(nc, name, I, pre, x_cols, X, C):
    F, HD = 32, 8
    CH = HEADS * F // P
    with ExitStack() as ctx:
        def sb(n, shape, dt=F32):
            return ctx.enter_context(nc.sbuf_tensor(f"{name}_{n}", shape, dt))
        qT = sb("qT", [P, TOK])
        kT = sb("kT", [P, TOK])
        v1 = sb("v1", [P, NT, D + 1])
        bd = sb("bd", [P, CH, P])
        own = sb("own", [P, F])
        w = sb("w", [P, 3 * D])
        qf = sb("qf", [P, CH, TOK])
        kf = sb("kf", [P, NT, CH * P])
        kv = sb("kv", [P, B, CH, 2, F])
        outT = sb("outT", [P, TOK])
        with Stage(nc, name + "_qkv") as st:
            ps = st.ps("ps", [P, 4, N])
            pv = st.ps("pv", [P, NT, P])
            loaded, made, ready, v_ready, bd_in, cleared = (
                st.sem(x) for x in ("loaded", "made", "ready", "v_ready", "bd_in", "cleared"))
            block = st.block()

            @block.sync
            def _(sp):
                sp.dma_start(w[:, :], I[pre + "w_qkv"]).then_inc(loaded, 16)
                sp.wait_ge(cleared, 1)
                for h in range(HEADS):
                    sp.dma_start(bd[h * HD:(h + 1) * HD, h // 4, h % 4 * F:(h % 4 + 1) * F],
                                 I[pre + "proj_matrix"][h, :, :]).then_inc(bd_in, 16)
                sp.wait_ge(bd_in, 16 * HEADS)

            @block.gpsimd
            def _(pool):
                pool.memset(own[:, :], 1.0).then_inc(made, 1)
                pool.wait_ge(made, 1)
                o = own[:, :].rearrange("p (h d) -> p h d", h=4)
                pool.affine_select(out=o, in_=o, compare_op=ALU.is_ge, fill=0.0, base=0,
                                   pattern=[[-F, 4], [0, HD]], channel_multiplier=1).then_inc(made, 1)
                pool.wait_ge(made, 2)
                pool.affine_select(out=o, in_=o, compare_op=ALU.is_ge, fill=0.0, base=F - 1,
                                   pattern=[[F, 4], [0, HD]], channel_multiplier=-1)

            @block.tensor
            def _(pe):
                pe.wait_ge(loaded, 16)
                for n in range(2):
                    for b in range(B):
                        pe.matmul(ps[:, 2 * n + b, :], w[:, n * D:(n + 1) * D], x_cols[:, b * N:(b + 1) * N],
                                  start=True, stop=True).then_inc(ready, 1)
                for t in range(NT):
                    last = pe.matmul(pv[:, t, :], x_cols[:, t * P:(t + 1) * P], w[:, 2 * D:3 * D],
                                     start=True, stop=True)
                last.then_inc(v_ready, 1)

            @block.scalar
            def _(act):
                for n, dst in enumerate((qT, kT)):
                    for b in range(B):
                        act.wait_ge(ready, 2 * n + b + 1)
                        act.activation(dst[:, b * N:(b + 1) * N], ps[:, 2 * n + b, :], ACT.Copy)

            @block.vector
            def _(dve):
                dve.memset(bd[:, :, :], 0.0).then_inc(cleared, 1)
                dve.memset(v1[:, :, D:D + 1], 1.0)
                dve.wait_ge(v_ready, 1)
                dve.tensor_copy(v1[:, :, 0:D], pv[:, :, :])

        with Stage(nc, name + "_feat") as st:
            low = st.sb("low", [P, 3, N])
            ps = st.ps("ps", [P, 3, N])
            raw, lowered, expd, done = (st.sem(x) for x in ("raw", "lowered", "expd", "done"))
            block = st.block()
            jobs = [(bd[:, c, :], qT[:, b * N:(b + 1) * N], qf[:, c, b * N:(b + 1) * N])
                    for b in range(B) for c in range(CH)]
            jobs += [(kT[:, t * P:(t + 1) * P], bd[:, :, :], kf[:, t, :]) for t in range(NT)]

            @block.tensor
            def _(pe):
                for k, (lhs, rhs, _) in enumerate(jobs):
                    if k >= 3:
                        pe.wait_ge(done, k - 2)
                    pe.matmul(ps[:, k % 3, :], lhs, rhs, start=True, stop=True).then_inc(raw, 1)

            @block.scalar
            def _(act):
                for k in range(len(jobs)):
                    act.wait_ge(lowered, k + 1)
                    act.activation(low[:, k % 3, :], low[:, k % 3, :], ACT.Exp).then_inc(expd, 1)

            @block.vector
            def _(dve):
                def finish(k):
                    dve.wait_ge(expd, k + 1)
                    dve.scalar_tensor_tensor(out=jobs[k][2], in0=ps[:, k % 3, :], scalar=0.0, in1=low[:, k % 3, :],
                                             op0=ALU.max, op1=ALU.add).then_inc(done, 1)

                for k in range(len(jobs)):
                    dve.wait_ge(raw, k + 1)
                    if k >= 3:
                        dve.wait_ge(done, k - 2)
                    dve.tensor_scalar(low[:, k % 3, :], ps[:, k % 3, :], 0.0, None, ALU.min).then_inc(lowered, 1)
                    if k >= 1:
                        finish(k - 1)
                finish(len(jobs) - 1)

        with Stage(nc, name + "_kv") as st:
            psK = st.ps("psK", [P, CH, N])
            psN = st.ps("psN", [P, 2, N])
            den = st.sb("den", [P, N])
            kv_out, kv_in, nd_out, nd_in, chain = (
                st.sem(x) for x in ("kv_out", "kv_in", "nd_out", "nd_in", "chain"))
            block = st.block()

            @block.tensor
            def _(pe):
                for b in range(B):
                    if b:
                        pe.wait_ge(kv_in, 1)
                    for c in range(CH):
                        for t in range(TPB):
                            last = pe.matmul(psK[:, c, 0:D + 1], kf[:, b * TPB + t, c * P:(c + 1) * P],
                                             v1[:, b * TPB + t, :], start=t == 0, stop=t == TPB - 1)
                    last.then_inc(kv_out, 1)
                for b in range(B):
                    pe.wait_ge(kv_in, b + 1)
                    if b:
                        pe.wait_ge(nd_in, b)
                    for n in range(2):
                        for c in range(CH):
                            last = pe.matmul(psN[c * F:(c + 1) * F, n, :], kv[:, b, c, n, :],
                                             qf[:, c, b * N:(b + 1) * N], start=True, stop=True,
                                             tile_position=(0, c * F))
                    last.then_inc(nd_out, 1)

            @block.vector
            def _(dve):
                link = Chain(dve, chain)
                for b in range(B):
                    dve.wait_ge(kv_out, b + 1)
                    for c in range(CH):
                        dve.tensor_tensor(kv[:, b, c, 0, :], psK[:, c, c * F:(c + 1) * F], own[:, :], ALU.mult)
                        last = dve.tensor_scalar(kv[:, b, c, 1, :], own[:, :], psK[:, c, D:D + 1], None, ALU.mult)
                    last.then_inc(kv_in, 1)
                for b in range(B):
                    dve.wait_ge(nd_out, b + 1)
                    link(dve.tensor_scalar(den[:, :], psN[:, 1, :], 1e-8, None, ALU.add))
                    link(dve.reciprocal(den[:, :], den[:, :]))
                    dve.tensor_tensor(outT[:, b * N:(b + 1) * N], psN[:, 0, :], den[:, :], ALU.mult).then_inc(nd_in, 1)
                    dve.wait_ge(nd_in, b + 1)

        columns_out(nc, name + "_o", outT, I[pre + "w_out"], X, I[pre + "b_out"])


def columns_out(nc, name, x_cols, w, X, bias, K=1):
    with Stage(nc, name) as st:
        ws = st.sb("w", [P, K, D])
        bs = st.sb("b", [P, D])
        y = st.ps("y", [P, NT, D])
        loaded, y_ready, chain = (st.sem(x) for x in ("loaded", "y_ready", "chain"))
        block = st.block()

        @block.sync
        def _(sp):
            sp.dma_start(ws[:, :, :], w.rearrange("(c p) n -> p c n", p=P)).then_inc(loaded, 16)
            sp.dma_start(bs[:, :], row_to_all(bias, D)).then_inc(loaded, 16)

        @block.tensor
        def _(pe):
            pe.wait_ge(loaded, 32)
            for t in range(NT):
                for k in range(K):
                    x = x_cols[:, t * P:(t + 1) * P] if K == 1 else x_cols[:, k, t * P:(t + 1) * P]
                    last = pe.matmul(y[:, t, :], x, ws[:, k, :], start=k == 0, stop=k == K - 1)
                if t % TPB == TPB - 1:
                    last.then_inc(y_ready, 1)

        @block.vector
        def _(dve):
            link = Chain(dve, chain)
            dve.wait_ge(loaded, 32)
            link(dve.tensor_tensor(X[:, :, :], X[:, :, :], bs[:, None, :].to_broadcast([P, NT, D]), ALU.add))
            for h in range(B):
                dve.wait_ge(y_ready, h + 1)
                part = X[:, h * TPB:(h + 1) * TPB, :]
                dve.tensor_tensor(part, part, y[:, h * TPB:(h + 1) * TPB, :], ALU.add)


def phase_ffn(nc, name, I, pre, x_cols, X, C):
    FCH = 4
    MAGIC = 12582912.0
    TURN = 6.283185307179586
    HI = 6.28125
    LO = TURN - HI
    PI = 3.1415925
    with ExitStack() as ctx:
        hidT = ctx.enter_context(nc.sbuf_tensor(f"{name}_hidT", [P, FCH, TOK], F32))
        with Stage(nc, name + "_h") as st:
            w1 = st.sb("w1", [P, FCH * P])
            vec = st.sb("vec", [P, 4, FCH])
            ang = st.sb("ang", [P, 2, FCH])
            kk = st.sb("kk", [P, 2, FCH])
            sc = st.sb("sc", [P, 2, FCH])
            amp = st.sb("amp", [P, FCH])
            h = st.sb("h", [P, 2, TOK])
            a = st.sb("a", [P, 2, TOK])
            k_ = st.sb("k", [P, 2, TOK])
            ps = st.ps("ps", [P, 2, TOK])
            loaded, chain, h_out, h_in, reduced, sined, ang_ready, sc_ready, done = (
                st.sem(x) for x in ("loaded", "chain", "h_out", "h_in", "reduced", "sined", "ang_ready",
                                    "sc_ready", "done"))
            relued = st.sem("relued")
            block = st.block()

            @block.sync
            def _(sp):
                sp.dma_start(w1[:, :], I[pre + "W1"]).then_inc(loaded, 16)
                for n, v in enumerate(("b1", "quantum_phases", "quantum_weights_real", "quantum_weights_imag")):
                    sp.dma_start(vec[:, n, :], I[pre + v]).then_inc(loaded, 16)

            @block.tensor
            def _(pe):
                pe.wait_ge(loaded, 80)
                for c in range(FCH):
                    if c >= 2:
                        pe.wait_ge(h_in, c - 1)
                    for b in range(B):
                        last = pe.matmul(ps[:, c % 2, b * N:(b + 1) * N], w1[:, c * P:(c + 1) * P],
                                         x_cols[:, b * N:(b + 1) * N], start=True, stop=True)
                    last.then_inc(h_out, 1)

            def reduce_angle(link, dve, x, k):
                link(dve.tensor_scalar(k, x, 1.0 / TURN, MAGIC, ALU.mult, ALU.add))
                link(dve.tensor_scalar(k, k, -MAGIC, None, ALU.add))
                link(dve.scalar_tensor_tensor(out=x, in0=k, scalar=-HI, in1=x, op0=ALU.mult, op1=ALU.add))
                link(dve.scalar_tensor_tensor(out=x, in0=k, scalar=-LO, in1=x, op0=ALU.mult, op1=ALU.add))
                link(dve.tensor_scalar(x, x, PI, -PI, ALU.min, ALU.max))

            @block.vector
            def _(dve):
                link = Chain(dve, chain)
                dve.wait_ge(loaded, 80)
                link(dve.tensor_copy(ang[:, 0, :], vec[:, 1, :]))
                link(dve.tensor_scalar(ang[:, 1, :], vec[:, 1, :], TURN / 4, None, ALU.add))
                reduce_angle(link, dve, ang[:, :, :], kk[:, :, :])
                dve.engine_nop().then_inc(ang_ready, 1)
                dve.wait_ge(sc_ready, 1)
                link(dve.tensor_tensor(sc[:, 1, :], sc[:, 1, :], vec[:, 2, :], ALU.mult))
                link(dve.tensor_tensor(sc[:, 0, :], sc[:, 0, :], vec[:, 3, :], ALU.mult))
                link(dve.tensor_tensor(amp[:, :], sc[:, 0, :], sc[:, 1, :], ALU.add))
                link(dve.tensor_tensor(amp[:, :], amp[:, :], vec[:, 3, :], ALU.mult))
                link(dve.tensor_scalar(amp[:, :], amp[:, :], 0.1, None, ALU.mult))

                def finish(c):
                    dve.wait_ge(sined, c + 1)
                    dve.scalar_tensor_tensor(out=h[:, c % 2, :], in0=a[:, c % 2, :], scalar=amp[:, c:c + 1],
                                             in1=h[:, c % 2, :], op0=ALU.mult, op1=ALU.add).then_inc(done, 1)

                for c in range(FCH):
                    dve.wait_ge(h_out, c + 1)
                    if c >= 2:
                        dve.wait_ge(relued, c - 1)
                    dve.tensor_scalar(h[:, c % 2, :], ps[:, c % 2, :], vec[:, 0, c:c + 1], None, ALU.add)\
                        .then_inc(h_in, 1)
                    dve.wait_ge(h_in, c + 1)
                    link(dve.tensor_scalar(a[:, c % 2, :], h[:, c % 2, :], 0.1, vec[:, 1, c:c + 1],
                                           ALU.mult, ALU.add))
                    reduce_angle(link, dve, a[:, c % 2, :], k_[:, c % 2, :])
                    dve.engine_nop().then_inc(reduced, 1)
                    if c >= 1:
                        finish(c - 1)
                finish(FCH - 1)

            @block.scalar
            def _(act):
                act.wait_ge(ang_ready, 1)
                act.activation(sc[:, :, :], ang[:, :, :], ACT.Sin).then_inc(sc_ready, 1)

                def relu(c):
                    act.wait_ge(done, c + 1)
                    act.activation(hidT[:, c, :], h[:, c % 2, :], ACT.Relu).then_inc(relued, 1)

                for c in range(FCH):
                    act.wait_ge(reduced, c + 1)
                    act.activation(a[:, c % 2, :], a[:, c % 2, :], ACT.Sin).then_inc(sined, 1)
                    if c >= 1:
                        relu(c - 1)
                relu(FCH - 1)

        columns_out(nc, name + "_o", hidT, I[pre + "W2"], X, I[pre + "b2"], K=FCH)


def expert_mlps(nc, name, x_cols, w1, b1, w2, b2, func, cT, c_scratch, dst):
    FCH = w1.shape[2] // P
    HALF = FCH * B
    STEPS = 2 * HALF
    with Stage(nc, name) as st:
        w1s = st.sb("w1", [P, 2, FCH * P])
        w2s = st.sb("w2", [P, 2, FCH, D])
        cb = st.sb("cb", [P, 2, TOK])
        b1s = st.sb("b1", [P, 2, FCH])
        b2s = st.sb("b2", [E, D])
        a = st.sb("a", [P, 4, N])
        hid = st.sb("hid", [P, 4, N])
        psH = st.ps("psH", [P, 4, N])
        psY = st.ps("psY", [P, B, N])
        loaded, stored, h_out, a_out, hid_ready, y_out = (
            st.sem(x) for x in ("loaded", "stored", "h_out", "a_out", "hid_ready", "y_out"))
        w_in = [st.sem(f"w_in{s}") for s in range(2)]
        block = st.block()

        def step(j):
            return j // HALF, j % HALF // B, j % B

        @block.sync
        def _(sp):
            sp.dma_start(c_scratch, cT[:, :]).then_inc(stored, 16)
            sp.dma_start(b2s[:, :], b2).then_inc(loaded, 16)
            sp.wait_ge(stored, 16)

            def load(it, s):
                e = it * 2 + s
                sp.dma_start(w1s[:, s, :], w1[bass.ds(e, 1), :, :].rearrange("a p n -> p (a n)"))\
                    .then_inc(w_in[s], 16)
                sp.dma_start(w2s[:, s, :, :], w2[bass.ds(e, 1), :, :].rearrange("a (c p) n -> p (a c) n", p=P))\
                    .then_inc(w_in[s], 16)
                sp.dma_start(b1s[:, s, :], b1[bass.ds(e, 1), :, :].rearrange("a p c -> p (a c)"))\
                    .then_inc(w_in[s], 16)
                sp.dma_start(cb[:, s, :], row_to_all(c_scratch[bass.ds(e, 1), :], TOK)).then_inc(w_in[s], 16)

            load(0, 0)
            load(0, 1)
            with sp.Fori(1, E // 2) as it:
                for s in range(2):
                    sp.wait_ge(y_out, it * STEPS - STEPS + HALF * (s + 1))
                    load(it, s)

        @block.tensor
        def _(pe):
            def down(it, j):
                s, f, h = step(j)
                pe.wait_ge(hid_ready, it * STEPS + j + 1)
                pe.matmul(psY[:, h, :], w2s[:, s, f, :], hid[:, j % 4, :], start=False, stop=False,
                          skip_group_check=True).then_inc(y_out, 1)

            def body(it, first):
                for j in range(STEPS):
                    s, f, h = step(j)
                    if j % HALF == 0:
                        pe.wait_ge(w_in[s], it * 64 + 64)
                    if not first or j >= 4:
                        pe.wait_ge(a_out, it * STEPS + j - 3)
                    pe.matmul(psH[:, j % 4, :], w1s[:, s, f * P:(f + 1) * P], x_cols[:, h * N:(h + 1) * N],
                              start=True, stop=True).then_inc(h_out, 1)
                    if j >= 2:
                        down(it, j - 2)
                down(it, STEPS - 2)
                down(it, STEPS - 1)

            pe.wait_ge(loaded, 16)
            for h in range(B):
                pe.matmul(psY[:, h, :], b2s[:, :], cT[:, h * N:(h + 1) * N], start=True, stop=False,
                          skip_group_check=True)
            body(0, True)
            with pe.Fori(1, E // 2) as it:
                body(it, False)

        @block.scalar
        def _(act):
            def body(it, first):
                for j in range(STEPS):
                    s, f, h = step(j)
                    if j % HALF == 0:
                        act.wait_ge(w_in[s], it * 64 + 64)
                    act.wait_ge(h_out, it * STEPS + j + 1)
                    if not first or j >= 4:
                        act.wait_ge(hid_ready, it * STEPS + j - 3)
                    act.activation(a[:, j % 4, :], psH[:, j % 4, :], func,
                                   bias=b1s[:, s, f:f + 1]).then_inc(a_out, 1)

            body(0, True)
            with act.Fori(1, E // 2) as it:
                body(it, False)
            act.wait_ge(y_out, E // 2 * STEPS)
            act.activation(dst[:, N:2 * N], psY[:, 1, :], ACT.Copy)

        @block.vector
        def _(dve):
            def body(it, first):
                for j in range(STEPS):
                    s, f, h = step(j)
                    if j % HALF == 0:
                        dve.wait_ge(w_in[s], it * 64 + 64)
                    dve.wait_ge(a_out, it * STEPS + j + 1)
                    if not first or j >= 4:
                        dve.wait_ge(y_out, it * STEPS + j - 3)
                    dve.tensor_tensor(hid[:, j % 4, :], a[:, j % 4, :], cb[:, s, h * N:(h + 1) * N], ALU.mult)\
                        .then_inc(hid_ready, 1)

            body(0, True)
            with dve.Fori(1, E // 2) as it:
                body(it, False)
            dve.wait_ge(y_out, E // 2 * STEPS)
            dve.tensor_copy(dst[:, 0:N], psY[:, 0, :])


def windowed_attention(nc, name, I, pre, x_cols, X, C):
    QT, WIN, HD, KV = 96, 32, 8, 2
    KW = QT + WIN - 1
    HALF = WIN // 2
    NU = -(-N // QT)
    PAD = NU * QT + WIN
    with ExitStack() as ctx:
        def sb(n, shape, dt=F32):
            return ctx.enter_context(nc.sbuf_tensor(f"{name}_{n}", shape, dt))
        xp = sb("xp", [P, B, PAD])
        qT = sb("qT", [P, 4, TOK])
        kT = sb("kT", [P, KV, B, PAD])
        vw = sb("vw", [P, B * NU, KV, HD + 1])
        OT = sb("OT", [P, TOK])
        with Stage(nc, name + "_qkv") as st:
            wq = st.sb("wq", [P, 4, 4, 32])
            wk = st.sb("wk", [P, KV, 4, 32])
            wv = st.sb("wv", [P, KV * HD])
            bq = st.sb("bq", [P, 4])
            bk = st.sb("bk", [P, KV])
            bv = st.sb("bv", [1, KV * HD])
            valid = st.sb("valid", [1, PAD])
            ps = st.ps("ps", [P, 4, N])
            pv = st.ps("pv", [P, B * NU, KV * HD])
            cleared, loaded, xp_ready, raw, evac, v_out = (
                st.sem(x) for x in ("cleared", "loaded", "xp_ready", "raw", "evac", "v_out"))
            block = st.block()
            n_loads = 16 * (4 + KV * 4 + 1 + 8 + 1)
            jobs = [(wq[:, c, :, :], x_cols[:, b * N:(b + 1) * N], qT[:, c, b * N:(b + 1) * N], bq[:, c:c + 1])
                    for c in range(4) for b in range(B)]
            jobs += [(wk[:, g, :, :], x_cols[:, b * N:(b + 1) * N], kT[:, g, b, HALF:HALF + N], bk[:, g:g + 1])
                     for g in range(KV) for b in range(B)]

            @block.sync
            def _(sp):
                sp.wait_ge(cleared, 4)
                for c in range(4):
                    sp.dma_start(wq[:, c, :, 0:HD], I[pre + "Wq"][:, c * 32:(c + 1) * 32]
                                 .rearrange("p (r d) -> p r d", d=HD)).then_inc(loaded, 16)
                for g in range(KV):
                    for r in range(4):
                        sp.dma_start(wk[:, g, r, 0:HD], I[pre + "Wk"][:, g * HD:(g + 1) * HD]).then_inc(loaded, 16)
                sp.dma_start(wv[:, :], I[pre + "Wv"]).then_inc(loaded, 16)
                for r in range(4):
                    sp.dma_start(bq[r * 32:r * 32 + HD, :], I[pre + "bq"][r, :, :]).then_inc(loaded, 16)
                    sp.dma_start(bk[r * 32:r * 32 + HD, :], I[pre + "bk"]).then_inc(loaded, 16)
                sp.dma_start(bv[:, :], dram_view(I[pre + "bv"], 0, [[KV * HD, 1], [1, KV * HD]])).then_inc(loaded, 16)

            @block.tensor
            def _(pe):
                pe.wait_ge(loaded, n_loads)
                for k, (lhs, rhs, _, _) in enumerate(jobs):
                    if k >= 4:
                        pe.wait_ge(evac, k - 3)
                    pe.matmul(ps[:, k % 4, :], lhs, rhs, start=True, stop=True).then_inc(raw, 1)
                pe.wait_ge(xp_ready, 3)
                for b in range(B):
                    for u in range(NU):
                        out = pv[0:KW, b * NU + u, :]
                        pe.matmul(out, xp[:, b, u * QT:u * QT + KW], wv[:, :], start=True, stop=False)
                        last = pe.matmul(out, valid[:, u * QT:u * QT + KW], bv[:, :], start=False, stop=True)
                last.then_inc(v_out, 1)

            @block.gpsimd
            def _(pool):
                pool.memset(xp[:, :, 0:HALF], 0.0)
                pool.memset(xp[:, :, HALF + N:PAD], 0.0)
                pool.tensor_copy(xp[:, :, HALF:HALF + N], x_cols[:, :].rearrange("p (b n) -> p b n", b=B))\
                    .then_inc(xp_ready, 1)
                pool.memset(valid[:, 0:HALF], 0.0)
                pool.memset(valid[:, HALF + N:PAD], 0.0).then_inc(xp_ready, 1)
                pool.memset(valid[:, HALF:HALF + N], 1.0).then_inc(xp_ready, 1)

            @block.vector
            def _(dve):
                dve.memset(wq[:, :, :, :], 0.0).then_inc(cleared, 1)
                dve.memset(wk[:, :, :, :], 0.0).then_inc(cleared, 1)
                dve.memset(bq[:, :], 0.0).then_inc(cleared, 1)
                dve.memset(bk[:, :], 0.0).then_inc(cleared, 1)
                dve.memset(kT[:, :, :, 0:HALF], 0.0)
                dve.memset(kT[:, :, :, HALF + N:PAD], 0.0)
                dve.memset(vw[:, :, :, HD:HD + 1], 1.0)
                dve.wait_ge(loaded, n_loads)
                for k, (_, _, dst, bias) in enumerate(jobs):
                    dve.wait_ge(raw, k + 1)
                    dve.tensor_scalar(dst, ps[:, k % 4, :], bias, None, ALU.add).then_inc(evac, 1)
                dve.wait_ge(v_out, 1)
                dve.tensor_copy(vw[0:KW, :, :, 0:HD], pv[0:KW, :, :].rearrange("p u (g d) -> p u g d", g=KV))

        units = [(b, u, min(QT, N - u * QT)) for b in range(B) for u in range(NU)]
        with Stage(nc, name + "_at") as st:
            band = st.sb("band", [P, 4, KW], BF16)
            S = st.sb("S", [P, HEADS, KW])
            Pm = st.sb("Pm", [P, HEADS, KW])
            PT = st.sb("PT", [P, HEADS, QT])
            nmax = st.sb("nmax", [P, HEADS])
            rinv = st.sb("rinv", [P, HEADS])
            O = st.sb("O", [P, HEADS, HD])
            psS = st.ps("psS", [P, 4, N])
            psT = st.ps("psT", [P, 2, N])
            psO = st.ps("psO", [P, N])
            made, s_out, s_in, expd, t_out, t_in, o_out, o_in, ot_out, ot_in, chain = (
                st.sem(x) for x in ("made", "s_out", "s_in", "expd", "t_out", "t_in", "o_out", "o_in",
                                    "ot_out", "ot_in", "chain"))
            t_in2 = st.sem("t_in2")
            block = st.block()

            @block.gpsimd
            def _(pool):
                pool.memset(band[:, :, :], 0.0).then_inc(made, 1)
                pool.wait_ge(made, 1)
                pool.affine_select(out=band[:, :, :], in_=band[:, :, :], compare_op=ALU.is_ge, fill=NEG, base=0,
                                   pattern=[[0, 4], [1, KW]], channel_multiplier=-1).then_inc(made, 1)
                pool.wait_ge(made, 2)
                pool.affine_select(out=band[:, :, :], in_=band[:, :, :], compare_op=ALU.is_ge, fill=NEG,
                                   base=WIN - 1, pattern=[[0, 4], [-1, KW]], channel_multiplier=1).then_inc(made, 1)

            @block.tensor
            def _(pe):
                def scores(k):
                    b, u, m = units[k]
                    if k:
                        pe.wait_ge(s_in, k)
                    for r in range(4):
                        pe.matmul(psS[0:m, r, 0:4 * KW], C.identb[:, 0:m], band[:, :, :], start=True, stop=False,
                                  skip_group_check=True)
                    for c in range(4):
                        for r in range(4):
                            rows = slice(32 * r, 32 * r + HD)
                            last = pe.matmul(psS[0:m, r, c * KW:(c + 1) * KW],
                                             qT[rows, c, b * N + u * QT:b * N + u * QT + m],
                                             kT[rows, c // 2, b, u * QT:u * QT + KW], start=False, stop=True,
                                             skip_group_check=True)
                    last.then_inc(s_out, 1)

                def values(k):
                    b, u, m = units[k]
                    pe.wait_ge(expd, k + 1)
                    for half in range(2):
                        n = 2 * k + half
                        if n:
                            pe.wait_ge(t_in, n)
                            pe.wait_ge(t_in2, n)
                        for y in range(8):
                            last = pe.transpose(psT[0:KW, y // 4, y % 4 * QT:y % 4 * QT + m],
                                                Pm[0:m, half * 8 + y, :], C.ident[0:m, 0:m])
                        last.then_inc(t_out, 1)
                    pe.wait_ge(t_in, 2 * k + 2)
                    pe.wait_ge(t_in2, 2 * k + 2)
                    if k:
                        pe.wait_ge(ot_in, k)
                    for y in range(HEADS):
                        r, c = y // 4, y % 4
                        h = 4 * c + r
                        last = pe.matmul(psO[0:m, h * (HD + 1):(h + 1) * (HD + 1)], PT[0:KW, y, 0:m],
                                         vw[0:KW, k, c // 2, :], start=True, stop=True)
                    last.then_inc(o_out, 1)

                def turn(k):
                    b, u, m = units[k]
                    pe.wait_ge(o_in, k + 1)
                    pe.transpose(psO[:, 256:256 + m], O[0:m, :, :], C.ident[0:m, 0:m]).then_inc(ot_out, 1)

                pe.wait_ge(made, 3)
                for k in range(len(units)):
                    scores(k)
                    if k:
                        values(k - 1)
                        turn(k - 1)
                values(len(units) - 1)
                turn(len(units) - 1)

            @block.scalar
            def _(act):
                for k, (b, u, m) in enumerate(units):
                    act.wait_ge(s_in, k + 1)
                    if k:
                        act.wait_ge(t_out, 2 * k)
                    act.activation(Pm[0:m, :, :], S[0:m, :, :], ACT.Exp).then_inc(expd, 1)
                    for half in range(2):
                        act.wait_ge(t_out, 2 * k + half + 1)
                        if k and not half:
                            act.wait_ge(o_out, k)
                        act.activation(PT[0:KW, half * 8:half * 8 + 4, 0:m],
                                       psT[0:KW, 0, 0:4 * QT].rearrange("p (y q) -> p y q", y=4)[:, :, 0:m],
                                       ACT.Copy).then_inc(t_in, 1)

            @block.vector
            def _(dve):
                link = Chain(dve, chain)

                def finish(k):
                    b, u, m = units[k]
                    for half in range(2):
                        dve.wait_ge(t_out, 2 * k + half + 1)
                        if k and not half:
                            dve.wait_ge(o_out, k)
                        dve.tensor_copy(PT[0:KW, half * 8 + 4:half * 8 + 8, 0:m],
                                        psT[0:KW, 1, 0:4 * QT].rearrange("p (y q) -> p y q", y=4)[:, :, 0:m])\
                            .then_inc(t_in2, 1)
                    dve.wait_ge(o_out, k + 1)
                    o = psO[0:m, 0:HEADS * (HD + 1)].rearrange("p (h d) -> p h d", h=HEADS)
                    link(dve.reciprocal(rinv[0:m, :], o[:, :, HD]))
                    dve.tensor_tensor(O[0:m, :, :], o[:, :, 0:HD],
                                      rinv[0:m, :].unsqueeze(2).to_broadcast([m, HEADS, HD]), ALU.mult)\
                        .then_inc(o_in, 1)
                    dve.wait_ge(ot_out, k + 1)
                    dve.tensor_copy(OT[:, b * N + u * QT:b * N + u * QT + m], psO[:, 256:256 + m]).then_inc(ot_in, 1)

                for k, (b, u, m) in enumerate(units):
                    dve.wait_ge(s_out, k + 1)
                    s = psS[0:m, :, 0:4 * KW].rearrange("p r (c j) -> p r c j", c=4)
                    link(dve.tensor_reduce(nmax[0:m, :].rearrange("p (r c) -> p r c", r=4), s, AX.X, ALU.max))
                    if k:
                        dve.wait_ge(expd, k)
                    dve.tensor_tensor(S[0:m, :, :].rearrange("p (r c) j -> p r c j", r=4), s,
                                      nmax[0:m, :].rearrange("p (r c) -> p r c", r=4).unsqueeze(3)
                                      .to_broadcast([m, 4, 4, KW]), ALU.subtract).then_inc(s_in, 1)
                    if k:
                        finish(k - 1)
                finish(len(units) - 1)

        columns_out(nc, name + "_o", OT, I[pre + "Wo"], X, I[pre + "bo"])


def layered_attention(nc, name, I, pre, Y, C):
    L, HD, LH, BK = 4, 16, 4, 64
    LW = LH * HD
    NB = N // BK
    FCH = 4
    with ExitStack() as ctx:
        def sb(n, shape, dt=F32):
            return ctx.enter_context(nc.sbuf_tensor(f"{name}_{n}", shape, dt))
        xn = sb("xn", [P, NT, D])
        xc = sb("xc", [P, TOK])
        qlT = sb("qlT", [P, TOK])
        klT = sb("klT", [P, TOK])
        v1 = sb("v1", [P, NT, D + 1])
        kg = sb("kg", [P, NT, LW])
        qgT = sb("qgT", [LW, TOK])
        ctxs = sb("ctxs", [LW, B * NB, LW])
        own = sb("own", [LW, LW])
        O = sb("O", [P, NT, D])
        OT = sb("OT", [P, TOK])
        hid = sb("hid", [P, FCH, TOK])
        with Stage(nc, name + "_own") as st:
            made = st.sem("made")
            block = st.block()

            @block.gpsimd
            def _(pool):
                pool.memset(own[:, :], 1.0).then_inc(made, 1)
                pool.wait_ge(made, 1)
                o = own[:, :].rearrange("p (h d) -> p h d", h=LH)
                pool.affine_select(out=o, in_=o, compare_op=ALU.is_ge, fill=0.0, base=0,
                                   pattern=[[-HD, LH], [0, HD]], channel_multiplier=1).then_inc(made, 1)
                pool.wait_ge(made, 2)
                pool.affine_select(out=o, in_=o, compare_op=ALU.is_ge, fill=0.0, base=HD - 1,
                                   pattern=[[HD, LH], [0, HD]], channel_multiplier=-1)

            @block.vector
            def _(dve):
                dve.memset(v1[:, :, D:D + 1], 1.0)

        with nc.Fori(0, L) as layer:
            def row(w):
                return I[pre + w][bass.ds(layer, 1), :]

            def matrix(w):
                return I[pre + w][bass.ds(layer, 1), :, :].rearrange("a p n -> (a p) n")

            layer_norm(nc, name + "_ln1", Y, xn, row("ln1_g"), row("ln1_b"), dst_cols=xc, ident=C.ident)
            with Stage(nc, name + "_qkv") as st:
                wl = st.sb("wl", [P, 2, LH, 32])
                wr = st.sb("wr", [P, 2 * D])
                qg = st.sb("qg", [P, NT * LH, HD])
                m = st.sb("m", [P, NT * LH])
                low = st.sb("low", [P, NT, LW])
                psL = st.ps("psL", [P, 4, N])
                psR = st.ps("psR", [P, NT, 2 * D])
                cleared, loaded, l_out, r_out, chain, shifted, expd, lowered, low_exp, q_ready, t_out = (
                    st.sem(x) for x in ("cleared", "loaded", "l_out", "r_out", "chain", "shifted", "expd",
                                        "lowered", "low_exp", "q_ready", "t_out"))
                psl_in = st.sem("psl_in")
                block = st.block()

                @block.sync
                def _(sp):
                    sp.dma_start(wr[:, 0:D], matrix("Wv")).then_inc(loaded, 16)
                    for n, w in enumerate(("Wq", "Wk")):
                        sp.dma_start(wr[:, D + n * LW:D + (n + 1) * LW], matrix(w)[:, LW:D]).then_inc(loaded, 16)
                    sp.wait_ge(cleared, 1)
                    for n, w in enumerate(("Wq", "Wk")):
                        sp.dma_start(wl[:, n, :, 0:HD], matrix(w)[:, 0:LW].rearrange("p (h d) -> p h d", h=LH))\
                            .then_inc(loaded, 16)

                @block.tensor
                def _(pe):
                    pe.wait_ge(loaded, 80)
                    for t in range(NT):
                        last = pe.matmul(psR[:, t, :], xc[:, t * P:(t + 1) * P], wr[:, :], start=True, stop=True)
                    last.then_inc(r_out, 1)
                    for n in range(2):
                        for b in range(B):
                            pe.matmul(psL[:, 2 * n + b, :], wl[:, n, :, :], xc[:, b * N:(b + 1) * N],
                                      start=True, stop=True).then_inc(l_out, 1)
                    pe.wait_ge(q_ready, 1)
                    pe.wait_ge(psl_in, 4)
                    for t in range(NT):
                        last = pe.transpose(psL[0:LW, t // TPB, t % TPB * P:(t % TPB + 1) * P],
                                            qg[:, t * LH:(t + 1) * LH, :], C.ident[:, :])
                    last.then_inc(t_out, 1)

                @block.scalar
                def _(act):
                    act.wait_ge(shifted, 1)
                    act.activation(qg[:, :, :], qg[:, :, :], ACT.Exp).then_inc(expd, 1)
                    act.wait_ge(lowered, 1)
                    act.activation(low[:, :, :], low[:, :, :], ACT.Exp).then_inc(low_exp, 1)
                    for n, (dst, scale) in enumerate(((qlT, HD ** -0.5), (klT, 1.0))):
                        for b in range(B):
                            act.wait_ge(l_out, 2 * n + b + 1)
                            act.activation(dst[:, b * N:(b + 1) * N], psL[:, 2 * n + b, :], ACT.Copy, scale=scale)\
                                .then_inc(psl_in, 1)

                @block.vector
                def _(dve):
                    link = Chain(dve, chain)
                    dve.memset(wl[:, :, :, :], 0.0).then_inc(cleared, 1)
                    dve.wait_ge(r_out, 1)
                    q = psR[:, :, D:D + LW].rearrange("p t (h d) -> p t h d", h=LH)
                    q4 = qg[:, :, :].rearrange("p (t h) d -> p t h d", t=NT)
                    m3 = m[:, :].rearrange("p (t h) -> p t h", t=NT)
                    over = m3.unsqueeze(3).to_broadcast([P, NT, LH, HD])
                    link(dve.tensor_reduce(m3, q, AX.X, ALU.max))
                    dve.tensor_tensor(q4, q, over, ALU.subtract).then_inc(shifted, 1)
                    k = psR[:, :, D + LW:D + 2 * LW]
                    dve.tensor_scalar(low[:, :, :], k, 0.0, None, ALU.min).then_inc(lowered, 1)
                    dve.tensor_copy(v1[:, :, 0:D], psR[:, :, 0:D])
                    dve.wait_ge(expd, 1)
                    link(dve.tensor_reduce(m[:, :], qg[:, :, :], AX.X, ALU.add))
                    link(dve.reciprocal(m[:, :], m[:, :]))
                    dve.tensor_tensor(q4, q4, over, ALU.mult).then_inc(q_ready, 1)
                    dve.wait_ge(low_exp, 1)
                    dve.scalar_tensor_tensor(out=kg[:, :, :], in0=k, scalar=0.0, in1=low[:, :, :],
                                             op0=ALU.max, op1=ALU.add)
                    dve.wait_ge(t_out, 1)
                    dve.tensor_copy(qgT[:, :], psL[0:LW, 0:2, :])

            with Stage(nc, name + "_glob") as st:
                cum = st.sb("cum", [LW, B, NB, LW + 1])
                rk = st.sb("rk", [LW, B, NB])
                psC = st.ps("psC", [LW, 2, B * NB // 2, P])
                psG = st.ps("psG", [P, NT, LW])
                c_out, c_ready, g_out, chain = (st.sem(x) for x in ("c_out", "c_ready", "g_out", "chain"))
                block = st.block()

                @block.tensor
                def _(pe):
                    for k in range(B * NB):
                        rows = slice(BK * (k % 2), BK * (k % 2) + BK)
                        last = pe.matmul(psC[:, k % 2, k // 2, 0:LW + 1], kg[rows, k // 2, :],
                                         v1[rows, k // 2, LW:D + 1], start=True, stop=True)
                    last.then_inc(c_out, 1)
                    pe.wait_ge(c_ready, 1)
                    for k in range(B * NB):
                        rows = slice(BK * (k % 2), BK * (k % 2) + BK)
                        last = pe.matmul(psG[rows, k // 2, :], qgT[:, k * BK:(k + 1) * BK], ctxs[:, k, :],
                                         start=True, stop=True)
                    last.then_inc(g_out, 1)

                @block.vector
                def _(dve):
                    link = Chain(dve, chain)
                    link(dve.memset(cum[:, :, 0, :], 0.0))
                    dve.wait_ge(c_out, 1)
                    raw = psC[:, :, :, 0:LW + 1].rearrange("p q (b t) d -> p q b t d", b=B)
                    for u in range(1, NB):
                        link(dve.tensor_tensor(cum[:, :, u, :], cum[:, :, u - 1, :],
                                               raw[:, (u - 1) % 2, :, (u - 1) // 2, :], ALU.add))
                    link(dve.tensor_scalar(rk[:, :, :], cum[:, :, :, LW], 1e-6, None, ALU.add))
                    link(dve.reciprocal(rk[:, :, :], rk[:, :, :]))
                    c3 = ctxs[:, :, :].rearrange("p (b u) d -> p b u d", b=B)
                    link(dve.tensor_tensor(c3, cum[:, :, :, 0:LW], rk[:, :, :].unsqueeze(3)
                                           .to_broadcast([LW, B, NB, LW]), ALU.mult))
                    dve.tensor_tensor(ctxs[:, :, :], ctxs[:, :, :],
                                      own[:, None, :].to_broadcast([LW, B * NB, LW]), ALU.mult).then_inc(c_ready, 1)
                    dve.wait_ge(g_out, 1)
                    dve.tensor_copy(O[:, :, LW:D], psG[:, :, :])

            with Stage(nc, name + "_loc") as st:
                Pm = st.sb("Pm", [P, 2, LH, 2 * P])
                PT = st.sb("PT", [P, LH, 2, P])
                nmax = st.sb("nmax", [P, 2, LH])
                rsum = st.sb("rsum", [P, 2, LH])
                rinv = st.sb("rinv", [P, LH])
                psS = st.ps("psS", [P, LH, N])
                psT = st.ps("psT", [P, LH, 2, P])
                psO = st.ps("psO", [P, LH, HD])
                s_out, maxed, expd, t_out, t_in, t_in2, o_out, o_in, chain = (
                    st.sem(x) for x in ("s_out", "maxed", "expd", "t_out", "t_in", "t_in2", "o_out", "o_in",
                                        "chain"))
                block = st.block()

                @block.tensor
                def _(pe):
                    def scores(t):
                        lo = 0 if t % TPB else P
                        if t:
                            pe.wait_ge(expd, LH * t)
                        for h in range(LH):
                            pe.matmul(psS[:, h, P:2 * P], C.identb[:, :], C.trib[:, :], start=True, stop=False,
                                      skip_group_check=True)
                        for h in range(LH):
                            rows = slice(32 * h, 32 * h + HD)
                            last = pe.matmul(psS[:, h, lo:2 * P], qlT[rows, t * P:(t + 1) * P],
                                             klT[rows, (t - 1) * P + lo:(t + 1) * P], start=False, stop=True,
                                             skip_group_check=True)
                        last.then_inc(s_out, 1)

                    def values(t):
                        lo = 0 if t % TPB else 1
                        pe.wait_ge(expd, LH * (t + 1))
                        if t:
                            pe.wait_ge(t_in, t)
                            pe.wait_ge(t_in2, t)
                        for h in range(LH):
                            for k in range(lo, 2):
                                last = pe.transpose(psT[:, h, k, :], Pm[:, t % 2, h, k * P:(k + 1) * P], C.ident[:, :])
                        last.then_inc(t_out, 1)
                        pe.wait_ge(t_in, t + 1)
                        pe.wait_ge(t_in2, t + 1)
                        if t:
                            pe.wait_ge(o_in, t)
                        for h in range(LH):
                            for k in range(lo, 2):
                                last = pe.matmul(psO[:, h, :], PT[:, h, k, :],
                                                 v1[:, t - 1 + k, h * HD:(h + 1) * HD], start=k == lo, stop=k == 1)
                        last.then_inc(o_out, 1)

                    for t in range(NT):
                        scores(t)
                        if t:
                            values(t - 1)
                    values(NT - 1)

                @block.scalar
                def _(act):
                    def copy(t):
                        lo = 0 if t % TPB else 1
                        act.wait_ge(t_out, t + 1)
                        if t:
                            act.wait_ge(o_out, t)
                        act.activation(PT[:, 0:2, lo:2, :], psT[:, 0:2, lo:2, :], ACT.Copy).then_inc(t_in, 1)

                    for t in range(NT):
                        lo = 0 if t % TPB else P
                        act.wait_ge(maxed, t + 1)
                        if t >= 2:
                            act.wait_ge(t_out, t - 1)
                        for h in range(LH):
                            act.activation(Pm[:, t % 2, h, lo:2 * P], psS[:, h, lo:2 * P], ACT.Exp,
                                           bias=nmax[:, t % 2, h:h + 1], accum_out=rsum[:, t % 2, h:h + 1])\
                                .then_inc(expd, 1)
                        if t:
                            copy(t - 1)
                    copy(NT - 1)

                @block.vector
                def _(dve):
                    link = Chain(dve, chain)

                    def finish(t):
                        lo = 0 if t % TPB else 1
                        dve.wait_ge(t_out, t + 1)
                        if t:
                            dve.wait_ge(o_out, t)
                        dve.tensor_copy(PT[:, 2:4, lo:2, :], psT[:, 2:4, lo:2, :]).then_inc(t_in2, 1)
                        link(dve.reciprocal(rinv[:, :], rsum[:, t % 2, :]))
                        dve.wait_ge(o_out, t + 1)
                        dve.tensor_tensor(O[:, t, 0:LW].rearrange("p (h d) -> p h d", h=LH), psO[:, :, :],
                                          rinv[:, :].unsqueeze(2).to_broadcast([P, LH, HD]), ALU.mult)\
                            .then_inc(o_in, 1)

                    for t in range(NT):
                        lo = 0 if t % TPB else P
                        dve.wait_ge(s_out, t + 1)
                        if t >= 2:
                            dve.wait_ge(expd, LH * (t - 1))
                        dve.tensor_reduce(nmax[:, t % 2, :], psS[:, :, lo:2 * P], AX.X, ALU.max, negate=True)\
                            .then_inc(maxed, 1)
                        if t:
                            dve.wait_ge(o_in, t - 1) if t > 1 else None
                            finish(t - 1)
                    dve.wait_ge(o_in, NT - 1)
                    finish(NT - 1)

            rows_to_columns(nc, name + "_ot", O, OT, C.ident)
            columns_out(nc, name + "_o", OT, matrix("Wo"), Y, row("bo"))
            layer_norm(nc, name + "_ln2", Y, xn, row("ln2_g"), row("ln2_b"), dst_cols=xc, ident=C.ident)
            with Stage(nc, name + "_ffn") as st:
                w1 = st.sb("w1", [P, FCH * P])
                b1 = st.sb("b1", [P, FCH])
                ps = st.ps("ps", [P, 4, N])
                loaded, h_out, h_in = (st.sem(x) for x in ("loaded", "h_out", "h_in"))
                block = st.block()

                @block.sync
                def _(sp):
                    sp.dma_start(w1[:, :], matrix("W1")).then_inc(loaded, 16)
                    sp.dma_start(b1[:, :], matrix("b1")).then_inc(loaded, 16)

                @block.tensor
                def _(pe):
                    pe.wait_ge(loaded, 32)
                    for k in range(FCH * B):
                        c, b = k // B, k % B
                        if k >= 4:
                            pe.wait_ge(h_in, k - 3)
                        pe.matmul(ps[:, k % 4, :], w1[:, c * P:(c + 1) * P], xc[:, b * N:(b + 1) * N],
                                  start=True, stop=True).then_inc(h_out, 1)

                @block.scalar
                def _(act):
                    act.wait_ge(loaded, 32)
                    for k in range(FCH * B):
                        c, b = k // B, k % B
                        act.wait_ge(h_out, k + 1)
                        act.activation(hid[:, c, b * N:(b + 1) * N], ps[:, k % 4, :], ACT.Gelu, bias=b1[:, c:c + 1])\
                            .then_inc(h_in, 1)

            columns_out(nc, name + "_o2", hid, matrix("W2"), Y, row("b2"), K=FCH)


def add_rows(nc, name, src, dst):
    with Stage(nc, name) as st:
        block = st.block()

        @block.vector
        def _(dve):
            dve.tensor_tensor(dst[:, :, :], dst[:, :, :], src[:, :, :], ALU.add)


class Constants:

    def __init__(self, nc, ctx, I):
        def sb(n, shape, dt=F32):
            return ctx.enter_context(nc.sbuf_tensor(n, shape, dt))
        self.ident = sb("ident", [P, P])
        self.flip = sb("flip", [P, P])
        self.identb = sb("identb", [P, P], BF16)
        self.ones = sb("ones", [P, P])
        self.upto = sb("upto", [P, P])
        self.desc = sb("desc", [P, E])
        self.onesb = sb("onesb", [1, P], BF16)
        self.trib = sb("trib", [P, P], BF16)
        self.mask_bf1 = sb("mask_bf1", [1, TOK], BF16)
        self.mask_bk0 = sb("mask_bk0", [1, TOK], BF16)
        masks = (("mask_BxS_bf1", self.mask_bf1), ("mask_BxS_bk0", self.mask_bk0))
        with Stage(nc, "consts") as st:
            raw = st.sb("raw", [1, 2, TOK], U8)
            desci = st.sb("desci", [P, E], I32)
            loaded, cleared = (st.sem(x) for x in ("loaded", "cleared"))
            block = st.block()

            @block.sync
            def _(sp):
                for n, (m, _) in enumerate(masks):
                    sp.dma_start(raw[:, n, :], dram_view(I[m], 0, [[TOK, 1], [1, TOK]])).then_inc(loaded, 16)

            @block.gpsimd
            def _(pool):
                for m, v in ((self.ident, 0.0), (self.identb, 0.0), (self.trib, 0.0), (self.flip, 0.0), (self.ones, 1.0),
                             (self.upto, 1.0)):
                    pool.memset(m[:, :], v).then_inc(cleared, 1)
                pool.iota(desci[:, :], pattern=[[-1, E]], base=E, channel_multiplier=0).then_inc(cleared, 1)
                pool.wait_ge(cleared, 7)
                pool.affine_select(out=self.upto[:, :], in_=self.upto[:, :], compare_op=ALU.is_ge, fill=0.0,
                                   base=0, pattern=[[1, P]], channel_multiplier=-1)
                for m in (self.ident, self.identb):
                    pool.affine_select(out=m[:, :], in_=m[:, :], compare_op=ALU.not_equal, fill=1.0, base=0,
                                       pattern=[[-1, P]], channel_multiplier=1)
                pool.affine_select(out=self.flip[:, :], in_=self.flip[:, :], compare_op=ALU.not_equal, fill=1.0,
                                   base=-(P - 1), pattern=[[1, P]], channel_multiplier=1)
                pool.affine_select(out=self.trib[:, :], in_=self.trib[:, :], compare_op=ALU.is_ge, fill=NEG,
                                   base=0, pattern=[[-1, P]], channel_multiplier=1)

            @block.vector
            def _(dve):
                dve.memset(self.onesb[:, :], 1.0)
                dve.wait_ge(cleared, 7)
                dve.tensor_copy(self.desc[:, :], desci[:, :])
                dve.wait_ge(loaded, 32)
                for n, (_, m) in enumerate(masks):
                    dve.tensor_scalar(m[:, :], raw[:, n, :], 1.0, -NEG, ALU.subtract, ALU.mult)


def load_rows(nc, name, x, X):
    with Stage(nc, name) as st:
        loaded = st.sem("loaded")
        block = st.block()

        @block.sync
        def _(sp):
            sp.dma_start(X[:, :, :], x.rearrange("(t p) d -> p t d", p=P)).then_inc(loaded, 16)
            sp.wait_ge(loaded, 16)


def store_rows(nc, name, X, out):
    with Stage(nc, name) as st:
        stored = st.sem("stored")
        block = st.block()

        @block.sync
        def _(sp):
            sp.dma_start(out.rearrange("(t p) d -> p t d", p=P), X[:, :, :]).then_inc(stored, 16)
            sp.wait_ge(stored, 16)


def program(nc, I, out, debug):
    Stage.cleared = []
    with ExitStack() as ctx:
        def sb(n, shape, dt=F32):
            return ctx.enter_context(nc.sbuf_tensor(n, shape, dt))
        C = Constants(nc, ctx, I)
        X = sb("X", [P, NT, D])
        Y = sb("Y", [P, NT, D])
        cols = sb("cols", [P, TOK])
        Z = sb("Z", [P, TOK])
        scratch = nc.dram_tensor("bias_table", (HEADS, TOEP), F32, kind="Internal").ap()
        c_scratch = nc.dram_tensor("expert_weights", (E, TOK), F32, kind="Internal").ap()

        def show(name, rows):
            if name in debug:
                store_rows(nc, "show_" + name, rows, debug[name])

        load_rows(nc, "load_x", I["x"], X)
        if RUN(0):
            cosine_attention(nc, "l0c", I, "L0_cond_", X, Y, C, scratch)
            show("L0_cond", Y)
        if RUN(1):
            distance_attention(nc, "l0a", I, "L0_attn_", Y, X, C, scratch)
            show("x0", X)
        if RUN(2):
            biased_attention(nc, "l0b", I, "L0_cond2_", X, Y, cols, C)
            show("L0_cond2", Y)
        if RUN(3):
            rerouted_experts(nc, "l0f", I, "L0_ffn_", cols, Z, C)
            add_columns(nc, "l0s", Z, X, C.ident)
            rows_to_columns(nc, "l0t", X, cols, C.ident)
            show("x1", X)
        if RUN(4):
            grouped_experts(nc, "l1c", I, "L1_cond_", cols, Z, C)
            if "L1_cond" in debug:
                add_columns(nc, "l1d", Z, Y, C.ident, add=False)
                show("L1_cond", Y)
            linear_attention(nc, "l1a", I, "L1_attn_", Z, X, C)
            show("x2", X)
        if RUN(5):
            biased_attention(nc, "l1b", I, "L1_cond2_", X, Y, cols, C)
            phase_ffn(nc, "l1f", I, "L1_ffn_", cols, X, C)
            rows_to_columns(nc, "l1t", X, cols, C.ident)
            show("x3", X)
        if RUN(6):
            grouped_experts(nc, "l2c", I, "L2_cond_", cols, Z, C)
            windowed_attention(nc, "l2a", I, "L2_attn_", Z, X, C)
            rows_to_columns(nc, "l2t", X, cols, C.ident)
            show("x4", X)
        if RUN(7):
            grouped_experts(nc, "l2b", I, "L2_cond2_", cols, Z, C)
            with ExitStack() as inner:
                cT = inner.enter_context(nc.sbuf_tensor("l2f_cT", [E, TOK], F32))
                route(nc, "l2f_r", Z, I["L2_ffn_Wr"], C, cT, softmax=False, bias=I["L2_ffn_br"], top=1)
                expert_mlps(nc, "l2f_x", Z, I["L2_ffn_W1"], I["L2_ffn_b1"], I["L2_ffn_W2"], I["L2_ffn_b2"],
                            ACT.Relu, cT, c_scratch, cols)
            add_columns(nc, "l2s", cols, X, C.ident)
            rows_to_columns(nc, "l2u", X, cols, C.ident)
            show("x5", X)
        if RUN(8):
            grouped_experts(nc, "l3c", I, "L3_cond_", cols, Z, C)
            add_columns(nc, "l3s", Z, Y, C.ident, add=False)
            show("L3_cond", Y)
            layered_attention(nc, "l3a", I, "L3_attn_", Y, C)
            show("L3_attn", Y)
            add_rows(nc, "l3r", Y, X)
            show("x6", X)
        if RUN(9):
            cosine_attention(nc, "l3b", I, "L3_cond2_", X, Y, C, scratch)
            show("L3_cond2", Y)
            rows_to_columns(nc, "l3t", Y, cols, C.ident)
            with ExitStack() as inner:
                cT = inner.enter_context(nc.sbuf_tensor("l3f_cT", [E, TOK], F32))
                route(nc, "l3f_r", cols, I["L3_ffn_router_w"], C, cT, bias=I["L3_ffn_router_b"],
                      capacity=-(-TOK * 5 // (E * 4)))
                expert_mlps(nc, "l3f_x", cols, I["L3_ffn_w1"], I["L3_ffn_b1"], I["L3_ffn_w2"], I["L3_ffn_b2"],
                            ACT.Gelu, cT, c_scratch, Z)
            add_columns(nc, "l3v", Z, X, C.ident)
            show("x7", X)
        store_rows(nc, "store", X, out)


def RUN(k):
    return k <= UPTO


LAYOUT = {
    "x": lambda a: a.reshape(TOK, D),
    "L0_attn_Wq": lambda a: a.T, "L0_attn_Wk": lambda a: a.T, "L0_attn_Wv": lambda a: a.T,
    "L0_attn_Wo": lambda a: a.T,
    "L0_attn_rel": lambda a: a[:, ::-1],
    "L0_ffn_gate_weight": lambda a: a.T,
    "L0_ffn_down": lambda a: a.transpose(0, 2, 1).reshape(E * P, D),
    "L0_ffn_gate": lambda a: a[:, :P, :].transpose(2, 0, 1).reshape(D, E * P),
    "L0_ffn_up": lambda a: a[:, P:, :].transpose(2, 0, 1).reshape(D, E * P),
    "cond_64_T": lambda a: a.T,
}
for _p in ("L1_cond_", "L2_cond_", "L2_cond2_", "L3_cond_"):
    LAYOUT.update({
        _p + "wt": lambda a: a.T, _p + "wg": lambda a: a.T,
        _p + "w_gate": lambda a: a.transpose(1, 0, 2).reshape(D, E * DH),
        _p + "w_up": lambda a: a.transpose(1, 0, 2).reshape(D, E * DH),
        _p + "w_down": lambda a: a.reshape(E * DH, D),
    })
for _v in ("b1", "quantum_phases", "quantum_weights_real", "quantum_weights_imag"):
    LAYOUT["L1_ffn_" + _v] = lambda a: a.reshape(-1, P).T
LAYOUT.update({
    "L2_attn_bq": lambda a: a.reshape(4, 4, 8).transpose(1, 2, 0),
    "L2_attn_bk": lambda a: a.reshape(2, 8).T,
    "L2_ffn_Wr": lambda a: a.T,
    "L2_ffn_W1": lambda a: a.transpose(0, 2, 1),
    "L2_ffn_W2": lambda a: a.transpose(0, 2, 1),
    "L2_ffn_b1": lambda a: a.reshape(E, -1, P).transpose(0, 2, 1),
    "L3_ffn_b1": lambda a: a.reshape(E, -1, P).transpose(0, 2, 1),
    "L3_attn_b1": lambda a: a.reshape(a.shape[0], -1, P).transpose(0, 2, 1),
})
PIECES = {"L0_ffn_gate_up_proj": ("L0_ffn_gate", "L0_ffn_up"), "L0_ffn_down_proj": ("L0_ffn_down",),
          "cond_64": ("cond_64", "cond_64_T")}


def kernel(**inputs):
    import numpy as _np
    import concourse.bacc as _bacc
    from concourse import mybir as _mybir
    from concourse.bass_utils import run_bass_kernel_spmd as _run

    nc = _bacc.Bacc("TRN2", target_bir_lowering=False, num_devices=1)
    arrays, I = {}, {}
    pieces = [(piece, a) for name, a in inputs.items() for piece in PIECES.get(name, (name,))]
    for name, a in pieces:
        a = _np.asarray(a)
        a = _np.ascontiguousarray(LAYOUT[name](a) if name in LAYOUT else a)
        arrays[f"in_{name}"] = a
        I[name] = nc.dram_tensor(f"in_{name}", a.shape, _mybir.dt.from_np(a.dtype), kind="ExternalInput").ap()
    out = nc.dram_tensor("out_0_dram", (TOK, D), _mybir.dt.float32, kind="ExternalOutput").ap()
    debug = {n: nc.dram_tensor("dbg_" + n, (TOK, D), _mybir.dt.float32, kind="ExternalOutput").ap()
             for n in DEBUG_NAMES}
    program(nc, I, out, debug)
    r = _run(nc, [arrays], core_ids=[0])
    return r.results[0]["out_0_dram"].reshape(B, N, D)
```

```python
from contextlib import ExitStack

import concourse.bass as bass
from concourse import mybir

F32 = mybir.dt.float32
BF16 = mybir.dt.bfloat16
I32 = mybir.dt.int32
U8 = mybir.dt.uint8
ALU = mybir.AluOpType
ACT = mybir.ActivationFunctionType
AX = mybir.AxisListType

P = 128
B, N, D = 2, 512, 128
TOK = B * N
NT = TOK // P
TPB = N // P
HEADS = 16
DH = 64
INNER = HEADS * DH
E = 8
NEG = -1.0e30
EPS = 1e-5
TOEP = N + P - 1

WARM = 4
DEBUG_NAMES = []
UPTO = 99


class Chain:

    def __init__(self, eng, sem):
        self.eng, self.sem, self.n = eng, sem, 0

    def __call__(self, ins, wait=True):
        ins.then_inc(self.sem, 1)
        self.n += 1
        if wait:
            self.eng.wait_ge(self.sem, self.n)

    def join(self):
        self.eng.wait_ge(self.sem, self.n)


class Stage:

    cleared = []

    def __init__(self, nc, name):
        self.nc, self.name, self.ctx, self.sems = nc, name, ExitStack(), []

    def sb(self, name, shape, dt=F32):
        return self.ctx.enter_context(self.nc.sbuf_tensor(f"{self.name}_{name}", shape, dt))

    def ps(self, name, shape, dt=F32):
        return self.ctx.enter_context(self.nc.psum_tensor(f"{self.name}_{name}", shape, dt))

    def sem(self, name):
        s = self.nc.alloc_semaphore(f"{self.name}_{name}")
        self.sems.append(s)
        return s

    def block(self):
        return self.ctx.enter_context(self.nc.Block())

    def __enter__(self):
        return self

    def __exit__(self, *a):
        done = self.ctx.__exit__(*a)
        if a[0] is None:
            for s in self.sems:
                self.nc.gpsimd.sem_clear(s)
            for s in Stage.cleared:
                self.nc.release_semaphore(s)
            Stage.cleared = self.sems
        return done


def dram_view(ap, offset, pattern):
    return bass.AP(tensor=ap.tensor, offset=offset, ap=pattern)


def row_to_all(ap, n, offset=0):
    if len(ap.shape) == 2 and ap.shape[0] == 1:
        return ap.partition_broadcast(P).rearrange("p a n -> p (a n)")
    return dram_view(ap, offset, [[0, P], [1, n]])


def rsqrt_rows(link, act_sqrt, var, root, r, t, eps):
    v = nc_vec(link)
    link(v.tensor_scalar(var, var, eps, None, ALU.add))
    act_sqrt()
    link(v.reciprocal(r, root))
    link(v.tensor_tensor(t, r, r, ALU.mult))
    link(v.tensor_tensor(t, t, var, ALU.mult))
    link(v.tensor_scalar(t, t, -0.5, 1.5, ALU.mult, ALU.add))
    link(v.tensor_tensor(r, r, t, ALU.mult))


def nc_vec(link):
    return link.eng


def layer_norm(nc, name, src, dst, gain, shift=None, dst_cols=None, ident=None, tiles=NT, silu=False):
    with Stage(nc, name) as st:
        g = st.sb("g", [P, D])
        s = st.sb("s", [P, D])
        stats = st.sb("stats", [P, tiles, 6])
        mv = st.sb("mv", [P, tiles, 2])
        var = st.sb("var", [P, tiles])
        root = st.sb("root", [P, tiles])
        rstd = st.sb("rstd", [P, tiles])
        tmp = st.sb("tmp", [P, tiles])
        turned = st.ps("turned", [P, tiles, P])
        loaded, chain, var_ready, root_ready, rows_ready, rows_silu, turned_ready, chain_act = (
            st.sem(x) for x in ("loaded", "chain", "var_ready", "root_ready", "rows_ready", "rows_silu",
                                "turned_ready", "chain_act"))
        n_loads = 16 * (1 + (shift is not None))
        block = st.block()

        @block.sync
        def _(sp):
            sp.dma_start(g[:, :], row_to_all(gain, D)).then_inc(loaded, 16)
            if shift is not None:
                sp.dma_start(s[:, :], row_to_all(shift, D)).then_inc(loaded, 16)

        @block.vector
        def _(dve):
            link = Chain(dve, chain)
            for t in range(tiles):
                link(dve.bn_stats(stats[:, t, :], src[:, t, :]), wait=False)
            for t in range(tiles):
                dve.wait_ge(chain, t + 1)
                link(dve.bn_aggr(mv[:, t, :], stats[:, t, :]), wait=False)
            link.join()
            link(dve.tensor_scalar(var[:, :], mv[:, :, 1], EPS, None, ALU.add))
            dve.engine_nop().then_inc(var_ready, 1)
            dve.wait_ge(root_ready, 1)
            link(dve.reciprocal(rstd[:, :], root[:, :]))
            link(dve.tensor_tensor(tmp[:, :], rstd[:, :], rstd[:, :], ALU.mult))
            link(dve.tensor_tensor(tmp[:, :], tmp[:, :], var[:, :], ALU.mult))
            link(dve.tensor_scalar(tmp[:, :], tmp[:, :], -0.5, 1.5, ALU.mult, ALU.add))
            link(dve.tensor_tensor(rstd[:, :], rstd[:, :], tmp[:, :], ALU.mult))
            for t in range(tiles):
                link(dve.tensor_scalar(dst[:, t, :], src[:, t, :], mv[:, t, 0:1], rstd[:, t:t + 1],
                                       ALU.subtract, ALU.mult), wait=False)
            dve.wait_ge(loaded, n_loads)
            link.join()
            for h in range(0, tiles, TPB):
                part = dst[:, h:h + TPB, :]
                mul = dve.tensor_tensor(part, part, g[:, None, :].to_broadcast([P, TPB, D]), ALU.mult)
                if shift is not None:
                    link(mul)
                    mul = dve.tensor_tensor(part, part, s[:, None, :].to_broadcast([P, TPB, D]), ALU.add)
                mul.then_inc(rows_ready, 1)
            if dst_cols is not None:
                dve.wait_ge(turned_ready, 1)
                dve.tensor_copy(dst_cols[:, 0:N], turned[:, 0:TPB, :])

        @block.scalar
        def _(act):
            act.wait_ge(var_ready, 1)
            act.activation(root[:, :], var[:, :], ACT.Sqrt).then_inc(root_ready, 1)
            if silu:
                for h in range(0, tiles, TPB):
                    act.wait_ge(rows_ready, h // TPB + 1)
                    part = dst[:, h:h + TPB, :]
                    act.activation(part, part, ACT.Silu).then_inc(rows_silu, 1)
            if dst_cols is not None and tiles > TPB:
                act.wait_ge(turned_ready, 2)
                act.activation(dst_cols[:, N:2 * N], turned[:, TPB:2 * TPB, :], ACT.Copy)

        @block.tensor
        def _(pe):
            if dst_cols is not None:
                for h in range(0, tiles, TPB):
                    pe.wait_ge(rows_silu if silu else rows_ready, h // TPB + 1)
                    for t in range(h, h + TPB):
                        last = pe.transpose(turned[:, t, :], dst[:, t, :], ident[:, :])
                    last.then_inc(turned_ready, 1)


def rows_to_columns(nc, name, src, dst_cols, ident):
    with Stage(nc, name) as st:
        turned = st.ps("turned", [P, NT, P])
        turned_ready = st.sem("turned_ready")
        block = st.block()

        @block.tensor
        def _(pe):
            for t in range(NT):
                last = pe.transpose(turned[:, t, :], src[:, t, :], ident[:, :])
                if t % TPB == TPB - 1:
                    last.then_inc(turned_ready, 1)

        @block.vector
        def _(dve):
            dve.wait_ge(turned_ready, 1)
            dve.tensor_copy(dst_cols[:, 0:N], turned[:, 0:TPB, :])

        @block.scalar
        def _(act):
            act.wait_ge(turned_ready, 2)
            act.activation(dst_cols[:, N:2 * N], turned[:, TPB:NT, :], ACT.Copy)


def add_columns(nc, name, cols, rows, ident, add=True):
    with Stage(nc, name) as st:
        turned = st.ps("turned", [P, NT, P])
        turned_ready = st.sem("turned_ready")
        block = st.block()

        @block.tensor
        def _(pe):
            for t in range(NT):
                last = pe.transpose(turned[:, t, :], cols[:, t * P:(t + 1) * P], ident[:, :])
                if t % TPB == TPB - 1:
                    last.then_inc(turned_ready, 1)

        @block.vector
        def _(dve):
            for h in range(2):
                dve.wait_ge(turned_ready, h + 1)
                part = rows[:, h * TPB:(h + 1) * TPB, :]
                if add:
                    dve.tensor_tensor(part, part, turned[:, h * TPB:(h + 1) * TPB, :], ALU.add)
                else:
                    dve.tensor_copy(part, turned[:, h * TPB:(h + 1) * TPB, :])


def shared_kv(nc, name, xn_cols, w_kv, null_kv, kT, k_null, v_rows, v_null, ident, k_gain=None, q_gain=None):
    with Stage(nc, name) as st:
        wkv = st.sb("wkv", [P, 2 * DH])
        kk = st.sb("kk", [P, NT, 2, DH])
        sq = st.sb("sq", [P, NT, DH])
        gain = st.sb("gain", [P, 2, DH])
        gcol = st.sb("gcol", [P, 2])
        nrm = st.sb("nrm", [P, NT + 1])
        root = st.sb("root", [P, NT + 1])
        rec = st.sb("rec", [P, NT + 1])
        tmp = st.sb("tmp", [P, NT + 1])
        sqn = st.sb("sqn", [P, 2])
        ones = st.sb("ones", [P, P])
        kv = st.ps("kv", [P, NT, 2 * DH])
        turned = st.ps("turned", [P, NT, P])
        nn = st.ps("nn", [P, 1])
        loaded, kv_ready, chain, k_ready, turned_ready, nrm_ready, root_ready, null_sq, null_len = (
            st.sem(x) for x in ("loaded", "kv_ready", "chain", "k_ready", "turned_ready", "nrm_ready",
                                "root_ready", "null_sq", "null_len"))
        n_loads = 16 * (4 + (6 if k_gain is not None else 0))
        block = st.block()

        @block.sync
        def _(sp):
            sp.dma_start(wkv[:, :], w_kv).then_inc(loaded, 16)
            sp.dma_start(v_null[:, :], row_to_all(null_kv, DH, DH)).then_inc(loaded, 16)
            for c in range(2):
                sp.dma_start(k_null[c * DH:(c + 1) * DH, c:c + 1], dram_view(null_kv, 0, [[1, DH], [1, 1]]))\
                    .then_inc(loaded, 16)
            if k_gain is not None:
                for n, v in enumerate((k_gain, q_gain)):
                    sp.dma_start(gain[:, n, :], row_to_all(v, DH)).then_inc(loaded, 16)
                    for c in range(2):
                        sp.dma_start(gcol[c * DH:(c + 1) * DH, n:n + 1], dram_view(v, 0, [[1, DH], [1, 1]]))\
                            .then_inc(loaded, 16)

        @block.tensor
        def _(pe):
            pe.wait_ge(loaded, n_loads)
            for t in range(NT):
                last = pe.matmul(kv[:, t, :], xn_cols[:, t * P:(t + 1) * P], wkv[:, :], start=True, stop=True)
                if t % TPB == TPB - 1:
                    last.then_inc(kv_ready, 1)
            if k_gain is not None:
                pe.wait_ge(null_sq, 1)
                pe.matmul(nn[:, :], ones[0:DH, :], sqn[0:DH, 0:1], start=True, stop=True).then_inc(null_len, 1)
            pe.wait_ge(k_ready, 1)
            for t in range(NT):
                last = pe.transpose(turned[:, t, :], kk[:, t, :, :], ident[:, :])
                if t % TPB == TPB - 1:
                    last.then_inc(turned_ready, 1)

        @block.scalar
        def _(act):
            if k_gain is not None:
                act.wait_ge(nrm_ready, 1)
                act.activation(root[:, :], nrm[:, :], ACT.Sqrt).then_inc(root_ready, 1)
            act.wait_ge(turned_ready, 2)
            act.activation(kT[DH:P, 1, :], turned[DH:P, :, :], ACT.Copy)

        @block.gpsimd
        def _(pool):
            pool.memset(kT[0:DH, 1, :], 0.0)
            pool.memset(kT[DH:P, 0, :], 0.0)

        @block.vector
        def _(dve):
            link = Chain(dve, chain)
            link(dve.memset(ones[:, :], 1.0), wait=False)
            link(dve.memset(k_null[DH:P, 0:1], 0.0), wait=False)
            link(dve.memset(k_null[0:DH, 1:2], 0.0))
            dve.wait_ge(loaded, n_loads)
            dve.wait_ge(kv_ready, 2)
            link(dve.tensor_tensor(v_rows[:, :, :], kv[:, :, DH:2 * DH],
                                   v_null[:, None, :].to_broadcast([P, NT, DH]), ALU.subtract), wait=False)
            if k_gain is None:
                for c in range(2):
                    link(dve.tensor_scalar(kk[:, :, c, :], kv[:, :, 0:DH], DH ** -0.5, None, ALU.mult), wait=False)
                link(dve.tensor_scalar(k_null[:, :], k_null[:, :], DH ** -0.5, None, ALU.mult))
            else:
                link(dve.tensor_copy(kk[:, :, 0, :], kv[:, :, 0:DH]))
                link(dve.tensor_tensor(sq[:, :, :], kk[:, :, 0, :], kk[:, :, 0, :], ALU.mult))
                link(dve.tensor_reduce(nrm[:, 0:NT], sq[:, :, :], AX.X, ALU.add))
                dve.tensor_tensor(sqn[:, :], k_null[:, :], k_null[:, :], ALU.mult).then_inc(null_sq, 1)
                dve.wait_ge(null_len, 1)
                link(dve.tensor_copy(nrm[:, NT:NT + 1], nn[:, :]))
                link(dve.tensor_scalar(nrm[:, :], nrm[:, :], 1e-24, None, ALU.max))
                dve.engine_nop().then_inc(nrm_ready, 1)
                dve.wait_ge(root_ready, 1)
                link(dve.reciprocal(rec[:, :], root[:, :]))
                link(dve.tensor_tensor(tmp[:, :], rec[:, :], rec[:, :], ALU.mult))
                link(dve.tensor_tensor(tmp[:, :], tmp[:, :], nrm[:, :], ALU.mult))
                link(dve.tensor_scalar(tmp[:, :], tmp[:, :], -0.5, 1.5, ALU.mult, ALU.add))
                link(dve.tensor_tensor(rec[:, :], rec[:, :], tmp[:, :], ALU.mult))
                link(dve.tensor_tensor(gain[:, 0, :], gain[:, 0, :], gain[:, 1, :], ALU.mult))
                link(dve.tensor_tensor(kk[:, :, 0, :], kk[:, :, 0, :],
                                       rec[:, 0:NT, None].to_broadcast([P, NT, DH]), ALU.mult))
                link(dve.tensor_tensor(kk[:, :, 0, :], kk[:, :, 0, :],
                                       gain[:, 0:1, :].to_broadcast([P, NT, DH]), ALU.mult))
                link(dve.tensor_copy(kk[:, :, 1, :], kk[:, :, 0, :]))
                link(dve.tensor_tensor(gcol[:, 0:1], gcol[:, 0:1], gcol[:, 1:2], ALU.mult))
                link(dve.tensor_scalar(k_null[:, :], k_null[:, :], rec[:, NT:NT + 1], gcol[:, 0:1],
                                       ALU.mult, ALU.mult))
            dve.engine_nop().then_inc(k_ready, 1)
            dve.wait_ge(turned_ready, 2)
            dve.tensor_copy(kT[0:DH, 0, :], turned[0:DH, :, :])


def query_lengths(nc, name, xn_cols, w_q, scale, rq):
    with Stage(nc, name) as st:
        wq = st.sb("wq", [P, INNER])
        sq = st.sb("sq", [P, 2, INNER])
        nrm = st.sb("nrm", [P, NT * HEADS])
        root = st.sb("root", [P, NT * HEADS])
        tmp = st.sb("tmp", [P, NT * HEADS])
        q = st.ps("q", [P, 2, INNER])
        loaded, q_ready, sq_ready, sq_read, nrm_ready, root_ready, chain = (
            st.sem(x) for x in ("loaded", "q_ready", "sq_ready", "sq_read", "nrm_ready", "root_ready", "chain"))
        block = st.block()

        @block.sync
        def _(sp):
            sp.dma_start(wq[:, :], w_q).then_inc(loaded, 16)

        @block.tensor
        def _(pe):
            pe.wait_ge(loaded, 16)
            for t in range(NT):
                if t >= 2:
                    pe.wait_ge(sq_ready, t - 1)
                for h in range(2):
                    last = pe.matmul(q[:, t % 2, h * N:(h + 1) * N], xn_cols[:, t * P:(t + 1) * P],
                                     wq[:, h * N:(h + 1) * N], start=True, stop=True)
                last.then_inc(q_ready, 1)

        @block.scalar
        def _(act):
            for t in range(NT):
                act.wait_ge(q_ready, t + 1)
                if t >= 2:
                    act.wait_ge(sq_read, t - 1)
                act.activation(sq[:, t % 2, :], q[:, t % 2, :], ACT.Square).then_inc(sq_ready, 1)
            act.wait_ge(nrm_ready, 1)
            act.activation(root[:, :], nrm[:, :], ACT.Sqrt).then_inc(root_ready, 1)

        @block.vector
        def _(dve):
            link = Chain(dve, chain)
            r = rq[:, :, :].rearrange("p t h -> p (t h)")
            for t in range(NT):
                dve.wait_ge(sq_ready, t + 1)
                dve.tensor_reduce(nrm[:, t * HEADS:(t + 1) * HEADS],
                                  sq[:, t % 2, :].rearrange("p (h d) -> p h d", h=HEADS), AX.X, ALU.add)\
                    .then_inc(sq_read, 1)
            dve.wait_ge(sq_read, NT)
            link(dve.tensor_scalar(nrm[:, :], nrm[:, :], 1e-24, None, ALU.max))
            dve.engine_nop().then_inc(nrm_ready, 1)
            dve.wait_ge(root_ready, 1)
            link(dve.reciprocal(r, root[:, :]))
            link(dve.tensor_tensor(tmp[:, :], r, r, ALU.mult))
            link(dve.tensor_tensor(tmp[:, :], tmp[:, :], nrm[:, :], ALU.mult))
            link(dve.tensor_scalar(tmp[:, :], tmp[:, :], -0.5 * scale, 1.5 * scale, ALU.mult, ALU.add))
            link(dve.tensor_tensor(r, r, tmp[:, :], ALU.mult))


def attend(nc, name, x_cols, w_q, O, v_rows, ident, identb, onesb, trib, dh=DH, w_k=None, q_scale=1.0, kT=None,
           nulls=None, v_null=None, key_mask=None, rq=None, side=None, toeplitz=None):
    null = int(nulls is not None)
    UNITS = 2 * B * TPB
    PAIRS = HEADS // 2
    TURN_LAG, COPY_LAG, VALUES_LAG, INV_LAG, OUT_LAG = 2, 3, 4, 3, 5
    SLOTS = 4
    with Stage(nc, name) as st:
        wbuf = st.sb("wbuf", [P, 2, P])
        qbuf = st.sb("qbuf", [P, B, N])
        kbuf = st.sb("kbuf", [P, B, 2, N]) if w_k is not None else None
        bias = st.sb("bias", [P, 4, TPB, N]) if side is not None else None
        S = st.sb("S", [P, SLOTS, N + 1])
        Pr = st.sb("Pr", [P, SLOTS, N + 1])
        PT = st.sb("PT", [P, 2, N])
        nmax = st.sb("nmax", [P, 8])
        rsum = st.sb("rsum", [P, 8])
        rinv = st.sb("rinv", [P, 8])
        psS = st.ps("psS", [P, SLOTS, N])
        psT = st.ps("psT", [P, 2, N])
        psO = st.ps("psO", [P, N])
        psQ = st.ps("psQ", [P, N])
        (w_in, q_out, q_in, s_out, biased, maxed, probs, pt_out, pt_in, pv_out, inv, o_in,
         consts, w_clear) = (
            st.sem(x) for x in ("w_in", "q_out", "q_in", "s_out", "biased", "maxed", "probs", "pt_out",
                                "pt_in", "pv_out", "inv", "o_in", "consts", "w_clear"))
        bias_in = [st.sem(f"bias_in{hh}") for hh in range(2)]
        NQ = 1 if w_k is None else 2
        W_INC = 16 * (2 if w_k is None else 4)
        block = st.block()

        def unit(u):
            b, hh, qt = u // (2 * TPB), u // TPB % 2, u % TPB
            return b, hh, qt, (qt + 1) * P

        def behind(step, pair, u, first):
            if u >= 0:
                step(pair, u, first)
            elif not first:
                step(pair - 1, UNITS + u, False)

        def mod4(pair, hh):
            return (pair % 2) * 2 + hh

        @block.sync
        def _(sp):
            if dh < DH:
                sp.wait_ge(w_clear, 1)

            def load_weights(pair):
                for n, w in enumerate((w_q, w_k)[:NQ]):
                    for hh in range(2):
                        sp.dma_start(wbuf[:, n, hh * DH:hh * DH + dh], w[:, bass.ds(pair * (2 * dh) + hh * dh, dh)])\
                            .then_inc(w_in, 16)

            def load_bias(pair, first):
                for hh in range(2):
                    if not first:
                        sp.wait_ge(biased, (1 + null) * (pair * UNITS - UNITS + TPB * hh + 1))
                    for qt in range(TPB):
                        n = (qt + 1) * P
                        src = side[bass.ds(pair * 2 + hh, 1), qt * P:(qt + 1) * P, 0:n]\
                            .rearrange("a p j -> p (a j)")
                        sp.dma_start(bias[:, bass.ds(mod4(pair, hh), 1), qt, N - n:N]
                                     .rearrange("p a j -> p (a j)"), src).then_inc(bias_in[hh], 16)

            load_weights(0)
            if side is not None:
                load_bias(0, True)
            with sp.Fori(1, PAIRS) as pair:
                sp.wait_ge(q_out, pair * (2 * NQ))
                load_weights(pair)
                if side is not None:
                    load_bias(pair, False)

        @block.tensor
        def _(pe):
            def project(pair, b):
                pe.wait_ge(w_in, pair * W_INC + W_INC)
                for n in range(NQ):
                    if b or n or not isinstance(pair, int) or pair:
                        pe.wait_ge(q_in, pair * (2 * NQ) + b * NQ + n)
                    pe.matmul(psQ[:, :], wbuf[:, n, :], x_cols[:, b * N:(b + 1) * N],
                              start=True, stop=True).then_inc(q_out, 1)

            def scores(pair, u, first):
                b, hh, qt, n = unit(u)
                g = pair * UNITS + u
                if u % (2 * TPB) == 0:
                    pe.wait_ge(q_in, pair * (2 * NQ) + (b + 1) * NQ)
                if not first or u >= SLOTS:
                    pe.wait_ge(biased, (g - SLOTS + 1) * (1 + null))
                q = qbuf[:, b, qt * P:(qt + 1) * P]
                keys = kbuf[:, b, hh, 0:n] if w_k is not None else kT[:, hh, b * N:b * N + n]
                out = psS[:, u % SLOTS, :]
                if key_mask is not None:
                    pe.matmul(out[:, 0:n], onesb[:, :], key_mask[:, b * N:b * N + n], start=True, stop=False,
                              skip_group_check=True)
                if side is not None:
                    pe.matmul(out[:, n - P:n], identb[:, :], trib[:, :], start=key_mask is None, stop=False,
                              skip_group_check=True)
                last = pe.matmul(out[:, 0:n], q, keys, start=key_mask is None and side is None, stop=True,
                                 skip_group_check=True)
                last.then_inc(s_out, 1)

            def turn(pair, u, first):
                _, _, qt, n = unit(u % UNITS)
                g = pair * UNITS + u
                pe.wait_ge(probs, g + 1)
                if not first or u >= 2:
                    pe.wait_ge(pt_in, g - 1)
                for k in range(qt + 1):
                    last = pe.transpose(psT[:, u % 2, k * P:(k + 1) * P],
                                        Pr[:, u % SLOTS, null + k * P:null + (k + 1) * P], ident[:, :])
                last.then_inc(pt_out, 1)

            def values(pair, u, first):
                b, hh, qt, n = unit(u % UNITS)
                g = pair * UNITS + u
                pe.wait_ge(pt_in, g + 1)
                if not first or u >= 1:
                    pe.wait_ge(o_in, g)
                for k in range(qt + 1):
                    v = v_rows[:, b * TPB + k, :] if kT is not None else \
                        v_rows[:, b * TPB + k, bass.ds(pair * (2 * dh) + hh * dh, dh)]
                    last = pe.matmul(psO[:, 0:dh], PT[:, u % 2, k * P:(k + 1) * P], v,
                                     start=k == 0, stop=k == qt)
                last.then_inc(pv_out, 1)

            def body(pair, first, last):
                for u in range(UNITS):
                    if u == 0:
                        project(pair, 1)
                    if u == UNITS // 2 and not last:
                        project(pair + 1, 0)
                    scores(pair, u, first)
                    behind(turn, pair, u - TURN_LAG, first)
                    behind(values, pair, u - VALUES_LAG, first)

            for _ in range(WARM):
                pe.matmul(psQ[:, :], x_cols[:, 0:P], x_cols[:, 0:N], start=True, stop=True)
            if w_k is not None:
                pe.wait_ge(consts, 2)
            project(0, 0)
            body(0, True, False)
            with pe.Fori(1, PAIRS - 1) as pair:
                body(pair, False, False)
            body(PAIRS - 1, False, True)
            for u in range(UNITS, UNITS + VALUES_LAG):
                if u - TURN_LAG < UNITS:
                    turn(PAIRS - 1, u - TURN_LAG, False)
                values(PAIRS - 1, u - VALUES_LAG, False)

        @block.scalar
        def _(act):
            def copy_q(pair, b, first):
                for n in range(NQ):
                    m = pair * (2 * NQ) + b * NQ + n
                    act.wait_ge(q_out, m + 1)
                    if n == 0 and not (first and (b or isinstance(pair, int) and pair == 0)):
                        act.wait_ge(s_out, pair * UNITS - UNITS // 2 * (1 - b))
                    if n == 0:
                        last = act.activation(qbuf[:, b, :], psQ[:, :], ACT.Copy, scale=q_scale)
                    else:
                        for hh in range(2):
                            rows = slice(hh * DH, (hh + 1) * DH)
                            last = act.activation(kbuf[rows, b, hh, :], psQ[rows, :], ACT.Copy)
                    last.then_inc(q_in, 1)

            def exps(pair, u, first):
                _, _, _, n = unit(u)
                g = pair * UNITS + u
                act.wait_ge(maxed, g + 1)
                if not first or u >= SLOTS:
                    act.wait_ge(pt_out, g - SLOTS + 1)
                w = n + null
                act.activation(Pr[:, u % SLOTS, 0:w], S[:, u % SLOTS, 0:w], ACT.Exp, bias=nmax[:, u % 8:u % 8 + 1],
                               accum_out=rsum[:, u % 8:u % 8 + 1]).then_inc(probs, 1)

            def copy_pt(pair, u, first):
                _, _, _, n = unit(u)
                g = pair * UNITS + u
                act.wait_ge(pt_out, g + 1)
                if not first or u >= 2:
                    act.wait_ge(pv_out, g - 1)
                act.activation(PT[:, u % 2, 0:n], psT[:, u % 2, 0:n], ACT.Copy).then_inc(pt_in, 1)

            def body(pair, first, last):
                for u in range(UNITS):
                    if u == 0:
                        copy_q(pair, 1, first)
                    if u == UNITS // 2 and not last:
                        copy_q(pair + 1, 0, False)
                    behind(copy_pt, pair, u - COPY_LAG, first)
                    exps(pair, u, first)

            copy_q(0, 0, True)
            body(0, True, False)
            with act.Fori(1, PAIRS - 1) as pair:
                body(pair, False, False)
            body(PAIRS - 1, False, True)
            for u in range(UNITS - COPY_LAG, UNITS):
                copy_pt(PAIRS - 1, u, False)

        @block.vector
        def _(dve):
            def score_bias(pair, u, first):
                b, hh, qt, n = unit(u)
                g = pair * UNITS + u
                if not first or u >= SLOTS:
                    dve.wait_ge(probs, g - SLOTS + 1)
                head = bass.ds(pair * 2 + hh, 1)
                if null:
                    dve.tensor_scalar(S[:, u % SLOTS, 0:1], nulls[:, b * TPB + qt, head], 1.0, None, ALU.mult)\
                        .then_inc(biased, 1)
                dve.wait_ge(s_out, g + 1)
                if side is not None and u in (0, TPB):
                    dve.wait_ge(bias_in[hh], pair * (16 * TPB) + 16 * TPB)
                if side is not None:
                    add = bias[:, bass.ds(mod4(pair, hh), 1), qt, N - n:N]
                else:
                    add = toeplitz[:, head, N - n:N]
                add = add.rearrange("p a j -> p (a j)")
                scale = 1.0 if rq is None else rq[:, b * TPB + qt, head]
                dve.scalar_tensor_tensor(out=S[:, u % SLOTS, null:null + n], in0=psS[:, u % SLOTS, 0:n],
                                         scalar=scale, in1=add, op0=ALU.mult, op1=ALU.add).then_inc(biased, 1)

            def row_maximum(pair, u, first):
                _, _, _, n = unit(u)
                dve.wait_ge(biased, (pair * UNITS + u + 1) * (1 + null))
                dve.tensor_reduce(nmax[:, u % 8:u % 8 + 1], S[:, u % SLOTS, 0:n + null], AX.X, ALU.max,
                                  negate=True).then_inc(maxed, 1)

            def inverse_sum(pair, u, first):
                dve.wait_ge(probs, pair * UNITS + u + 1)
                dve.reciprocal(rinv[:, u % 8:u % 8 + 1], rsum[:, u % 8:u % 8 + 1]).then_inc(inv, 1)

            def outputs(pair, u, first):
                b, hh, qt, _ = unit(u)
                s = u % 8
                dve.wait_ge(inv, pair * UNITS + u + 1)
                dve.wait_ge(pv_out, pair * UNITS + u + 1)
                dst = O[:, b * TPB + qt, bass.ds(pair * (2 * dh) + hh * dh, dh)]
                if null:
                    dve.scalar_tensor_tensor(out=dst, in0=psO[:, 0:dh], scalar=rinv[:, s:s + 1],
                                             in1=v_null[:, :], op0=ALU.mult, op1=ALU.add).then_inc(o_in, 1)
                else:
                    dve.tensor_scalar(dst, psO[:, 0:dh], rinv[:, s:s + 1], None, ALU.mult)\
                        .then_inc(o_in, 1)

            def body(pair, first, last):
                for u in range(UNITS):
                    behind(outputs, pair, u - OUT_LAG, first)
                    score_bias(pair, u, first)
                    behind(inverse_sum, pair, u - INV_LAG, first)
                    row_maximum(pair, u, first)

            if dh < DH:
                dve.memset(wbuf[:, :, :], 0.0).then_inc(w_clear, 1)
            if w_k is not None:
                dve.memset(kbuf[0:DH, :, 1, :], 0.0).then_inc(consts, 1)
                dve.memset(kbuf[DH:P, :, 0, :], 0.0).then_inc(consts, 1)
            body(0, True, False)
            with dve.Fori(1, PAIRS - 1) as pair:
                body(pair, False, False)
            body(PAIRS - 1, False, True)
            for u in range(UNITS - OUT_LAG, UNITS):
                if u + OUT_LAG - INV_LAG < UNITS:
                    inverse_sum(PAIRS - 1, u + OUT_LAG - INV_LAG, False)
                outputs(PAIRS - 1, u, False)


def null_scores(nc, name, xn_cols, w_q, k_null, bias, nulls, ident, rq=None):
    with Stage(nc, name) as st:
        wq = st.sb("wq", [P, HEADS, DH])
        prod = st.sb("prod", [P, HEADS, DH])
        wn = st.sb("wn", [P, HEADS])
        nb = st.sb("nb", [P, HEADS])
        spread = st.sb("spread", [P, P])
        row = st.ps("row", [P, N])
        y = st.ps("y", [P, NT, HEADS])
        loaded, spread_ready, row_ready, wn_ready, y_ready, chain = (
            st.sem(x) for x in ("loaded", "spread_ready", "row_ready", "wn_ready", "y_ready", "chain"))
        block = st.block()

        @block.sync
        def _(sp):
            sp.dma_start(wq[:, :, :].rearrange("p h d -> p (h d)"), w_q).then_inc(loaded, 16)
            sp.dma_start(nb[:, :], row_to_all(bias, HEADS)).then_inc(loaded, 16)

        @block.tensor
        def _(pe):
            pe.wait_ge(spread_ready, 1)
            pe.matmul(row[:, 0:DH], spread[:, :], ident[:, 0:DH], start=True, stop=True).then_inc(row_ready, 1)
            pe.wait_ge(wn_ready, 1)
            for t in range(NT):
                last = pe.matmul(y[:, t, :], xn_cols[:, t * P:(t + 1) * P], wn[:, :], start=True, stop=True)
            last.then_inc(y_ready, 1)

        @block.vector
        def _(dve):
            link = Chain(dve, chain)
            dve.tensor_copy(spread[:, :], k_null[:, 0:1].to_broadcast([P, P])).then_inc(spread_ready, 1)
            dve.wait_ge(loaded, 32)
            dve.wait_ge(row_ready, 1)
            link(dve.tensor_tensor(prod[:, :, :], wq[:, :, :], row[:, None, 0:DH].to_broadcast([P, HEADS, DH]),
                                   ALU.mult))
            dve.tensor_reduce(wn[:, :], prod[:, :, :], AX.X, ALU.add).then_inc(wn_ready, 1)
            dve.wait_ge(y_ready, 1)
            if rq is not None:
                link(dve.tensor_tensor(nulls[:, :, :], y[:, :, :], rq[:, :, :], ALU.mult))
                dve.tensor_tensor(nulls[:, :, :], nulls[:, :, :], nb[:, None, :].to_broadcast([P, NT, HEADS]), ALU.add)
            else:
                dve.tensor_tensor(nulls[:, :, :], y[:, :, :], nb[:, None, :].to_broadcast([P, NT, HEADS]), ALU.add)


def project_rows(nc, name, O, width, w_out, dst, addends, ident):
    CH = width // P
    with Stage(nc, name) as st:
        w = st.sb("w", [P, CH, D])
        OT = st.sb("OT", [P, 2, CH, P])
        turned = st.ps("turned", [P, 2, CH * P if CH > 1 else N])
        y = st.ps("y", [P, 2, N])
        loaded, turned_ready, ot_ready, y_ready, y_read, chain = (
            st.sem(x) for x in ("loaded", "turned_ready", "ot_ready", "y_ready", "y_read", "chain"))
        block = st.block()

        @block.sync
        def _(sp):
            sp.dma_start(w[:, :, :], w_out.rearrange("(c p) n -> p c n", p=P)).then_inc(loaded, 16)

        @block.tensor
        def _(pe):
            def product(t):
                if t == 0:
                    pe.wait_ge(loaded, 16)
                pe.wait_ge(ot_ready, t + 1)
                if t >= 2:
                    pe.wait_ge(y_read, t - 1)
                for c in range(CH):
                    last = pe.matmul(y[:, t % 2, 0:D], OT[:, t % 2, c, :], w[:, c, :], start=c == 0, stop=c == CH - 1)
                last.then_inc(y_ready, 1)

            for t in range(NT):
                if t >= 2:
                    pe.wait_ge(ot_ready, t - 1)
                for c in range(CH):
                    last = pe.transpose(turned[:, t % 2, c * P:(c + 1) * P], O[:, t, c * P:(c + 1) * P], ident[:, :])
                last.then_inc(turned_ready, 1)
                if t >= 1:
                    product(t - 1)
            product(NT - 1)

        @block.scalar
        def _(act):
            for t in range(NT):
                act.wait_ge(turned_ready, t + 1)
                if t >= 2:
                    act.wait_ge(y_ready, t - 1)
                act.activation(OT[:, t % 2, :, :], turned[:, t % 2, 0:CH * P], ACT.Copy).then_inc(ot_ready, 1)

        @block.vector
        def _(dve):
            link = Chain(dve, chain)
            for t in range(NT):
                dve.wait_ge(y_ready, t + 1)
                if not addends:
                    dve.tensor_copy(dst[:, t, :], y[:, t % 2, 0:D]).then_inc(y_read, 1)
                    continue
                dve.tensor_tensor(dst[:, t, :], y[:, t % 2, 0:D], addends[0](t), ALU.add).then_inc(y_read, 1)
                for a in addends[1:]:
                    dve.wait_ge(y_read, t + 1)
                    link(dve.tensor_tensor(dst[:, t, :], dst[:, t, :], a(t), ALU.add))


def toeplitz_from_table(nc, name, table, scratch, T, C):
    with Stage(nc, name) as st:
        turned = st.sb("turned", [P, HEADS, N])
        ps = st.ps("ps", [P, 4, N])
        stored, flipped, out_v, out_a = (st.sem(x) for x in ("stored", "flipped", "out_v", "out_a"))
        spread = [st.sem(f"spread{h}") for h in range(4)]
        block = st.block()

        @block.sync
        def _(sp):
            sp.dma_start(scratch, table[:, :]).then_inc(stored, 16)
            sp.wait_ge(stored, 16)
            for q in range(4):
                sp.dma_start(turned[:, q * 4:(q + 1) * 4, :],
                             dram_view(scratch, q * 4 * TOEP, [[1, P], [TOEP, 4], [1, N]])).then_inc(spread[q], 16)

        @block.tensor
        def _(pe):
            for h in range(HEADS):
                if h % 4 == 0:
                    pe.wait_ge(spread[h // 4], 16)
                if h >= 4:
                    pe.wait_ge((out_v, out_a)[h % 2], (h - 4) // 2 + 1)
                pe.matmul(ps[:, h % 4, :], C.flip[:, :], turned[:, h, :], start=True, stop=True)\
                    .then_inc(flipped, 1)

        @block.scalar
        def _(act):
            for h in range(1, HEADS, 2):
                act.wait_ge(flipped, h + 1)
                act.activation(T[:, h, 0:N], ps[:, h % 4, :], ACT.Copy).then_inc(out_a, 1)

        @block.vector
        def _(dve):
            for h in range(0, HEADS, 2):
                dve.wait_ge(flipped, h + 1)
                dve.tensor_copy(T[:, h, 0:N], ps[:, h % 4, :]).then_inc(out_v, 1)


def position_bias(nc, name, I, pre, T, scratch, C):
    ident = C.ident
    h = nc.sbuf_tensor
    with ExitStack() as ctx:
        rows = ctx.enter_context(h(f"{name}_rows", [P, TPB, D], F32))
        cols = ctx.enter_context(h(f"{name}_cols", [P, N], F32))
        table = ctx.enter_context(h(f"{name}_table", [HEADS, TOEP], F32))
        with Stage(nc, name + "_in") as st:
            w0 = st.sb("w0", [P, D])
            b0 = st.sb("b0", [P, D])
            posi = st.sb("posi", [P, TPB], I32)
            pos = st.sb("pos", [P, TPB])
            loaded, made, conv = (st.sem(x) for x in ("loaded", "made", "conv"))
            block = st.block()

            @block.sync
            def _(sp):
                sp.dma_start(w0[:, :], row_to_all(I[pre + "w0"], D)).then_inc(loaded, 16)
                sp.dma_start(b0[:, :], row_to_all(I[pre + "b0"], D)).then_inc(loaded, 16)

            @block.gpsimd
            def _(pool):
                pool.iota(posi[:, :], pattern=[[-P, TPB]], base=N - 1, channel_multiplier=-1).then_inc(made, 1)

            @block.vector
            def _(dve):
                dve.wait_ge(made, 1)
                dve.tensor_copy(pos[:, :], posi[:, :]).then_inc(conv, 1)
                dve.wait_ge(conv, 1)
                dve.wait_ge(loaded, 32)
                for t in range(TPB):
                    dve.scalar_tensor_tensor(out=rows[:, t, :], in0=w0[:, :], scalar=pos[:, t:t + 1], in1=b0[:, :],
                                             op0=ALU.mult, op1=ALU.add)

        layer_norm(nc, name + "_n0", rows, rows, I[pre + "g0"], dst_cols=cols, ident=ident, tiles=TPB, silu=True)
        with Stage(nc, name + "_mid") as st:
            w1 = st.sb("w1", [P, D])
            b1 = st.sb("b1", [P, D])
            y = st.ps("y", [P, TPB, D])
            loaded, y_ready = (st.sem(x) for x in ("loaded", "y_ready"))
            block = st.block()

            @block.sync
            def _(sp):
                sp.dma_start(w1[:, :], I[pre + "w1"]).then_inc(loaded, 16)
                sp.dma_start(b1[:, :], row_to_all(I[pre + "b1"], D)).then_inc(loaded, 16)

            @block.tensor
            def _(pe):
                pe.wait_ge(loaded, 32)
                for t in range(TPB):
                    last = pe.matmul(y[:, t, :], cols[:, t * P:(t + 1) * P], w1[:, :], start=True, stop=True)
                last.then_inc(y_ready, 1)

            @block.vector
            def _(dve):
                dve.wait_ge(y_ready, 1)
                dve.wait_ge(loaded, 32)
                dve.tensor_tensor(rows[:, :, :], y[:, :, :], b1[:, None, :].to_broadcast([P, TPB, D]), ALU.add)

        layer_norm(nc, name + "_n1", rows, rows, I[pre + "g1"], dst_cols=cols, ident=ident, tiles=TPB, silu=True)
        with Stage(nc, name + "_out") as st:
            w2 = st.sb("w2", [P, HEADS])
            b2 = st.sb("b2", [HEADS, 1])
            y = st.ps("y", [HEADS, N])
            loaded, y_ready = (st.sem(x) for x in ("loaded", "y_ready"))
            block = st.block()

            @block.sync
            def _(sp):
                sp.dma_start(w2[:, :], I[pre + "w2"]).then_inc(loaded, 16)
                sp.dma_start(b2[:, :], dram_view(I[pre + "b2"], 0, [[1, HEADS], [1, 1]])).then_inc(loaded, 16)

            @block.tensor
            def _(pe):
                pe.wait_ge(loaded, 32)
                pe.matmul(y[:, :], w2[:, :], cols[:, :], start=True, stop=True).then_inc(y_ready, 1)

            @block.vector
            def _(dve):
                dve.memset(table[:, N:TOEP], NEG)
                dve.wait_ge(loaded, 32)
                dve.wait_ge(y_ready, 1)
                dve.tensor_scalar(table[:, 0:N], y[:, :], b2[:, 0:1], None, ALU.add)

        toeplitz_from_table(nc, name + "_spread", table, scratch, T, C)


def distance_bias(nc, name, rel, T, scratch, C):
    R = rel.shape[1]
    with ExitStack() as ctx:
        table = ctx.enter_context(nc.sbuf_tensor(f"{name}_table", [HEADS, TOEP], F32))
        with Stage(nc, name + "_in") as st:
            r = st.sb("r", [HEADS, R])
            loaded = st.sem("loaded")
            block = st.block()

            @block.sync
            def _(sp):
                sp.dma_start(r[:, :], rel).then_inc(loaded, 16)

            @block.vector
            def _(dve):
                dve.memset(table[:, N:TOEP], NEG)
                dve.wait_ge(loaded, 16)
                dve.tensor_copy(table[:, N - R + 1:N], r[:, 1:R])
                dve.tensor_copy(table[:, 0:N - R + 1], r[:, 0:1].to_broadcast([HEADS, N - R + 1]))
        toeplitz_from_table(nc, name + "_spread", table, scratch, T, C)


def cosine_attention(nc, name, I, pre, src, dst, C, scratch):
    with ExitStack() as ctx:
        def sb(n, shape, dt=F32):
            return ctx.enter_context(nc.sbuf_tensor(f"{name}_{n}", shape, dt))
        T = sb("T", [P, HEADS, N])
        xn = sb("xn", [P, NT, D])
        xn_cols = sb("xn_cols", [P, TOK])
        kT = sb("kT", [P, 2, TOK])
        k_null = sb("k_null", [P, 2])
        nulls = sb("nulls", [P, NT, HEADS])
        v_rows = sb("v_rows", [P, NT, DH])
        v_null = sb("v_null", [P, DH])
        rq = sb("rq", [P, NT, HEADS])
        O = sb("O", [P, NT, INNER])
        position_bias(nc, name + "_pos", I, pre, T, scratch, C)
        layer_norm(nc, name + "_ln", src, xn, I[pre + "g_norm"], dst_cols=xn_cols, ident=C.ident)
        shared_kv(nc, name + "_kv", xn_cols, I[pre + "Wkv"], I["cond_64"], kT, k_null, v_rows, v_null, C.ident,
                  I[pre + "k_scale"], I[pre + "q_scale"])
        query_lengths(nc, name + "_ql", xn_cols, I[pre + "Wq"], 8.0, rq)
        null_scores(nc, name + "_ns", xn_cols, I[pre + "Wq"], k_null, I[pre + "null_attn_bias"], nulls, C.ident, rq)
        attend(nc, name + "_at", xn_cols, I[pre + "Wq"], O, v_rows, C.ident, C.identb, C.onesb, C.trib, kT=kT,
               nulls=nulls, v_null=v_null, key_mask=C.mask_bf1, rq=rq, toeplitz=T)
        project_rows(nc, name + "_o", O, INNER, I[pre + "Wout"], dst, (), C.ident)
    layer_norm(nc, name + "_ln2", dst, dst, I[pre + "g_out"])


def biased_attention(nc, name, I, pre, src, dst, dst_cols, C):
    with ExitStack() as ctx:
        def sb(n, shape, dt=F32):
            return ctx.enter_context(nc.sbuf_tensor(f"{name}_{n}", shape, dt))
        xn = sb("xn", [P, NT, D])
        xn_cols = sb("xn_cols", [P, TOK])
        kT = sb("kT", [P, 2, TOK])
        k_null = sb("k_null", [P, 2])
        nulls = sb("nulls", [P, NT, HEADS])
        v_rows = sb("v_rows", [P, NT, DH])
        v_null = sb("v_null", [P, DH])
        O = sb("O", [P, NT, INNER])
        layer_norm(nc, name + "_ln", src, xn, I[pre + "g_in"], dst_cols=xn_cols, ident=C.ident)
        shared_kv(nc, name + "_kv", xn_cols, I[pre + "Wkv"], I["cond_64"], kT, k_null, v_rows, v_null, C.ident)
        null_scores(nc, name + "_ns", xn_cols, I[pre + "Wq"], k_null, I[pre + "null_attn_bias"], nulls, C.ident)
        attend(nc, name + "_at", xn_cols, I[pre + "Wq"], O, v_rows, C.ident, C.identb, C.onesb, C.trib, kT=kT,
               nulls=nulls, v_null=v_null, key_mask=C.mask_bk0,
               side=I["fside_16xSxS_0"])
        project_rows(nc, name + "_o", O, INNER, I[pre + "Wo"], dst, (), C.ident)
    layer_norm(nc, name + "_ln2", dst, dst, I[pre + "g_out"], dst_cols=dst_cols, ident=C.ident)


def distance_attention(nc, name, I, pre, src, X, C, scratch):
    with ExitStack() as ctx:
        def sb(n, shape, dt=F32):
            return ctx.enter_context(nc.sbuf_tensor(f"{name}_{n}", shape, dt))
        T = sb("T", [P, HEADS, N])
        xn = sb("xn", [P, NT, D])
        xn_cols = sb("xn_cols", [P, TOK])
        v_rows = sb("v_rows", [P, NT, D])
        O = sb("O", [P, NT, D])
        distance_bias(nc, name + "_b", I[pre + "rel"], T, scratch, C)
        layer_norm(nc, name + "_ln", src, xn, I[pre + "ln_gamma"], I[pre + "ln_beta"], dst_cols=xn_cols,
                   ident=C.ident)
        linear_rows(nc, name + "_v", xn_cols, I[pre + "Wv"], D, v_rows)
        attend(nc, name + "_at", xn_cols, I[pre + "Wq"], O, v_rows, C.ident, C.identb, C.onesb, C.trib, dh=8,
               w_k=I[pre + "Wk"], q_scale=8 ** -0.5, toeplitz=T)
        project_rows(nc, name + "_o", O, D, I[pre + "Wo"], X,
                     (lambda t: X[:, t, :], lambda t: src[:, t, :]), C.ident)


def linear_rows(nc, name, x_cols, w, width, dst):
    with Stage(nc, name) as st:
        ws = st.sb("w", [P, width])
        y = st.ps("y", [P, NT, width])
        loaded, y_ready = (st.sem(x) for x in ("loaded", "y_ready"))
        block = st.block()

        @block.sync
        def _(sp):
            sp.dma_start(ws[:, :], w).then_inc(loaded, 16)

        @block.tensor
        def _(pe):
            pe.wait_ge(loaded, 16)
            for t in range(NT):
                last = pe.matmul(y[:, t, :], x_cols[:, t * P:(t + 1) * P], ws[:, :], start=True, stop=True)
            last.then_inc(y_ready, 1)

        @block.vector
        def _(dve):
            dve.wait_ge(y_ready, 1)
            dve.tensor_copy(dst[:, :, :], y[:, :, :])


def first_maximum(link, dve, s, best, onehot, place, C):
    shape = [s.shape[0], s.shape[1], E]
    desc = C.desc[0:shape[0], None, :].to_broadcast(shape)
    link(dve.tensor_reduce(best, s, AX.X, ALU.max))
    link(dve.tensor_tensor(onehot, s, best.unsqueeze(2).to_broadcast(shape), ALU.is_equal))
    link(dve.tensor_tensor(onehot, onehot, desc, ALU.mult))
    link(dve.tensor_reduce(place, onehot, AX.X, ALU.max))
    link(dve.tensor_tensor(onehot, desc, place.unsqueeze(2).to_broadcast(shape), ALU.is_equal))


def route(nc, name, x_cols, w, C, cT, softmax=True, temper=1.0, group=None, bias=None, top=2, norm=None,
          capacity=None, similarity=None):
    with Stage(nc, name) as st:
        ws = st.sb("w", [P, E])
        wg = st.sb("wg", [DH, E])
        gcol = st.sb("gcol", [DH, B])
        gb = st.sb("gb", [DH, B, P])
        br = st.sb("br", [P, E])
        s = st.sb("s", [P, NT, E])
        r = st.sb("r", [P, NT, E])
        oh1 = st.sb("oh1", [P, NT, E])
        oh2 = st.sb("oh2", [P, NT, E])
        m1, m2, den, place = (st.sb(x, [P, NT]) for x in ("m1", "m2", "den", "place"))
        sim = st.sb("sim", [E, 1, E])
        simm = st.sb("simm", [E, 1, E])
        move = st.sb("move", [E, 1, E])
        prim = st.sb("prim", [E, 1, E])
        cond = st.sb("cond", [E, 4])
        c0 = st.sb("c0", [E, TOK])
        L = st.ps("L", [P, NT, E])
        cnt = st.ps("cnt", [P, NT, E])
        tot = st.ps("tot", [P, NT, E])
        turned = st.ps("turned", [E, TOK])
        moved = st.ps("moved", [E, TOK])
        loaded, gb_ready, logits, chain, shifted, expd, w_ready, turned_ready, c0_ready, moved_ready, counted, mask_ready = (
            st.sem(x) for x in ("loaded", "gb_ready", "logits", "chain", "shifted", "expd", "w_ready",
                                "turned_ready", "c0_ready", "moved_ready", "counted", "mask_ready"))
        n_loads = 16 * (1 + (2 if group else 0) + (bias is not None) + (similarity is not None))
        block = st.block()

        @block.sync
        def _(sp):
            sp.dma_start(ws[:, :], w).then_inc(loaded, 16)
            if group:
                sp.dma_start(wg[:, :], group[0]).then_inc(loaded, 16)
                sp.dma_start(gcol[:, :], group[1]).then_inc(loaded, 16)
            if bias is not None:
                sp.dma_start(br[:, :], row_to_all(bias, E)).then_inc(loaded, 16)
            if similarity is not None:
                sp.dma_start(sim[:, 0, :], similarity).then_inc(loaded, 16)

        @block.tensor
        def _(pe):
            pe.wait_ge(loaded, n_loads)
            if group:
                pe.wait_ge(gb_ready, 1)
            for t in range(NT):
                last = pe.matmul(L[:, t, :], x_cols[:, t * P:(t + 1) * P], ws[:, :], start=True, stop=not group)
                if group:
                    last = pe.matmul(L[:, t, :], gb[:, t // TPB, :], wg[:, :], start=False, stop=True)
            last.then_inc(logits, 1)
            if similarity is not None:
                pe.wait_ge(mask_ready, 1)
                for t in range(NT):
                    pe.matmul(cnt[0:E, 0, :], C.ones[:, 0:E], oh1[:, t, :], start=t == 0, stop=t == NT - 1)
                for t in range(NT):
                    last = pe.matmul(tot[0:E, 0, 0:1], oh1[:, t, :], C.ones[:, 0:1], start=t == 0, stop=t == NT - 1)
                last.then_inc(counted, 1)
            if capacity is not None:
                pe.wait_ge(mask_ready, 1)
                pe.matmul(cnt[:, :, :], C.upto[:, :], oh2[:, :, :], start=True, stop=True)
                pe.matmul(tot[:, :, :], C.ones[:, :], oh2[:, :, :], start=True, stop=True).then_inc(counted, 1)
            pe.wait_ge(w_ready, 1)
            for t in range(NT):
                last = pe.transpose(turned[:, t * P:(t + 1) * P], r[:, t, :], C.ident[:, :])
            last.then_inc(turned_ready, 1)
            if similarity is not None:
                pe.wait_ge(c0_ready, 1)
                for h in range(B):
                    last = pe.matmul(moved[:, h * N:(h + 1) * N], move[:, 0, :], c0[:, h * N:(h + 1) * N],
                                     start=True, stop=True)
                last.then_inc(moved_ready, 1)

        @block.scalar
        def _(act):
            if softmax:
                act.wait_ge(shifted, 1)
                act.activation(s[:, :, :], s[:, :, :], ACT.Exp, scale=temper).then_inc(expd, 1)

        @block.vector
        def _(dve):
            link = Chain(dve, chain)
            dve.wait_ge(loaded, n_loads)
            if group:
                for b in range(B):
                    last = dve.tensor_copy(gb[:, b, :], gcol[:, b:b + 1].to_broadcast([DH, P]))
                last.then_inc(gb_ready, 1)
            dve.wait_ge(logits, 1)

            def over(x):
                return x[:, :].unsqueeze(2).to_broadcast([P, NT, E])

            if bias is not None:
                link(dve.tensor_tensor(s[:, :, :], L[:, :, :], br[:, None, :].to_broadcast([P, NT, E]), ALU.add))
            else:
                link(dve.tensor_copy(s[:, :, :], L[:, :, :]))
            if softmax:
                link(dve.tensor_reduce(m1[:, :], s[:, :, :], AX.X, ALU.max))
                link(dve.tensor_tensor(s[:, :, :], s[:, :, :], over(m1), ALU.subtract))
                dve.engine_nop().then_inc(shifted, 1)
                dve.wait_ge(expd, 1)
                link(dve.tensor_reduce(den[:, :], s[:, :, :], AX.X, ALU.add))
                link(dve.reciprocal(den[:, :], den[:, :]))
                link(dve.tensor_tensor(s[:, :, :], s[:, :, :], over(den), ALU.mult))
            first_maximum(link, dve, s[:, :, :], m1[:, :], oh1[:, :, :], place[:, :], C)
            if similarity is not None:
                dve.engine_nop().then_inc(mask_ready, 1)
            if top == 1:
                link(dve.tensor_copy(r[:, :, :], oh1[:, :, :]))
            else:
                link(dve.scalar_tensor_tensor(out=r[:, :, :], in0=oh1[:, :, :], scalar=-4.0, in1=s[:, :, :],
                                              op0=ALU.mult, op1=ALU.add))
                first_maximum(link, dve, r[:, :, :], m2[:, :], oh2[:, :, :], place[:, :], C)
                link(dve.tensor_tensor(oh2[:, :, :], oh1[:, :, :], oh2[:, :, :], ALU.add))
                link(dve.tensor_tensor(r[:, :, :], s[:, :, :], oh2[:, :, :], ALU.mult))
            if norm is not None:
                link(dve.tensor_tensor(den[:, :], m1[:, :], m2[:, :], ALU.add))
                link(dve.tensor_scalar(den[:, :], den[:, :], norm[1], None, norm[0]))
                link(dve.reciprocal(den[:, :], den[:, :]))
                link(dve.tensor_tensor(r[:, :, :], r[:, :, :], over(den), ALU.mult))
            if capacity is not None:
                dve.engine_nop().then_inc(mask_ready, 1)
                dve.wait_ge(counted, 1)
                link(dve.memset(s[:, 0, :], 0.0))
                for t in range(1, NT):
                    link(dve.tensor_tensor(s[:, t, :], s[:, t - 1, :], tot[:, t - 1, :], ALU.add))
                link(dve.tensor_tensor(s[:, :, :], s[:, :, :], cnt[:, :, :], ALU.add))
                link(dve.tensor_scalar(s[:, :, :], s[:, :, :], float(capacity), None, ALU.is_le))
                link(dve.tensor_tensor(r[:, :, :], r[:, :, :], s[:, :, :], ALU.mult))
            if similarity is not None:
                dve.wait_ge(counted, 1)
                link(dve.tensor_scalar(prim[:, :, :], cnt[0:E, 0:1, :], 1.0, None, ALU.min))
                link(dve.tensor_tensor(simm[:, :, :], sim[:, :, :], prim[:, :, :], ALU.mult))
                link(dve.tensor_scalar(prim[:, :, :], prim[:, :, :], 1.0, -NEG, ALU.subtract, ALU.mult))
                link(dve.tensor_tensor(simm[:, :, :], simm[:, :, :], prim[:, :, :], ALU.add))
                first_maximum(link, dve, simm[:, :, :], cond[:, 0:1], move[:, :, :], cond[:, 1:2], C)
                link(dve.tensor_scalar(cond[:, 2:3], tot[0:E, 0, 0:1], 0.5, None, ALU.is_lt))
                link(dve.tensor_scalar(cond[:, 0:1], cond[:, 0:1], 0.7, cond[:, 2:3], ALU.is_ge, ALU.mult))
                link(dve.tensor_scalar(cond[:, 3:4], cond[:, 0:1], -1.0, 1.0, ALU.mult, ALU.add))
                link(dve.tensor_scalar(move[:, 0, :], move[:, 0, :], cond[:, 0:1], None, ALU.mult))
                link(dve.scalar_tensor_tensor(out=move[:, 0, :], in0=C.ident[0:E, 0:E], scalar=cond[:, 3:4],
                                              in1=move[:, 0, :], op0=ALU.mult, op1=ALU.add))
            dve.engine_nop().then_inc(w_ready, 1)
            dve.wait_ge(turned_ready, 1)
            if similarity is None:
                dve.tensor_copy(cT[:, :], turned[:, :])
            else:
                dve.tensor_copy(c0[:, :], turned[:, :]).then_inc(c0_ready, 1)
                dve.wait_ge(moved_ready, 1)
                dve.tensor_copy(cT[:, :], moved[:, :])


def gated_experts(nc, name, x_cols, w_gate, w_up, w_down, chunk, n_chunks, shared, leaky, cT, C, dst):
    per = P // chunk
    units = n_chunks * P
    steps = [(c, h) for c in range(n_chunks) for h in range(B)]
    if shared:
        steps = [(-1, h) for h in range(B)] + steps
    with Stage(nc, name) as st:
        wg = st.sb("wg", [P, units])
        wu = st.sb("wu", [P, units])
        wd = st.sb("wd", [P, n_chunks, D])
        sg = st.sb("sg", [P, 3, P])
        sel = st.sb("sel", [E, n_chunks, P])
        gs = st.sb("gs", [P, 2, N])
        lk = st.sb("lk", [P, 2, N])
        hid = st.sb("hid", [P, 2, N])
        psG = st.ps("psG", [P, N])
        psU = st.ps("psU", [P, 2, N])
        psB = st.ps("psB", [P, 2, N])
        psY = st.ps("psY", [P, B, N])
        (loaded, sel_made, g_out, u_out, g_in, chain, hid_ready, y_out, scaled) = (
            st.sem(x) for x in ("loaded", "sel_made", "g_out", "u_out", "g_in", "chain", "hid_ready", "y_out",
                                "scaled"))
        shared_in = st.sem("shared_in")
        block = st.block()

        @block.sync
        def _(sp):
            if shared:
                for n, w in enumerate(shared):
                    sp.dma_start(sg[:, n, :], w).then_inc(shared_in, 16)
            sp.dma_start(wg[:, :], w_gate).then_inc(loaded, 16)
            sp.dma_start(wu[:, :], w_up).then_inc(loaded, 16)
            sp.dma_start(wd[:, :, :], w_down.rearrange("(c p) n -> p c n", p=P)).then_inc(loaded, 16)

        @block.gpsimd
        def _(pool):
            pool.memset(sel[:, :, :], 0.0).then_inc(sel_made, 1)
            pool.wait_ge(sel_made, 1)
            v = sel[:, :, :].rearrange("e c (k m) -> e c k m", k=per)
            pool.affine_select(out=v, in_=v, compare_op=ALU.not_equal, fill=1.0, base=0,
                               pattern=[[-per, n_chunks], [-1, per], [0, chunk]], channel_multiplier=1)\
                .then_inc(sel_made, 1)

        @block.tensor
        def _(pe):
            def down(k):
                c, h = steps[k]
                pe.wait_ge(hid_ready, k + 1)
                w = sg[:, 2, :] if c < 0 else wd[:, c, :]
                pe.matmul(psY[:, h, :], w, hid[:, k % 2, :], start=k < 2, stop=k >= len(steps) - 2,
                          skip_group_check=True).then_inc(y_out, 1)

            pe.wait_ge(sel_made, 2)
            for k, (c, h) in enumerate(steps):
                if c < 0:
                    pe.wait_ge(shared_in, 48)
                else:
                    pe.wait_ge(loaded, 48)
                x = x_cols[:, h * N:(h + 1) * N]
                if k >= 1:
                    pe.wait_ge(g_in, k)
                g, u = (sg[:, 0, :], sg[:, 1, :]) if c < 0 else (wg[:, c * P:(c + 1) * P], wu[:, c * P:(c + 1) * P])
                pe.matmul(psG[:, :], g, x, start=True, stop=True).then_inc(g_out, 1)
                if k >= 2:
                    pe.wait_ge(hid_ready, k - 1)
                last = pe.matmul(psU[:, k % 2, :], u, x, start=True, stop=True)
                if c >= 0:
                    last = pe.matmul(psB[:, k % 2, :], sel[:, c, :], cT[:, h * N:(h + 1) * N], start=True, stop=True)
                last.then_inc(u_out, 1)
                if k >= 1:
                    down(k - 1)
            down(len(steps) - 1)

        @block.scalar
        def _(act):
            for k in range(len(steps)):
                act.wait_ge(g_out, k + 1)
                if k >= 2:
                    act.wait_ge(scaled, k - 1)
                act.activation(gs[:, k % 2, :], psG[:, :], ACT.Copy if leaky else ACT.Silu).then_inc(g_in, 1)
            act.wait_ge(y_out, len(steps))
            act.activation(dst[:, N:2 * N], psY[:, 1, :], ACT.Copy)

        @block.vector
        def _(dve):
            link = Chain(dve, chain)
            for k, (c, h) in enumerate(steps):
                dve.wait_ge(g_in, k + 1)
                a = gs[:, k % 2, :]
                if leaky:
                    link(dve.scalar_tensor_tensor(out=lk[:, k % 2, :], in0=a, scalar=0.01, in1=a,
                                                  op0=ALU.mult, op1=ALU.max))
                    a = lk[:, k % 2, :]
                dve.wait_ge(u_out, k + 1)
                if k >= 2:
                    dve.wait_ge(y_out, k - 1)
                mul = dve.tensor_tensor(hid[:, k % 2, :], a, psU[:, k % 2, :], ALU.mult)
                mul.then_inc(scaled, 1)
                dve.wait_ge(scaled, k + 1)
                if c >= 0:
                    dve.tensor_tensor(hid[:, k % 2, :], hid[:, k % 2, :], psB[:, k % 2, :], ALU.mult)\
                        .then_inc(hid_ready, 1)
                else:
                    dve.engine_nop().then_inc(hid_ready, 1)
            dve.wait_ge(y_out, len(steps))
            dve.tensor_copy(dst[:, 0:N], psY[:, 0, :])


def grouped_experts(nc, name, I, pre, x_cols, dst, C):
    with ExitStack() as ctx:
        cT = ctx.enter_context(nc.sbuf_tensor(f"{name}_cT", [E, TOK], F32))
        route(nc, name + "_r", x_cols, I[pre + "wt"], C, cT, temper=0.5, group=(I[pre + "wg"], I["cond_64_T"]),
              norm=(ALU.add, 1e-20))
        gated_experts(nc, name + "_x", x_cols, I[pre + "w_gate"], I[pre + "w_up"],
                      I[pre + "w_down"], DH, E * DH // P,
                      tuple(I[pre + w] for w in ("sw_gate", "sw_up", "sw_down")), True, cT, C, dst)


def rerouted_experts(nc, name, I, pre, x_cols, dst, C):
    with ExitStack() as ctx:
        cT = ctx.enter_context(nc.sbuf_tensor(f"{name}_cT", [E, TOK], F32))
        route(nc, name + "_r", x_cols, I[pre + "gate_weight"], C, cT, norm=(ALU.max, 1e-12),
              similarity=I[pre + "similarity_matrix"])
        gated_experts(nc, name + "_x", x_cols, I[pre + "gate"], I[pre + "up"], I[pre + "down"], P, E, None,
                      False, cT, C, dst)


def linear_attention(nc, name, I, pre, x_cols, X, C):
    F, HD = 32, 8
    CH = HEADS * F // P
    with ExitStack() as ctx:
        def sb(n, shape, dt=F32):
            return ctx.enter_context(nc.sbuf_tensor(f"{name}_{n}", shape, dt))
        qT = sb("qT", [P, TOK])
        kT = sb("kT", [P, TOK])
        v1 = sb("v1", [P, NT, D + 1])
        bd = sb("bd", [P, CH, P])
        own = sb("own", [P, F])
        w = sb("w", [P, 3 * D])
        qf = sb("qf", [P, CH, TOK])
        kf = sb("kf", [P, NT, CH * P])
        kv = sb("kv", [P, B, CH, 2, F])
        outT = sb("outT", [P, TOK])
        with Stage(nc, name + "_qkv") as st:
            ps = st.ps("ps", [P, 4, N])
            pv = st.ps("pv", [P, NT, P])
            loaded, made, ready, v_ready, bd_in, cleared = (
                st.sem(x) for x in ("loaded", "made", "ready", "v_ready", "bd_in", "cleared"))
            block = st.block()

            @block.sync
            def _(sp):
                sp.dma_start(w[:, :], I[pre + "w_qkv"]).then_inc(loaded, 16)
                sp.wait_ge(cleared, 1)
                for h in range(HEADS):
                    sp.dma_start(bd[h * HD:(h + 1) * HD, h // 4, h % 4 * F:(h % 4 + 1) * F],
                                 I[pre + "proj_matrix"][h, :, :]).then_inc(bd_in, 16)
                sp.wait_ge(bd_in, 16 * HEADS)

            @block.gpsimd
            def _(pool):
                pool.memset(own[:, :], 1.0).then_inc(made, 1)
                pool.wait_ge(made, 1)
                o = own[:, :].rearrange("p (h d) -> p h d", h=4)
                pool.affine_select(out=o, in_=o, compare_op=ALU.is_ge, fill=0.0, base=0,
                                   pattern=[[-F, 4], [0, HD]], channel_multiplier=1).then_inc(made, 1)
                pool.wait_ge(made, 2)
                pool.affine_select(out=o, in_=o, compare_op=ALU.is_ge, fill=0.0, base=F - 1,
                                   pattern=[[F, 4], [0, HD]], channel_multiplier=-1)

            @block.tensor
            def _(pe):
                pe.wait_ge(loaded, 16)
                for n in range(2):
                    for b in range(B):
                        pe.matmul(ps[:, 2 * n + b, :], w[:, n * D:(n + 1) * D], x_cols[:, b * N:(b + 1) * N],
                                  start=True, stop=True).then_inc(ready, 1)
                for t in range(NT):
                    last = pe.matmul(pv[:, t, :], x_cols[:, t * P:(t + 1) * P], w[:, 2 * D:3 * D],
                                     start=True, stop=True)
                last.then_inc(v_ready, 1)

            @block.scalar
            def _(act):
                for n, dst in enumerate((qT, kT)):
                    for b in range(B):
                        act.wait_ge(ready, 2 * n + b + 1)
                        act.activation(dst[:, b * N:(b + 1) * N], ps[:, 2 * n + b, :], ACT.Copy)

            @block.vector
            def _(dve):
                dve.memset(bd[:, :, :], 0.0).then_inc(cleared, 1)
                dve.memset(v1[:, :, D:D + 1], 1.0)
                dve.wait_ge(v_ready, 1)
                dve.tensor_copy(v1[:, :, 0:D], pv[:, :, :])

        with Stage(nc, name + "_feat") as st:
            low = st.sb("low", [P, 3, N])
            ps = st.ps("ps", [P, 3, N])
            raw, lowered, expd, done = (st.sem(x) for x in ("raw", "lowered", "expd", "done"))
            block = st.block()
            jobs = [(bd[:, c, :], qT[:, b * N:(b + 1) * N], qf[:, c, b * N:(b + 1) * N])
                    for b in range(B) for c in range(CH)]
            jobs += [(kT[:, t * P:(t + 1) * P], bd[:, :, :], kf[:, t, :]) for t in range(NT)]

            @block.tensor
            def _(pe):
                for k, (lhs, rhs, _) in enumerate(jobs):
                    if k >= 3:
                        pe.wait_ge(done, k - 2)
                    pe.matmul(ps[:, k % 3, :], lhs, rhs, start=True, stop=True).then_inc(raw, 1)

            @block.scalar
            def _(act):
                for k in range(len(jobs)):
                    act.wait_ge(lowered, k + 1)
                    act.activation(low[:, k % 3, :], low[:, k % 3, :], ACT.Exp).then_inc(expd, 1)

            @block.vector
            def _(dve):
                def finish(k):
                    dve.wait_ge(expd, k + 1)
                    dve.scalar_tensor_tensor(out=jobs[k][2], in0=ps[:, k % 3, :], scalar=0.0, in1=low[:, k % 3, :],
                                             op0=ALU.max, op1=ALU.add).then_inc(done, 1)

                for k in range(len(jobs)):
                    dve.wait_ge(raw, k + 1)
                    if k >= 3:
                        dve.wait_ge(done, k - 2)
                    dve.tensor_scalar(low[:, k % 3, :], ps[:, k % 3, :], 0.0, None, ALU.min).then_inc(lowered, 1)
                    if k >= 1:
                        finish(k - 1)
                finish(len(jobs) - 1)

        with Stage(nc, name + "_kv") as st:
            psK = st.ps("psK", [P, CH, N])
            psN = st.ps("psN", [P, 2, N])
            den = st.sb("den", [P, N])
            kv_out, kv_in, nd_out, nd_in, chain = (
                st.sem(x) for x in ("kv_out", "kv_in", "nd_out", "nd_in", "chain"))
            block = st.block()

            @block.tensor
            def _(pe):
                for b in range(B):
                    if b:
                        pe.wait_ge(kv_in, 1)
                    for c in range(CH):
                        for t in range(TPB):
                            last = pe.matmul(psK[:, c, 0:D + 1], kf[:, b * TPB + t, c * P:(c + 1) * P],
                                             v1[:, b * TPB + t, :], start=t == 0, stop=t == TPB - 1)
                    last.then_inc(kv_out, 1)
                for b in range(B):
                    pe.wait_ge(kv_in, b + 1)
                    if b:
                        pe.wait_ge(nd_in, b)
                    for n in range(2):
                        for c in range(CH):
                            last = pe.matmul(psN[c * F:(c + 1) * F, n, :], kv[:, b, c, n, :],
                                             qf[:, c, b * N:(b + 1) * N], start=True, stop=True,
                                             tile_position=(0, c * F))
                    last.then_inc(nd_out, 1)

            @block.vector
            def _(dve):
                link = Chain(dve, chain)
                for b in range(B):
                    dve.wait_ge(kv_out, b + 1)
                    for c in range(CH):
                        dve.tensor_tensor(kv[:, b, c, 0, :], psK[:, c, c * F:(c + 1) * F], own[:, :], ALU.mult)
                        last = dve.tensor_scalar(kv[:, b, c, 1, :], own[:, :], psK[:, c, D:D + 1], None, ALU.mult)
                    last.then_inc(kv_in, 1)
                for b in range(B):
                    dve.wait_ge(nd_out, b + 1)
                    link(dve.tensor_scalar(den[:, :], psN[:, 1, :], 1e-8, None, ALU.add))
                    link(dve.reciprocal(den[:, :], den[:, :]))
                    dve.tensor_tensor(outT[:, b * N:(b + 1) * N], psN[:, 0, :], den[:, :], ALU.mult).then_inc(nd_in, 1)
                    dve.wait_ge(nd_in, b + 1)

        columns_out(nc, name + "_o", outT, I[pre + "w_out"], X, I[pre + "b_out"])


def columns_out(nc, name, x_cols, w, X, bias, K=1):
    with Stage(nc, name) as st:
        ws = st.sb("w", [P, K, D])
        bs = st.sb("b", [P, D])
        y = st.ps("y", [P, NT, D])
        loaded, y_ready, chain = (st.sem(x) for x in ("loaded", "y_ready", "chain"))
        block = st.block()

        @block.sync
        def _(sp):
            sp.dma_start(ws[:, :, :], w.rearrange("(c p) n -> p c n", p=P)).then_inc(loaded, 16)
            sp.dma_start(bs[:, :], row_to_all(bias, D)).then_inc(loaded, 16)

        @block.tensor
        def _(pe):
            pe.wait_ge(loaded, 32)
            for t in range(NT):
                for k in range(K):
                    x = x_cols[:, t * P:(t + 1) * P] if K == 1 else x_cols[:, k, t * P:(t + 1) * P]
                    last = pe.matmul(y[:, t, :], x, ws[:, k, :], start=k == 0, stop=k == K - 1)
                if t % TPB == TPB - 1:
                    last.then_inc(y_ready, 1)

        @block.vector
        def _(dve):
            link = Chain(dve, chain)
            dve.wait_ge(loaded, 32)
            link(dve.tensor_tensor(X[:, :, :], X[:, :, :], bs[:, None, :].to_broadcast([P, NT, D]), ALU.add))
            for h in range(B):
                dve.wait_ge(y_ready, h + 1)
                part = X[:, h * TPB:(h + 1) * TPB, :]
                dve.tensor_tensor(part, part, y[:, h * TPB:(h + 1) * TPB, :], ALU.add)


def phase_ffn(nc, name, I, pre, x_cols, X, C):
    FCH = 4
    MAGIC = 12582912.0
    TURN = 6.283185307179586
    HI = 6.28125
    LO = TURN - HI
    PI = 3.1415925
    with ExitStack() as ctx:
        hidT = ctx.enter_context(nc.sbuf_tensor(f"{name}_hidT", [P, FCH, TOK], F32))
        with Stage(nc, name + "_h") as st:
            w1 = st.sb("w1", [P, FCH * P])
            vec = st.sb("vec", [P, 4, FCH])
            ang = st.sb("ang", [P, 2, FCH])
            kk = st.sb("kk", [P, 2, FCH])
            sc = st.sb("sc", [P, 2, FCH])
            amp = st.sb("amp", [P, FCH])
            h = st.sb("h", [P, 2, TOK])
            a = st.sb("a", [P, 2, TOK])
            k_ = st.sb("k", [P, 2, TOK])
            ps = st.ps("ps", [P, 2, TOK])
            loaded, chain, h_out, h_in, reduced, sined, ang_ready, sc_ready, done = (
                st.sem(x) for x in ("loaded", "chain", "h_out", "h_in", "reduced", "sined", "ang_ready",
                                    "sc_ready", "done"))
            relued = st.sem("relued")
            block = st.block()

            @block.sync
            def _(sp):
                sp.dma_start(w1[:, :], I[pre + "W1"]).then_inc(loaded, 16)
                for n, v in enumerate(("b1", "quantum_phases", "quantum_weights_real", "quantum_weights_imag")):
                    sp.dma_start(vec[:, n, :], I[pre + v]).then_inc(loaded, 16)

            @block.tensor
            def _(pe):
                pe.wait_ge(loaded, 80)
                for c in range(FCH):
                    if c >= 2:
                        pe.wait_ge(h_in, c - 1)
                    for b in range(B):
                        last = pe.matmul(ps[:, c % 2, b * N:(b + 1) * N], w1[:, c * P:(c + 1) * P],
                                         x_cols[:, b * N:(b + 1) * N], start=True, stop=True)
                    last.then_inc(h_out, 1)

            def reduce_angle(link, dve, x, k):
                link(dve.tensor_scalar(k, x, 1.0 / TURN, MAGIC, ALU.mult, ALU.add))
                link(dve.tensor_scalar(k, k, -MAGIC, None, ALU.add))
                link(dve.scalar_tensor_tensor(out=x, in0=k, scalar=-HI, in1=x, op0=ALU.mult, op1=ALU.add))
                link(dve.scalar_tensor_tensor(out=x, in0=k, scalar=-LO, in1=x, op0=ALU.mult, op1=ALU.add))
                link(dve.tensor_scalar(x, x, PI, -PI, ALU.min, ALU.max))

            @block.vector
            def _(dve):
                link = Chain(dve, chain)
                dve.wait_ge(loaded, 80)
                link(dve.tensor_copy(ang[:, 0, :], vec[:, 1, :]))
                link(dve.tensor_scalar(ang[:, 1, :], vec[:, 1, :], TURN / 4, None, ALU.add))
                reduce_angle(link, dve, ang[:, :, :], kk[:, :, :])
                dve.engine_nop().then_inc(ang_ready, 1)
                dve.wait_ge(sc_ready, 1)
                link(dve.tensor_tensor(sc[:, 1, :], sc[:, 1, :], vec[:, 2, :], ALU.mult))
                link(dve.tensor_tensor(sc[:, 0, :], sc[:, 0, :], vec[:, 3, :], ALU.mult))
                link(dve.tensor_tensor(amp[:, :], sc[:, 0, :], sc[:, 1, :], ALU.add))
                link(dve.tensor_tensor(amp[:, :], amp[:, :], vec[:, 3, :], ALU.mult))
                link(dve.tensor_scalar(amp[:, :], amp[:, :], 0.1, None, ALU.mult))

                def finish(c):
                    dve.wait_ge(sined, c + 1)
                    dve.scalar_tensor_tensor(out=h[:, c % 2, :], in0=a[:, c % 2, :], scalar=amp[:, c:c + 1],
                                             in1=h[:, c % 2, :], op0=ALU.mult, op1=ALU.add).then_inc(done, 1)

                for c in range(FCH):
                    dve.wait_ge(h_out, c + 1)
                    if c >= 2:
                        dve.wait_ge(relued, c - 1)
                    dve.tensor_scalar(h[:, c % 2, :], ps[:, c % 2, :], vec[:, 0, c:c + 1], None, ALU.add)\
                        .then_inc(h_in, 1)
                    dve.wait_ge(h_in, c + 1)
                    link(dve.tensor_scalar(a[:, c % 2, :], h[:, c % 2, :], 0.1, vec[:, 1, c:c + 1],
                                           ALU.mult, ALU.add))
                    reduce_angle(link, dve, a[:, c % 2, :], k_[:, c % 2, :])
                    dve.engine_nop().then_inc(reduced, 1)
                    if c >= 1:
                        finish(c - 1)
                finish(FCH - 1)

            @block.scalar
            def _(act):
                act.wait_ge(ang_ready, 1)
                act.activation(sc[:, :, :], ang[:, :, :], ACT.Sin).then_inc(sc_ready, 1)

                def relu(c):
                    act.wait_ge(done, c + 1)
                    act.activation(hidT[:, c, :], h[:, c % 2, :], ACT.Relu).then_inc(relued, 1)

                for c in range(FCH):
                    act.wait_ge(reduced, c + 1)
                    act.activation(a[:, c % 2, :], a[:, c % 2, :], ACT.Sin).then_inc(sined, 1)
                    if c >= 1:
                        relu(c - 1)
                relu(FCH - 1)

        columns_out(nc, name + "_o", hidT, I[pre + "W2"], X, I[pre + "b2"], K=FCH)


def expert_mlps(nc, name, x_cols, w1, b1, w2, b2, func, cT, c_scratch, dst):
    FCH = w1.shape[2] // P
    HALF = FCH * B
    STEPS = 2 * HALF
    with Stage(nc, name) as st:
        w1s = st.sb("w1", [P, 2, FCH * P])
        w2s = st.sb("w2", [P, 2, FCH, D])
        cb = st.sb("cb", [P, 2, TOK])
        b1s = st.sb("b1", [P, 2, FCH])
        b2s = st.sb("b2", [E, D])
        a = st.sb("a", [P, 4, N])
        hid = st.sb("hid", [P, 4, N])
        psH = st.ps("psH", [P, 4, N])
        psY = st.ps("psY", [P, B, N])
        loaded, stored, h_out, a_out, hid_ready, y_out = (
            st.sem(x) for x in ("loaded", "stored", "h_out", "a_out", "hid_ready", "y_out"))
        w_in = [st.sem(f"w_in{s}") for s in range(2)]
        block = st.block()

        def step(j):
            return j // HALF, j % HALF // B, j % B

        @block.sync
        def _(sp):
            sp.dma_start(c_scratch, cT[:, :]).then_inc(stored, 16)
            sp.dma_start(b2s[:, :], b2).then_inc(loaded, 16)
            sp.wait_ge(stored, 16)

            def load(it, s):
                e = it * 2 + s
                sp.dma_start(w1s[:, s, :], w1[bass.ds(e, 1), :, :].rearrange("a p n -> p (a n)"))\
                    .then_inc(w_in[s], 16)
                sp.dma_start(w2s[:, s, :, :], w2[bass.ds(e, 1), :, :].rearrange("a (c p) n -> p (a c) n", p=P))\
                    .then_inc(w_in[s], 16)
                sp.dma_start(b1s[:, s, :], b1[bass.ds(e, 1), :, :].rearrange("a p c -> p (a c)"))\
                    .then_inc(w_in[s], 16)
                sp.dma_start(cb[:, s, :], row_to_all(c_scratch[bass.ds(e, 1), :], TOK)).then_inc(w_in[s], 16)

            load(0, 0)
            load(0, 1)
            with sp.Fori(1, E // 2) as it:
                for s in range(2):
                    sp.wait_ge(y_out, it * STEPS - STEPS + HALF * (s + 1))
                    load(it, s)

        @block.tensor
        def _(pe):
            def down(it, j):
                s, f, h = step(j)
                pe.wait_ge(hid_ready, it * STEPS + j + 1)
                pe.matmul(psY[:, h, :], w2s[:, s, f, :], hid[:, j % 4, :], start=False, stop=False,
                          skip_group_check=True).then_inc(y_out, 1)

            def body(it, first):
                for j in range(STEPS):
                    s, f, h = step(j)
                    if j % HALF == 0:
                        pe.wait_ge(w_in[s], it * 64 + 64)
                    if not first or j >= 4:
                        pe.wait_ge(a_out, it * STEPS + j - 3)
                    pe.matmul(psH[:, j % 4, :], w1s[:, s, f * P:(f + 1) * P], x_cols[:, h * N:(h + 1) * N],
                              start=True, stop=True).then_inc(h_out, 1)
                    if j >= 2:
                        down(it, j - 2)
                down(it, STEPS - 2)
                down(it, STEPS - 1)

            pe.wait_ge(loaded, 16)
            for h in range(B):
                pe.matmul(psY[:, h, :], b2s[:, :], cT[:, h * N:(h + 1) * N], start=True, stop=False,
                          skip_group_check=True)
            body(0, True)
            with pe.Fori(1, E // 2) as it:
                body(it, False)

        @block.scalar
        def _(act):
            def body(it, first):
                for j in range(STEPS):
                    s, f, h = step(j)
                    if j % HALF == 0:
                        act.wait_ge(w_in[s], it * 64 + 64)
                    act.wait_ge(h_out, it * STEPS + j + 1)
                    if not first or j >= 4:
                        act.wait_ge(hid_ready, it * STEPS + j - 3)
                    act.activation(a[:, j % 4, :], psH[:, j % 4, :], func,
                                   bias=b1s[:, s, f:f + 1]).then_inc(a_out, 1)

            body(0, True)
            with act.Fori(1, E // 2) as it:
                body(it, False)
            act.wait_ge(y_out, E // 2 * STEPS)
            act.activation(dst[:, N:2 * N], psY[:, 1, :], ACT.Copy)

        @block.vector
        def _(dve):
            def body(it, first):
                for j in range(STEPS):
                    s, f, h = step(j)
                    if j % HALF == 0:
                        dve.wait_ge(w_in[s], it * 64 + 64)
                    dve.wait_ge(a_out, it * STEPS + j + 1)
                    if not first or j >= 4:
                        dve.wait_ge(y_out, it * STEPS + j - 3)
                    dve.tensor_tensor(hid[:, j % 4, :], a[:, j % 4, :], cb[:, s, h * N:(h + 1) * N], ALU.mult)\
                        .then_inc(hid_ready, 1)

            body(0, True)
            with dve.Fori(1, E // 2) as it:
                body(it, False)
            dve.wait_ge(y_out, E // 2 * STEPS)
            dve.tensor_copy(dst[:, 0:N], psY[:, 0, :])


def windowed_attention(nc, name, I, pre, x_cols, X, C):
    QT, WIN, HD, KV = 96, 32, 8, 2
    KW = QT + WIN - 1
    HALF = WIN // 2
    NU = -(-N // QT)
    PAD = NU * QT + WIN
    with ExitStack() as ctx:
        def sb(n, shape, dt=F32):
            return ctx.enter_context(nc.sbuf_tensor(f"{name}_{n}", shape, dt))
        xp = sb("xp", [P, B, PAD])
        qT = sb("qT", [P, 4, TOK])
        kT = sb("kT", [P, KV, 4, B, PAD])
        vw = sb("vw", [P, B * NU, KV, HD + 1])
        OT = sb("OT", [P, TOK])
        with Stage(nc, name + "_qkv") as st:
            wq = st.sb("wq", [P, 4, 4, 32])
            wk = st.sb("wk", [P, KV, 4, 32])
            wv = st.sb("wv", [P, KV * HD])
            bq = st.sb("bq", [P, 4])
            bk = st.sb("bk", [P, KV])
            bv = st.sb("bv", [1, KV * HD])
            valid = st.sb("valid", [1, PAD])
            ps = st.ps("ps", [P, 4, N])
            pk = st.ps("pk", [P, 2, N])
            pv = st.ps("pv", [P, B * NU, KV * HD])
            cleared, loaded, xp_ready, raw, evac, k_raw, k_evac, k_clear, v_out = (
                st.sem(x) for x in ("cleared", "loaded", "xp_ready", "raw", "evac", "k_raw", "k_evac", "k_clear",
                                    "v_out"))
            block = st.block()
            n_loads = 16 * (4 + KV * 4 + 1 + 8 + 1)
            jobs = [(wq[:, c, :, :], x_cols[:, b * N:(b + 1) * N], qT[:, c, b * N:(b + 1) * N], bq[:, c:c + 1])
                    for c in range(4) for b in range(B)]
            key_jobs = [(g, b) for g in range(KV) for b in range(B)]

            @block.sync
            def _(sp):
                sp.wait_ge(cleared, 4)
                for c in range(4):
                    sp.dma_start(wq[:, c, :, 0:HD], I[pre + "Wq"][:, c * 32:(c + 1) * 32]
                                 .rearrange("p (r d) -> p r d", d=HD)).then_inc(loaded, 16)
                for g in range(KV):
                    for r in range(4):
                        sp.dma_start(wk[:, g, r, 0:HD], I[pre + "Wk"][:, g * HD:(g + 1) * HD]).then_inc(loaded, 16)
                sp.dma_start(wv[:, :], I[pre + "Wv"]).then_inc(loaded, 16)
                for r in range(4):
                    sp.dma_start(bq[r * 32:r * 32 + HD, :], I[pre + "bq"][r, :, :]).then_inc(loaded, 16)
                    sp.dma_start(bk[r * 32:r * 32 + HD, :], I[pre + "bk"]).then_inc(loaded, 16)
                sp.dma_start(bv[:, :], dram_view(I[pre + "bv"], 0, [[KV * HD, 1], [1, KV * HD]])).then_inc(loaded, 16)

            @block.tensor
            def _(pe):
                pe.wait_ge(loaded, n_loads)
                for k, (g, b) in enumerate(key_jobs):
                    if k >= 2:
                        pe.wait_ge(k_evac, k - 1)
                    pe.matmul(pk[:, k % 2, :], wk[:, g, :, :], x_cols[:, b * N:(b + 1) * N], start=True, stop=True)\
                        .then_inc(k_raw, 1)
                for k, (lhs, rhs, _, _) in enumerate(jobs):
                    if k >= 4:
                        pe.wait_ge(evac, k - 3)
                    pe.matmul(ps[:, k % 4, :], lhs, rhs, start=True, stop=True).then_inc(raw, 1)
                pe.wait_ge(xp_ready, 3)
                for b in range(B):
                    for u in range(NU):
                        out = pv[0:KW, b * NU + u, :]
                        pe.matmul(out, xp[:, b, u * QT:u * QT + KW], wv[:, :], start=True, stop=False)
                        last = pe.matmul(out, valid[:, u * QT:u * QT + KW], bv[:, :], start=False, stop=True)
                last.then_inc(v_out, 1)

            @block.scalar
            def _(act):
                act.wait_ge(loaded, n_loads)
                act.wait_ge(k_clear, 2)
                for k, (g, b) in enumerate(key_jobs):
                    act.wait_ge(k_raw, k + 1)
                    for h in range(4):
                        rows = slice(32 * h, 32 * h + 32)
                        last = act.activation(kT[rows, g, h, b, HALF:HALF + N], pk[rows, k % 2, :], ACT.Identity,
                                              bias=bk[rows, g:g + 1])
                    last.then_inc(k_evac, 1)

            @block.gpsimd
            def _(pool):
                pool.memset(kT[:, 1, :, :, :], 0.0).then_inc(k_clear, 1)
                pool.memset(xp[:, :, 0:HALF], 0.0)
                pool.memset(xp[:, :, HALF + N:PAD], 0.0)
                pool.tensor_copy(xp[:, :, HALF:HALF + N], x_cols[:, :].rearrange("p (b n) -> p b n", b=B))\
                    .then_inc(xp_ready, 1)
                pool.memset(valid[:, 0:HALF], 0.0)
                pool.memset(valid[:, HALF + N:PAD], 0.0).then_inc(xp_ready, 1)
                pool.memset(valid[:, HALF:HALF + N], 1.0).then_inc(xp_ready, 1)

            @block.vector
            def _(dve):
                dve.memset(wq[:, :, :, :], 0.0).then_inc(cleared, 1)
                dve.memset(wk[:, :, :, :], 0.0).then_inc(cleared, 1)
                dve.memset(bq[:, :], 0.0).then_inc(cleared, 1)
                dve.memset(bk[:, :], 0.0).then_inc(cleared, 1)
                dve.memset(kT[:, 0, :, :, :], 0.0).then_inc(k_clear, 1)
                dve.memset(vw[:, :, :, HD:HD + 1], 1.0)
                dve.wait_ge(loaded, n_loads)
                for k, (_, _, dst, bias) in enumerate(jobs):
                    dve.wait_ge(raw, k + 1)
                    dve.tensor_scalar(dst, ps[:, k % 4, :], bias, None, ALU.add).then_inc(evac, 1)
                dve.wait_ge(v_out, 1)
                dve.tensor_copy(vw[0:KW, :, :, 0:HD], pv[0:KW, :, :].rearrange("p u (g d) -> p u g d", g=KV))

        units = [(b, u, min(QT, N - u * QT)) for b in range(B) for u in range(NU)]
        with Stage(nc, name + "_at") as st:
            band = st.sb("band", [P, 4, KW], BF16)
            S = st.sb("S", [P, HEADS, KW])
            Pm = st.sb("Pm", [P, HEADS, KW])
            PT = st.sb("PT", [P, HEADS, QT])
            nmax = st.sb("nmax", [P, HEADS])
            rinv = st.sb("rinv", [P, HEADS])
            O = st.sb("O", [P, HEADS, HD])
            psS = st.ps("psS", [P, 4, N])
            psT = st.ps("psT", [P, 2, N])
            psO = st.ps("psO", [P, N])
            psX = st.ps("psX", [P, N])
            made, s_out, maxed, s_in, expd, t_out, t_in, o_out, inv, o_in, ot_out, ot_in = (
                st.sem(x) for x in ("made", "s_out", "maxed", "s_in", "expd", "t_out", "t_in", "o_out", "inv",
                                    "o_in", "ot_out", "ot_in"))
            block = st.block()

            @block.gpsimd
            def _(pool):
                pool.memset(band[:, :, :], 0.0).then_inc(made, 1)
                pool.wait_ge(made, 1)
                pool.affine_select(out=band[:, :, :], in_=band[:, :, :], compare_op=ALU.is_ge, fill=NEG, base=0,
                                   pattern=[[0, 4], [1, KW]], channel_multiplier=-1).then_inc(made, 1)
                pool.wait_ge(made, 2)
                pool.affine_select(out=band[:, :, :], in_=band[:, :, :], compare_op=ALU.is_ge, fill=NEG,
                                   base=WIN - 1, pattern=[[0, 4], [-1, KW]], channel_multiplier=1).then_inc(made, 1)

            @block.tensor
            def _(pe):
                def scores(k):
                    b, u, m = units[k]
                    if k:
                        pe.wait_ge(s_in, k)
                    for c in range(4):
                        pe.matmul(psS[0:m, c, 0:4 * KW], C.identb[:, 0:m], band[:, :, :], start=True, stop=False,
                                  skip_group_check=True)
                        last = pe.matmul(psS[0:m, c, 0:4 * KW], qT[:, c, b * N + u * QT:b * N + u * QT + m],
                                         kT[:, c // 2, :, b, u * QT:u * QT + KW], start=False, stop=True,
                                         skip_group_check=True)
                    last.then_inc(s_out, 1)

                def turn_group(k, j):
                    b, u, m = units[k]
                    n = 4 * k + j
                    if n >= 2:
                        pe.wait_ge(t_in, n - 1)
                    for y in range(4):
                        last = pe.transpose(psT[0:KW, j % 2, y * QT:y * QT + m], Pm[0:m, 4 * j + y, :],
                                            C.ident[0:m, 0:m])
                    last.then_inc(t_out, 1)

                def values_group(k, j):
                    b, u, m = units[k]
                    pe.wait_ge(t_in, 4 * k + j + 1)
                    if k and j == 0:
                        pe.wait_ge(o_in, k)
                    for h in range(4 * j, 4 * j + 4):
                        last = pe.matmul(psO[0:m, h * (HD + 1):(h + 1) * (HD + 1)], PT[0:KW, h, 0:m],
                                         vw[0:KW, k, j // 2, :], start=True, stop=True)
                    if j == 3:
                        last.then_inc(o_out, 1)

                def values(k):
                    pe.wait_ge(expd, k + 1)
                    for j in range(5):
                        if j < 4:
                            turn_group(k, j)
                        if j >= 1:
                            values_group(k, j - 1)

                def turn(k):
                    b, u, m = units[k]
                    pe.wait_ge(o_in, k + 1)
                    if k:
                        pe.wait_ge(ot_in, k)
                    pe.transpose(psX[:, 0:m], O[0:m, :, :], C.ident[0:m, 0:m]).then_inc(ot_out, 1)

                pe.wait_ge(made, 3)
                for k in range(len(units) + 2):
                    if k < len(units):
                        scores(k)
                    if k >= 2:
                        turn(k - 2)
                    if 1 <= k <= len(units):
                        values(k - 1)

            @block.scalar
            def _(act):
                for k in range(len(units) + 2):
                    if k >= 2:
                        b, u, m = units[k - 2]
                        act.wait_ge(ot_out, k - 1)
                        act.activation(OT[:, b * N + u * QT:b * N + u * QT + m], psX[:, 0:m], ACT.Copy)\
                            .then_inc(ot_in, 1)
                    if 1 <= k <= len(units):
                        b, u, m = units[k - 1]
                        for j in range(4):
                            act.wait_ge(t_out, 4 * (k - 1) + j + 1)
                            if k >= 2 and j == 0:
                                act.wait_ge(o_out, k - 1)
                            act.activation(PT[0:KW, 4 * j:4 * j + 4, 0:m],
                                           psT[0:KW, j % 2, 0:4 * QT].rearrange("p (y q) -> p y q", y=4)[:, :, 0:m],
                                           ACT.Copy).then_inc(t_in, 1)
                    if k < len(units):
                        b, u, m = units[k]
                        act.wait_ge(s_in, k + 1)
                        act.activation(Pm[0:m, :, :], S[0:m, :, :], ACT.Exp).then_inc(expd, 1)

            @block.vector
            def _(dve):
                def finish(k):
                    b, u, m = units[k]
                    dve.wait_ge(o_out, k + 1)
                    o = psO[0:m, 0:HEADS * (HD + 1)].rearrange("p (h d) -> p h d", h=HEADS)
                    dve.reciprocal(rinv[0:m, :], o[:, :, HD]).then_inc(inv, 1)
                    dve.wait_ge(inv, k + 1)
                    if k:
                        dve.wait_ge(ot_out, k)
                    dve.tensor_tensor(O[0:m, :, :], o[:, :, 0:HD],
                                      rinv[0:m, :].unsqueeze(2).to_broadcast([m, HEADS, HD]), ALU.mult)\
                        .then_inc(o_in, 1)

                for k, (b, u, m) in enumerate(units):
                    dve.wait_ge(s_out, k + 1)
                    s = psS[0:m, :, 0:4 * KW].rearrange("p c (r j) -> p c r j", r=4)
                    n4 = nmax[0:m, :].rearrange("p (c r) -> p c r", c=4)
                    dve.tensor_reduce(n4, s, AX.X, ALU.max).then_inc(maxed, 1)
                    dve.wait_ge(maxed, k + 1)
                    if k:
                        dve.wait_ge(expd, k)
                    dve.tensor_tensor(S[0:m, :, :].rearrange("p (c r) j -> p c r j", c=4), s,
                                      n4.unsqueeze(3).to_broadcast([m, 4, 4, KW]), ALU.subtract).then_inc(s_in, 1)
                    if k:
                        finish(k - 1)
                finish(len(units) - 1)

        columns_out(nc, name + "_o", OT, I[pre + "Wo"], X, I[pre + "bo"])


def layered_attention(nc, name, I, pre, Y, C):
    L, HD, LH, BK = 4, 16, 4, 64
    LW = LH * HD
    NB = N // BK
    FCH = 4
    with ExitStack() as ctx:
        def sb(n, shape, dt=F32):
            return ctx.enter_context(nc.sbuf_tensor(f"{name}_{n}", shape, dt))
        xn = sb("xn", [P, NT, D])
        xc = sb("xc", [P, TOK])
        qlT = sb("qlT", [P, TOK])
        klT = sb("klT", [P, LH, TOK])
        v1 = sb("v1", [P, NT, D + 1])
        kg = sb("kg", [P, NT, LW])
        qgT = sb("qgT", [LW, TOK])
        ctxs = sb("ctxs", [LW, B * NB, LW])
        own = sb("own", [LW, LW])
        O = sb("O", [P, NT, D])
        OT = sb("OT", [P, TOK])
        hid = sb("hid", [P, FCH, TOK])
        with Stage(nc, name + "_own") as st:
            made = st.sem("made")
            block = st.block()

            @block.gpsimd
            def _(pool):
                pool.memset(own[:, :], 1.0).then_inc(made, 1)
                pool.wait_ge(made, 1)
                o = own[:, :].rearrange("p (h d) -> p h d", h=LH)
                pool.affine_select(out=o, in_=o, compare_op=ALU.is_ge, fill=0.0, base=0,
                                   pattern=[[-HD, LH], [0, HD]], channel_multiplier=1).then_inc(made, 1)
                pool.wait_ge(made, 2)
                pool.affine_select(out=o, in_=o, compare_op=ALU.is_ge, fill=0.0, base=HD - 1,
                                   pattern=[[HD, LH], [0, HD]], channel_multiplier=-1)

            @block.vector
            def _(dve):
                dve.memset(v1[:, :, D:D + 1], 1.0)
                dve.memset(klT[:, :, :], 0.0)

        with nc.Fori(0, L) as layer:
            def row(w):
                return I[pre + w][bass.ds(layer, 1), :]

            def matrix(w):
                return I[pre + w][bass.ds(layer, 1), :, :].rearrange("a p n -> (a p) n")

            layer_norm(nc, name + "_ln1", Y, xn, row("ln1_g"), row("ln1_b"), dst_cols=xc, ident=C.ident)
            with Stage(nc, name + "_qkv") as st:
                wl = st.sb("wl", [P, 2, LH, 32])
                wr = st.sb("wr", [P, 2 * D])
                qg = st.sb("qg", [P, NT * LH, HD])
                m = st.sb("m", [P, NT * LH])
                low = st.sb("low", [P, NT, LW])
                psL = st.ps("psL", [P, 4, N])
                psR = st.ps("psR", [P, NT, 2 * D])
                cleared, loaded, l_out, r_out, chain, shifted, expd, lowered, low_exp, q_ready, t_out = (
                    st.sem(x) for x in ("cleared", "loaded", "l_out", "r_out", "chain", "shifted", "expd",
                                        "lowered", "low_exp", "q_ready", "t_out"))
                psl_in = st.sem("psl_in")
                block = st.block()

                @block.sync
                def _(sp):
                    sp.dma_start(wr[:, 0:D], matrix("Wv")).then_inc(loaded, 16)
                    for n, w in enumerate(("Wq", "Wk")):
                        sp.dma_start(wr[:, D + n * LW:D + (n + 1) * LW], matrix(w)[:, LW:D]).then_inc(loaded, 16)
                    sp.wait_ge(cleared, 1)
                    for n, w in enumerate(("Wq", "Wk")):
                        sp.dma_start(wl[:, n, :, 0:HD], matrix(w)[:, 0:LW].rearrange("p (h d) -> p h d", h=LH))\
                            .then_inc(loaded, 16)

                @block.tensor
                def _(pe):
                    pe.wait_ge(loaded, 80)
                    for t in range(NT):
                        last = pe.matmul(psR[:, t, :], xc[:, t * P:(t + 1) * P], wr[:, :], start=True, stop=True)
                    last.then_inc(r_out, 1)
                    for n in range(2):
                        for b in range(B):
                            pe.matmul(psL[:, 2 * n + b, :], wl[:, n, :, :], xc[:, b * N:(b + 1) * N],
                                      start=True, stop=True).then_inc(l_out, 1)
                    pe.wait_ge(q_ready, 1)
                    pe.wait_ge(psl_in, 2)
                    for t in range(NT):
                        last = pe.transpose(psL[0:LW, t // TPB, t % TPB * P:(t % TPB + 1) * P],
                                            qg[:, t * LH:(t + 1) * LH, :], C.ident[:, :])
                    last.then_inc(t_out, 1)

                @block.scalar
                def _(act):
                    act.wait_ge(shifted, 1)
                    act.activation(qg[:, :, :], qg[:, :, :], ACT.Exp).then_inc(expd, 1)
                    act.wait_ge(lowered, 1)
                    act.activation(low[:, :, :], low[:, :, :], ACT.Exp).then_inc(low_exp, 1)
                    for b in range(B):
                        act.wait_ge(l_out, b + 1)
                        act.activation(qlT[:, b * N:(b + 1) * N], psL[:, b, :], ACT.Copy, scale=HD ** -0.5)\
                            .then_inc(psl_in, 1)
                    act.wait_ge(l_out, 4)
                    for h in range(LH):
                        rows = slice(32 * h, 32 * h + 32)
                        act.activation(klT[rows, h, :].rearrange("p (b j) -> p b j", b=B), psL[rows, 2:4, :], ACT.Copy)

                @block.vector
                def _(dve):
                    link = Chain(dve, chain)
                    dve.memset(wl[:, :, :, :], 0.0).then_inc(cleared, 1)
                    dve.wait_ge(r_out, 1)
                    q = psR[:, :, D:D + LW].rearrange("p t (h d) -> p t h d", h=LH)
                    q4 = qg[:, :, :].rearrange("p (t h) d -> p t h d", t=NT)
                    m3 = m[:, :].rearrange("p (t h) -> p t h", t=NT)
                    over = m3.unsqueeze(3).to_broadcast([P, NT, LH, HD])
                    link(dve.tensor_reduce(m3, q, AX.X, ALU.max))
                    dve.tensor_tensor(q4, q, over, ALU.subtract).then_inc(shifted, 1)
                    k = psR[:, :, D + LW:D + 2 * LW]
                    dve.tensor_scalar(low[:, :, :], k, 0.0, None, ALU.min).then_inc(lowered, 1)
                    dve.tensor_copy(v1[:, :, 0:D], psR[:, :, 0:D])
                    dve.wait_ge(expd, 1)
                    link(dve.tensor_reduce(m[:, :], qg[:, :, :], AX.X, ALU.add))
                    link(dve.reciprocal(m[:, :], m[:, :]))
                    dve.tensor_tensor(q4, q4, over, ALU.mult).then_inc(q_ready, 1)
                    dve.wait_ge(low_exp, 1)
                    dve.scalar_tensor_tensor(out=kg[:, :, :], in0=k, scalar=0.0, in1=low[:, :, :],
                                             op0=ALU.max, op1=ALU.add)
                    dve.wait_ge(t_out, 1)
                    dve.tensor_copy(qgT[:, :], psL[0:LW, 0:2, :])

            with Stage(nc, name + "_glob") as st:
                cum = st.sb("cum", [LW, B, NB, LW + 1])
                rk = st.sb("rk", [LW, B, NB])
                psC = st.ps("psC", [LW, 2, B * NB // 2, P])
                psG = st.ps("psG", [P, NT, LW])
                c_out, c_ready, g_out, chain = (st.sem(x) for x in ("c_out", "c_ready", "g_out", "chain"))
                block = st.block()

                @block.tensor
                def _(pe):
                    for k in range(B * NB):
                        rows = slice(BK * (k % 2), BK * (k % 2) + BK)
                        last = pe.matmul(psC[:, k % 2, k // 2, 0:LW + 1], kg[rows, k // 2, :],
                                         v1[rows, k // 2, LW:D + 1], start=True, stop=True)
                    last.then_inc(c_out, 1)
                    pe.wait_ge(c_ready, 1)
                    for k in range(B * NB):
                        rows = slice(BK * (k % 2), BK * (k % 2) + BK)
                        last = pe.matmul(psG[rows, k // 2, :], qgT[:, k * BK:(k + 1) * BK], ctxs[:, k, :],
                                         start=True, stop=True)
                    last.then_inc(g_out, 1)

                @block.vector
                def _(dve):
                    link = Chain(dve, chain)
                    link(dve.memset(cum[:, :, 0, :], 0.0))
                    dve.wait_ge(c_out, 1)
                    raw = psC[:, :, :, 0:LW + 1].rearrange("p q (b t) d -> p q b t d", b=B)
                    for u in range(1, NB):
                        link(dve.tensor_tensor(cum[:, :, u, :], cum[:, :, u - 1, :],
                                               raw[:, (u - 1) % 2, :, (u - 1) // 2, :], ALU.add))
                    link(dve.tensor_scalar(rk[:, :, :], cum[:, :, :, LW], 1e-6, None, ALU.add))
                    link(dve.reciprocal(rk[:, :, :], rk[:, :, :]))
                    c3 = ctxs[:, :, :].rearrange("p (b u) d -> p b u d", b=B)
                    link(dve.tensor_tensor(c3, cum[:, :, :, 0:LW], rk[:, :, :].unsqueeze(3)
                                           .to_broadcast([LW, B, NB, LW]), ALU.mult))
                    dve.tensor_tensor(ctxs[:, :, :], ctxs[:, :, :],
                                      own[:, None, :].to_broadcast([LW, B * NB, LW]), ALU.mult).then_inc(c_ready, 1)
                    dve.wait_ge(g_out, 1)
                    dve.tensor_copy(O[:, :, LW:D], psG[:, :, :])

            with Stage(nc, name + "_loc") as st:
                Pm = st.sb("Pm", [P, 2, LH, 2 * P])
                PT = st.sb("PT", [P, LH, 2, P])
                nmax = st.sb("nmax", [P, 2, LH])
                rsum = st.sb("rsum", [P, 4, LH])
                rinv = st.sb("rinv", [P, LH])
                psS = st.ps("psS", [P, 2, LH, 2 * P])
                psT = st.ps("psT", [P, LH, 2, P])
                psO = st.ps("psO", [P, LH, HD])
                s_out, maxed, expd, t_out, t_in, t_in2, o_out, o_in, inv = (
                    st.sem(x) for x in ("s_out", "maxed", "expd", "t_out", "t_in", "t_in2", "o_out", "o_in", "inv"))
                block = st.block()

                @block.tensor
                def _(pe):
                    def scores(t):
                        lo = 0 if t % TPB else P
                        if t >= 2:
                            pe.wait_ge(expd, LH * (t - 1))
                        for h in range(0, LH, 2):
                            pe.matmul(psS[:, t % 2, h:h + 2, P:2 * P], C.identb[:, :],
                                      C.trib[:, None, :].to_broadcast([P, 2, P]), start=True, stop=False,
                                      skip_group_check=True)
                            for hh in (h, h + 1):
                                last = pe.matmul(psS[:, t % 2, hh, lo:2 * P], qlT[:, t * P:(t + 1) * P],
                                                 klT[:, hh, (t - 1) * P + lo:(t + 1) * P], start=False, stop=True,
                                                 skip_group_check=True)
                        last.then_inc(s_out, 1)

                    def turn(t):
                        lo = 0 if t % TPB else 1
                        pe.wait_ge(expd, LH * (t + 1))
                        if t:
                            pe.wait_ge(t_in, t)
                            pe.wait_ge(t_in2, t)
                        for h in range(LH):
                            for k in range(lo, 2):
                                last = pe.transpose(psT[:, h, k, :], Pm[:, t % 2, h, k * P:(k + 1) * P], C.ident[:, :])
                        last.then_inc(t_out, 1)

                    def values(t):
                        lo = 0 if t % TPB else 1
                        pe.wait_ge(t_in, t + 1)
                        pe.wait_ge(t_in2, t + 1)
                        if t:
                            pe.wait_ge(o_in, t)
                        for h in range(LH):
                            for k in range(lo, 2):
                                last = pe.matmul(psO[:, h, :], PT[:, h, k, :],
                                                 v1[:, t - 1 + k, h * HD:(h + 1) * HD], start=k == lo, stop=k == 1)
                        last.then_inc(o_out, 1)

                    for t in range(NT + 2):
                        if t < NT:
                            scores(t)
                        if t >= 2:
                            values(t - 2)
                        if 1 <= t <= NT:
                            turn(t - 1)

                @block.scalar
                def _(act):
                    for t in range(NT + 2):
                        if t >= 2:
                            lo = 0 if (t - 2) % TPB else 1
                            act.wait_ge(t_out, t - 1)
                            if t >= 3:
                                act.wait_ge(o_out, t - 2)
                            act.activation(PT[:, 0:2, lo:2, :], psT[:, 0:2, lo:2, :], ACT.Copy).then_inc(t_in, 1)
                        if t < NT:
                            lo = 0 if t % TPB else P
                            act.wait_ge(maxed, t + 1)
                            for h in range(LH):
                                act.activation(Pm[:, t % 2, h, lo:2 * P], psS[:, t % 2, h, lo:2 * P], ACT.Exp,
                                               bias=nmax[:, t % 2, h:h + 1], accum_out=rsum[:, t % 4, h:h + 1])\
                                    .then_inc(expd, 1)

                @block.vector
                def _(dve):
                    for t in range(NT + 3):
                        if 2 <= t < NT + 2:
                            lo = 0 if (t - 2) % TPB else 1
                            dve.wait_ge(t_out, t - 1)
                            if t >= 3:
                                dve.wait_ge(o_out, t - 2)
                            dve.tensor_copy(PT[:, 2:4, lo:2, :], psT[:, 2:4, lo:2, :]).then_inc(t_in2, 1)
                        if t >= 3:
                            if t >= 4:
                                dve.wait_ge(o_in, t - 3)
                            dve.reciprocal(rinv[:, :], rsum[:, (t - 3) % 4, :]).then_inc(inv, 1)
                            dve.wait_ge(inv, t - 2)
                            dve.wait_ge(o_out, t - 2)
                            dve.tensor_tensor(O[:, t - 3, 0:LW].rearrange("p (h d) -> p h d", h=LH), psO[:, :, :],
                                              rinv[:, :].unsqueeze(2).to_broadcast([P, LH, HD]), ALU.mult)\
                                .then_inc(o_in, 1)
                        if t < NT:
                            lo = 0 if t % TPB else P
                            dve.wait_ge(s_out, t + 1)
                            if t >= 2:
                                dve.wait_ge(expd, LH * (t - 1))
                            dve.tensor_reduce(nmax[:, t % 2, :], psS[:, t % 2, :, lo:2 * P], AX.X, ALU.max,
                                              negate=True).then_inc(maxed, 1)

            rows_to_columns(nc, name + "_ot", O, OT, C.ident)
            columns_out(nc, name + "_o", OT, matrix("Wo"), Y, row("bo"))
            layer_norm(nc, name + "_ln2", Y, xn, row("ln2_g"), row("ln2_b"), dst_cols=xc, ident=C.ident)
            with Stage(nc, name + "_ffn") as st:
                w1 = st.sb("w1", [P, FCH * P])
                b1 = st.sb("b1", [P, FCH])
                ps = st.ps("ps", [P, 4, N])
                loaded, h_out, h_in = (st.sem(x) for x in ("loaded", "h_out", "h_in"))
                block = st.block()

                @block.sync
                def _(sp):
                    sp.dma_start(w1[:, :], matrix("W1")).then_inc(loaded, 16)
                    sp.dma_start(b1[:, :], matrix("b1")).then_inc(loaded, 16)

                @block.tensor
                def _(pe):
                    pe.wait_ge(loaded, 32)
                    for k in range(FCH * B):
                        c, b = k // B, k % B
                        if k >= 4:
                            pe.wait_ge(h_in, k - 3)
                        pe.matmul(ps[:, k % 4, :], w1[:, c * P:(c + 1) * P], xc[:, b * N:(b + 1) * N],
                                  start=True, stop=True).then_inc(h_out, 1)

                @block.scalar
                def _(act):
                    act.wait_ge(loaded, 32)
                    for k in range(FCH * B):
                        c, b = k // B, k % B
                        act.wait_ge(h_out, k + 1)
                        act.activation(hid[:, c, b * N:(b + 1) * N], ps[:, k % 4, :], ACT.Gelu, bias=b1[:, c:c + 1])\
                            .then_inc(h_in, 1)

            columns_out(nc, name + "_o2", hid, matrix("W2"), Y, row("b2"), K=FCH)


def add_rows(nc, name, src, dst):
    with Stage(nc, name) as st:
        block = st.block()

        @block.vector
        def _(dve):
            dve.tensor_tensor(dst[:, :, :], dst[:, :, :], src[:, :, :], ALU.add)


class Constants:

    def __init__(self, nc, ctx, I):
        def sb(n, shape, dt=F32):
            return ctx.enter_context(nc.sbuf_tensor(n, shape, dt))
        self.ident = sb("ident", [P, P])
        self.flip = sb("flip", [P, P])
        self.identb = sb("identb", [P, P], BF16)
        self.ones = sb("ones", [P, P])
        self.upto = sb("upto", [P, P])
        self.desc = sb("desc", [P, E])
        self.onesb = sb("onesb", [1, P], BF16)
        self.trib = sb("trib", [P, P], BF16)
        self.mask_bf1 = sb("mask_bf1", [1, TOK], BF16)
        self.mask_bk0 = sb("mask_bk0", [1, TOK], BF16)
        masks = (("mask_BxS_bf1", self.mask_bf1), ("mask_BxS_bk0", self.mask_bk0))
        with Stage(nc, "consts") as st:
            raw = st.sb("raw", [1, 2, TOK], U8)
            desci = st.sb("desci", [P, E], I32)
            loaded, cleared = (st.sem(x) for x in ("loaded", "cleared"))
            block = st.block()

            @block.sync
            def _(sp):
                for n, (m, _) in enumerate(masks):
                    sp.dma_start(raw[:, n, :], dram_view(I[m], 0, [[TOK, 1], [1, TOK]])).then_inc(loaded, 16)

            @block.gpsimd
            def _(pool):
                for m, v in ((self.ident, 0.0), (self.identb, 0.0), (self.trib, 0.0), (self.flip, 0.0), (self.ones, 1.0),
                             (self.upto, 1.0)):
                    pool.memset(m[:, :], v).then_inc(cleared, 1)
                pool.iota(desci[:, :], pattern=[[-1, E]], base=E, channel_multiplier=0).then_inc(cleared, 1)
                pool.wait_ge(cleared, 7)
                pool.affine_select(out=self.upto[:, :], in_=self.upto[:, :], compare_op=ALU.is_ge, fill=0.0,
                                   base=0, pattern=[[1, P]], channel_multiplier=-1)
                for m in (self.ident, self.identb):
                    pool.affine_select(out=m[:, :], in_=m[:, :], compare_op=ALU.not_equal, fill=1.0, base=0,
                                       pattern=[[-1, P]], channel_multiplier=1)
                pool.affine_select(out=self.flip[:, :], in_=self.flip[:, :], compare_op=ALU.not_equal, fill=1.0,
                                   base=-(P - 1), pattern=[[1, P]], channel_multiplier=1)
                pool.affine_select(out=self.trib[:, :], in_=self.trib[:, :], compare_op=ALU.is_ge, fill=NEG,
                                   base=0, pattern=[[-1, P]], channel_multiplier=1)

            @block.vector
            def _(dve):
                dve.memset(self.onesb[:, :], 1.0)
                dve.wait_ge(cleared, 7)
                dve.tensor_copy(self.desc[:, :], desci[:, :])
                dve.wait_ge(loaded, 32)
                for n, (_, m) in enumerate(masks):
                    dve.tensor_scalar(m[:, :], raw[:, n, :], 1.0, -NEG, ALU.subtract, ALU.mult)


def load_rows(nc, name, x, X):
    with Stage(nc, name) as st:
        loaded = st.sem("loaded")
        block = st.block()

        @block.sync
        def _(sp):
            sp.dma_start(X[:, :, :], x.rearrange("(t p) d -> p t d", p=P)).then_inc(loaded, 16)
            sp.wait_ge(loaded, 16)


def store_rows(nc, name, X, out):
    with Stage(nc, name) as st:
        stored = st.sem("stored")
        block = st.block()

        @block.sync
        def _(sp):
            sp.dma_start(out.rearrange("(t p) d -> p t d", p=P), X[:, :, :]).then_inc(stored, 16)
            sp.wait_ge(stored, 16)


def program(nc, I, out, debug):
    Stage.cleared = []
    with ExitStack() as ctx:
        def sb(n, shape, dt=F32):
            return ctx.enter_context(nc.sbuf_tensor(n, shape, dt))
        C = Constants(nc, ctx, I)
        X = sb("X", [P, NT, D])
        Y = sb("Y", [P, NT, D])
        cols = sb("cols", [P, TOK])
        Z = sb("Z", [P, TOK])
        scratch = nc.dram_tensor("bias_table", (HEADS, TOEP), F32, kind="Internal").ap()
        c_scratch = nc.dram_tensor("expert_weights", (E, TOK), F32, kind="Internal").ap()

        def show(name, rows):
            if name in debug:
                store_rows(nc, "show_" + name, rows, debug[name])

        load_rows(nc, "load_x", I["x"], X)
        if RUN(0):
            cosine_attention(nc, "l0c", I, "L0_cond_", X, Y, C, scratch)
            show("L0_cond", Y)
        if RUN(1):
            distance_attention(nc, "l0a", I, "L0_attn_", Y, X, C, scratch)
            show("x0", X)
        if RUN(2):
            biased_attention(nc, "l0b", I, "L0_cond2_", X, Y, cols, C)
            show("L0_cond2", Y)
        if RUN(3):
            rerouted_experts(nc, "l0f", I, "L0_ffn_", cols, Z, C)
            add_columns(nc, "l0s", Z, X, C.ident)
            rows_to_columns(nc, "l0t", X, cols, C.ident)
            show("x1", X)
        if RUN(4):
            grouped_experts(nc, "l1c", I, "L1_cond_", cols, Z, C)
            if "L1_cond" in debug:
                add_columns(nc, "l1d", Z, Y, C.ident, add=False)
                show("L1_cond", Y)
            linear_attention(nc, "l1a", I, "L1_attn_", Z, X, C)
            show("x2", X)
        if RUN(5):
            biased_attention(nc, "l1b", I, "L1_cond2_", X, Y, cols, C)
            phase_ffn(nc, "l1f", I, "L1_ffn_", cols, X, C)
            rows_to_columns(nc, "l1t", X, cols, C.ident)
            show("x3", X)
        if RUN(6):
            grouped_experts(nc, "l2c", I, "L2_cond_", cols, Z, C)
            windowed_attention(nc, "l2a", I, "L2_attn_", Z, X, C)
            rows_to_columns(nc, "l2t", X, cols, C.ident)
            show("x4", X)
        if RUN(7):
            grouped_experts(nc, "l2b", I, "L2_cond2_", cols, Z, C)
            with ExitStack() as inner:
                cT = inner.enter_context(nc.sbuf_tensor("l2f_cT", [E, TOK], F32))
                route(nc, "l2f_r", Z, I["L2_ffn_Wr"], C, cT, softmax=False, bias=I["L2_ffn_br"], top=1)
                expert_mlps(nc, "l2f_x", Z, I["L2_ffn_W1"], I["L2_ffn_b1"], I["L2_ffn_W2"], I["L2_ffn_b2"],
                            ACT.Relu, cT, c_scratch, cols)
            add_columns(nc, "l2s", cols, X, C.ident)
            rows_to_columns(nc, "l2u", X, cols, C.ident)
            show("x5", X)
        if RUN(8):
            grouped_experts(nc, "l3c", I, "L3_cond_", cols, Z, C)
            add_columns(nc, "l3s", Z, Y, C.ident, add=False)
            show("L3_cond", Y)
            layered_attention(nc, "l3a", I, "L3_attn_", Y, C)
            show("L3_attn", Y)
            add_rows(nc, "l3r", Y, X)
            show("x6", X)
        if RUN(9):
            cosine_attention(nc, "l3b", I, "L3_cond2_", X, Y, C, scratch)
            show("L3_cond2", Y)
            rows_to_columns(nc, "l3t", Y, cols, C.ident)
            with ExitStack() as inner:
                cT = inner.enter_context(nc.sbuf_tensor("l3f_cT", [E, TOK], F32))
                route(nc, "l3f_r", cols, I["L3_ffn_router_w"], C, cT, bias=I["L3_ffn_router_b"],
                      capacity=-(-TOK * 5 // (E * 4)))
                expert_mlps(nc, "l3f_x", cols, I["L3_ffn_w1"], I["L3_ffn_b1"], I["L3_ffn_w2"], I["L3_ffn_b2"],
                            ACT.Gelu, cT, c_scratch, Z)
            add_columns(nc, "l3v", Z, X, C.ident)
            show("x7", X)
        store_rows(nc, "store", X, out)


def RUN(k):
    return k <= UPTO


LAYOUT = {
    "x": lambda a: a.reshape(TOK, D),
    "L0_attn_Wq": lambda a: a.T, "L0_attn_Wk": lambda a: a.T, "L0_attn_Wv": lambda a: a.T,
    "L0_attn_Wo": lambda a: a.T,
    "L0_attn_rel": lambda a: a[:, ::-1],
    "L0_ffn_gate_weight": lambda a: a.T,
    "L0_ffn_down": lambda a: a.transpose(0, 2, 1).reshape(E * P, D),
    "L0_ffn_gate": lambda a: a[:, :P, :].transpose(2, 0, 1).reshape(D, E * P),
    "L0_ffn_up": lambda a: a[:, P:, :].transpose(2, 0, 1).reshape(D, E * P),
    "cond_64_T": lambda a: a.T,
}
for _p in ("L1_cond_", "L2_cond_", "L2_cond2_", "L3_cond_"):
    LAYOUT.update({
        _p + "wt": lambda a: a.T, _p + "wg": lambda a: a.T,
        _p + "w_gate": lambda a: a.transpose(1, 0, 2).reshape(D, E * DH),
        _p + "w_up": lambda a: a.transpose(1, 0, 2).reshape(D, E * DH),
        _p + "w_down": lambda a: a.reshape(E * DH, D),
    })
for _v in ("b1", "quantum_phases", "quantum_weights_real", "quantum_weights_imag"):
    LAYOUT["L1_ffn_" + _v] = lambda a: a.reshape(-1, P).T
LAYOUT.update({
    "L2_attn_bq": lambda a: a.reshape(4, 4, 8).transpose(1, 2, 0),
    "L2_attn_bk": lambda a: a.reshape(2, 8).T,
    "L2_ffn_Wr": lambda a: a.T,
    "L2_ffn_W1": lambda a: a.transpose(0, 2, 1),
    "L2_ffn_W2": lambda a: a.transpose(0, 2, 1),
    "L2_ffn_b1": lambda a: a.reshape(E, -1, P).transpose(0, 2, 1),
    "L3_ffn_b1": lambda a: a.reshape(E, -1, P).transpose(0, 2, 1),
    "L3_attn_b1": lambda a: a.reshape(a.shape[0], -1, P).transpose(0, 2, 1),
})
PIECES = {"L0_ffn_gate_up_proj": ("L0_ffn_gate", "L0_ffn_up"), "L0_ffn_down_proj": ("L0_ffn_down",),
          "cond_64": ("cond_64", "cond_64_T")}


def kernel(**inputs):
    import numpy as _np
    import concourse.bacc as _bacc
    from concourse import mybir as _mybir
    from concourse.bass_utils import run_bass_kernel_spmd as _run

    nc = _bacc.Bacc("TRN2", target_bir_lowering=False, num_devices=1)
    arrays, I = {}, {}
    pieces = [(piece, a) for name, a in inputs.items() for piece in PIECES.get(name, (name,))]
    for name, a in pieces:
        a = _np.asarray(a)
        a = _np.ascontiguousarray(LAYOUT[name](a) if name in LAYOUT else a)
        arrays[f"in_{name}"] = a
        I[name] = nc.dram_tensor(f"in_{name}", a.shape, _mybir.dt.from_np(a.dtype), kind="ExternalInput").ap()
    out = nc.dram_tensor("out_0_dram", (TOK, D), _mybir.dt.float32, kind="ExternalOutput").ap()
    debug = {n: nc.dram_tensor("dbg_" + n, (TOK, D), _mybir.dt.float32, kind="ExternalOutput").ap()
             for n in DEBUG_NAMES}
    program(nc, I, out, debug)
    r = _run(nc, [arrays], core_ids=[0])
    return r.results[0]["out_0_dram"].reshape(B, N, D)
```

```python
from contextlib import ExitStack

import concourse.bass as bass
from concourse import mybir

F32 = mybir.dt.float32
BF16 = mybir.dt.bfloat16
I32 = mybir.dt.int32
U8 = mybir.dt.uint8
ALU = mybir.AluOpType
ACT = mybir.ActivationFunctionType
AX = mybir.AxisListType

P = 128
B, N, D = 2, 512, 128
TOK = B * N
NT = TOK // P
TPB = N // P
HEADS = 16
DH = 64
INNER = HEADS * DH
E = 8
NEG = -1.0e30
EPS = 1e-5
TOEP = N + P - 1

WARM = 2


class Chain:

    def __init__(self, eng, sem):
        self.eng, self.sem, self.n = eng, sem, 0

    def __call__(self, ins, wait=True):
        ins.then_inc(self.sem, 1)
        self.n += 1
        if wait:
            self.eng.wait_ge(self.sem, self.n)

    def join(self):
        self.eng.wait_ge(self.sem, self.n)


class Stage:

    cleared = []

    def __init__(self, nc, name):
        self.nc, self.name, self.ctx, self.sems = nc, name, ExitStack(), []

    def sb(self, name, shape, dt=F32):
        return self.ctx.enter_context(self.nc.sbuf_tensor(f"{self.name}_{name}", shape, dt))

    def ps(self, name, shape, dt=F32):
        return self.ctx.enter_context(self.nc.psum_tensor(f"{self.name}_{name}", shape, dt))

    def sem(self, name):
        s = self.nc.alloc_semaphore(f"{self.name}_{name}")
        self.sems.append(s)
        return s

    def load_ahead(self, sp, ahead):
        self.ahead_in = self.sem("ahead_in")
        for dst, src in ahead:
            sp.dma_start(dst, src).then_inc(self.ahead_in, 16)

    def wait_ahead(self, sp, ahead):
        if ahead:
            sp.wait_ge(self.ahead_in, 16 * len(ahead))

    def block(self):
        return self.ctx.enter_context(self.nc.Block())

    def __enter__(self):
        return self

    def __exit__(self, *a):
        done = self.ctx.__exit__(*a)
        if a[0] is None:
            for s in self.sems:
                self.nc.gpsimd.sem_clear(s)
            for s in Stage.cleared:
                self.nc.release_semaphore(s)
            Stage.cleared = self.sems
        return done


def dram_view(ap, offset, pattern):
    return bass.AP(tensor=ap.tensor, offset=offset, ap=pattern)


def row_to_all(ap, n, offset=0):
    if len(ap.shape) == 2 and ap.shape[0] == 1:
        return ap.partition_broadcast(P).rearrange("p a n -> p (a n)")
    return dram_view(ap, offset, [[0, P], [1, n]])


def load_table(act, st, func, x):
    act.activation(st.sb(f"table_{func.name}", [P, 1])[:, :], x, func, scale=0.0)


def column(ap, n):
    if len(ap.shape) == 2:
        return ap.rearrange("a n -> n a")
    return dram_view(ap, 0, [[1, n], [1, 1]])


def layer_norm(nc, name, src, dst, gain, shift=None, dst_cols=None, ident=None, tiles=NT, silu=False, ahead=()):
    only_cols = dst is None
    with Stage(nc, name) as st:
        g = st.sb("g", [P, 1 if only_cols else D])
        s = st.sb("s", [P, 1])
        xn = st.sb("xn", [P, tiles, D]) if only_cols else dst
        stats = st.sb("stats", [P, tiles, 6])
        mv = st.sb("mv", [P, tiles, 2])
        var = st.sb("var", [P, tiles])
        root = st.sb("root", [P, tiles])
        rstd = st.sb("rstd", [P, tiles])
        tmp = st.sb("tmp", [P, tiles])
        turned = st.ps("turned", [P, tiles, P])
        loaded, chain, var_ready, root_ready, rows_ready, turned_ready = (
            st.sem(x) for x in ("loaded", "chain", "var_ready", "root_ready", "rows_ready", "turned_ready"))
        n_loads = 16 * (1 + (shift is not None))
        block = st.block()

        @block.sync
        def _(sp):
            if only_cols:
                sp.dma_start(g[:, :], column(gain, D)).then_inc(loaded, 16)
                if shift is not None:
                    sp.dma_start(s[:, :], column(shift, D)).then_inc(loaded, 16)
            else:
                sp.dma_start(g[:, :], row_to_all(gain, D)).then_inc(loaded, 16)
            st.load_ahead(sp, ahead)
            st.wait_ahead(sp, ahead)

        @block.vector
        def _(dve):
            link = Chain(dve, chain)
            for t in range(tiles):
                link(dve.bn_stats(stats[:, t, :], src[:, t, :]), wait=False)
            for t in range(tiles):
                dve.wait_ge(chain, t + 1)
                link(dve.bn_aggr(mv[:, t, :], stats[:, t, :]), wait=False)
            link.join()
            link(dve.tensor_scalar(var[:, :], mv[:, :, 1], EPS, None, ALU.add))
            dve.engine_nop().then_inc(var_ready, 1)
            dve.wait_ge(root_ready, 1)
            link(dve.reciprocal(rstd[:, :], root[:, :]))
            link(dve.tensor_tensor(tmp[:, :], rstd[:, :], rstd[:, :], ALU.mult))
            link(dve.tensor_tensor(tmp[:, :], tmp[:, :], var[:, :], ALU.mult))
            link(dve.tensor_scalar(tmp[:, :], tmp[:, :], -0.5, 1.5, ALU.mult, ALU.add))
            link(dve.tensor_tensor(rstd[:, :], rstd[:, :], tmp[:, :], ALU.mult))
            for t in range(tiles):
                norm = dve.tensor_scalar(xn[:, t, :], src[:, t, :], mv[:, t, 0:1], rstd[:, t:t + 1],
                                         ALU.subtract, ALU.mult)
                if not only_cols:
                    link(norm, wait=False)
                elif t % TPB == TPB - 1:
                    norm.then_inc(rows_ready, 1)
            if not only_cols:
                dve.wait_ge(loaded, n_loads)
                link.join()
                for h in range(0, tiles, TPB):
                    part = dst[:, h:h + TPB, :]
                    dve.tensor_tensor(part, part, g[:, None, :].to_broadcast([P, TPB, D]), ALU.mult)\
                        .then_inc(rows_ready, 1)
            if dst_cols is not None and not silu:
                dve.wait_ge(turned_ready, 1)
                if only_cols:
                    dve.wait_ge(loaded, n_loads)
                    if shift is not None:
                        dve.tensor_scalar(dst_cols[:, 0:N], turned[:, 0:TPB, :].rearrange("p t q -> p (t q)"), g[:, :],
                                          s[:, :], ALU.mult, ALU.add)
                    else:
                        dve.tensor_scalar(dst_cols[:, 0:N], turned[:, 0:TPB, :].rearrange("p t q -> p (t q)"), g[:, :],
                                          None, ALU.mult)
                else:
                    dve.tensor_copy(dst_cols[:, 0:N], turned[:, 0:TPB, :])

        @block.scalar
        def _(act):
            load_table(act, st, ACT.Sqrt, src[:, 0, 0:1])
            act.wait_ge(var_ready, 1)
            act.activation(root[:, :], var[:, :], ACT.Sqrt).then_inc(root_ready, 1)
            if silu:
                load_table(act, st, ACT.Silu, src[:, 0, 0:1])
                act.wait_ge(loaded, n_loads)
                act.wait_ge(turned_ready, 1)
                act.activation(dst_cols[:, 0:N], turned[:, 0:TPB, :], ACT.Silu, scale=g[:, :])
            elif dst_cols is not None:
                if only_cols:
                    act.wait_ge(loaded, n_loads)
                act.wait_ge(turned_ready, 2)
                cols, last = dst_cols[:, N:2 * N], turned[:, TPB:2 * TPB, :]
                if not only_cols:
                    act.activation(cols, last, ACT.Copy)
                elif shift is None:
                    act.activation(cols, last, ACT.Identity, scale=g[:, :])
                else:
                    act.activation(cols, last, ACT.Identity, scale=g[:, :], bias=s[:, :])

        @block.tensor
        def _(pe):
            if dst_cols is not None:
                for h in range(0, tiles, TPB):
                    pe.wait_ge(rows_ready, h // TPB + 1)
                    for t in range(h, h + TPB):
                        last = pe.transpose(turned[:, t, :], xn[:, t, :], ident[:, :])
                    last.then_inc(turned_ready, 1)


def rows_to_columns(nc, name, src, dst_cols, ident):
    with Stage(nc, name) as st:
        turned = st.ps("turned", [P, NT, P])
        turned_ready = st.sem("turned_ready")
        block = st.block()

        @block.tensor
        def _(pe):
            for t in range(NT):
                last = pe.transpose(turned[:, t, :], src[:, t, :], ident[:, :])
                if t % TPB == TPB - 1:
                    last.then_inc(turned_ready, 1)

        @block.vector
        def _(dve):
            dve.wait_ge(turned_ready, 1)
            dve.tensor_copy(dst_cols[:, 0:N], turned[:, 0:TPB, :])

        @block.scalar
        def _(act):
            act.wait_ge(turned_ready, 2)
            act.activation(dst_cols[:, N:2 * N], turned[:, TPB:NT, :], ACT.Copy)


def add_columns(nc, name, cols, rows, ident, add=True):
    with Stage(nc, name) as st:
        turned = st.ps("turned", [P, NT, P])
        turned_ready = st.sem("turned_ready")
        block = st.block()

        @block.tensor
        def _(pe):
            for t in range(NT):
                last = pe.transpose(turned[:, t, :], cols[:, t * P:(t + 1) * P], ident[:, :])
                if t % TPB == TPB - 1:
                    last.then_inc(turned_ready, 1)

        @block.vector
        def _(dve):
            for h in range(2):
                dve.wait_ge(turned_ready, h + 1)
                part = rows[:, h * TPB:(h + 1) * TPB, :]
                if add:
                    dve.tensor_tensor(part, part, turned[:, h * TPB:(h + 1) * TPB, :], ALU.add)
                else:
                    dve.tensor_copy(part, turned[:, h * TPB:(h + 1) * TPB, :])


def shared_kv(nc, name, xn_cols, wkv, null_kv, mask, kT, k_null, v_rows, v_null, ident, k_gain=None, q_gain=None):
    with Stage(nc, name) as st:
        kk = st.sb("kk", [P, NT, 2, DH])
        sq = st.sb("sq", [P, NT, DH])
        gain = st.sb("gain", [P, 2, DH])
        gcol = st.sb("gcol", [P, 2])
        nrm = st.sb("nrm", [P, NT + 1])
        root = st.sb("root", [P, NT + 1])
        rec = st.sb("rec", [P, NT + 1])
        tmp = st.sb("tmp", [P, NT + 1])
        sqn = st.sb("sqn", [P, 2])
        ones = st.sb("ones", [P, P])
        kv = st.ps("kv", [P, NT, 2 * DH])
        turned = st.ps("turned", [P, NT, P])
        nn = st.ps("nn", [P, 1])
        loaded, kv_ready, chain, k_ready, turned_ready, nrm_ready, root_ready, null_sq, null_len = (
            st.sem(x) for x in ("loaded", "kv_ready", "chain", "k_ready", "turned_ready", "nrm_ready",
                                "root_ready", "null_sq", "null_len"))
        k_clear = st.sem("k_clear")
        n_loads = 16 * (3 + (6 if k_gain is not None else 0))
        block = st.block()

        @block.sync
        def _(sp):
            sp.dma_start(v_null[:, :], row_to_all(null_kv, DH, DH)).then_inc(loaded, 16)
            for c in range(2):
                sp.dma_start(k_null[c * DH:(c + 1) * DH, c:c + 1], dram_view(null_kv, 0, [[1, DH], [1, 1]]))\
                    .then_inc(loaded, 16)
            if k_gain is not None:
                for n, v in enumerate((k_gain, q_gain)):
                    sp.dma_start(gain[:, n, :], row_to_all(v, DH)).then_inc(loaded, 16)
                    for c in range(2):
                        sp.dma_start(gcol[c * DH:(c + 1) * DH, n:n + 1], dram_view(v, 0, [[1, DH], [1, 1]]))\
                            .then_inc(loaded, 16)

        @block.tensor
        def _(pe):
            for t in range(NT):
                last = pe.matmul(kv[:, t, :], xn_cols[:, t * P:(t + 1) * P], wkv[:, :], start=True, stop=True)
                if t % TPB == TPB - 1:
                    last.then_inc(kv_ready, 1)
            if k_gain is not None:
                pe.wait_ge(null_sq, 1)
                pe.matmul(nn[:, :], ones[0:DH, :], sqn[0:DH, 0:1], start=True, stop=True).then_inc(null_len, 1)
            pe.wait_ge(k_ready, 1)
            for t in range(NT):
                last = pe.transpose(turned[:, t, :], kk[:, t, :, :], ident[:, :])
                if t % TPB == TPB - 1:
                    last.then_inc(turned_ready, 1)

        @block.scalar
        def _(act):
            if k_gain is not None:
                act.wait_ge(nrm_ready, 1)
                act.activation(root[:, :], nrm[:, :], ACT.Sqrt).then_inc(root_ready, 1)
            act.wait_ge(turned_ready, 2)
            act.activation(kT[DH:P, 1, :], turned[DH:P, :, :], ACT.Copy)

        @block.gpsimd
        def _(pool):
            pool.memset(kT[0:DH, 1, :], 0.0).then_inc(k_clear, 1)
            pool.memset(kT[DH:P, 0, :], 0.0).then_inc(k_clear, 1)
            pool.wait_ge(k_clear, 2)
            pool.tensor_copy(kT[0:1, 1, :], mask[0:1, :])
            pool.tensor_copy(kT[DH:DH + 1, 0, :], mask[DH:DH + 1, :])

        @block.vector
        def _(dve):
            link = Chain(dve, chain)
            link(dve.memset(ones[:, :], 1.0), wait=False)
            link(dve.memset(k_null[DH:P, 0:1], 0.0), wait=False)
            link(dve.memset(k_null[0:DH, 1:2], 0.0))
            dve.wait_ge(loaded, n_loads)
            dve.wait_ge(kv_ready, 2)
            link(dve.tensor_tensor(v_rows[:, :, :], kv[:, :, DH:2 * DH],
                                   v_null[:, None, :].to_broadcast([P, NT, DH]), ALU.subtract), wait=False)
            if k_gain is None:
                for c in range(2):
                    link(dve.tensor_scalar(kk[:, :, c, :], kv[:, :, 0:DH], DH ** -0.5, None, ALU.mult), wait=False)
                link(dve.tensor_scalar(k_null[:, :], k_null[:, :], DH ** -0.5, None, ALU.mult))
            else:
                link(dve.tensor_copy(kk[:, :, 0, :], kv[:, :, 0:DH]))
                link(dve.tensor_tensor(sq[:, :, :], kk[:, :, 0, :], kk[:, :, 0, :], ALU.mult))
                link(dve.tensor_reduce(nrm[:, 0:NT], sq[:, :, :], AX.X, ALU.add))
                dve.tensor_tensor(sqn[:, :], k_null[:, :], k_null[:, :], ALU.mult).then_inc(null_sq, 1)
                dve.wait_ge(null_len, 1)
                link(dve.tensor_copy(nrm[:, NT:NT + 1], nn[:, :]))
                link(dve.tensor_scalar(nrm[:, :], nrm[:, :], 1e-24, None, ALU.max))
                dve.engine_nop().then_inc(nrm_ready, 1)
                dve.wait_ge(root_ready, 1)
                link(dve.reciprocal(rec[:, :], root[:, :]))
                link(dve.tensor_tensor(tmp[:, :], rec[:, :], rec[:, :], ALU.mult))
                link(dve.tensor_tensor(tmp[:, :], tmp[:, :], nrm[:, :], ALU.mult))
                link(dve.tensor_scalar(tmp[:, :], tmp[:, :], -0.5, 1.5, ALU.mult, ALU.add))
                link(dve.tensor_tensor(rec[:, :], rec[:, :], tmp[:, :], ALU.mult))
                link(dve.tensor_tensor(gain[:, 0, :], gain[:, 0, :], gain[:, 1, :], ALU.mult))
                link(dve.tensor_tensor(kk[:, :, 0, :], kk[:, :, 0, :],
                                       rec[:, 0:NT, None].to_broadcast([P, NT, DH]), ALU.mult))
                link(dve.tensor_tensor(kk[:, :, 0, :], kk[:, :, 0, :],
                                       gain[:, 0:1, :].to_broadcast([P, NT, DH]), ALU.mult))
                link(dve.tensor_copy(kk[:, :, 1, :], kk[:, :, 0, :]))
                link(dve.tensor_tensor(gcol[:, 0:1], gcol[:, 0:1], gcol[:, 1:2], ALU.mult))
                link(dve.tensor_scalar(k_null[:, :], k_null[:, :], rec[:, NT:NT + 1], gcol[:, 0:1],
                                       ALU.mult, ALU.mult))
            dve.engine_nop().then_inc(k_ready, 1)
            dve.wait_ge(turned_ready, 2)
            dve.tensor_copy(kT[0:DH, 0, :], turned[0:DH, :, :])


def query_lengths(nc, name, xn_cols, wq, scale, rq):
    with Stage(nc, name) as st:
        sq = st.sb("sq", [P, 2, INNER])
        nrm = st.sb("nrm", [P, NT * HEADS])
        root = st.sb("root", [P, NT * HEADS])
        tmp = st.sb("tmp", [P, NT * HEADS])
        q = st.ps("q", [P, 2, INNER])
        q_ready, sq_ready, sq_read, nrm_ready, root_ready, chain = (
            st.sem(x) for x in ("q_ready", "sq_ready", "sq_read", "nrm_ready", "root_ready", "chain"))
        block = st.block()

        @block.tensor
        def _(pe):
            for t in range(NT):
                if t >= 2:
                    pe.wait_ge(sq_ready, t - 1)
                for h in range(2):
                    last = pe.matmul(q[:, t % 2, h * N:(h + 1) * N], xn_cols[:, t * P:(t + 1) * P],
                                     wq[:, h * N:(h + 1) * N], start=True, stop=True)
                last.then_inc(q_ready, 1)

        @block.scalar
        def _(act):
            for t in range(NT):
                act.wait_ge(q_ready, t + 1)
                if t >= 2:
                    act.wait_ge(sq_read, t - 1)
                act.activation(sq[:, t % 2, :], q[:, t % 2, :], ACT.Square).then_inc(sq_ready, 1)
            act.wait_ge(nrm_ready, 1)
            act.activation(root[:, :], nrm[:, :], ACT.Sqrt).then_inc(root_ready, 1)

        @block.vector
        def _(dve):
            link = Chain(dve, chain)
            r = rq[:, :, :].rearrange("p t h -> p (t h)")
            for t in range(NT):
                dve.wait_ge(sq_ready, t + 1)
                dve.tensor_reduce(nrm[:, t * HEADS:(t + 1) * HEADS],
                                  sq[:, t % 2, :].rearrange("p (h d) -> p h d", h=HEADS), AX.X, ALU.add)\
                    .then_inc(sq_read, 1)
            dve.wait_ge(sq_read, NT)
            link(dve.tensor_scalar(nrm[:, :], nrm[:, :], 1e-24, None, ALU.max))
            dve.engine_nop().then_inc(nrm_ready, 1)
            dve.wait_ge(root_ready, 1)
            link(dve.reciprocal(r, root[:, :]))
            link(dve.tensor_tensor(tmp[:, :], r, r, ALU.mult))
            link(dve.tensor_tensor(tmp[:, :], tmp[:, :], nrm[:, :], ALU.mult))
            link(dve.tensor_scalar(tmp[:, :], tmp[:, :], -0.5 * scale, 1.5 * scale, ALU.mult, ALU.add))
            link(dve.tensor_tensor(r, r, tmp[:, :], ALU.mult))


def attend(nc, name, x_cols, w_q, O, v_rows, ident, identb, trib, dh=DH, w_k=None, q_scale=1.0, kT=None,
           nulls=None, v_null=None, masked=False, rq=None, side=None, toeplitz=None, ahead=()):
    null = int(nulls is not None)
    UNITS = 2 * B * TPB
    PAIRS = HEADS // 2
    TURN_LAG, COPY_LAG, VALUES_LAG, INV_LAG, OUT_LAG = 3, 4, 5, 3, 6
    SLOTS = 4
    with Stage(nc, name) as st:
        wbuf = st.sb("wbuf", [P, 2, P])
        qbuf = st.sb("qbuf", [P, B, 1 + masked, N])
        kbuf = st.sb("kbuf", [P, B, 2, N]) if w_k is not None else None
        bias = st.sb("bias", [P, 4, TPB, N]) if side is not None else None
        S = st.sb("S", [P, SLOTS, N + 1])
        Pr = st.sb("Pr", [P, SLOTS, N + 1])
        PT = st.sb("PT", [P, 2, N])
        nmax = st.sb("nmax", [P, 8])
        rsum = st.sb("rsum", [P, 8])
        rinv = st.sb("rinv", [P, 8])
        psS = st.ps("psS", [P, SLOTS, N])
        psT = st.ps("psT", [P, 2, N])
        psO = st.ps("psO", [P, 2, N])
        (w_in, q_out, q_in, s_out, biased, maxed, probs, pt_out, pt_in, pv_out, inv, o_in,
         consts, w_clear) = (
            st.sem(x) for x in ("w_in", "q_out", "q_in", "s_out", "biased", "maxed", "probs", "pt_out",
                                "pt_in", "pv_out", "inv", "o_in", "consts", "w_clear"))
        bias_in = [st.sem(f"bias_in{hh}") for hh in range(2)]
        NQ = 1 if w_k is None else 2
        W_INC = 16 * (2 if w_k is None else 4)
        block = st.block()

        def unit(u):
            b, hh, qt = u // (2 * TPB), u // TPB % 2, u % TPB
            return b, hh, qt, (qt + 1) * P

        def behind(step, pair, u, first):
            if u >= 0:
                step(pair, u, first)
            elif not first:
                step(pair - 1, UNITS + u, False)

        def mod4(pair, hh):
            return (pair % 2) * 2 + hh

        @block.sync
        def _(sp):
            if dh < DH:
                sp.wait_ge(w_clear, 1)

            def load_weights(pair):
                for n, w in enumerate((w_q, w_k)[:NQ]):
                    for hh in range(2):
                        sp.dma_start(wbuf[:, n, hh * DH:hh * DH + dh], w[:, bass.ds(pair * (2 * dh) + hh * dh, dh)])\
                            .then_inc(w_in, 16)

            def load_bias(pair, first):
                for hh in range(2):
                    if not first:
                        sp.wait_ge(biased, (1 + null) * (pair * UNITS - UNITS + TPB * hh + 1))
                    for qt in range(TPB):
                        n = (qt + 1) * P
                        src = side[bass.ds(pair * 2 + hh, 1), qt * P:(qt + 1) * P, 0:n]\
                            .rearrange("a p j -> p (a j)")
                        sp.dma_start(bias[:, bass.ds(mod4(pair, hh), 1), qt, N - n:N]
                                     .rearrange("p a j -> p (a j)"), src).then_inc(bias_in[hh], 16)

            load_weights(0)
            st.load_ahead(sp, ahead)
            if side is not None:
                load_bias(0, True)
            with sp.Fori(1, PAIRS) as pair:
                sp.wait_ge(q_out, pair * (2 * NQ))
                load_weights(pair)
                if side is not None:
                    load_bias(pair, False)
            st.wait_ahead(sp, ahead)

        @block.tensor
        def _(pe):
            def project(pair, b, units_before):
                pe.wait_ge(w_in, pair * W_INC + W_INC)
                if units_before is not None:
                    pe.wait_ge(biased, (units_before - SLOTS + 1 + NQ) * (1 + null))
                for n in range(NQ):
                    if units_before is None and b:
                        pe.wait_ge(q_in, NQ)
                    pe.matmul(psS[:, 1 + n, :], wbuf[:, n, :], x_cols[:, b * N:(b + 1) * N],
                              start=True, stop=True).then_inc(q_out, 1)

            def scores(pair, u, first, last):
                b, hh, qt, n = unit(u)
                g = pair * UNITS + u
                if u % (2 * TPB) == 0:
                    pe.wait_ge(q_in, pair * (2 * NQ) + (b + 1) * NQ)
                if u % (2 * TPB) == 1 and not (last and b):
                    pe.wait_ge(q_in, pair * (2 * NQ) + (b + 2) * NQ)
                if not first or u >= SLOTS:
                    pe.wait_ge(biased, (g - SLOTS + 1) * (1 + null))
                q = qbuf[:, b, hh * masked, qt * P:(qt + 1) * P]
                keys = kbuf[:, b, hh, 0:n] if w_k is not None else kT[:, hh, b * N:b * N + n]
                out = psS[:, u % SLOTS, :]
                if side is not None:
                    pe.matmul(out[:, n - P:n], identb[:, :], trib[:, :], start=True, stop=False,
                              skip_group_check=True)
                done = pe.matmul(out[:, 0:n], q, keys, start=side is None, stop=True,
                                 skip_group_check=True)
                done.then_inc(s_out, 1)

            def turn(pair, u, first):
                _, _, qt, n = unit(u % UNITS)
                g = pair * UNITS + u
                pe.wait_ge(probs, g + 1)
                if not first or u >= 2:
                    pe.wait_ge(pt_in, g - 1)
                for k in range(qt + 1):
                    last = pe.transpose(psT[:, u % 2, k * P:(k + 1) * P],
                                        Pr[:, u % SLOTS, null + k * P:null + (k + 1) * P], ident[:, :])
                last.then_inc(pt_out, 1)

            def values(pair, u, first):
                b, hh, qt, n = unit(u % UNITS)
                g = pair * UNITS + u
                pe.wait_ge(pt_in, g + 1)
                if not first or u >= 2:
                    pe.wait_ge(o_in, g - 1)
                for k in range(qt + 1):
                    v = v_rows[:, b * TPB + k, :] if kT is not None else \
                        v_rows[:, b * TPB + k, bass.ds(pair * (2 * dh) + hh * dh, dh)]
                    last = pe.matmul(psO[:, u % 2, 0:dh], PT[:, u % 2, k * P:(k + 1) * P], v,
                                     start=k == 0, stop=k == qt)
                last.then_inc(pv_out, 1)

            def body(pair, first, last):
                for u in range(UNITS):
                    if u == 0:
                        project(pair, 1, None if first else pair * UNITS)
                    if u == UNITS // 2 and not last:
                        project(pair + 1, 0, pair * UNITS + u)
                    scores(pair, u, first, last)
                    behind(turn, pair, u - TURN_LAG, first)
                    behind(values, pair, u - VALUES_LAG, first)

            for _ in range(WARM):
                pe.matmul(psS[:, 0, :], x_cols[:, 0:P], x_cols[:, 0:N], start=True, stop=True)
            if w_k is not None or masked:
                pe.wait_ge(consts, 2)
            project(0, 0, None)
            body(0, True, False)
            with pe.Fori(1, PAIRS - 1) as pair:
                body(pair, False, False)
            body(PAIRS - 1, False, True)
            for u in range(UNITS, UNITS + VALUES_LAG):
                if u - TURN_LAG < UNITS:
                    turn(PAIRS - 1, u - TURN_LAG, False)
                values(PAIRS - 1, u - VALUES_LAG, False)

        @block.scalar
        def _(act):
            def copy_q(pair, b, first):
                for n in range(NQ):
                    m = pair * (2 * NQ) + b * NQ + n
                    act.wait_ge(q_out, m + 1)
                    if n == 0 and not (first and (b or isinstance(pair, int) and pair == 0)):
                        act.wait_ge(s_out, pair * UNITS - UNITS // 2 * (1 - b))
                    if n == 0 and masked:
                        for hh in range(2):
                            rows = slice(hh * DH, (hh + 1) * DH)
                            last = act.activation(qbuf[rows, b, hh, :], psS[rows, 1 + n, :], ACT.Copy, scale=q_scale)
                    elif n == 0:
                        last = act.activation(qbuf[:, b, 0, :], psS[:, 1 + n, :], ACT.Copy, scale=q_scale)
                    else:
                        for hh in range(2):
                            rows = slice(hh * DH, (hh + 1) * DH)
                            last = act.activation(kbuf[rows, b, hh, :], psS[rows, 1 + n, :], ACT.Copy)
                    last.then_inc(q_in, 1)

            def exps(pair, u, first):
                _, _, _, n = unit(u)
                g = pair * UNITS + u
                act.wait_ge(maxed, g + 1)
                if not first or u >= SLOTS:
                    act.wait_ge(pt_out, g - SLOTS + 1)
                w = n + null
                act.activation(Pr[:, u % SLOTS, 0:w], S[:, u % SLOTS, 0:w], ACT.Exp, bias=nmax[:, u % 8:u % 8 + 1],
                               accum_out=rsum[:, u % 8:u % 8 + 1]).then_inc(probs, 1)

            def copy_pt(pair, u, first):
                _, _, _, n = unit(u)
                g = pair * UNITS + u
                act.wait_ge(pt_out, g + 1)
                if not first or u >= 2:
                    act.wait_ge(pv_out, g - 1)
                act.activation(PT[:, u % 2, 0:n], psT[:, u % 2, 0:n], ACT.Copy).then_inc(pt_in, 1)

            def body(pair, first, last):
                for u in range(UNITS):
                    if u == 0:
                        copy_q(pair, 1, first)
                    if u == UNITS // 2 and not last:
                        copy_q(pair + 1, 0, False)
                    behind(copy_pt, pair, u - COPY_LAG, first)
                    exps(pair, u, first)

            load_table(act, st, ACT.Exp, x_cols[:, 0:1])
            copy_q(0, 0, True)
            body(0, True, False)
            with act.Fori(1, PAIRS - 1) as pair:
                body(pair, False, False)
            body(PAIRS - 1, False, True)
            for u in range(UNITS - COPY_LAG, UNITS):
                copy_pt(PAIRS - 1, u, False)

        @block.vector
        def _(dve):
            def score_bias(pair, u, first):
                b, hh, qt, n = unit(u)
                g = pair * UNITS + u
                if not first or u >= SLOTS:
                    dve.wait_ge(probs, g - SLOTS + 1)
                head = bass.ds(pair * 2 + hh, 1)
                if null:
                    dve.tensor_scalar(S[:, u % SLOTS, 0:1], nulls[:, b * TPB + qt, head], 1.0, None, ALU.mult)\
                        .then_inc(biased, 1)
                dve.wait_ge(s_out, g + 1)
                if side is not None and u in (0, TPB):
                    dve.wait_ge(bias_in[hh], pair * (16 * TPB) + 16 * TPB)
                if side is not None:
                    add = bias[:, bass.ds(mod4(pair, hh), 1), qt, N - n:N]
                else:
                    add = toeplitz[:, head, N - n:N]
                add = add.rearrange("p a j -> p (a j)")
                scale = 1.0 if rq is None else rq[:, b * TPB + qt, head]
                dve.scalar_tensor_tensor(out=S[:, u % SLOTS, null:null + n], in0=psS[:, u % SLOTS, 0:n],
                                         scalar=scale, in1=add, op0=ALU.mult, op1=ALU.add).then_inc(biased, 1)

            def row_maximum(pair, u, first):
                _, _, _, n = unit(u)
                dve.wait_ge(biased, (pair * UNITS + u + 1) * (1 + null))
                dve.tensor_reduce(nmax[:, u % 8:u % 8 + 1], S[:, u % SLOTS, 0:n + null], AX.X, ALU.max,
                                  negate=True).then_inc(maxed, 1)

            def inverse_sum(pair, u, first):
                dve.wait_ge(probs, pair * UNITS + u + 1)
                dve.reciprocal(rinv[:, u % 8:u % 8 + 1], rsum[:, u % 8:u % 8 + 1]).then_inc(inv, 1)

            def outputs(pair, u, first):
                b, hh, qt, _ = unit(u)
                s = u % 8
                dve.wait_ge(inv, pair * UNITS + u + 1)
                dve.wait_ge(pv_out, pair * UNITS + u + 1)
                dst = O[:, b * TPB + qt, bass.ds(pair * (2 * dh) + hh * dh, dh)]
                if null:
                    dve.scalar_tensor_tensor(out=dst, in0=psO[:, u % 2, 0:dh], scalar=rinv[:, s:s + 1],
                                             in1=v_null[:, :], op0=ALU.mult, op1=ALU.add).then_inc(o_in, 1)
                else:
                    dve.tensor_scalar(dst, psO[:, u % 2, 0:dh], rinv[:, s:s + 1], None, ALU.mult)\
                        .then_inc(o_in, 1)

            def body(pair, first, last):
                for u in range(UNITS):
                    behind(outputs, pair, u - OUT_LAG, first)
                    score_bias(pair, u, first)
                    behind(inverse_sum, pair, u - INV_LAG, first)
                    row_maximum(pair, u, first)

            if dh < DH:
                dve.memset(wbuf[:, :, :], 0.0).then_inc(w_clear, 1)
            if masked:
                dve.memset(qbuf[0:DH, :, 1, :], 1.0).then_inc(consts, 1)
                dve.memset(qbuf[DH:P, :, 0, :], 1.0).then_inc(consts, 1)
            if w_k is not None:
                dve.memset(kbuf[0:DH, :, 1, :], 0.0).then_inc(consts, 1)
                dve.memset(kbuf[DH:P, :, 0, :], 0.0).then_inc(consts, 1)
            body(0, True, False)
            with dve.Fori(1, PAIRS - 1) as pair:
                body(pair, False, False)
            body(PAIRS - 1, False, True)
            for u in range(UNITS - OUT_LAG, UNITS):
                if u + OUT_LAG - INV_LAG < UNITS:
                    inverse_sum(PAIRS - 1, u + OUT_LAG - INV_LAG, False)
                outputs(PAIRS - 1, u, False)


def null_scores(nc, name, xn_cols, wq, k_null, bias, nulls, ident, rq=None):
    with Stage(nc, name) as st:
        prod = st.sb("prod", [P, HEADS, DH])
        wn = st.sb("wn", [P, HEADS])
        nb = st.sb("nb", [P, HEADS])
        spread = st.sb("spread", [P, P])
        row = st.ps("row", [P, N])
        y = st.ps("y", [P, NT, HEADS])
        loaded, spread_ready, row_ready, wn_ready, y_ready, chain = (
            st.sem(x) for x in ("loaded", "spread_ready", "row_ready", "wn_ready", "y_ready", "chain"))
        block = st.block()

        @block.sync
        def _(sp):
            sp.dma_start(nb[:, :], row_to_all(bias, HEADS)).then_inc(loaded, 16)

        @block.tensor
        def _(pe):
            pe.wait_ge(spread_ready, 1)
            pe.matmul(row[:, 0:DH], spread[:, :], ident[:, 0:DH], start=True, stop=True).then_inc(row_ready, 1)
            pe.wait_ge(wn_ready, 1)
            for t in range(NT):
                last = pe.matmul(y[:, t, :], xn_cols[:, t * P:(t + 1) * P], wn[:, :], start=True, stop=True)
            last.then_inc(y_ready, 1)

        @block.vector
        def _(dve):
            link = Chain(dve, chain)
            dve.tensor_copy(spread[:, :], k_null[:, 0:1].to_broadcast([P, P])).then_inc(spread_ready, 1)
            dve.wait_ge(row_ready, 1)
            link(dve.tensor_tensor(prod[:, :, :], wq[:, :].rearrange("p (h d) -> p h d", h=HEADS), row[:, None, 0:DH].to_broadcast([P, HEADS, DH]),
                                   ALU.mult))
            dve.tensor_reduce(wn[:, :], prod[:, :, :], AX.X, ALU.add).then_inc(wn_ready, 1)
            dve.wait_ge(y_ready, 1)
            dve.wait_ge(loaded, 16)
            if rq is not None:
                link(dve.tensor_tensor(nulls[:, :, :], y[:, :, :], rq[:, :, :], ALU.mult))
                dve.tensor_tensor(nulls[:, :, :], nulls[:, :, :], nb[:, None, :].to_broadcast([P, NT, HEADS]), ALU.add)
            else:
                dve.tensor_tensor(nulls[:, :, :], y[:, :, :], nb[:, None, :].to_broadcast([P, NT, HEADS]), ALU.add)


def project_rows(nc, name, O, width, w, dst, addends, ident):
    CH = width // P
    with Stage(nc, name) as st:
        OT = st.sb("OT", [P, 2, CH, P])
        turned = st.ps("turned", [P, 2, CH * P if CH > 1 else N])
        y = st.ps("y", [P, 2, N])
        turned_ready, ot_ready, y_ready, y_read, chain = (
            st.sem(x) for x in ("turned_ready", "ot_ready", "y_ready", "y_read", "chain"))
        block = st.block()

        @block.tensor
        def _(pe):
            def product(t):
                pe.wait_ge(ot_ready, t + 1)
                if t >= 2:
                    pe.wait_ge(y_read, t - 1)
                for c in range(CH):
                    last = pe.matmul(y[:, t % 2, 0:D], OT[:, t % 2, c, :], w[:, c, :], start=c == 0, stop=c == CH - 1)
                last.then_inc(y_ready, 1)

            for t in range(NT):
                if t >= 2:
                    pe.wait_ge(ot_ready, t - 1)
                for c in range(CH):
                    last = pe.transpose(turned[:, t % 2, c * P:(c + 1) * P], O[:, t, c * P:(c + 1) * P], ident[:, :])
                last.then_inc(turned_ready, 1)
                if t >= 1:
                    product(t - 1)
            product(NT - 1)

        @block.scalar
        def _(act):
            for t in range(NT):
                act.wait_ge(turned_ready, t + 1)
                if t >= 2:
                    act.wait_ge(y_ready, t - 1)
                act.activation(OT[:, t % 2, :, :], turned[:, t % 2, 0:CH * P], ACT.Copy).then_inc(ot_ready, 1)

        @block.vector
        def _(dve):
            link = Chain(dve, chain)
            for t in range(NT):
                dve.wait_ge(y_ready, t + 1)
                if not addends:
                    dve.tensor_copy(dst[:, t, :], y[:, t % 2, 0:D]).then_inc(y_read, 1)
                    continue
                dve.tensor_tensor(dst[:, t, :], y[:, t % 2, 0:D], addends[0](t), ALU.add).then_inc(y_read, 1)
                for a in addends[1:]:
                    dve.wait_ge(y_read, t + 1)
                    link(dve.tensor_tensor(dst[:, t, :], dst[:, t, :], a(t), ALU.add))


def toeplitz_from_table(nc, name, table, scratch, T, C):
    with Stage(nc, name) as st:
        turned = st.sb("turned", [P, HEADS, N])
        ps = st.ps("ps", [P, 4, N])
        stored, flipped, out_v, out_a = (st.sem(x) for x in ("stored", "flipped", "out_v", "out_a"))
        spread = [st.sem(f"spread{h}") for h in range(4)]
        block = st.block()

        @block.sync
        def _(sp):
            sp.dma_start(scratch, table[:, :]).then_inc(stored, 16)
            sp.wait_ge(stored, 16)
            for q in range(4):
                sp.dma_start(turned[:, q * 4:(q + 1) * 4, :],
                             dram_view(scratch, q * 4 * TOEP, [[1, P], [TOEP, 4], [1, N]])).then_inc(spread[q], 16)

        @block.tensor
        def _(pe):
            for h in range(HEADS):
                if h % 4 == 0:
                    pe.wait_ge(spread[h // 4], 16)
                if h >= 4:
                    pe.wait_ge((out_v, out_a)[h % 2], (h - 4) // 2 + 1)
                pe.matmul(ps[:, h % 4, :], C.flip[:, :], turned[:, h, :], start=True, stop=True)\
                    .then_inc(flipped, 1)

        @block.scalar
        def _(act):
            for h in range(1, HEADS, 2):
                act.wait_ge(flipped, h + 1)
                act.activation(T[:, h, 0:N], ps[:, h % 4, :], ACT.Copy).then_inc(out_a, 1)

        @block.vector
        def _(dve):
            for h in range(0, HEADS, 2):
                dve.wait_ge(flipped, h + 1)
                dve.tensor_copy(T[:, h, 0:N], ps[:, h % 4, :]).then_inc(out_v, 1)


def position_bias(nc, name, I, pre, T, scratch, C):
    ident = C.ident
    h = nc.sbuf_tensor
    with ExitStack() as ctx:
        rows = ctx.enter_context(h(f"{name}_rows", [P, TPB, D], F32))
        cols = ctx.enter_context(h(f"{name}_cols", [P, N], F32))
        table = ctx.enter_context(h(f"{name}_table", [HEADS, TOEP], F32))
        with Stage(nc, name + "_in") as st:
            w0 = st.sb("w0", [P, D])
            b0 = st.sb("b0", [P, D])
            posi = st.sb("posi", [P, TPB], I32)
            pos = st.sb("pos", [P, TPB])
            loaded, made, conv = (st.sem(x) for x in ("loaded", "made", "conv"))
            block = st.block()

            @block.sync
            def _(sp):
                sp.dma_start(w0[:, :], row_to_all(I[pre + "w0"], D)).then_inc(loaded, 16)
                sp.dma_start(b0[:, :], row_to_all(I[pre + "b0"], D)).then_inc(loaded, 16)

            @block.gpsimd
            def _(pool):
                pool.iota(posi[:, :], pattern=[[-P, TPB]], base=N - 1, channel_multiplier=-1).then_inc(made, 1)

            @block.vector
            def _(dve):
                dve.wait_ge(made, 1)
                dve.tensor_copy(pos[:, :], posi[:, :]).then_inc(conv, 1)
                dve.wait_ge(conv, 1)
                dve.wait_ge(loaded, 32)
                for t in range(TPB):
                    dve.scalar_tensor_tensor(out=rows[:, t, :], in0=w0[:, :], scalar=pos[:, t:t + 1], in1=b0[:, :],
                                             op0=ALU.mult, op1=ALU.add)

        layer_norm(nc, name + "_n0", rows, None, I[pre + "g0"], dst_cols=cols, ident=ident, tiles=TPB, silu=True)
        with Stage(nc, name + "_mid") as st:
            w1 = st.sb("w1", [P, D])
            b1 = st.sb("b1", [P, D])
            y = st.ps("y", [P, TPB, D])
            loaded, y_ready = (st.sem(x) for x in ("loaded", "y_ready"))
            block = st.block()

            @block.sync
            def _(sp):
                sp.dma_start(w1[:, :], I[pre + "w1"]).then_inc(loaded, 16)
                sp.dma_start(b1[:, :], row_to_all(I[pre + "b1"], D)).then_inc(loaded, 16)

            @block.tensor
            def _(pe):
                pe.wait_ge(loaded, 32)
                for t in range(TPB):
                    last = pe.matmul(y[:, t, :], cols[:, t * P:(t + 1) * P], w1[:, :], start=True, stop=True)
                last.then_inc(y_ready, 1)

            @block.vector
            def _(dve):
                dve.wait_ge(y_ready, 1)
                dve.wait_ge(loaded, 32)
                dve.tensor_tensor(rows[:, :, :], y[:, :, :], b1[:, None, :].to_broadcast([P, TPB, D]), ALU.add)

        layer_norm(nc, name + "_n1", rows, None, I[pre + "g1"], dst_cols=cols, ident=ident, tiles=TPB, silu=True)
        with Stage(nc, name + "_out") as st:
            w2 = st.sb("w2", [P, HEADS])
            b2 = st.sb("b2", [HEADS, 1])
            y = st.ps("y", [HEADS, N])
            loaded, y_ready = (st.sem(x) for x in ("loaded", "y_ready"))
            block = st.block()

            @block.sync
            def _(sp):
                sp.dma_start(w2[:, :], I[pre + "w2"]).then_inc(loaded, 16)
                sp.dma_start(b2[:, :], dram_view(I[pre + "b2"], 0, [[1, HEADS], [1, 1]])).then_inc(loaded, 16)

            @block.tensor
            def _(pe):
                pe.wait_ge(loaded, 32)
                pe.matmul(y[:, :], w2[:, :], cols[:, :], start=True, stop=True).then_inc(y_ready, 1)

            @block.vector
            def _(dve):
                dve.memset(table[:, N:TOEP], NEG)
                dve.wait_ge(loaded, 32)
                dve.wait_ge(y_ready, 1)
                dve.tensor_scalar(table[:, 0:N], y[:, :], b2[:, 0:1], None, ALU.add)

        toeplitz_from_table(nc, name + "_spread", table, scratch, T, C)


def distance_bias(nc, name, rel, T, scratch, C):
    R = rel.shape[1]
    with ExitStack() as ctx:
        table = ctx.enter_context(nc.sbuf_tensor(f"{name}_table", [HEADS, TOEP], F32))
        with Stage(nc, name + "_in") as st:
            r = st.sb("r", [HEADS, R])
            loaded = st.sem("loaded")
            block = st.block()

            @block.sync
            def _(sp):
                sp.dma_start(r[:, :], rel).then_inc(loaded, 16)

            @block.vector
            def _(dve):
                dve.memset(table[:, N:TOEP], NEG)
                dve.wait_ge(loaded, 16)
                dve.tensor_copy(table[:, N - R + 1:N], r[:, 1:R])
                dve.tensor_copy(table[:, 0:N - R + 1], r[:, 0:1].to_broadcast([HEADS, N - R + 1]))
        toeplitz_from_table(nc, name + "_spread", table, scratch, T, C)


def cosine_attention(nc, name, I, pre, src, dst, C, scratch):
    with ExitStack() as ctx:
        def sb(n, shape, dt=F32):
            return ctx.enter_context(nc.sbuf_tensor(f"{name}_{n}", shape, dt))
        T = sb("T", [P, HEADS, N])
        wq = sb("wq", [P, INNER])
        wkv = sb("wkv", [P, 2 * DH])
        wo = sb("wo", [P, INNER // P, D])
        xn_cols = sb("xn_cols", [P, TOK])
        kT = sb("kT", [P, 2, TOK])
        k_null = sb("k_null", [P, 2])
        nulls = sb("nulls", [P, NT, HEADS])
        v_rows = sb("v_rows", [P, NT, DH])
        v_null = sb("v_null", [P, DH])
        rq = sb("rq", [P, NT, HEADS])
        O = sb("O", [P, NT, INNER])
        position_bias(nc, name + "_pos", I, pre, T, scratch, C)
        layer_norm(nc, name + "_ln", src, None, I[pre + "g_norm"], dst_cols=xn_cols, ident=C.ident,
                   ahead=((wkv[:, :], I[pre + "Wkv"]), (wq[:, :], I[pre + "Wq"])))
        shared_kv(nc, name + "_kv", xn_cols, wkv, I["cond_64"], C.mask_bf1, kT, k_null, v_rows, v_null, C.ident,
                  I[pre + "k_scale"], I[pre + "q_scale"])
        query_lengths(nc, name + "_ql", xn_cols, wq, 8.0, rq)
        null_scores(nc, name + "_ns", xn_cols, wq, k_null, I[pre + "null_attn_bias"], nulls, C.ident, rq)
        attend(nc, name + "_at", xn_cols, I[pre + "Wq"], O, v_rows, C.ident, C.identb, C.trib, kT=kT,
               nulls=nulls, v_null=v_null, masked=True, rq=rq, toeplitz=T,
               ahead=((wo[:, :, :], I[pre + "Wout"].rearrange("(c p) n -> p c n", p=P)),))
        project_rows(nc, name + "_o", O, INNER, wo, dst, (), C.ident)
    layer_norm(nc, name + "_ln2", dst, dst, I[pre + "g_out"])


def biased_attention(nc, name, I, pre, src, dst, dst_cols, C):
    with ExitStack() as ctx:
        def sb(n, shape, dt=F32):
            return ctx.enter_context(nc.sbuf_tensor(f"{name}_{n}", shape, dt))
        wq = sb("wq", [P, INNER])
        wkv = sb("wkv", [P, 2 * DH])
        wo = sb("wo", [P, INNER // P, D])
        xn_cols = sb("xn_cols", [P, TOK])
        kT = sb("kT", [P, 2, TOK])
        k_null = sb("k_null", [P, 2])
        nulls = sb("nulls", [P, NT, HEADS])
        v_rows = sb("v_rows", [P, NT, DH])
        v_null = sb("v_null", [P, DH])
        O = sb("O", [P, NT, INNER])
        layer_norm(nc, name + "_ln", src, None, I[pre + "g_in"], dst_cols=xn_cols, ident=C.ident,
                   ahead=((wkv[:, :], I[pre + "Wkv"]), (wq[:, :], I[pre + "Wq"])))
        shared_kv(nc, name + "_kv", xn_cols, wkv, I["cond_64"], C.mask_bk0, kT, k_null, v_rows, v_null, C.ident)
        null_scores(nc, name + "_ns", xn_cols, wq, k_null, I[pre + "null_attn_bias"], nulls, C.ident)
        attend(nc, name + "_at", xn_cols, I[pre + "Wq"], O, v_rows, C.ident, C.identb, C.trib, kT=kT,
               nulls=nulls, v_null=v_null, masked=True,
               side=I["fside_16xSxS_0"],
               ahead=((wo[:, :, :], I[pre + "Wo"].rearrange("(c p) n -> p c n", p=P)),))
        project_rows(nc, name + "_o", O, INNER, wo, dst, (), C.ident)
    layer_norm(nc, name + "_ln2", dst, dst, I[pre + "g_out"], dst_cols=dst_cols, ident=C.ident)


def distance_attention(nc, name, I, pre, src, X, C, scratch):
    with ExitStack() as ctx:
        def sb(n, shape, dt=F32):
            return ctx.enter_context(nc.sbuf_tensor(f"{name}_{n}", shape, dt))
        T = sb("T", [P, HEADS, N])
        wv = sb("wv", [P, D])
        wo = sb("wo", [P, 1, D])
        xn_cols = sb("xn_cols", [P, TOK])
        v_rows = sb("v_rows", [P, NT, D])
        O = sb("O", [P, NT, D])
        distance_bias(nc, name + "_b", I[pre + "rel"], T, scratch, C)
        layer_norm(nc, name + "_ln", src, None, I[pre + "ln_gamma"], I[pre + "ln_beta"], dst_cols=xn_cols,
                   ident=C.ident, ahead=((wv[:, :], I[pre + "Wv"]),))
        linear_rows(nc, name + "_v", xn_cols, wv, D, v_rows)
        attend(nc, name + "_at", xn_cols, I[pre + "Wq"], O, v_rows, C.ident, C.identb, C.trib, dh=8,
               w_k=I[pre + "Wk"], q_scale=8 ** -0.5, toeplitz=T, ahead=((wo[:, 0, :], I[pre + "Wo"]),))
        project_rows(nc, name + "_o", O, D, wo, X,
                     (lambda t: X[:, t, :], lambda t: src[:, t, :]), C.ident)


def linear_rows(nc, name, x_cols, w, width, dst):
    with Stage(nc, name) as st:
        y = st.ps("y", [P, NT, width])
        y_ready = st.sem("y_ready")
        block = st.block()

        @block.tensor
        def _(pe):
            for t in range(NT):
                last = pe.matmul(y[:, t, :], x_cols[:, t * P:(t + 1) * P], w[:, :], start=True, stop=True)
            last.then_inc(y_ready, 1)

        @block.vector
        def _(dve):
            dve.wait_ge(y_ready, 1)
            dve.tensor_copy(dst[:, :, :], y[:, :, :])


def first_maximum(link, dve, s, best, onehot, place, C):
    shape = [s.shape[0], s.shape[1], E]
    desc = C.desc[0:shape[0], None, :].to_broadcast(shape)
    link(dve.tensor_reduce(best, s, AX.X, ALU.max))
    link(dve.tensor_tensor(onehot, s, best.unsqueeze(2).to_broadcast(shape), ALU.is_equal))
    link(dve.tensor_tensor(onehot, onehot, desc, ALU.mult))
    link(dve.tensor_reduce(place, onehot, AX.X, ALU.max))
    link(dve.tensor_tensor(onehot, desc, place.unsqueeze(2).to_broadcast(shape), ALU.is_equal))


def route(nc, name, x_cols, w, C, cT, softmax=True, temper=1.0, group=None, bias=None, top=2, norm=None,
          capacity=None, similarity=None, ahead=()):
    with Stage(nc, name) as st:
        ws = st.sb("w", [P, E])
        wg = st.sb("wg", [DH, E])
        gcol = st.sb("gcol", [DH, B])
        gb = st.sb("gb", [DH, B, P])
        br = st.sb("br", [P, E])
        s = st.sb("s", [P, NT, E])
        r = st.sb("r", [P, NT, E])
        oh1 = st.sb("oh1", [P, NT, E])
        oh2 = st.sb("oh2", [P, NT, E])
        m1, m2, den, place = (st.sb(x, [P, NT]) for x in ("m1", "m2", "den", "place"))
        sim = st.sb("sim", [E, 1, E])
        simm = st.sb("simm", [E, 1, E])
        move = st.sb("move", [E, 1, E])
        prim = st.sb("prim", [E, 1, E])
        cond = st.sb("cond", [E, 4])
        c0 = st.sb("c0", [E, TOK])
        L = st.ps("L", [P, NT, E])
        cnt = st.ps("cnt", [P, NT, E])
        tot = st.ps("tot", [P, NT, E])
        turned = st.ps("turned", [E, TOK])
        moved = st.ps("moved", [E, TOK])
        loaded, gb_ready, logits, chain, shifted, expd, w_ready, turned_ready, c0_ready, moved_ready, counted, mask_ready = (
            st.sem(x) for x in ("loaded", "gb_ready", "logits", "chain", "shifted", "expd", "w_ready",
                                "turned_ready", "c0_ready", "moved_ready", "counted", "mask_ready"))
        n_loads = 16 * (1 + (2 if group else 0) + (bias is not None) + (similarity is not None))
        block = st.block()

        @block.sync
        def _(sp):
            sp.dma_start(ws[:, :], w).then_inc(loaded, 16)
            if group:
                sp.dma_start(wg[:, :], group[0]).then_inc(loaded, 16)
                sp.dma_start(gcol[:, :], group[1]).then_inc(loaded, 16)
            if bias is not None:
                sp.dma_start(br[:, :], row_to_all(bias, E)).then_inc(loaded, 16)
            if similarity is not None:
                sp.dma_start(sim[:, 0, :], similarity).then_inc(loaded, 16)
            st.load_ahead(sp, ahead)
            st.wait_ahead(sp, ahead)

        @block.tensor
        def _(pe):
            pe.wait_ge(loaded, n_loads)
            if group:
                pe.wait_ge(gb_ready, 1)
            for t in range(NT):
                last = pe.matmul(L[:, t, :], x_cols[:, t * P:(t + 1) * P], ws[:, :], start=True, stop=not group)
                if group:
                    last = pe.matmul(L[:, t, :], gb[:, t // TPB, :], wg[:, :], start=False, stop=True)
            last.then_inc(logits, 1)
            if similarity is not None:
                pe.wait_ge(mask_ready, 1)
                for t in range(NT):
                    pe.matmul(cnt[0:E, 0, :], C.ones[:, 0:E], oh1[:, t, :], start=t == 0, stop=t == NT - 1)
                for t in range(NT):
                    last = pe.matmul(tot[0:E, 0, 0:1], oh1[:, t, :], C.ones[:, 0:1], start=t == 0, stop=t == NT - 1)
                last.then_inc(counted, 1)
            if capacity is not None:
                pe.wait_ge(mask_ready, 1)
                pe.matmul(cnt[:, :, :], C.upto[:, :], oh2[:, :, :], start=True, stop=True)
                pe.matmul(tot[:, :, :], C.ones[:, :], oh2[:, :, :], start=True, stop=True).then_inc(counted, 1)
            pe.wait_ge(w_ready, 1)
            for t in range(NT):
                last = pe.transpose(turned[:, t * P:(t + 1) * P], r[:, t, :], C.ident[:, :])
            last.then_inc(turned_ready, 1)
            if similarity is not None:
                pe.wait_ge(c0_ready, 1)
                for h in range(B):
                    last = pe.matmul(moved[:, h * N:(h + 1) * N], move[:, 0, :], c0[:, h * N:(h + 1) * N],
                                     start=True, stop=True)
                last.then_inc(moved_ready, 1)

        @block.scalar
        def _(act):
            if softmax:
                load_table(act, st, ACT.Exp, x_cols[:, 0:1])
                act.wait_ge(shifted, 1)
                act.activation(s[:, :, :], s[:, :, :], ACT.Exp, scale=temper).then_inc(expd, 1)

        @block.vector
        def _(dve):
            link = Chain(dve, chain)
            dve.wait_ge(loaded, n_loads)
            if group:
                for b in range(B):
                    last = dve.tensor_copy(gb[:, b, :], gcol[:, b:b + 1].to_broadcast([DH, P]))
                last.then_inc(gb_ready, 1)
            dve.wait_ge(logits, 1)

            def over(x):
                return x[:, :].unsqueeze(2).to_broadcast([P, NT, E])

            if bias is not None:
                link(dve.tensor_tensor(s[:, :, :], L[:, :, :], br[:, None, :].to_broadcast([P, NT, E]), ALU.add))
            else:
                link(dve.tensor_copy(s[:, :, :], L[:, :, :]))
            if softmax:
                link(dve.tensor_reduce(m1[:, :], s[:, :, :], AX.X, ALU.max))
                link(dve.tensor_tensor(s[:, :, :], s[:, :, :], over(m1), ALU.subtract))
                dve.engine_nop().then_inc(shifted, 1)
                dve.wait_ge(expd, 1)
                link(dve.tensor_reduce(den[:, :], s[:, :, :], AX.X, ALU.add))
                link(dve.reciprocal(den[:, :], den[:, :]))
                link(dve.tensor_tensor(s[:, :, :], s[:, :, :], over(den), ALU.mult))
            first_maximum(link, dve, s[:, :, :], m1[:, :], oh1[:, :, :], place[:, :], C)
            if similarity is not None:
                dve.engine_nop().then_inc(mask_ready, 1)
            if top == 1:
                link(dve.tensor_copy(r[:, :, :], oh1[:, :, :]))
            else:
                link(dve.scalar_tensor_tensor(out=r[:, :, :], in0=oh1[:, :, :], scalar=-4.0, in1=s[:, :, :],
                                              op0=ALU.mult, op1=ALU.add))
                first_maximum(link, dve, r[:, :, :], m2[:, :], oh2[:, :, :], place[:, :], C)
                link(dve.tensor_tensor(oh2[:, :, :], oh1[:, :, :], oh2[:, :, :], ALU.add))
                link(dve.tensor_tensor(r[:, :, :], s[:, :, :], oh2[:, :, :], ALU.mult))
            if norm is not None:
                link(dve.tensor_tensor(den[:, :], m1[:, :], m2[:, :], ALU.add))
                link(dve.tensor_scalar(den[:, :], den[:, :], norm[1], None, norm[0]))
                link(dve.reciprocal(den[:, :], den[:, :]))
                link(dve.tensor_tensor(r[:, :, :], r[:, :, :], over(den), ALU.mult))
            if capacity is not None:
                dve.engine_nop().then_inc(mask_ready, 1)
                dve.wait_ge(counted, 1)
                link(dve.memset(s[:, 0, :], 0.0))
                for t in range(1, NT):
                    link(dve.tensor_tensor(s[:, t, :], s[:, t - 1, :], tot[:, t - 1, :], ALU.add))
                link(dve.tensor_tensor(s[:, :, :], s[:, :, :], cnt[:, :, :], ALU.add))
                link(dve.tensor_scalar(s[:, :, :], s[:, :, :], float(capacity), None, ALU.is_le))
                link(dve.tensor_tensor(r[:, :, :], r[:, :, :], s[:, :, :], ALU.mult))
            if similarity is not None:
                dve.wait_ge(counted, 1)
                link(dve.tensor_scalar(prim[:, :, :], cnt[0:E, 0:1, :], 1.0, None, ALU.min))
                link(dve.tensor_tensor(simm[:, :, :], sim[:, :, :], prim[:, :, :], ALU.mult))
                link(dve.tensor_scalar(prim[:, :, :], prim[:, :, :], 1.0, -NEG, ALU.subtract, ALU.mult))
                link(dve.tensor_tensor(simm[:, :, :], simm[:, :, :], prim[:, :, :], ALU.add))
                first_maximum(link, dve, simm[:, :, :], cond[:, 0:1], move[:, :, :], cond[:, 1:2], C)
                link(dve.tensor_scalar(cond[:, 2:3], tot[0:E, 0, 0:1], 0.5, None, ALU.is_lt))
                link(dve.tensor_scalar(cond[:, 0:1], cond[:, 0:1], 0.7, cond[:, 2:3], ALU.is_ge, ALU.mult))
                link(dve.tensor_scalar(cond[:, 3:4], cond[:, 0:1], -1.0, 1.0, ALU.mult, ALU.add))
                link(dve.tensor_scalar(move[:, 0, :], move[:, 0, :], cond[:, 0:1], None, ALU.mult))
                link(dve.scalar_tensor_tensor(out=move[:, 0, :], in0=C.ident[0:E, 0:E], scalar=cond[:, 3:4],
                                              in1=move[:, 0, :], op0=ALU.mult, op1=ALU.add))
            dve.engine_nop().then_inc(w_ready, 1)
            dve.wait_ge(turned_ready, 1)
            if similarity is None:
                dve.tensor_copy(cT[:, :], turned[:, :])
            else:
                dve.tensor_copy(c0[:, :], turned[:, :]).then_inc(c0_ready, 1)
                dve.wait_ge(moved_ready, 1)
                dve.tensor_copy(cT[:, :], moved[:, :])


def gated_experts(nc, name, x_cols, wg, wu, wd, sg, chunk, n_chunks, leaky, cT, C, dst):
    per = P // chunk
    steps = [(c, h) for c in range(n_chunks) for h in range(B)]
    if sg is not None:
        steps = [(-1, h) for h in range(B)] + steps
    with Stage(nc, name) as st:
        sel = st.sb("sel", [E, n_chunks, P])
        gs = st.sb("gs", [P, 2, N])
        lk = st.sb("lk", [P, 2, N])
        hid = st.sb("hid", [P, 2, N])
        psG = st.ps("psG", [P, N])
        psU = st.ps("psU", [P, 2, N])
        psB = st.ps("psB", [P, 2, N])
        psY = st.ps("psY", [P, B, N])
        (sel_made, g_out, u_out, g_in, chain, hid_ready, y_out, scaled) = (
            st.sem(x) for x in ("sel_made", "g_out", "u_out", "g_in", "chain", "hid_ready", "y_out",
                                "scaled"))
        block = st.block()

        @block.gpsimd
        def _(pool):
            pool.memset(sel[:, :, :], 0.0).then_inc(sel_made, 1)
            pool.wait_ge(sel_made, 1)
            v = sel[:, :, :].rearrange("e c (k m) -> e c k m", k=per)
            pool.affine_select(out=v, in_=v, compare_op=ALU.not_equal, fill=1.0, base=0,
                               pattern=[[-per, n_chunks], [-1, per], [0, chunk]], channel_multiplier=1)\
                .then_inc(sel_made, 1)

        @block.tensor
        def _(pe):
            def down(k):
                c, h = steps[k]
                pe.wait_ge(hid_ready, k + 1)
                w = sg[:, 2, :] if c < 0 else wd[:, c, :]
                pe.matmul(psY[:, h, :], w, hid[:, k % 2, :], start=k < 2, stop=k >= len(steps) - 2,
                          skip_group_check=True).then_inc(y_out, 1)

            pe.wait_ge(sel_made, 2)
            for k, (c, h) in enumerate(steps):
                x = x_cols[:, h * N:(h + 1) * N]
                if k >= 1:
                    pe.wait_ge(g_in, k)
                g, u = (sg[:, 0, :], sg[:, 1, :]) if c < 0 else (wg[:, c * P:(c + 1) * P], wu[:, c * P:(c + 1) * P])
                pe.matmul(psG[:, :], g, x, start=True, stop=True).then_inc(g_out, 1)
                if k >= 2:
                    pe.wait_ge(hid_ready, k - 1)
                last = pe.matmul(psU[:, k % 2, :], u, x, start=True, stop=True)
                if c >= 0:
                    last = pe.matmul(psB[:, k % 2, :], sel[:, c, :], cT[:, h * N:(h + 1) * N], start=True, stop=True)
                last.then_inc(u_out, 1)
                if k >= 1:
                    down(k - 1)
            down(len(steps) - 1)

        @block.scalar
        def _(act):
            if not leaky:
                load_table(act, st, ACT.Silu, x_cols[:, 0:1])
            for k in range(len(steps)):
                act.wait_ge(g_out, k + 1)
                if k >= 2:
                    act.wait_ge(scaled, k - 1)
                act.activation(gs[:, k % 2, :], psG[:, :], ACT.Copy if leaky else ACT.Silu).then_inc(g_in, 1)
            act.wait_ge(y_out, len(steps))
            act.activation(dst[:, N:2 * N], psY[:, 1, :], ACT.Copy)

        @block.vector
        def _(dve):
            link = Chain(dve, chain)
            for k, (c, h) in enumerate(steps):
                dve.wait_ge(g_in, k + 1)
                a = gs[:, k % 2, :]
                if leaky:
                    link(dve.scalar_tensor_tensor(out=lk[:, k % 2, :], in0=a, scalar=0.01, in1=a,
                                                  op0=ALU.mult, op1=ALU.max))
                    a = lk[:, k % 2, :]
                dve.wait_ge(u_out, k + 1)
                if k >= 2:
                    dve.wait_ge(y_out, k - 1)
                mul = dve.tensor_tensor(hid[:, k % 2, :], a, psU[:, k % 2, :], ALU.mult)
                mul.then_inc(scaled, 1)
                dve.wait_ge(scaled, k + 1)
                if c >= 0:
                    dve.tensor_tensor(hid[:, k % 2, :], hid[:, k % 2, :], psB[:, k % 2, :], ALU.mult)\
                        .then_inc(hid_ready, 1)
                else:
                    dve.engine_nop().then_inc(hid_ready, 1)
            dve.wait_ge(y_out, len(steps))
            dve.tensor_copy(dst[:, 0:N], psY[:, 0, :])


def grouped_experts(nc, name, I, pre, x_cols, dst, C):
    units = E * DH
    with ExitStack() as ctx:
        cT, wg, wu, wd, sg = (
            ctx.enter_context(nc.sbuf_tensor(f"{name}_{n}", shape, F32))
            for n, shape in (("cT", [E, TOK]), ("wg", [P, units]), ("wu", [P, units]), ("wd", [P, units // P, D]),
                             ("sg", [P, 3, P])))
        route(nc, name + "_r", x_cols, I[pre + "wt"], C, cT, temper=0.5, group=(I[pre + "wg"], I["cond_64_T"]),
              norm=(ALU.add, 1e-20),
              ahead=((wg[:, :], I[pre + "w_gate"]), (wu[:, :], I[pre + "w_up"]),
                     (wd[:, :, :], I[pre + "w_down"].rearrange("(c p) n -> p c n", p=P)),
                     *((sg[:, n, :], I[pre + w]) for n, w in enumerate(("sw_gate", "sw_up", "sw_down")))))
        gated_experts(nc, name + "_x", x_cols, wg, wu, wd, sg, DH, units // P, True, cT, C, dst)


def rerouted_experts(nc, name, I, pre, x_cols, dst, C):
    units = E * P
    with ExitStack() as ctx:
        cT, wg, wu, wd = (
            ctx.enter_context(nc.sbuf_tensor(f"{name}_{n}", shape, F32))
            for n, shape in (("cT", [E, TOK]), ("wg", [P, units]), ("wu", [P, units]), ("wd", [P, E, D])))
        route(nc, name + "_r", x_cols, I[pre + "gate_weight"], C, cT, norm=(ALU.max, 1e-12),
              similarity=I[pre + "similarity_matrix"],
              ahead=((wg[:, :], I[pre + "gate"]), (wu[:, :], I[pre + "up"]),
                     (wd[:, :, :], I[pre + "down"].rearrange("(c p) n -> p c n", p=P))))
        gated_experts(nc, name + "_x", x_cols, wg, wu, wd, None, P, E, False, cT, C, dst)


def linear_attention(nc, name, I, pre, x_cols, X, C):
    F, HD = 32, 8
    CH = HEADS * F // P
    with ExitStack() as ctx:
        def sb(n, shape, dt=F32):
            return ctx.enter_context(nc.sbuf_tensor(f"{name}_{n}", shape, dt))
        qT = sb("qT", [P, TOK])
        kT = sb("kT", [P, TOK])
        v1 = sb("v1", [P, NT, D + 1])
        bd = sb("bd", [P, CH, P])
        own = sb("own", [P, F])
        w = sb("w", [P, 3 * D])
        qf = sb("qf", [P, CH, TOK])
        kf = sb("kf", [P, NT, CH * P])
        kv = sb("kv", [P, B, CH, 2, F])
        outT = sb("outT", [P, TOK])
        with Stage(nc, name + "_qkv") as st:
            ps = st.ps("ps", [P, 4, N])
            pv = st.ps("pv", [P, NT, P])
            loaded, made, ready, v_ready, bd_in, cleared = (
                st.sem(x) for x in ("loaded", "made", "ready", "v_ready", "bd_in", "cleared"))
            block = st.block()

            @block.sync
            def _(sp):
                sp.dma_start(w[:, :], I[pre + "w_qkv"]).then_inc(loaded, 16)
                sp.wait_ge(cleared, 1)
                for h in range(HEADS):
                    sp.dma_start(bd[h * HD:(h + 1) * HD, h // 4, h % 4 * F:(h % 4 + 1) * F],
                                 I[pre + "proj_matrix"][h, :, :]).then_inc(bd_in, 16)
                sp.wait_ge(bd_in, 16 * HEADS)

            @block.gpsimd
            def _(pool):
                pool.memset(own[:, :], 1.0).then_inc(made, 1)
                pool.wait_ge(made, 1)
                o = own[:, :].rearrange("p (h d) -> p h d", h=4)
                pool.affine_select(out=o, in_=o, compare_op=ALU.is_ge, fill=0.0, base=0,
                                   pattern=[[-F, 4], [0, HD]], channel_multiplier=1).then_inc(made, 1)
                pool.wait_ge(made, 2)
                pool.affine_select(out=o, in_=o, compare_op=ALU.is_ge, fill=0.0, base=F - 1,
                                   pattern=[[F, 4], [0, HD]], channel_multiplier=-1)

            @block.tensor
            def _(pe):
                pe.wait_ge(loaded, 16)
                for n in range(2):
                    for b in range(B):
                        pe.matmul(ps[:, 2 * n + b, :], w[:, n * D:(n + 1) * D], x_cols[:, b * N:(b + 1) * N],
                                  start=True, stop=True).then_inc(ready, 1)
                for t in range(NT):
                    last = pe.matmul(pv[:, t, :], x_cols[:, t * P:(t + 1) * P], w[:, 2 * D:3 * D],
                                     start=True, stop=True)
                last.then_inc(v_ready, 1)

            @block.scalar
            def _(act):
                for n, dst in enumerate((qT, kT)):
                    for b in range(B):
                        act.wait_ge(ready, 2 * n + b + 1)
                        act.activation(dst[:, b * N:(b + 1) * N], ps[:, 2 * n + b, :], ACT.Copy)

            @block.vector
            def _(dve):
                dve.memset(bd[:, :, :], 0.0).then_inc(cleared, 1)
                dve.memset(v1[:, :, D:D + 1], 1.0)
                dve.wait_ge(v_ready, 1)
                dve.tensor_copy(v1[:, :, 0:D], pv[:, :, :])

        with Stage(nc, name + "_feat") as st:
            low = st.sb("low", [P, 3, N])
            ps = st.ps("ps", [P, 3, N])
            raw, lowered, expd, done = (st.sem(x) for x in ("raw", "lowered", "expd", "done"))
            block = st.block()
            jobs = [(bd[:, c, :], qT[:, b * N:(b + 1) * N], qf[:, c, b * N:(b + 1) * N])
                    for b in range(B) for c in range(CH)]
            jobs += [(kT[:, t * P:(t + 1) * P], bd[:, :, :], kf[:, t, :]) for t in range(NT)]

            @block.tensor
            def _(pe):
                for k, (lhs, rhs, _) in enumerate(jobs):
                    if k >= 3:
                        pe.wait_ge(done, k - 2)
                    pe.matmul(ps[:, k % 3, :], lhs, rhs, start=True, stop=True).then_inc(raw, 1)

            @block.scalar
            def _(act):
                for k in range(len(jobs)):
                    act.wait_ge(lowered, k + 1)
                    act.activation(low[:, k % 3, :], low[:, k % 3, :], ACT.Exp).then_inc(expd, 1)

            @block.vector
            def _(dve):
                def finish(k):
                    dve.wait_ge(expd, k + 1)
                    dve.scalar_tensor_tensor(out=jobs[k][2], in0=ps[:, k % 3, :], scalar=0.0, in1=low[:, k % 3, :],
                                             op0=ALU.max, op1=ALU.add).then_inc(done, 1)

                for k in range(len(jobs)):
                    dve.wait_ge(raw, k + 1)
                    if k >= 3:
                        dve.wait_ge(done, k - 2)
                    dve.tensor_scalar(low[:, k % 3, :], ps[:, k % 3, :], 0.0, None, ALU.min).then_inc(lowered, 1)
                    if k >= 1:
                        finish(k - 1)
                finish(len(jobs) - 1)

        with Stage(nc, name + "_kv") as st:
            psK = st.ps("psK", [P, CH, N])
            psN = st.ps("psN", [P, 2, N])
            den = st.sb("den", [P, N])
            kv_out, kv_in, nd_out, nd_in, chain = (
                st.sem(x) for x in ("kv_out", "kv_in", "nd_out", "nd_in", "chain"))
            block = st.block()

            @block.tensor
            def _(pe):
                for b in range(B):
                    if b:
                        pe.wait_ge(kv_in, 1)
                    for c in range(CH):
                        for t in range(TPB):
                            last = pe.matmul(psK[:, c, 0:D + 1], kf[:, b * TPB + t, c * P:(c + 1) * P],
                                             v1[:, b * TPB + t, :], start=t == 0, stop=t == TPB - 1)
                    last.then_inc(kv_out, 1)
                for b in range(B):
                    pe.wait_ge(kv_in, b + 1)
                    if b:
                        pe.wait_ge(nd_in, b)
                    for n in range(2):
                        for c in range(CH):
                            last = pe.matmul(psN[c * F:(c + 1) * F, n, :], kv[:, b, c, n, :],
                                             qf[:, c, b * N:(b + 1) * N], start=True, stop=True,
                                             tile_position=(0, c * F))
                    last.then_inc(nd_out, 1)

            @block.vector
            def _(dve):
                link = Chain(dve, chain)
                for b in range(B):
                    dve.wait_ge(kv_out, b + 1)
                    for c in range(CH):
                        dve.tensor_tensor(kv[:, b, c, 0, :], psK[:, c, c * F:(c + 1) * F], own[:, :], ALU.mult)
                        last = dve.tensor_scalar(kv[:, b, c, 1, :], own[:, :], psK[:, c, D:D + 1], None, ALU.mult)
                    last.then_inc(kv_in, 1)
                for b in range(B):
                    dve.wait_ge(nd_out, b + 1)
                    link(dve.tensor_scalar(den[:, :], psN[:, 1, :], 1e-8, None, ALU.add))
                    link(dve.reciprocal(den[:, :], den[:, :]))
                    dve.tensor_tensor(outT[:, b * N:(b + 1) * N], psN[:, 0, :], den[:, :], ALU.mult).then_inc(nd_in, 1)
                    dve.wait_ge(nd_in, b + 1)

        columns_out(nc, name + "_o", outT, I[pre + "w_out"], X, I[pre + "b_out"])


def columns_out(nc, name, x_cols, w, X, bias, K=1, held=None):
    with Stage(nc, name) as st:
        ws, bs = held or (st.sb("w", [P, K, D]), st.sb("b", [P, D]))
        n_loads = 0 if held else 32
        y = st.ps("y", [P, NT, D])
        loaded, y_ready, chain = (st.sem(x) for x in ("loaded", "y_ready", "chain"))
        block = st.block()

        @block.sync
        def _(sp):
            if not held:
                sp.dma_start(ws[:, :, :], w.rearrange("(c p) n -> p c n", p=P)).then_inc(loaded, 16)
                sp.dma_start(bs[:, :], row_to_all(bias, D)).then_inc(loaded, 16)

        @block.tensor
        def _(pe):
            if n_loads:
                pe.wait_ge(loaded, n_loads)
            for t in range(NT):
                for k in range(K):
                    x = x_cols[:, t * P:(t + 1) * P] if K == 1 else x_cols[:, k, t * P:(t + 1) * P]
                    last = pe.matmul(y[:, t, :], x, ws[:, k, :], start=k == 0, stop=k == K - 1)
                if t % TPB == TPB - 1:
                    last.then_inc(y_ready, 1)

        @block.vector
        def _(dve):
            link = Chain(dve, chain)
            if n_loads:
                dve.wait_ge(loaded, n_loads)
            link(dve.tensor_tensor(X[:, :, :], X[:, :, :], bs[:, None, :].to_broadcast([P, NT, D]), ALU.add))
            for h in range(B):
                dve.wait_ge(y_ready, h + 1)
                part = X[:, h * TPB:(h + 1) * TPB, :]
                dve.tensor_tensor(part, part, y[:, h * TPB:(h + 1) * TPB, :], ALU.add)


def phase_ffn(nc, name, I, pre, x_cols, X, C):
    FCH = 4
    MAGIC = 12582912.0
    TURN = 6.283185307179586
    HI = 6.28125
    LO = TURN - HI
    PI = 3.1415925
    with ExitStack() as ctx:
        hidT = ctx.enter_context(nc.sbuf_tensor(f"{name}_hidT", [P, FCH, TOK], F32))
        with Stage(nc, name + "_h") as st:
            w1 = st.sb("w1", [P, FCH * P])
            vec = st.sb("vec", [P, 4, FCH])
            ang = st.sb("ang", [P, 2, FCH])
            kk = st.sb("kk", [P, 2, FCH])
            sc = st.sb("sc", [P, 2, FCH])
            amp = st.sb("amp", [P, FCH])
            h = st.sb("h", [P, 2, TOK])
            a = st.sb("a", [P, 2, TOK])
            k_ = st.sb("k", [P, 2, TOK])
            ps = st.ps("ps", [P, 2, TOK])
            loaded, chain, h_out, h_in, reduced, sined, ang_ready, sc_ready, done = (
                st.sem(x) for x in ("loaded", "chain", "h_out", "h_in", "reduced", "sined", "ang_ready",
                                    "sc_ready", "done"))
            relued = st.sem("relued")
            block = st.block()

            @block.sync
            def _(sp):
                sp.dma_start(w1[:, :], I[pre + "W1"]).then_inc(loaded, 16)
                for n, v in enumerate(("b1", "quantum_phases", "quantum_weights_real", "quantum_weights_imag")):
                    sp.dma_start(vec[:, n, :], I[pre + v]).then_inc(loaded, 16)

            @block.tensor
            def _(pe):
                pe.wait_ge(loaded, 80)
                for c in range(FCH):
                    if c >= 2:
                        pe.wait_ge(h_in, c - 1)
                    for b in range(B):
                        last = pe.matmul(ps[:, c % 2, b * N:(b + 1) * N], w1[:, c * P:(c + 1) * P],
                                         x_cols[:, b * N:(b + 1) * N], start=True, stop=True)
                    last.then_inc(h_out, 1)

            def reduce_angle(link, dve, x, k):
                link(dve.tensor_scalar(k, x, 1.0 / TURN, MAGIC, ALU.mult, ALU.add))
                link(dve.tensor_scalar(k, k, -MAGIC, None, ALU.add))
                link(dve.scalar_tensor_tensor(out=x, in0=k, scalar=-HI, in1=x, op0=ALU.mult, op1=ALU.add))
                link(dve.scalar_tensor_tensor(out=x, in0=k, scalar=-LO, in1=x, op0=ALU.mult, op1=ALU.add))
                link(dve.tensor_scalar(x, x, PI, -PI, ALU.min, ALU.max))

            @block.vector
            def _(dve):
                link = Chain(dve, chain)
                dve.wait_ge(loaded, 80)
                link(dve.tensor_copy(ang[:, 0, :], vec[:, 1, :]))
                link(dve.tensor_scalar(ang[:, 1, :], vec[:, 1, :], TURN / 4, None, ALU.add))
                reduce_angle(link, dve, ang[:, :, :], kk[:, :, :])
                dve.engine_nop().then_inc(ang_ready, 1)
                dve.wait_ge(sc_ready, 1)
                link(dve.tensor_tensor(sc[:, 1, :], sc[:, 1, :], vec[:, 2, :], ALU.mult))
                link(dve.tensor_tensor(sc[:, 0, :], sc[:, 0, :], vec[:, 3, :], ALU.mult))
                link(dve.tensor_tensor(amp[:, :], sc[:, 0, :], sc[:, 1, :], ALU.add))
                link(dve.tensor_tensor(amp[:, :], amp[:, :], vec[:, 3, :], ALU.mult))
                link(dve.tensor_scalar(amp[:, :], amp[:, :], 0.1, None, ALU.mult))

                def finish(c):
                    dve.wait_ge(sined, c + 1)
                    dve.scalar_tensor_tensor(out=h[:, c % 2, :], in0=a[:, c % 2, :], scalar=amp[:, c:c + 1],
                                             in1=h[:, c % 2, :], op0=ALU.mult, op1=ALU.add).then_inc(done, 1)

                for c in range(FCH):
                    dve.wait_ge(h_out, c + 1)
                    if c >= 2:
                        dve.wait_ge(relued, c - 1)
                    dve.tensor_scalar(h[:, c % 2, :], ps[:, c % 2, :], vec[:, 0, c:c + 1], None, ALU.add)\
                        .then_inc(h_in, 1)
                    dve.wait_ge(h_in, c + 1)
                    link(dve.tensor_scalar(a[:, c % 2, :], h[:, c % 2, :], 0.1, vec[:, 1, c:c + 1],
                                           ALU.mult, ALU.add))
                    reduce_angle(link, dve, a[:, c % 2, :], k_[:, c % 2, :])
                    dve.engine_nop().then_inc(reduced, 1)
                    if c >= 1:
                        finish(c - 1)
                finish(FCH - 1)

            @block.scalar
            def _(act):
                load_table(act, st, ACT.Sin, x_cols[:, 0:1])
                act.wait_ge(ang_ready, 1)
                act.activation(sc[:, :, :], ang[:, :, :], ACT.Sin).then_inc(sc_ready, 1)

                def relu(c):
                    act.wait_ge(done, c + 1)
                    act.activation(hidT[:, c, :], h[:, c % 2, :], ACT.Relu).then_inc(relued, 1)

                for c in range(FCH):
                    act.wait_ge(reduced, c + 1)
                    act.activation(a[:, c % 2, :], a[:, c % 2, :], ACT.Sin).then_inc(sined, 1)
                    if c >= 1:
                        relu(c - 1)
                relu(FCH - 1)

        columns_out(nc, name + "_o", hidT, I[pre + "W2"], X, I[pre + "b2"], K=FCH)


def expert_mlps(nc, name, x_cols, w1, b1, w2, b2, func, cT, c_scratch, dst):
    FCH = w1.shape[2] // P
    HALF = FCH * B
    STEPS = 2 * HALF
    with Stage(nc, name) as st:
        w1s = st.sb("w1", [P, 2, FCH * P])
        w2s = st.sb("w2", [P, 2, FCH, D])
        cb = st.sb("cb", [P, 2, TOK])
        b1s = st.sb("b1", [P, 2, FCH])
        b2s = st.sb("b2", [E, D])
        a = st.sb("a", [P, 4, N])
        hid = st.sb("hid", [P, 4, N])
        psH = st.ps("psH", [P, 4, N])
        psY = st.ps("psY", [P, B, N])
        loaded, stored, h_out, a_out, hid_ready, y_out = (
            st.sem(x) for x in ("loaded", "stored", "h_out", "a_out", "hid_ready", "y_out"))
        w_in = [st.sem(f"w_in{s}") for s in range(2)]
        block = st.block()

        def step(j):
            return j // HALF, j % HALF // B, j % B

        @block.sync
        def _(sp):
            sp.dma_start(c_scratch, cT[:, :]).then_inc(stored, 16)
            sp.dma_start(b2s[:, :], b2).then_inc(loaded, 16)

            def load_weights(it, s):
                e = it * 2 + s
                sp.dma_start(w1s[:, s, :], w1[bass.ds(e, 1), :, :].rearrange("a p n -> p (a n)"))\
                    .then_inc(w_in[s], 16)
                sp.dma_start(w2s[:, s, :, :], w2[bass.ds(e, 1), :, :].rearrange("a (c p) n -> p (a c) n", p=P))\
                    .then_inc(w_in[s], 16)
                sp.dma_start(b1s[:, s, :], b1[bass.ds(e, 1), :, :].rearrange("a p c -> p (a c)"))\
                    .then_inc(w_in[s], 16)

            def load_factors(it, s):
                sp.dma_start(cb[:, s, :], row_to_all(c_scratch[bass.ds(it * 2 + s, 1), :], TOK)).then_inc(w_in[s], 16)

            for s in range(2):
                load_weights(0, s)
            sp.wait_ge(stored, 16)
            for s in range(2):
                load_factors(0, s)
            with sp.Fori(1, E // 2) as it:
                for s in range(2):
                    sp.wait_ge(y_out, it * STEPS - STEPS + HALF * (s + 1))
                    load_weights(it, s)
                    load_factors(it, s)

        @block.tensor
        def _(pe):
            def down(it, j):
                s, f, h = step(j)
                pe.wait_ge(hid_ready, it * STEPS + j + 1)
                pe.matmul(psY[:, h, :], w2s[:, s, f, :], hid[:, j % 4, :], start=False, stop=False,
                          skip_group_check=True).then_inc(y_out, 1)

            def body(it, first):
                for j in range(STEPS):
                    s, f, h = step(j)
                    if j % HALF == 0:
                        pe.wait_ge(w_in[s], it * 64 + 64)
                    if not first or j >= 4:
                        pe.wait_ge(a_out, it * STEPS + j - 3)
                    pe.matmul(psH[:, j % 4, :], w1s[:, s, f * P:(f + 1) * P], x_cols[:, h * N:(h + 1) * N],
                              start=True, stop=True).then_inc(h_out, 1)
                    if j >= 2:
                        down(it, j - 2)
                down(it, STEPS - 2)
                down(it, STEPS - 1)

            pe.wait_ge(loaded, 16)
            for h in range(B):
                pe.matmul(psY[:, h, :], b2s[:, :], cT[:, h * N:(h + 1) * N], start=True, stop=False,
                          skip_group_check=True)
            body(0, True)
            with pe.Fori(1, E // 2) as it:
                body(it, False)

        @block.scalar
        def _(act):
            load_table(act, st, func, x_cols[:, 0:1])

            def body(it, first):
                for j in range(STEPS):
                    s, f, h = step(j)
                    if j % HALF == 0:
                        act.wait_ge(w_in[s], it * 64 + 64)
                    act.wait_ge(h_out, it * STEPS + j + 1)
                    if not first or j >= 4:
                        act.wait_ge(hid_ready, it * STEPS + j - 3)
                    act.activation(a[:, j % 4, :], psH[:, j % 4, :], func,
                                   bias=b1s[:, s, f:f + 1]).then_inc(a_out, 1)

            body(0, True)
            with act.Fori(1, E // 2) as it:
                body(it, False)
            act.wait_ge(y_out, E // 2 * STEPS)
            act.activation(dst[:, N:2 * N], psY[:, 1, :], ACT.Copy)

        @block.vector
        def _(dve):
            def body(it, first):
                for j in range(STEPS):
                    s, f, h = step(j)
                    if j % HALF == 0:
                        dve.wait_ge(w_in[s], it * 64 + 64)
                    dve.wait_ge(a_out, it * STEPS + j + 1)
                    if not first or j >= 4:
                        dve.wait_ge(y_out, it * STEPS + j - 3)
                    dve.tensor_tensor(hid[:, j % 4, :], a[:, j % 4, :], cb[:, s, h * N:(h + 1) * N], ALU.mult)\
                        .then_inc(hid_ready, 1)

            body(0, True)
            with dve.Fori(1, E // 2) as it:
                body(it, False)
            dve.wait_ge(y_out, E // 2 * STEPS)
            dve.tensor_copy(dst[:, 0:N], psY[:, 0, :])


def windowed_attention(nc, name, I, pre, x_cols, X, C):
    QT, WIN, HD, KV = 96, 32, 8, 2
    KW = QT + WIN - 1
    HALF = WIN // 2
    NU = -(-N // QT)
    PAD = NU * QT + WIN
    with ExitStack() as ctx:
        def sb(n, shape, dt=F32):
            return ctx.enter_context(nc.sbuf_tensor(f"{name}_{n}", shape, dt))
        xp = sb("xp", [P, B, PAD])
        qT = sb("qT", [P, 4, TOK])
        kT = sb("kT", [P, KV, 4, B, PAD])
        vw = sb("vw", [P, B * NU, KV, HD + 1])
        OT = sb("OT", [P, TOK])
        with Stage(nc, name + "_qkv") as st:
            wq = st.sb("wq", [P, 4, 4, 32])
            wk = st.sb("wk", [P, KV, 4, 32])
            wv = st.sb("wv", [P, KV * HD])
            bq = st.sb("bq", [P, 4])
            bk = st.sb("bk", [P, KV])
            bv = st.sb("bv", [1, KV * HD])
            valid = st.sb("valid", [1, PAD])
            ps = st.ps("ps", [P, 4, N])
            pk = st.ps("pk", [P, 2, N])
            pv = st.ps("pv", [P, B * NU, KV * HD])
            cleared, loaded, xp_ready, raw, evac, k_raw, k_evac, k_clear, v_out = (
                st.sem(x) for x in ("cleared", "loaded", "xp_ready", "raw", "evac", "k_raw", "k_evac", "k_clear",
                                    "v_out"))
            block = st.block()
            n_loads = 16 * (4 + KV * 4 + 1 + 8 + 1)
            jobs = [(wq[:, c, :, :], x_cols[:, b * N:(b + 1) * N], qT[:, c, b * N:(b + 1) * N], bq[:, c:c + 1])
                    for c in range(4) for b in range(B)]
            key_jobs = [(g, b) for g in range(KV) for b in range(B)]

            @block.sync
            def _(sp):
                sp.wait_ge(cleared, 4)
                for c in range(4):
                    sp.dma_start(wq[:, c, :, 0:HD], I[pre + "Wq"][:, c * 32:(c + 1) * 32]
                                 .rearrange("p (r d) -> p r d", d=HD)).then_inc(loaded, 16)
                for g in range(KV):
                    for r in range(4):
                        sp.dma_start(wk[:, g, r, 0:HD], I[pre + "Wk"][:, g * HD:(g + 1) * HD]).then_inc(loaded, 16)
                sp.dma_start(wv[:, :], I[pre + "Wv"]).then_inc(loaded, 16)
                for r in range(4):
                    sp.dma_start(bq[r * 32:r * 32 + HD, :], I[pre + "bq"][r, :, :]).then_inc(loaded, 16)
                    sp.dma_start(bk[r * 32:r * 32 + HD, :], I[pre + "bk"]).then_inc(loaded, 16)
                sp.dma_start(bv[:, :], dram_view(I[pre + "bv"], 0, [[KV * HD, 1], [1, KV * HD]])).then_inc(loaded, 16)

            @block.tensor
            def _(pe):
                pe.wait_ge(loaded, n_loads)
                for k, (g, b) in enumerate(key_jobs):
                    if k >= 2:
                        pe.wait_ge(k_evac, k - 1)
                    pe.matmul(pk[:, k % 2, :], wk[:, g, :, :], x_cols[:, b * N:(b + 1) * N], start=True, stop=True)\
                        .then_inc(k_raw, 1)
                for k, (lhs, rhs, _, _) in enumerate(jobs):
                    if k >= 4:
                        pe.wait_ge(evac, k - 3)
                    pe.matmul(ps[:, k % 4, :], lhs, rhs, start=True, stop=True).then_inc(raw, 1)
                pe.wait_ge(xp_ready, 3)
                for b in range(B):
                    for u in range(NU):
                        out = pv[0:KW, b * NU + u, :]
                        pe.matmul(out, xp[:, b, u * QT:u * QT + KW], wv[:, :], start=True, stop=False)
                        last = pe.matmul(out, valid[:, u * QT:u * QT + KW], bv[:, :], start=False, stop=True)
                last.then_inc(v_out, 1)

            @block.scalar
            def _(act):
                act.wait_ge(loaded, n_loads)
                act.wait_ge(k_clear, 2)
                for k, (g, b) in enumerate(key_jobs):
                    act.wait_ge(k_raw, k + 1)
                    for h in range(4):
                        rows = slice(32 * h, 32 * h + 32)
                        last = act.activation(kT[rows, g, h, b, HALF:HALF + N], pk[rows, k % 2, :], ACT.Identity,
                                              bias=bk[rows, g:g + 1])
                    last.then_inc(k_evac, 1)

            @block.gpsimd
            def _(pool):
                pool.memset(kT[:, 1, :, :, :], 0.0).then_inc(k_clear, 1)
                pool.memset(xp[:, :, 0:HALF], 0.0)
                pool.memset(xp[:, :, HALF + N:PAD], 0.0)
                pool.tensor_copy(xp[:, :, HALF:HALF + N], x_cols[:, :].rearrange("p (b n) -> p b n", b=B))\
                    .then_inc(xp_ready, 1)
                pool.memset(valid[:, 0:HALF], 0.0)
                pool.memset(valid[:, HALF + N:PAD], 0.0).then_inc(xp_ready, 1)
                pool.memset(valid[:, HALF:HALF + N], 1.0).then_inc(xp_ready, 1)

            @block.vector
            def _(dve):
                dve.memset(wq[:, :, :, :], 0.0).then_inc(cleared, 1)
                dve.memset(wk[:, :, :, :], 0.0).then_inc(cleared, 1)
                dve.memset(bq[:, :], 0.0).then_inc(cleared, 1)
                dve.memset(bk[:, :], 0.0).then_inc(cleared, 1)
                dve.memset(kT[:, 0, :, :, :], 0.0).then_inc(k_clear, 1)
                dve.memset(vw[:, :, :, HD:HD + 1], 1.0)
                dve.wait_ge(loaded, n_loads)
                for k, (_, _, dst, bias) in enumerate(jobs):
                    dve.wait_ge(raw, k + 1)
                    dve.tensor_scalar(dst, ps[:, k % 4, :], bias, None, ALU.add).then_inc(evac, 1)
                dve.wait_ge(v_out, 1)
                dve.tensor_copy(vw[0:KW, :, :, 0:HD], pv[0:KW, :, :].rearrange("p u (g d) -> p u g d", g=KV))

        units = [(b, u, min(QT, N - u * QT)) for b in range(B) for u in range(NU)]
        with Stage(nc, name + "_at") as st:
            band = st.sb("band", [P, 4, KW], BF16)
            S = st.sb("S", [P, HEADS, KW])
            Pm = st.sb("Pm", [P, HEADS, KW])
            PT = st.sb("PT", [P, HEADS, QT])
            nmax = st.sb("nmax", [P, HEADS])
            rinv = st.sb("rinv", [P, HEADS])
            O = st.sb("O", [P, HEADS, HD])
            psS = st.ps("psS", [P, 4, N])
            psT = st.ps("psT", [P, 2, N])
            psO = st.ps("psO", [P, N])
            psX = st.ps("psX", [P, N])
            made, s_out, maxed, s_in, expd, t_out, t_in, o_out, inv, o_in, ot_out, ot_in = (
                st.sem(x) for x in ("made", "s_out", "maxed", "s_in", "expd", "t_out", "t_in", "o_out", "inv",
                                    "o_in", "ot_out", "ot_in"))
            block = st.block()

            @block.gpsimd
            def _(pool):
                pool.memset(band[:, :, :], 0.0).then_inc(made, 1)
                pool.wait_ge(made, 1)
                pool.affine_select(out=band[:, :, :], in_=band[:, :, :], compare_op=ALU.is_ge, fill=NEG, base=0,
                                   pattern=[[0, 4], [1, KW]], channel_multiplier=-1).then_inc(made, 1)
                pool.wait_ge(made, 2)
                pool.affine_select(out=band[:, :, :], in_=band[:, :, :], compare_op=ALU.is_ge, fill=NEG,
                                   base=WIN - 1, pattern=[[0, 4], [-1, KW]], channel_multiplier=1).then_inc(made, 1)

            @block.tensor
            def _(pe):
                def scores(k):
                    b, u, m = units[k]
                    if k:
                        pe.wait_ge(s_in, k)
                    for c in range(4):
                        pe.matmul(psS[0:m, c, 0:4 * KW], C.identb[:, 0:m], band[:, :, :], start=True, stop=False,
                                  skip_group_check=True)
                        last = pe.matmul(psS[0:m, c, 0:4 * KW], qT[:, c, b * N + u * QT:b * N + u * QT + m],
                                         kT[:, c // 2, :, b, u * QT:u * QT + KW], start=False, stop=True,
                                         skip_group_check=True)
                    last.then_inc(s_out, 1)

                def turn_group(k, j):
                    b, u, m = units[k]
                    n = 4 * k + j
                    if n >= 2:
                        pe.wait_ge(t_in, n - 1)
                    for y in range(4):
                        last = pe.transpose(psT[0:KW, j % 2, y * QT:y * QT + m], Pm[0:m, 4 * j + y, :],
                                            C.ident[0:m, 0:m])
                    last.then_inc(t_out, 1)

                def values_group(k, j):
                    b, u, m = units[k]
                    pe.wait_ge(t_in, 4 * k + j + 1)
                    if k and j == 0:
                        pe.wait_ge(o_in, k)
                    for h in range(4 * j, 4 * j + 4):
                        last = pe.matmul(psO[0:m, h * (HD + 1):(h + 1) * (HD + 1)], PT[0:KW, h, 0:m],
                                         vw[0:KW, k, j // 2, :], start=True, stop=True)
                    if j == 3:
                        last.then_inc(o_out, 1)

                def values(k):
                    pe.wait_ge(expd, k + 1)
                    for j in range(5):
                        if j < 4:
                            turn_group(k, j)
                        if j >= 1:
                            values_group(k, j - 1)

                def turn(k):
                    b, u, m = units[k]
                    pe.wait_ge(o_in, k + 1)
                    if k:
                        pe.wait_ge(ot_in, k)
                    pe.transpose(psX[:, 0:m], O[0:m, :, :], C.ident[0:m, 0:m]).then_inc(ot_out, 1)

                pe.wait_ge(made, 3)
                for k in range(len(units) + 2):
                    if k < len(units):
                        scores(k)
                    if k >= 2:
                        turn(k - 2)
                    if 1 <= k <= len(units):
                        values(k - 1)

            @block.scalar
            def _(act):
                load_table(act, st, ACT.Exp, qT[:, 0, 0:1])
                for k in range(len(units) + 2):
                    if k >= 2:
                        b, u, m = units[k - 2]
                        act.wait_ge(ot_out, k - 1)
                        act.activation(OT[:, b * N + u * QT:b * N + u * QT + m], psX[:, 0:m], ACT.Copy)\
                            .then_inc(ot_in, 1)
                    if 1 <= k <= len(units):
                        b, u, m = units[k - 1]
                        for j in range(4):
                            act.wait_ge(t_out, 4 * (k - 1) + j + 1)
                            if k >= 2 and j == 0:
                                act.wait_ge(o_out, k - 1)
                            act.activation(PT[0:KW, 4 * j:4 * j + 4, 0:m],
                                           psT[0:KW, j % 2, 0:4 * QT].rearrange("p (y q) -> p y q", y=4)[:, :, 0:m],
                                           ACT.Copy).then_inc(t_in, 1)
                    if k < len(units):
                        b, u, m = units[k]
                        act.wait_ge(s_in, k + 1)
                        act.activation(Pm[0:m, :, :], S[0:m, :, :], ACT.Exp).then_inc(expd, 1)

            @block.vector
            def _(dve):
                def finish(k):
                    b, u, m = units[k]
                    dve.wait_ge(o_out, k + 1)
                    o = psO[0:m, 0:HEADS * (HD + 1)].rearrange("p (h d) -> p h d", h=HEADS)
                    dve.reciprocal(rinv[0:m, :], o[:, :, HD]).then_inc(inv, 1)
                    dve.wait_ge(inv, k + 1)
                    if k:
                        dve.wait_ge(ot_out, k)
                    dve.tensor_tensor(O[0:m, :, :], o[:, :, 0:HD],
                                      rinv[0:m, :].unsqueeze(2).to_broadcast([m, HEADS, HD]), ALU.mult)\
                        .then_inc(o_in, 1)

                for k, (b, u, m) in enumerate(units):
                    dve.wait_ge(s_out, k + 1)
                    s = psS[0:m, :, 0:4 * KW].rearrange("p c (r j) -> p c r j", r=4)
                    n4 = nmax[0:m, :].rearrange("p (c r) -> p c r", c=4)
                    dve.tensor_reduce(n4, s, AX.X, ALU.max).then_inc(maxed, 1)
                    dve.wait_ge(maxed, k + 1)
                    if k:
                        dve.wait_ge(expd, k)
                    dve.tensor_tensor(S[0:m, :, :].rearrange("p (c r) j -> p c r j", c=4), s,
                                      n4.unsqueeze(3).to_broadcast([m, 4, 4, KW]), ALU.subtract).then_inc(s_in, 1)
                    if k:
                        finish(k - 1)
                finish(len(units) - 1)

        columns_out(nc, name + "_o", OT, I[pre + "Wo"], X, I[pre + "bo"])


def layered_attention(nc, name, I, pre, Y, C):
    L, HD, LH, BK = 4, 16, 4, 64
    LW = LH * HD
    NB = N // BK
    FCH = 4
    with ExitStack() as ctx:
        def sb(n, shape, dt=F32):
            return ctx.enter_context(nc.sbuf_tensor(f"{name}_{n}", shape, dt))
        wl = sb("wl", [P, 2, LH, 32])
        wr = sb("wr", [P, 2 * D])
        wo = sb("wo", [P, 1, D])
        bo = sb("bo", [P, D])
        w1 = sb("w1", [P, FCH * P])
        b1 = sb("b1", [P, FCH])
        w2 = sb("w2", [P, FCH, D])
        b2 = sb("b2", [P, D])
        xc = sb("xc", [P, TOK])
        qlT = sb("qlT", [P, TOK])
        klT = sb("klT", [P, LH, TOK])
        v1 = sb("v1", [P, NT, D + 1])
        kg = sb("kg", [P, NT, LW])
        qgT = sb("qgT", [LW, TOK])
        ctxs = sb("ctxs", [LW, B * NB, LW])
        own = sb("own", [LW, LW])
        O = sb("O", [P, NT, D])
        OT = sb("OT", [P, TOK])
        hid = sb("hid", [P, FCH, TOK])
        with Stage(nc, name + "_own") as st:
            made = st.sem("made")
            block = st.block()

            @block.gpsimd
            def _(pool):
                pool.memset(own[:, :], 1.0).then_inc(made, 1)
                pool.wait_ge(made, 1)
                o = own[:, :].rearrange("p (h d) -> p h d", h=LH)
                pool.affine_select(out=o, in_=o, compare_op=ALU.is_ge, fill=0.0, base=0,
                                   pattern=[[-HD, LH], [0, HD]], channel_multiplier=1).then_inc(made, 1)
                pool.wait_ge(made, 2)
                pool.affine_select(out=o, in_=o, compare_op=ALU.is_ge, fill=0.0, base=HD - 1,
                                   pattern=[[HD, LH], [0, HD]], channel_multiplier=-1)

            @block.vector
            def _(dve):
                dve.memset(v1[:, :, D:D + 1], 1.0)
                dve.memset(klT[:, :, :], 0.0)
                dve.memset(wl[:, :, :, :], 0.0)

        with nc.Fori(0, L) as layer:
            def row(w):
                return I[pre + w][bass.ds(layer, 1), :]

            def matrix(w):
                return I[pre + w][bass.ds(layer, 1), :, :].rearrange("a p n -> (a p) n")

            def local(w):
                return matrix(w)[:, 0:LW].rearrange("p (h d) -> p h d", h=LH)

            layer_norm(nc, name + "_ln1", Y, None, row("ln1_g"), row("ln1_b"), dst_cols=xc, ident=C.ident,
                       ahead=((wr[:, 0:D], matrix("Wv")), (wr[:, D:D + LW], matrix("Wq")[:, LW:D]),
                              (wr[:, D + LW:2 * D], matrix("Wk")[:, LW:D]), (wl[:, 0, :, 0:HD], local("Wq")),
                              (wl[:, 1, :, 0:HD], local("Wk")), (wo[:, 0, :], matrix("Wo")),
                              (bo[:, :], row_to_all(row("bo"), D))))
            with Stage(nc, name + "_qkv") as st:
                qg = st.sb("qg", [P, NT * LH, HD])
                m = st.sb("m", [P, NT * LH])
                low = st.sb("low", [P, NT, LW])
                psL = st.ps("psL", [P, 4, N])
                psR = st.ps("psR", [P, NT, 2 * D])
                l_out, r_out, chain, shifted, expd, lowered, low_exp, q_ready, t_out = (
                    st.sem(x) for x in ("l_out", "r_out", "chain", "shifted", "expd",
                                        "lowered", "low_exp", "q_ready", "t_out"))
                psl_in = st.sem("psl_in")
                block = st.block()

                @block.tensor
                def _(pe):
                    for t in range(NT):
                        last = pe.matmul(psR[:, t, :], xc[:, t * P:(t + 1) * P], wr[:, :], start=True, stop=True)
                    last.then_inc(r_out, 1)
                    for n in range(2):
                        for b in range(B):
                            pe.matmul(psL[:, 2 * n + b, :], wl[:, n, :, :], xc[:, b * N:(b + 1) * N],
                                      start=True, stop=True).then_inc(l_out, 1)
                    pe.wait_ge(q_ready, 1)
                    pe.wait_ge(psl_in, 2)
                    for t in range(NT):
                        last = pe.transpose(psL[0:LW, t // TPB, t % TPB * P:(t % TPB + 1) * P],
                                            qg[:, t * LH:(t + 1) * LH, :], C.ident[:, :])
                    last.then_inc(t_out, 1)

                @block.scalar
                def _(act):
                    load_table(act, st, ACT.Exp, xc[:, 0:1])
                    act.wait_ge(shifted, 1)
                    act.activation(qg[:, :, :], qg[:, :, :], ACT.Exp).then_inc(expd, 1)
                    act.wait_ge(lowered, 1)
                    act.activation(low[:, :, :], low[:, :, :], ACT.Exp).then_inc(low_exp, 1)
                    for b in range(B):
                        act.wait_ge(l_out, b + 1)
                        act.activation(qlT[:, b * N:(b + 1) * N], psL[:, b, :], ACT.Copy, scale=HD ** -0.5)\
                            .then_inc(psl_in, 1)
                    act.wait_ge(l_out, 4)
                    for h in range(LH):
                        rows = slice(32 * h, 32 * h + 32)
                        act.activation(klT[rows, h, :].rearrange("p (b j) -> p b j", b=B), psL[rows, 2:4, :], ACT.Copy)

                @block.vector
                def _(dve):
                    link = Chain(dve, chain)
                    dve.wait_ge(r_out, 1)
                    q = psR[:, :, D:D + LW].rearrange("p t (h d) -> p t h d", h=LH)
                    q4 = qg[:, :, :].rearrange("p (t h) d -> p t h d", t=NT)
                    m3 = m[:, :].rearrange("p (t h) -> p t h", t=NT)
                    over = m3.unsqueeze(3).to_broadcast([P, NT, LH, HD])
                    link(dve.tensor_reduce(m3, q, AX.X, ALU.max))
                    dve.tensor_tensor(q4, q, over, ALU.subtract).then_inc(shifted, 1)
                    k = psR[:, :, D + LW:D + 2 * LW]
                    dve.tensor_scalar(low[:, :, :], k, 0.0, None, ALU.min).then_inc(lowered, 1)
                    dve.tensor_copy(v1[:, :, 0:D], psR[:, :, 0:D])
                    dve.wait_ge(expd, 1)
                    link(dve.tensor_reduce(m[:, :], qg[:, :, :], AX.X, ALU.add))
                    link(dve.reciprocal(m[:, :], m[:, :]))
                    dve.tensor_tensor(q4, q4, over, ALU.mult).then_inc(q_ready, 1)
                    dve.wait_ge(low_exp, 1)
                    dve.scalar_tensor_tensor(out=kg[:, :, :], in0=k, scalar=0.0, in1=low[:, :, :],
                                             op0=ALU.max, op1=ALU.add)
                    dve.wait_ge(t_out, 1)
                    dve.tensor_copy(qgT[:, :], psL[0:LW, 0:2, :])

            with Stage(nc, name + "_glob") as st:
                cum = st.sb("cum", [LW, B, NB, LW + 1])
                rk = st.sb("rk", [LW, B, NB])
                psC = st.ps("psC", [LW, 2, B * NB // 2, P])
                psG = st.ps("psG", [P, NT, LW])
                c_out, c_ready, g_out, chain = (st.sem(x) for x in ("c_out", "c_ready", "g_out", "chain"))
                block = st.block()

                @block.tensor
                def _(pe):
                    for k in range(B * NB):
                        rows = slice(BK * (k % 2), BK * (k % 2) + BK)
                        last = pe.matmul(psC[:, k % 2, k // 2, 0:LW + 1], kg[rows, k // 2, :],
                                         v1[rows, k // 2, LW:D + 1], start=True, stop=True)
                    last.then_inc(c_out, 1)
                    pe.wait_ge(c_ready, 1)
                    for k in range(B * NB):
                        rows = slice(BK * (k % 2), BK * (k % 2) + BK)
                        last = pe.matmul(psG[rows, k // 2, :], qgT[:, k * BK:(k + 1) * BK], ctxs[:, k, :],
                                         start=True, stop=True)
                    last.then_inc(g_out, 1)

                @block.vector
                def _(dve):
                    link = Chain(dve, chain)
                    link(dve.memset(cum[:, :, 0, :], 0.0))
                    dve.wait_ge(c_out, 1)
                    raw = psC[:, :, :, 0:LW + 1].rearrange("p q (b t) d -> p q b t d", b=B)
                    for u in range(1, NB):
                        link(dve.tensor_tensor(cum[:, :, u, :], cum[:, :, u - 1, :],
                                               raw[:, (u - 1) % 2, :, (u - 1) // 2, :], ALU.add))
                    link(dve.tensor_scalar(rk[:, :, :], cum[:, :, :, LW], 1e-6, None, ALU.add))
                    link(dve.reciprocal(rk[:, :, :], rk[:, :, :]))
                    c3 = ctxs[:, :, :].rearrange("p (b u) d -> p b u d", b=B)
                    link(dve.tensor_tensor(c3, cum[:, :, :, 0:LW], rk[:, :, :].unsqueeze(3)
                                           .to_broadcast([LW, B, NB, LW]), ALU.mult))
                    dve.tensor_tensor(ctxs[:, :, :], ctxs[:, :, :],
                                      own[:, None, :].to_broadcast([LW, B * NB, LW]), ALU.mult).then_inc(c_ready, 1)
                    dve.wait_ge(g_out, 1)
                    dve.tensor_copy(O[:, :, LW:D], psG[:, :, :])

            with Stage(nc, name + "_loc") as st:
                Pm = st.sb("Pm", [P, 2, LH, 2 * P])
                PT = st.sb("PT", [P, LH, 2, P])
                nmax = st.sb("nmax", [P, 2, LH])
                rsum = st.sb("rsum", [P, 4, LH])
                rinv = st.sb("rinv", [P, LH])
                psS = st.ps("psS", [P, 2, LH, 2 * P])
                psT = st.ps("psT", [P, LH, 2, P])
                psO = st.ps("psO", [P, LH, HD])
                s_out, maxed, expd, t_out, t_in, t_in2, o_out, o_in, inv = (
                    st.sem(x) for x in ("s_out", "maxed", "expd", "t_out", "t_in", "t_in2", "o_out", "o_in", "inv"))
                block = st.block()

                @block.tensor
                def _(pe):
                    def scores(t):
                        lo = 0 if t % TPB else P
                        if t >= 2:
                            pe.wait_ge(expd, LH * (t - 1))
                        for h in range(0, LH, 2):
                            pe.matmul(psS[:, t % 2, h:h + 2, P:2 * P], C.identb[:, :],
                                      C.trib[:, None, :].to_broadcast([P, 2, P]), start=True, stop=False,
                                      skip_group_check=True)
                            for hh in (h, h + 1):
                                last = pe.matmul(psS[:, t % 2, hh, lo:2 * P], qlT[:, t * P:(t + 1) * P],
                                                 klT[:, hh, (t - 1) * P + lo:(t + 1) * P], start=False, stop=True,
                                                 skip_group_check=True)
                        last.then_inc(s_out, 1)

                    def turn(t):
                        lo = 0 if t % TPB else 1
                        pe.wait_ge(expd, LH * (t + 1))
                        if t:
                            pe.wait_ge(t_in, t)
                            pe.wait_ge(t_in2, t)
                        for h in range(LH):
                            for k in range(lo, 2):
                                last = pe.transpose(psT[:, h, k, :], Pm[:, t % 2, h, k * P:(k + 1) * P], C.ident[:, :])
                        last.then_inc(t_out, 1)

                    def values(t):
                        lo = 0 if t % TPB else 1
                        pe.wait_ge(t_in, t + 1)
                        pe.wait_ge(t_in2, t + 1)
                        if t:
                            pe.wait_ge(o_in, t)
                        for h in range(LH):
                            for k in range(lo, 2):
                                last = pe.matmul(psO[:, h, :], PT[:, h, k, :],
                                                 v1[:, t - 1 + k, h * HD:(h + 1) * HD], start=k == lo, stop=k == 1)
                        last.then_inc(o_out, 1)

                    for t in range(NT + 2):
                        if t < NT:
                            scores(t)
                        if t >= 2:
                            values(t - 2)
                        if 1 <= t <= NT:
                            turn(t - 1)

                @block.scalar
                def _(act):
                    load_table(act, st, ACT.Exp, xc[:, 0:1])
                    for t in range(NT + 2):
                        if t >= 2:
                            lo = 0 if (t - 2) % TPB else 1
                            act.wait_ge(t_out, t - 1)
                            if t >= 3:
                                act.wait_ge(o_out, t - 2)
                            act.activation(PT[:, 0:2, lo:2, :], psT[:, 0:2, lo:2, :], ACT.Copy).then_inc(t_in, 1)
                        if t < NT:
                            lo = 0 if t % TPB else P
                            act.wait_ge(maxed, t + 1)
                            for h in range(LH):
                                act.activation(Pm[:, t % 2, h, lo:2 * P], psS[:, t % 2, h, lo:2 * P], ACT.Exp,
                                               bias=nmax[:, t % 2, h:h + 1], accum_out=rsum[:, t % 4, h:h + 1])\
                                    .then_inc(expd, 1)

                @block.vector
                def _(dve):
                    for t in range(NT + 3):
                        if 2 <= t < NT + 2:
                            lo = 0 if (t - 2) % TPB else 1
                            dve.wait_ge(t_out, t - 1)
                            if t >= 3:
                                dve.wait_ge(o_out, t - 2)
                            dve.tensor_copy(PT[:, 2:4, lo:2, :], psT[:, 2:4, lo:2, :]).then_inc(t_in2, 1)
                        if t >= 3:
                            if t >= 4:
                                dve.wait_ge(o_in, t - 3)
                            dve.reciprocal(rinv[:, :], rsum[:, (t - 3) % 4, :]).then_inc(inv, 1)
                            dve.wait_ge(inv, t - 2)
                            dve.wait_ge(o_out, t - 2)
                            dve.tensor_tensor(O[:, t - 3, 0:LW].rearrange("p (h d) -> p h d", h=LH), psO[:, :, :],
                                              rinv[:, :].unsqueeze(2).to_broadcast([P, LH, HD]), ALU.mult)\
                                .then_inc(o_in, 1)
                        if t < NT:
                            lo = 0 if t % TPB else P
                            dve.wait_ge(s_out, t + 1)
                            if t >= 2:
                                dve.wait_ge(expd, LH * (t - 1))
                            dve.tensor_reduce(nmax[:, t % 2, :], psS[:, t % 2, :, lo:2 * P], AX.X, ALU.max,
                                              negate=True).then_inc(maxed, 1)

            rows_to_columns(nc, name + "_ot", O, OT, C.ident)
            columns_out(nc, name + "_o", OT, None, Y, None, held=(wo, bo))
            layer_norm(nc, name + "_ln2", Y, None, row("ln2_g"), row("ln2_b"), dst_cols=xc, ident=C.ident,
                       ahead=((w1[:, :], matrix("W1")), (b1[:, :], matrix("b1")),
                              (w2[:, :, :], matrix("W2").rearrange("(c p) n -> p c n", p=P)),
                              (b2[:, :], row_to_all(row("b2"), D))))
            with Stage(nc, name + "_ffn") as st:
                ps = st.ps("ps", [P, 4, N])
                h_out, h_in = (st.sem(x) for x in ("h_out", "h_in"))
                block = st.block()

                @block.tensor
                def _(pe):
                    for k in range(FCH * B):
                        c, b = k // B, k % B
                        if k >= 4:
                            pe.wait_ge(h_in, k - 3)
                        pe.matmul(ps[:, k % 4, :], w1[:, c * P:(c + 1) * P], xc[:, b * N:(b + 1) * N],
                                  start=True, stop=True).then_inc(h_out, 1)

                @block.scalar
                def _(act):
                    load_table(act, st, ACT.Gelu, xc[:, 0:1])
                    for k in range(FCH * B):
                        c, b = k // B, k % B
                        act.wait_ge(h_out, k + 1)
                        act.activation(hid[:, c, b * N:(b + 1) * N], ps[:, k % 4, :], ACT.Gelu, bias=b1[:, c:c + 1])\
                            .then_inc(h_in, 1)

            columns_out(nc, name + "_o2", hid, None, Y, None, K=FCH, held=(w2, b2))


def add_rows(nc, name, src, dst):
    with Stage(nc, name) as st:
        block = st.block()

        @block.vector
        def _(dve):
            dve.tensor_tensor(dst[:, :, :], dst[:, :, :], src[:, :, :], ALU.add)


class Constants:

    def __init__(self, nc, ctx, I):
        def sb(n, shape, dt=F32):
            return ctx.enter_context(nc.sbuf_tensor(n, shape, dt))
        self.ident = sb("ident", [P, P])
        self.flip = sb("flip", [P, P])
        self.identb = sb("identb", [P, P], BF16)
        self.ones = sb("ones", [P, P])
        self.upto = sb("upto", [P, P])
        self.desc = sb("desc", [P, E])
        self.trib = sb("trib", [P, P], BF16)
        self.mask_bf1 = sb("mask_bf1", [P, TOK])
        self.mask_bk0 = sb("mask_bk0", [P, TOK])
        masks = (("mask_BxS_bf1", self.mask_bf1), ("mask_BxS_bk0", self.mask_bk0))
        with Stage(nc, "consts") as st:
            raw = st.sb("raw", [P, 2, TOK], U8)
            desci = st.sb("desci", [P, E], I32)
            loaded, cleared = (st.sem(x) for x in ("loaded", "cleared"))
            block = st.block()

            @block.sync
            def _(sp):
                for n, (m, _) in enumerate(masks):
                    for p in (0, DH):
                        sp.dma_start(raw[p:p + 1, n, :], dram_view(I[m], 0, [[TOK, 1], [1, TOK]]))\
                            .then_inc(loaded, 16)

            @block.gpsimd
            def _(pool):
                for m, v in ((self.ident, 0.0), (self.identb, 0.0), (self.trib, 0.0), (self.flip, 0.0), (self.ones, 1.0),
                             (self.upto, 1.0)):
                    pool.memset(m[:, :], v).then_inc(cleared, 1)
                pool.iota(desci[:, :], pattern=[[-1, E]], base=E, channel_multiplier=0).then_inc(cleared, 1)
                pool.wait_ge(cleared, 7)
                pool.affine_select(out=self.upto[:, :], in_=self.upto[:, :], compare_op=ALU.is_ge, fill=0.0,
                                   base=0, pattern=[[1, P]], channel_multiplier=-1)
                for m in (self.ident, self.identb):
                    pool.affine_select(out=m[:, :], in_=m[:, :], compare_op=ALU.not_equal, fill=1.0, base=0,
                                       pattern=[[-1, P]], channel_multiplier=1)
                pool.affine_select(out=self.flip[:, :], in_=self.flip[:, :], compare_op=ALU.not_equal, fill=1.0,
                                   base=-(P - 1), pattern=[[1, P]], channel_multiplier=1)
                pool.affine_select(out=self.trib[:, :], in_=self.trib[:, :], compare_op=ALU.is_ge, fill=NEG,
                                   base=0, pattern=[[-1, P]], channel_multiplier=1)

            @block.vector
            def _(dve):
                dve.wait_ge(cleared, 7)
                dve.tensor_copy(self.desc[:, :], desci[:, :])
                dve.wait_ge(loaded, 64)
                for n, (_, m) in enumerate(masks):
                    for p in (0, DH):
                        dve.tensor_scalar(m[p:p + 1, :], raw[p:p + 1, n, :], 1.0, -NEG, ALU.subtract, ALU.mult)


def load_rows(nc, name, x, X):
    with Stage(nc, name) as st:
        loaded = st.sem("loaded")
        block = st.block()

        @block.sync
        def _(sp):
            sp.dma_start(X[:, :, :], x.rearrange("(t p) d -> p t d", p=P)).then_inc(loaded, 16)
            sp.wait_ge(loaded, 16)


def store_rows(nc, name, X, out):
    with Stage(nc, name) as st:
        stored = st.sem("stored")
        block = st.block()

        @block.sync
        def _(sp):
            sp.dma_start(out.rearrange("(t p) d -> p t d", p=P), X[:, :, :]).then_inc(stored, 16)
            sp.wait_ge(stored, 16)


def program(nc, I, out):
    Stage.cleared = []
    with ExitStack() as ctx:
        def sb(n, shape, dt=F32):
            return ctx.enter_context(nc.sbuf_tensor(n, shape, dt))
        C = Constants(nc, ctx, I)
        X = sb("X", [P, NT, D])
        Y = sb("Y", [P, NT, D])
        cols = sb("cols", [P, TOK])
        Z = sb("Z", [P, TOK])
        scratch = nc.dram_tensor("bias_table", (HEADS, TOEP), F32, kind="Internal").ap()
        c_scratch = nc.dram_tensor("expert_weights", (E, TOK), F32, kind="Internal").ap()

        load_rows(nc, "load_x", I["x"], X)
        cosine_attention(nc, "l0c", I, "L0_cond_", X, Y, C, scratch)
        distance_attention(nc, "l0a", I, "L0_attn_", Y, X, C, scratch)
        biased_attention(nc, "l0b", I, "L0_cond2_", X, Y, cols, C)
        rerouted_experts(nc, "l0f", I, "L0_ffn_", cols, Z, C)
        add_columns(nc, "l0s", Z, X, C.ident)
        rows_to_columns(nc, "l0t", X, cols, C.ident)
        grouped_experts(nc, "l1c", I, "L1_cond_", cols, Z, C)
        linear_attention(nc, "l1a", I, "L1_attn_", Z, X, C)
        biased_attention(nc, "l1b", I, "L1_cond2_", X, Y, cols, C)
        phase_ffn(nc, "l1f", I, "L1_ffn_", cols, X, C)
        rows_to_columns(nc, "l1t", X, cols, C.ident)
        grouped_experts(nc, "l2c", I, "L2_cond_", cols, Z, C)
        windowed_attention(nc, "l2a", I, "L2_attn_", Z, X, C)
        rows_to_columns(nc, "l2t", X, cols, C.ident)
        grouped_experts(nc, "l2b", I, "L2_cond2_", cols, Z, C)
        with ExitStack() as inner:
            cT = inner.enter_context(nc.sbuf_tensor("l2f_cT", [E, TOK], F32))
            route(nc, "l2f_r", Z, I["L2_ffn_Wr"], C, cT, softmax=False, bias=I["L2_ffn_br"], top=1)
            expert_mlps(nc, "l2f_x", Z, I["L2_ffn_W1"], I["L2_ffn_b1"], I["L2_ffn_W2"], I["L2_ffn_b2"],
                        ACT.Relu, cT, c_scratch, cols)
        add_columns(nc, "l2s", cols, X, C.ident)
        rows_to_columns(nc, "l2u", X, cols, C.ident)
        grouped_experts(nc, "l3c", I, "L3_cond_", cols, Z, C)
        add_columns(nc, "l3s", Z, Y, C.ident, add=False)
        layered_attention(nc, "l3a", I, "L3_attn_", Y, C)
        add_rows(nc, "l3r", Y, X)
        cosine_attention(nc, "l3b", I, "L3_cond2_", X, Y, C, scratch)
        rows_to_columns(nc, "l3t", Y, cols, C.ident)
        with ExitStack() as inner:
            cT = inner.enter_context(nc.sbuf_tensor("l3f_cT", [E, TOK], F32))
            route(nc, "l3f_r", cols, I["L3_ffn_router_w"], C, cT, bias=I["L3_ffn_router_b"],
                  capacity=-(-TOK * 5 // (E * 4)))
            expert_mlps(nc, "l3f_x", cols, I["L3_ffn_w1"], I["L3_ffn_b1"], I["L3_ffn_w2"], I["L3_ffn_b2"],
                        ACT.Gelu, cT, c_scratch, Z)
        add_columns(nc, "l3v", Z, X, C.ident)
        store_rows(nc, "store", X, out)


LAYOUT = {
    "x": lambda a: a.reshape(TOK, D),
    "L0_attn_Wq": lambda a: a.T, "L0_attn_Wk": lambda a: a.T, "L0_attn_Wv": lambda a: a.T,
    "L0_attn_Wo": lambda a: a.T,
    "L0_attn_rel": lambda a: a[:, ::-1],
    "L0_ffn_gate_weight": lambda a: a.T,
    "L0_ffn_down": lambda a: a.transpose(0, 2, 1).reshape(E * P, D),
    "L0_ffn_gate": lambda a: a[:, :P, :].transpose(2, 0, 1).reshape(D, E * P),
    "L0_ffn_up": lambda a: a[:, P:, :].transpose(2, 0, 1).reshape(D, E * P),
    "cond_64_T": lambda a: a.T,
}
for _p in ("L1_cond_", "L2_cond_", "L2_cond2_", "L3_cond_"):
    LAYOUT.update({
        _p + "wt": lambda a: a.T, _p + "wg": lambda a: a.T,
        _p + "w_gate": lambda a: a.transpose(1, 0, 2).reshape(D, E * DH),
        _p + "w_up": lambda a: a.transpose(1, 0, 2).reshape(D, E * DH),
        _p + "w_down": lambda a: a.reshape(E * DH, D),
    })
for _v in ("b1", "quantum_phases", "quantum_weights_real", "quantum_weights_imag"):
    LAYOUT["L1_ffn_" + _v] = lambda a: a.reshape(-1, P).T
LAYOUT.update({
    "L2_attn_bq": lambda a: a.reshape(4, 4, 8).transpose(1, 2, 0),
    "L2_attn_bk": lambda a: a.reshape(2, 8).T,
    "L2_ffn_Wr": lambda a: a.T,
    "L2_ffn_W1": lambda a: a.transpose(0, 2, 1),
    "L2_ffn_W2": lambda a: a.transpose(0, 2, 1),
    "L2_ffn_b1": lambda a: a.reshape(E, -1, P).transpose(0, 2, 1),
    "L3_ffn_b1": lambda a: a.reshape(E, -1, P).transpose(0, 2, 1),
    "L3_attn_b1": lambda a: a.reshape(a.shape[0], -1, P).transpose(0, 2, 1),
})
PIECES = {"L0_ffn_gate_up_proj": ("L0_ffn_gate", "L0_ffn_up"), "L0_ffn_down_proj": ("L0_ffn_down",),
          "cond_64": ("cond_64", "cond_64_T")}


def kernel(**inputs):
    import numpy as _np
    import concourse.bacc as _bacc
    from concourse import mybir as _mybir
    from concourse.bass_utils import run_bass_kernel_spmd as _run

    nc = _bacc.Bacc("TRN2", target_bir_lowering=False, num_devices=1)
    arrays, I = {}, {}
    pieces = [(piece, a) for name, a in inputs.items() for piece in PIECES.get(name, (name,))]
    for name, a in pieces:
        a = _np.asarray(a)
        a = _np.ascontiguousarray(LAYOUT[name](a) if name in LAYOUT else a)
        arrays[f"in_{name}"] = a
        I[name] = nc.dram_tensor(f"in_{name}", a.shape, _mybir.dt.from_np(a.dtype), kind="ExternalInput").ap()
    out = nc.dram_tensor("out_0_dram", (TOK, D), _mybir.dt.float32, kind="ExternalOutput").ap()
    program(nc, I, out)
    r = _run(nc, [arrays], core_ids=[0])
    return r.results[0]["out_0_dram"].reshape(B, N, D)
```
